# Optimizing a Trainium2 kernel written in Bass

```python
import numpy as np
import jax
import jax.numpy as jnp

def _softmax(x, axis=-1):
    return jax.nn.softmax(x, axis=axis)

def _gelu(x):
    return jax.nn.gelu(x, approximate=True)

def _silu(x):
    return jax.nn.silu(x)

def _sigmoid(x):
    return jax.nn.sigmoid(x)

def _layernorm(x, axis=-1, eps=1e-05):
    m = jnp.mean(x, axis=axis, keepdims=True)
    v = jnp.var(x, axis=axis, keepdims=True)
    return (x - m) / jnp.sqrt(v + eps)

def _scatter_add(tgt, idx, src, axis=0):
    return tgt.at[idx].add(src)

def _segment_sum(src, seg, n):
    return jax.ops.segment_sum(src, seg, n)
kernel_name = 'mk_seq_preln_d4_jaxref_r8_63116b'

def setup_inputs(seed: int=0):
    np.random.seed(seed)
    _w = jnp.asarray

    def _L0_attn_setup():
        import jax, jax.numpy as jnp
        import numpy as np
        D_MODEL = 128
        NUM_HEADS = 16
        HEAD_DIM = D_MODEL // NUM_HEADS
        key = jax.random.key(seed)
        ks = jax.random.split(key, 7)
        B, T, C = (4, 256, D_MODEL)
        s = 1.0 / np.sqrt(C)
        return {'x': jax.random.normal(ks[0], (B, T, C), dtype=jnp.float32), 'ln_gamma': jnp.ones((C,), dtype=jnp.float32), 'ln_beta': jnp.zeros((C,), dtype=jnp.float32), 'w_qkv': jax.random.normal(ks[1], (C, 3 * C), dtype=jnp.float32) * s, 'b_qkv': jnp.zeros((3 * C,), dtype=jnp.float32), 'w_out': jax.random.normal(ks[2], (C, C), dtype=jnp.float32) * s, 'b_out': jnp.zeros((C,), dtype=jnp.float32)}
    _L0_attn_in = _L0_attn_setup()

    def _L0_ffn_setup():
        import jax, jax.numpy as jnp
        import numpy as np
        EPS = 1e-05
        N_HEADS = 16
        TOP_K = 2

        def _ln(x, g, b):
            m = x.mean(-1, keepdims=True)
            v = ((x - m) ** 2).mean(-1, keepdims=True)
            return (x - m) / jnp.sqrt(v + EPS) * g + b

        def _block_fwd(x, ln1_g, ln1_b, ln2_g, ln2_b, Wq, bq, Wk, bk, Wv, bv, Wo, bo, Wr, br, e_w1, e_b1, e_w2, e_b2):
            B, S, D = x.shape
            H = N_HEADS
            hd = D // H
            h = _ln(x, ln1_g, ln1_b)
            q = (h @ Wq + bq).reshape(B, S, H, hd).transpose(0, 2, 1, 3)
            k = (h @ Wk + bk).reshape(B, S, H, hd).transpose(0, 2, 1, 3)
            v = (h @ Wv + bv).reshape(B, S, H, hd).transpose(0, 2, 1, 3)
            scores = jnp.einsum('bhqd,bhkd->bhqk', q, k) / hd ** 0.5
            causal = jnp.tril(jnp.ones((S, S), dtype=bool))
            scores = jnp.where(causal, scores, -jnp.inf)
            attn = jax.nn.softmax(scores, axis=-1)
            o = jnp.einsum('bhqk,bhkd->bhqd', attn, v).transpose(0, 2, 1, 3).reshape(B, S, D)
            a = o @ Wo + bo + x
            h2 = _ln(a, ln2_g, ln2_b)
            logits = h2 @ Wr + br
            topv = jax.lax.top_k(logits, TOP_K)[0]
            kmask = logits >= topv[..., -1:]
            w = jax.nn.softmax(jnp.where(kmask, logits, -jnp.inf), axis=-1)
            mid = jax.nn.gelu(jnp.einsum('bsd,edf->bsef', h2, e_w1) + e_b1, approximate=False)
            eo = jnp.einsum('bsef,efd->bsed', mid, e_w2) + e_b2
            moe = jnp.einsum('bse,bsed->bsd', w, eo)
            return moe + a
        key = jax.random.key(seed)
        B, S, D, E = (1, 256, 128, 8)
        F = 4 * D
        ks = jax.random.split(key, 8)

        def n(k, shape):
            return jax.random.normal(k, shape, jnp.float32) * 0.02
        return dict(x=jax.random.normal(ks[0], (B, S, D), jnp.float32), ln1_g=jnp.ones((D,), jnp.float32), ln1_b=jnp.zeros((D,), jnp.float32), ln2_g=jnp.ones((D,), jnp.float32), ln2_b=jnp.zeros((D,), jnp.float32), Wq=n(ks[1], (D, D)), bq=jnp.zeros((D,), jnp.float32), Wk=n(ks[2], (D, D)), bk=jnp.zeros((D,), jnp.float32), Wv=n(ks[3], (D, D)), bv=jnp.zeros((D,), jnp.float32), Wo=n(ks[4], (D, D)), bo=jnp.zeros((D,), jnp.float32), Wr=n(ks[5], (D, E)), br=jnp.zeros((E,), jnp.float32), e_w1=n(ks[6], (E, D, F)), e_b1=jnp.zeros((E, F), jnp.float32), e_w2=n(ks[7], (E, F, D)), e_b2=jnp.zeros((E, D), jnp.float32))
    _L0_ffn_in = _L0_ffn_setup()

    def _L1_attn_setup():
        import jax, jax.numpy as jnp
        import numpy as np
        BATCH, L, D_MODEL = (2, 128, 128)
        D_STATE, D_CONV, EXPAND = (16, 4, 2)
        D_INNER = EXPAND * D_MODEL
        DT_RANK = max(1, -(-D_MODEL // 16))

        def _forward(x, W_in, conv_w, conv_b, W_x, W_dt, b_dt, A_log, D, W_out):
            xv = x @ W_in
            xc = jnp.transpose(xv, (0, 2, 1))
            xc = jax.lax.conv_general_dilated(xc, conv_w, window_strides=(1,), padding=[(D_CONV - 1, 0)], dimension_numbers=('NCH', 'OIH', 'NCH'), feature_group_count=D_INNER)
            xv = jnp.transpose(xc, (0, 2, 1)) + conv_b
            xv = jax.nn.silu(xv)
            ssm = xv @ W_x
            dt_raw = ssm[..., :DT_RANK]
            Bp = ssm[..., DT_RANK:DT_RANK + D_STATE]
            Cp = ssm[..., DT_RANK + D_STATE:]
            delta = jax.nn.softplus(dt_raw @ W_dt + b_dt)
            A = -jnp.exp(A_log)
            dA = jnp.exp(delta[..., None] * A)
            dBx = delta[..., None] * Bp[:, :, None, :] * xv[..., None]

            def comb(c1, c2):
                a1, b1 = c1
                a2, b2 = c2
                return (a1 * a2, a2 * b1 + b2)
            _, h = jax.lax.associative_scan(comb, (dA, dBx), axis=1)
            y = jnp.einsum('bldn,bln->bld', h, Cp)
            y = y + xv * D
            return y @ W_out
        key = jax.random.key(seed)
        ks = jax.random.split(key, 10)
        s = 0.02
        x = jax.random.normal(ks[0], (BATCH, L, D_MODEL), jnp.float32)
        W_in = jax.random.normal(ks[1], (D_MODEL, D_INNER), jnp.float32) * s
        conv_w = jax.random.normal(ks[2], (D_INNER, 1, D_CONV), jnp.float32) * s
        conv_b = jax.random.normal(ks[3], (D_INNER,), jnp.float32) * s
        W_x = jax.random.normal(ks[4], (D_INNER, DT_RANK + 2 * D_STATE), jnp.float32) * s
        W_dt = jax.random.normal(ks[5], (DT_RANK, D_INNER), jnp.float32) * s
        b_dt = jax.random.normal(ks[6], (D_INNER,), jnp.float32) * s
        A_log = jnp.log(jnp.broadcast_to(jnp.arange(1, D_STATE + 1, dtype=jnp.float32), (D_INNER, D_STATE)))
        D = jnp.ones((D_INNER,), jnp.float32)
        W_out = jax.random.normal(ks[7], (D_INNER, D_MODEL), jnp.float32) * s
        return {'x': x, 'W_in': W_in, 'conv_w': conv_w, 'conv_b': conv_b, 'W_x': W_x, 'W_dt': W_dt, 'b_dt': b_dt, 'A_log': A_log, 'D': D, 'W_out': W_out}
    _L1_attn_in = _L1_attn_setup()

    def _L1_ffn_setup():
        import jax, jax.numpy as jnp
        import numpy as np
        THRESH_FACTOR = 0.7

        def ternary_quantize(w):
            delta = THRESH_FACTOR * jnp.mean(jnp.abs(w))
            return jnp.where(w > delta, 1.0, jnp.where(w < -delta, -1.0, 0.0)).astype(w.dtype)
        key = jax.random.key(seed)
        k1, k2, k3 = jax.random.split(key, 3)
        B, S, D_IN, D_OUT = (8, 512, 128, 128)
        inp = {'input': jax.random.normal(k1, (B, S, D_IN), dtype=jnp.float32), 'weight': jax.random.normal(k2, (D_OUT, D_IN), dtype=jnp.float32) * (1.0 / np.sqrt(D_IN)), 'alpha': jnp.ones((1,), dtype=jnp.float32), 'bias': jax.random.normal(k3, (D_OUT,), dtype=jnp.float32) * (1.0 / np.sqrt(D_IN))}
        return inp
    _L1_ffn_in = _L1_ffn_setup()

    def _L2_attn_setup():
        import jax, jax.numpy as jnp
        import numpy as np
        import math
        H = 16
        EPS = 1e-06

        def _apply_kernel(x, orf):
            m, d_k = orf.shape
            proj = jnp.einsum('bhld,md->bhlm', x, orf) / d_k ** 0.25
            norm = jnp.sum(x * x, axis=-1, keepdims=True) / (2.0 * math.sqrt(d_k))
            return (jnp.exp(proj - norm) + EPS) / math.sqrt(m)
        key = jax.random.key(seed)
        ks = jax.random.split(key, 10)
        B, L, D, m = (4, 512, 128, 32)
        d_k = D // H
        s = 1.0 / math.sqrt(D)
        return {'x': jax.random.normal(ks[0], (B, L, D), jnp.float32), 'Wq': jax.random.normal(ks[1], (D, D), jnp.float32) * s, 'bq': jax.random.normal(ks[2], (D,), jnp.float32) * s, 'Wk': jax.random.normal(ks[3], (D, D), jnp.float32) * s, 'bk': jax.random.normal(ks[4], (D,), jnp.float32) * s, 'Wv': jax.random.normal(ks[5], (D, D), jnp.float32) * s, 'bv': jax.random.normal(ks[6], (D,), jnp.float32) * s, 'Wo': jax.random.normal(ks[7], (D, D), jnp.float32) * s, 'bo': jax.random.normal(ks[8], (D,), jnp.float32) * s, 'orf': jax.random.normal(ks[9], (m, d_k), jnp.float32)}
    _L2_attn_in = _L2_attn_setup()

    def _L2_ffn_setup():
        import jax, jax.numpy as jnp
        import numpy as np
        H = 16
        TOP_K = 2
        LN_EPS = 1e-05
        key = jax.random.key(seed)
        ks = jax.random.split(key, 8)
        B, S, E, NE = (2, 128, 128, 8)
        w = lambda k, shp: jax.random.normal(k, shp, dtype=jnp.float32) * 0.02
        return {'x': jax.random.normal(ks[0], (B, S, E), dtype=jnp.float32), 'rW1': w(ks[1], (E // 2, E)), 'rb1': jnp.zeros((E // 2,), jnp.float32), 'ln_g': jnp.ones((E // 2,), jnp.float32), 'ln_b': jnp.zeros((E // 2,), jnp.float32), 'rW2': w(ks[2], (NE, E // 2)), 'rb2': jnp.zeros((NE,), jnp.float32), 'qW': w(ks[3], (NE, E, E)), 'qb': jnp.zeros((NE, E), jnp.float32), 'kW': w(ks[4], (NE, E, E)), 'kb': jnp.zeros((NE, E), jnp.float32), 'vW': w(ks[5], (NE, E, E)), 'vb': jnp.zeros((NE, E), jnp.float32), 'oW': w(ks[6], (NE, E, E)), 'ob': jnp.zeros((NE, E), jnp.float32)}
    _L2_ffn_in = _L2_ffn_setup()

    def _L3_attn_setup():
        import jax, jax.numpy as jnp
        import numpy as np
        key = jax.random.key(seed)
        ks = jax.random.split(key, 8)
        B, L, D, N, K = (4, 512, 128, 64, 4)
        return {'x': jax.random.normal(ks[0], (B, L, D), dtype=jnp.float32), 'conv_w': jax.random.normal(ks[1], (K, 1, D), dtype=jnp.float32) * 0.1, 'conv_b': jnp.zeros((D,), dtype=jnp.float32), 'Wp': jax.random.normal(ks[2], (D, 2 * N), dtype=jnp.float32) * (1.0 / np.sqrt(D)), 'bp': jnp.zeros((2 * N,), dtype=jnp.float32), 'Ws': jax.random.normal(ks[3], (D, N), dtype=jnp.float32) * (1.0 / np.sqrt(D)), 'bs': jnp.zeros((N,), dtype=jnp.float32), 'A_log': jax.random.normal(ks[4], (N,), dtype=jnp.float32) * 0.02, 'dt_log': jax.random.normal(ks[5], (N,), dtype=jnp.float32) * 0.02, 'Wo': jax.random.normal(ks[6], (N, D), dtype=jnp.float32) * (1.0 / np.sqrt(N)), 'bo': jnp.zeros((D,), dtype=jnp.float32)}
    _L3_attn_in = _L3_attn_setup()

    def _L3_ffn_setup():
        import jax, jax.numpy as jnp
        import numpy as np
        H = 128
        I = 512
        E = 4
        LN_EPS = 1e-12

        def _layer_norm(x, gamma, beta, eps=LN_EPS):
            mu = jnp.mean(x, axis=-1, keepdims=True)
            var = jnp.mean(jnp.square(x - mu), axis=-1, keepdims=True)
            return (x - mu) * jax.lax.rsqrt(var + eps) * gamma + beta
        key = jax.random.key(seed)
        ks = jax.random.split(key, 8)
        B, S = (4, 64)
        scale = 0.02
        return {'hidden_states': jax.random.normal(ks[0], (B, S, H), jnp.float32), 'W_router': jax.random.normal(ks[1], (H, E), jnp.float32) * scale, 'W1': jax.random.normal(ks[2], (E, H, I), jnp.float32) * scale, 'b1': jax.random.normal(ks[3], (E, I), jnp.float32) * scale, 'Wo': jax.random.normal(ks[4], (I, H), jnp.float32) * scale, 'bo': jax.random.normal(ks[5], (H,), jnp.float32) * scale, 'ln_gamma': jnp.ones((H,), jnp.float32), 'ln_beta': jnp.zeros((H,), jnp.float32)}
    _L3_ffn_in = _L3_ffn_setup()
    _d = {'L0_attn_x': _L0_attn_in['x'], 'L0_attn_ln_gamma': _L0_attn_in['ln_gamma'], 'L0_attn_ln_beta': _L0_attn_in['ln_beta'], 'L0_attn_w_qkv': _L0_attn_in['w_qkv'], 'L0_attn_b_qkv': _L0_attn_in['b_qkv'], 'L0_attn_w_out': _L0_attn_in['w_out'], 'L0_attn_b_out': _L0_attn_in['b_out'], 'L0_ffn_ln1_g': _L0_ffn_in['ln1_g'], 'L0_ffn_ln1_b': _L0_ffn_in['ln1_b'], 'L0_ffn_ln2_g': _L0_ffn_in['ln2_g'], 'L0_ffn_ln2_b': _L0_ffn_in['ln2_b'], 'L0_ffn_Wq': _L0_ffn_in['Wq'], 'L0_ffn_bq': _L0_ffn_in['bq'], 'L0_ffn_Wk': _L0_ffn_in['Wk'], 'L0_ffn_bk': _L0_ffn_in['bk'], 'L0_ffn_Wv': _L0_ffn_in['Wv'], 'L0_ffn_bv': _L0_ffn_in['bv'], 'L0_ffn_Wo': _L0_ffn_in['Wo'], 'L0_ffn_bo': _L0_ffn_in['bo'], 'L0_ffn_Wr': _L0_ffn_in['Wr'], 'L0_ffn_br': _L0_ffn_in['br'], 'L0_ffn_e_w1': _L0_ffn_in['e_w1'], 'L0_ffn_e_b1': _L0_ffn_in['e_b1'], 'L0_ffn_e_w2': _L0_ffn_in['e_w2'], 'L0_ffn_e_b2': _L0_ffn_in['e_b2'], 'L1_attn_W_in': _L1_attn_in['W_in'], 'L1_attn_conv_w': _L1_attn_in['conv_w'], 'L1_attn_conv_b': _L1_attn_in['conv_b'], 'L1_attn_W_x': _L1_attn_in['W_x'], 'L1_attn_W_dt': _L1_attn_in['W_dt'], 'L1_attn_b_dt': _L1_attn_in['b_dt'], 'L1_attn_A_log': _L1_attn_in['A_log'], 'L1_attn_D': _L1_attn_in['D'], 'L1_attn_W_out': _L1_attn_in['W_out'], 'L1_ffn_weight': _L1_ffn_in['weight'], 'L1_ffn_alpha': _L1_ffn_in['alpha'], 'L1_ffn_bias': _L1_ffn_in['bias'], 'L2_attn_Wq': _L2_attn_in['Wq'], 'L2_attn_bq': _L2_attn_in['bq'], 'L2_attn_Wk': _L2_attn_in['Wk'], 'L2_attn_bk': _L2_attn_in['bk'], 'L2_attn_Wv': _L2_attn_in['Wv'], 'L2_attn_bv': _L2_attn_in['bv'], 'L2_attn_Wo': _L2_attn_in['Wo'], 'L2_attn_bo': _L2_attn_in['bo'], 'L2_attn_orf': _L2_attn_in['orf'], 'L2_ffn_rW1': _L2_ffn_in['rW1'], 'L2_ffn_rb1': _L2_ffn_in['rb1'], 'L2_ffn_ln_g': _L2_ffn_in['ln_g'], 'L2_ffn_ln_b': _L2_ffn_in['ln_b'], 'L2_ffn_rW2': _L2_ffn_in['rW2'], 'L2_ffn_rb2': _L2_ffn_in['rb2'], 'L2_ffn_qW': _L2_ffn_in['qW'], 'L2_ffn_qb': _L2_ffn_in['qb'], 'L2_ffn_kW': _L2_ffn_in['kW'], 'L2_ffn_kb': _L2_ffn_in['kb'], 'L2_ffn_vW': _L2_ffn_in['vW'], 'L2_ffn_vb': _L2_ffn_in['vb'], 'L2_ffn_oW': _L2_ffn_in['oW'], 'L2_ffn_ob': _L2_ffn_in['ob'], 'L3_attn_conv_w': _L3_attn_in['conv_w'], 'L3_attn_conv_b': _L3_attn_in['conv_b'], 'L3_attn_Wp': _L3_attn_in['Wp'], 'L3_attn_bp': _L3_attn_in['bp'], 'L3_attn_Ws': _L3_attn_in['Ws'], 'L3_attn_bs': _L3_attn_in['bs'], 'L3_attn_A_log': _L3_attn_in['A_log'], 'L3_attn_dt_log': _L3_attn_in['dt_log'], 'L3_attn_Wo': _L3_attn_in['Wo'], 'L3_attn_bo': _L3_attn_in['bo'], 'L3_ffn_W_router': _L3_ffn_in['W_router'], 'L3_ffn_W1': _L3_ffn_in['W1'], 'L3_ffn_b1': _L3_ffn_in['b1'], 'L3_ffn_Wo': _L3_ffn_in['Wo'], 'L3_ffn_bo': _L3_ffn_in['bo'], 'L3_ffn_ln_gamma': _L3_ffn_in['ln_gamma'], 'L3_ffn_ln_beta': _L3_ffn_in['ln_beta']}
    _x0 = _d['L0_attn_x']
    _d['L0_attn_x'] = jax.random.normal(jax.random.fold_in(jax.random.key(seed), 1), (1, 2048, 128), dtype=_x0.dtype)
    del _x0
    return _d

def reference(L0_attn_x, L0_attn_ln_gamma, L0_attn_ln_beta, L0_attn_w_qkv, L0_attn_b_qkv, L0_attn_w_out, L0_attn_b_out, L0_ffn_ln1_g, L0_ffn_ln1_b, L0_ffn_ln2_g, L0_ffn_ln2_b, L0_ffn_Wq, L0_ffn_bq, L0_ffn_Wk, L0_ffn_bk, L0_ffn_Wv, L0_ffn_bv, L0_ffn_Wo, L0_ffn_bo, L0_ffn_Wr, L0_ffn_br, L0_ffn_e_w1, L0_ffn_e_b1, L0_ffn_e_w2, L0_ffn_e_b2, L1_attn_W_in, L1_attn_conv_w, L1_attn_conv_b, L1_attn_W_x, L1_attn_W_dt, L1_attn_b_dt, L1_attn_A_log, L1_attn_D, L1_attn_W_out, L1_ffn_weight, L1_ffn_alpha, L1_ffn_bias, L2_attn_Wq, L2_attn_bq, L2_attn_Wk, L2_attn_bk, L2_attn_Wv, L2_attn_bv, L2_attn_Wo, L2_attn_bo, L2_attn_orf, L2_ffn_rW1, L2_ffn_rb1, L2_ffn_ln_g, L2_ffn_ln_b, L2_ffn_rW2, L2_ffn_rb2, L2_ffn_qW, L2_ffn_qb, L2_ffn_kW, L2_ffn_kb, L2_ffn_vW, L2_ffn_vb, L2_ffn_oW, L2_ffn_ob, L3_attn_conv_w, L3_attn_conv_b, L3_attn_Wp, L3_attn_bp, L3_attn_Ws, L3_attn_bs, L3_attn_A_log, L3_attn_dt_log, L3_attn_Wo, L3_attn_bo, L3_ffn_W_router, L3_ffn_W1, L3_ffn_b1, L3_ffn_Wo, L3_ffn_bo, L3_ffn_ln_gamma, L3_ffn_ln_beta):

    def _L0_attn_ref(x, ln_gamma, ln_beta, w_qkv, b_qkv, w_out, b_out):
        import jax, jax.numpy as jnp
        import numpy as np
        D_MODEL = 128
        NUM_HEADS = 16
        HEAD_DIM = D_MODEL // NUM_HEADS
        B, T, C = x.shape
        residual = x
        mu = jnp.mean(x, axis=-1, keepdims=True)
        var = jnp.var(x, axis=-1, keepdims=True)
        h = (x - mu) * jax.lax.rsqrt(var + 1e-05) * ln_gamma + ln_beta
        qkv = (h @ w_qkv + b_qkv).reshape(B, T, 3, NUM_HEADS, HEAD_DIM)
        qkv = jnp.transpose(qkv, (2, 0, 3, 1, 4))
        q, k, v = (qkv[0], qkv[1], qkv[2])
        scores = jnp.einsum('bhqd,bhkd->bhqk', q, k) / np.sqrt(HEAD_DIM)
        attn = jax.nn.softmax(scores, axis=-1)
        out = jnp.einsum('bhqk,bhkd->bhqd', attn, v)
        out = jnp.transpose(out, (0, 2, 1, 3)).reshape(B, T, C)
        out = out @ w_out + b_out
        return residual + out

    def _L0_ffn_ref(x, ln1_g, ln1_b, ln2_g, ln2_b, Wq, bq, Wk, bk, Wv, bv, Wo, bo, Wr, br, e_w1, e_b1, e_w2, e_b2):
        import jax, jax.numpy as jnp
        import numpy as np
        EPS = 1e-05
        N_HEADS = 16
        TOP_K = 2

        def _ln(x, g, b):
            m = x.mean(-1, keepdims=True)
            v = ((x - m) ** 2).mean(-1, keepdims=True)
            return (x - m) / jnp.sqrt(v + EPS) * g + b

        def _block_fwd(x, ln1_g, ln1_b, ln2_g, ln2_b, Wq, bq, Wk, bk, Wv, bv, Wo, bo, Wr, br, e_w1, e_b1, e_w2, e_b2):
            B, S, D = x.shape
            H = N_HEADS
            hd = D // H
            h = _ln(x, ln1_g, ln1_b)
            q = (h @ Wq + bq).reshape(B, S, H, hd).transpose(0, 2, 1, 3)
            k = (h @ Wk + bk).reshape(B, S, H, hd).transpose(0, 2, 1, 3)
            v = (h @ Wv + bv).reshape(B, S, H, hd).transpose(0, 2, 1, 3)
            scores = jnp.einsum('bhqd,bhkd->bhqk', q, k) / hd ** 0.5
            causal = jnp.tril(jnp.ones((S, S), dtype=bool))
            scores = jnp.where(causal, scores, -jnp.inf)
            attn = jax.nn.softmax(scores, axis=-1)
            o = jnp.einsum('bhqk,bhkd->bhqd', attn, v).transpose(0, 2, 1, 3).reshape(B, S, D)
            a = o @ Wo + bo + x
            h2 = _ln(a, ln2_g, ln2_b)
            logits = h2 @ Wr + br
            topv = jax.lax.top_k(logits, TOP_K)[0]
            kmask = logits >= topv[..., -1:]
            w = jax.nn.softmax(jnp.where(kmask, logits, -jnp.inf), axis=-1)
            mid = jax.nn.gelu(jnp.einsum('bsd,edf->bsef', h2, e_w1) + e_b1, approximate=False)
            eo = jnp.einsum('bsef,efd->bsed', mid, e_w2) + e_b2
            moe = jnp.einsum('bse,bsed->bsd', w, eo)
            return moe + a
        return _block_fwd(x, ln1_g, ln1_b, ln2_g, ln2_b, Wq, bq, Wk, bk, Wv, bv, Wo, bo, Wr, br, e_w1, e_b1, e_w2, e_b2)

    def _L1_attn_ref(x, W_in, conv_w, conv_b, W_x, W_dt, b_dt, A_log, D, W_out):
        import jax, jax.numpy as jnp
        import numpy as np
        BATCH, L, D_MODEL = (2, 128, 128)
        D_STATE, D_CONV, EXPAND = (16, 4, 2)
        D_INNER = EXPAND * D_MODEL
        DT_RANK = max(1, -(-D_MODEL // 16))

        def _forward(x, W_in, conv_w, conv_b, W_x, W_dt, b_dt, A_log, D, W_out):
            xv = x @ W_in
            xc = jnp.transpose(xv, (0, 2, 1))
            xc = jax.lax.conv_general_dilated(xc, conv_w, window_strides=(1,), padding=[(D_CONV - 1, 0)], dimension_numbers=('NCH', 'OIH', 'NCH'), feature_group_count=D_INNER)
            xv = jnp.transpose(xc, (0, 2, 1)) + conv_b
            xv = jax.nn.silu(xv)
            ssm = xv @ W_x
            dt_raw = ssm[..., :DT_RANK]
            Bp = ssm[..., DT_RANK:DT_RANK + D_STATE]
            Cp = ssm[..., DT_RANK + D_STATE:]
            delta = jax.nn.softplus(dt_raw @ W_dt + b_dt)
            A = -jnp.exp(A_log)
            dA = jnp.exp(delta[..., None] * A)
            dBx = delta[..., None] * Bp[:, :, None, :] * xv[..., None]

            def comb(c1, c2):
                a1, b1 = c1
                a2, b2 = c2
                return (a1 * a2, a2 * b1 + b2)
            _, h = jax.lax.associative_scan(comb, (dA, dBx), axis=1)
            y = jnp.einsum('bldn,bln->bld', h, Cp)
            y = y + xv * D
            return y @ W_out
        return _forward(x, W_in, conv_w, conv_b, W_x, W_dt, b_dt, A_log, D, W_out)

    def _L1_ffn_ref(input, weight, alpha, bias):
        import jax, jax.numpy as jnp
        import numpy as np
        THRESH_FACTOR = 0.7

        def ternary_quantize(w):
            delta = THRESH_FACTOR * jnp.mean(jnp.abs(w))
            return jnp.where(w > delta, 1.0, jnp.where(w < -delta, -1.0, 0.0)).astype(w.dtype)
        w_ternary = ternary_quantize(weight)
        w_eff = w_ternary * alpha
        out = jnp.einsum('bsd,od->bso', input, w_eff) + bias
        return out

    def _L2_attn_ref(x, Wq, bq, Wk, bk, Wv, bv, Wo, bo, orf):
        import jax, jax.numpy as jnp
        import numpy as np
        import math
        H = 16
        EPS = 1e-06

        def _apply_kernel(x, orf):
            m, d_k = orf.shape
            proj = jnp.einsum('bhld,md->bhlm', x, orf) / d_k ** 0.25
            norm = jnp.sum(x * x, axis=-1, keepdims=True) / (2.0 * math.sqrt(d_k))
            return (jnp.exp(proj - norm) + EPS) / math.sqrt(m)
        B, L, D = x.shape
        d_k = D // H

        def split(y):
            return y.reshape(B, L, H, d_k).transpose(0, 2, 1, 3)
        q = split(x @ Wq.T + bq)
        k = split(x @ Wk.T + bk)
        v = split(x @ Wv.T + bv)
        q_phi = _apply_kernel(q, orf)
        k_phi = _apply_kernel(k, orf)
        kv = jnp.einsum('bhlm,bhld->bhmd', k_phi, v)
        ksum = jnp.sum(k_phi, axis=2)
        num = jnp.einsum('bhlm,bhmd->bhld', q_phi, kv)
        den = jnp.einsum('bhlm,bhm->bhl', q_phi, ksum)
        out = num / den[..., None]
        out = out.transpose(0, 2, 1, 3).reshape(B, L, D)
        return out @ Wo.T + bo

    def _L2_ffn_ref(x, rW1, rb1, ln_g, ln_b, rW2, rb2, qW, qb, kW, kb, vW, vb, oW, ob):
        import jax, jax.numpy as jnp
        import numpy as np
        H = 16
        TOP_K = 2
        LN_EPS = 1e-05
        B, S, E = x.shape
        NE = qW.shape[0]
        Dh = E // H
        scale = 1.0 / jnp.sqrt(jnp.asarray(Dh, x.dtype))
        h = x @ rW1.T + rb1
        mu = h.mean(-1, keepdims=True)
        var = ((h - mu) ** 2).mean(-1, keepdims=True)
        h = (h - mu) * jax.lax.rsqrt(var + LN_EPS) * ln_g + ln_b
        h = jax.nn.relu(h)
        logits = h @ rW2.T + rb2
        probs = jax.nn.softmax(logits, axis=-1)
        tp, ti = jax.lax.top_k(probs, TOP_K)
        tp = tp / tp.sum(-1, keepdims=True)
        expert_mask = (jax.nn.one_hot(ti, NE, dtype=probs.dtype) * tp[..., None]).sum(-2)
        gates = jnp.moveaxis(expert_mask, -1, 0)

        def expert_step(acc, params):
            qw, qb_, kw, kb_, vw, vb_, ow, ob_, g = params
            q = (x @ qw.T + qb_).reshape(B, S, H, Dh).transpose(0, 2, 1, 3)
            k = (x @ kw.T + kb_).reshape(B, S, H, Dh).transpose(0, 2, 1, 3)
            v = (x @ vw.T + vb_).reshape(B, S, H, Dh).transpose(0, 2, 1, 3)
            scores = jnp.einsum('bhqd,bhkd->bhqk', q, k) * scale
            p = jax.nn.softmax(scores, axis=-1)
            o = jnp.einsum('bhqk,bhkd->bhqd', p, v)
            o = o.transpose(0, 2, 1, 3).reshape(B, S, E) @ ow.T + ob_
            return (acc + o * g[..., None], None)
        out, _ = jax.lax.scan(expert_step, jnp.zeros_like(x), (qW, qb, kW, kb, vW, vb, oW, ob, gates))
        return out

    def _L3_attn_ref(x, conv_w, conv_b, Wp, bp, Ws, bs, A_log, dt_log, Wo, bo):
        import jax, jax.numpy as jnp
        import numpy as np
        B, L, D = x.shape
        K = conv_w.shape[0]
        N = Ws.shape[1]
        x_pad = jnp.pad(x, ((0, 0), (K - 1, 0), (0, 0)))
        conv = conv_b + sum((x_pad[:, k:k + L, :] * conv_w[k, 0] for k in range(K)))
        proj = conv @ Wp + bp
        B_t = jax.nn.softplus(proj[..., :N])
        C_t = jnp.tanh(proj[..., N:])
        u = x @ Ws + bs
        A = -jax.nn.softplus(A_log)
        dt = jax.nn.softplus(dt_log)
        decay = 1.0 + dt * A

        def step(state, inputs):
            u_t, b_t, c_t = inputs
            state = decay * state + dt * b_t * u_t
            return (state, c_t * state)
        init = jnp.zeros((B, N), dtype=x.dtype)
        xs = tuple((jnp.swapaxes(a, 0, 1) for a in (u, B_t, C_t)))
        _, ys = jax.lax.scan(step, init, xs, unroll=4)
        y = jnp.swapaxes(ys, 0, 1)
        return y @ Wo + bo

    def _L3_ffn_ref(hidden_states, W_router, W1, b1, Wo, bo, ln_gamma, ln_beta):
        import jax, jax.numpy as jnp
        import numpy as np
        H = 128
        I = 512
        E = 4
        LN_EPS = 1e-12

        def _layer_norm(x, gamma, beta, eps=LN_EPS):
            mu = jnp.mean(x, axis=-1, keepdims=True)
            var = jnp.mean(jnp.square(x - mu), axis=-1, keepdims=True)
            return (x - mu) * jax.lax.rsqrt(var + eps) * gamma + beta
        B, S, _ = hidden_states.shape
        x = hidden_states.reshape(-1, H)
        logits = x @ W_router
        expert_idx = jnp.argmax(logits, axis=-1)
        h = jnp.einsum('th,ehi->tei', x, W1) + b1
        h = jax.nn.gelu(h, approximate=False)
        onehot = jax.nn.one_hot(expert_idx, E, dtype=x.dtype)
        intermediate = jnp.einsum('te,tei->ti', onehot, h)
        y = intermediate @ Wo + bo + x
        y = _layer_norm(y, ln_gamma, ln_beta)
        return y.reshape(B, S, H)
    x = L0_attn_x
    x = x + _L0_attn_ref(_layernorm(x, axis=-1), L0_attn_ln_gamma, L0_attn_ln_beta, L0_attn_w_qkv, L0_attn_b_qkv, L0_attn_w_out, L0_attn_b_out)
    x = x + _L0_ffn_ref(_layernorm(x, axis=-1), L0_ffn_ln1_g, L0_ffn_ln1_b, L0_ffn_ln2_g, L0_ffn_ln2_b, L0_ffn_Wq, L0_ffn_bq, L0_ffn_Wk, L0_ffn_bk, L0_ffn_Wv, L0_ffn_bv, L0_ffn_Wo, L0_ffn_bo, L0_ffn_Wr, L0_ffn_br, L0_ffn_e_w1, L0_ffn_e_b1, L0_ffn_e_w2, L0_ffn_e_b2)
    x = x + _L1_attn_ref(_layernorm(x, axis=-1), L1_attn_W_in, L1_attn_conv_w, L1_attn_conv_b, L1_attn_W_x, L1_attn_W_dt, L1_attn_b_dt, L1_attn_A_log, L1_attn_D, L1_attn_W_out)
    x = x + _L1_ffn_ref(_layernorm(x, axis=-1), L1_ffn_weight, L1_ffn_alpha, L1_ffn_bias)
    x = x + _L2_attn_ref(_layernorm(x, axis=-1), L2_attn_Wq, L2_attn_bq, L2_attn_Wk, L2_attn_bk, L2_attn_Wv, L2_attn_bv, L2_attn_Wo, L2_attn_bo, L2_attn_orf)
    x = x + _L2_ffn_ref(_layernorm(x, axis=-1), L2_ffn_rW1, L2_ffn_rb1, L2_ffn_ln_g, L2_ffn_ln_b, L2_ffn_rW2, L2_ffn_rb2, L2_ffn_qW, L2_ffn_qb, L2_ffn_kW, L2_ffn_kb, L2_ffn_vW, L2_ffn_vb, L2_ffn_oW, L2_ffn_ob)
    x = x + _L3_attn_ref(_layernorm(x, axis=-1), L3_attn_conv_w, L3_attn_conv_b, L3_attn_Wp, L3_attn_bp, L3_attn_Ws, L3_attn_bs, L3_attn_A_log, L3_attn_dt_log, L3_attn_Wo, L3_attn_bo)
    x = x + _L3_ffn_ref(_layernorm(x, axis=-1), L3_ffn_W_router, L3_ffn_W1, L3_ffn_b1, L3_ffn_Wo, L3_ffn_bo, L3_ffn_ln_gamma, L3_ffn_ln_beta)
    return x

_drawn_inputs = setup_inputs


def setup_inputs(seed=0):
    import zlib

    import numpy as np

    out = dict(_drawn_inputs(seed))
    spreads = {'L0_attn_ln_gamma': (1.0, 0.2),
     'L0_attn_ln_beta': (0.0, 0.1),
     'L0_attn_b_qkv': (0.0, 0.1),
     'L0_attn_b_out': (0.0, 0.1),
     'L0_ffn_ln1_g': (1.0, 0.2),
     'L0_ffn_ln1_b': (0.0, 0.1),
     'L0_ffn_ln2_g': (1.0, 0.2),
     'L0_ffn_ln2_b': (0.0, 0.1),
     'L0_ffn_bq': (0.0, 0.1),
     'L0_ffn_bk': (0.0, 0.1),
     'L0_ffn_bv': (0.0, 0.1),
     'L0_ffn_bo': (0.0, 0.1),
     'L0_ffn_br': (0.0, 0.1),
     'L0_ffn_e_b1': (0.0, 0.1),
     'L0_ffn_e_b2': (0.0, 0.1),
     'L1_attn_D': (1.0, 0.2),
     'L2_ffn_rb1': (0.0, 0.1),
     'L2_ffn_ln_g': (1.0, 0.2),
     'L2_ffn_ln_b': (0.0, 0.1),
     'L2_ffn_rb2': (0.0, 0.1),
     'L2_ffn_qb': (0.0, 0.1),
     'L2_ffn_kb': (0.0, 0.1),
     'L2_ffn_vb': (0.0, 0.1),
     'L2_ffn_ob': (0.0, 0.1),
     'L3_attn_conv_b': (0.0, 0.1),
     'L3_attn_bp': (0.0, 0.1),
     'L3_attn_bs': (0.0, 0.1),
     'L3_attn_bo': (0.0, 0.1),
     'L3_ffn_ln_gamma': (1.0, 0.2),
     'L3_ffn_ln_beta': (0.0, 0.1)}
    factors = {}
    for name, (base, spread) in spreads.items():
        noise = np.random.default_rng([zlib.crc32(name.encode()), seed]).standard_normal(out[name].shape)
        drawn = base * np.exp(spread * noise) if base else spread * noise
        out[name] = jnp.asarray(drawn.astype(out[name].dtype))
    for name, factor in factors.items():
        out[name] = (out[name] * factor).astype(out[name].dtype)
    return out
```

```python
import concourse.bass as bass
from concourse import mybir
from contextlib import ExitStack
import numpy as np

F32 = mybir.dt.float32
BF16 = mybir.dt.bfloat16
ALU = mybir.AluOpType
ACT = mybir.ActivationFunctionType
X = mybir.AxisListType.X

P = 128
T = 2048
NT = T // P
NC = T // 512
H = 16
HD = P // H
NPAIR = H // 2
PARTS_Q = (0, 0, 0, 1, 1, 2)
PARTS_K = (0, 1, 2, 0, 1, 0)
RUNS_K = ((0, 3), (3, 2), (5, 1))
NR = len(PARTS_Q)
ROWS = NR * HD
SCALE = HD ** -0.5
MASKED = -1e30


class Chain:

    def __init__(self, eng, sem):
        self.eng, self.sem, self.n = eng, sem, 0

    def __call__(self, ins):
        self.n += 1
        ins.then_inc(self.sem, 1)
        self.eng.wait_ge(self.sem, self.n)


class Core:

    def __init__(self, nc, ctx):
        self.nc, self.layer, self.sems = nc, "", []
        sb = self.sb
        self.x = sb(ctx, "x_residual", [P, NT, P], F32)
        self.n = sb(ctx, "x_normalised", [P, NT, P], F32)
        self.heads = sb(ctx, "heads_out", [P, NT + 1, P], F32)
        self.a = self.heads[:, 1:NT + 1, :]
        self.b = sb(ctx, "tokens_b", [P, NT, P], F32)
        self.nT = sb(ctx, "channels_n", [P, T], F32)
        self.qk = sb(ctx, "channels_qk", [P, 2, T], F32)
        self.qT, self.kT = self.qk[:, 0, :], self.qk[:, 1, :]
        self.stat = sb(ctx, "ln_stat", [P, 5, NT], F32)
        self.ident = sb(ctx, "identity", [P, P], F32)
        self.identb = sb(ctx, "identity_bf16", [P, P], BF16)
        self.ps = ctx.enter_context(nc.psum_tensor("psum", [P, 8, 512], F32))

    def sb(self, ctx, name, shape, dtype):
        return ctx.enter_context(self.nc.sbuf_tensor(f"{self.layer}{name}", shape, dtype))

    def sem(self, name):
        s = self.nc.alloc_semaphore(name=f"{self.layer}{name}")
        self.sems.append(s)
        return s

    def end_sublayer(self):
        self.nc.clear_and_free_semaphores(self.sems)
        self.sems = []
        self.nc.all_engine_barrier()


def row_view(v, n):
    return v.rearrange("(a n) -> a n", a=1).to_broadcast([P, n])


def column(v):
    return v.rearrange("(p a) -> p a", a=1)


def head_order(v):
    return v.rearrange("c (p j d) -> c j d p", p=NPAIR, j=2)


def split_heads(v):
    return v.rearrange("c (j d p) -> c j d p", p=NPAIR, j=2)


def head_column(v):
    return v.rearrange("(p j d a) -> j d p a", p=NPAIR, j=2, a=1)


def token_bcast(stat):
    return stat.unsqueeze(2).to_broadcast([P, NT, P])


def layer_norm_vector(c, dve, link, src, dst, square, var_ready, std_ready, count, eps):
    v, st = c.nc.vector, c.stat
    link(v.tensor_reduce(st[:, 0, :], src, X, ALU.add))
    link(v.tensor_scalar(st[:, 1, :], st[:, 0, :], 1.0 / P, None, ALU.mult))
    link(v.tensor_tensor(dst, src, token_bcast(st[:, 1, :]), ALU.subtract))
    link(v.tensor_tensor(square, dst, dst, ALU.mult))
    link(v.tensor_reduce(st[:, 2, :], square, X, ALU.add))
    v.tensor_scalar(st[:, 3, :], st[:, 2, :], 1.0 / P, eps, ALU.mult, ALU.add).then_inc(var_ready, 1)
    dve.wait_ge(std_ready, count)
    link(v.reciprocal(st[:, 4, :], st[:, 2, :]))
    return v.tensor_tensor(dst, dst, token_bcast(st[:, 4, :]), ALU.mult)


def layer_norm_scalar(c, act, var_ready, std_ready, count):
    act.wait_ge(var_ready, count)
    c.nc.scalar.activation(c.stat[:, 2, :], c.stat[:, 3, :], ACT.Sqrt).then_inc(std_ready, 1)


def transpose_tokens(c, src, bank0, done):
    for t in range(NT):
        ins = c.nc.tensor.transpose(c.ps[:, bank0 + t // 4, (t % 4) * P:(t % 4 + 1) * P], src[:, t, :], c.ident[:, :])
        if t % 4 == 3:
            ins.then_inc(done, 1)


def project_channels(c, w, rhs, bank0, done):
    for k in range(NC):
        c.nc.tensor.matmul(c.ps[:, bank0 + k, :], w, rhs[:, k * 512:(k + 1) * 512], start=True, stop=True).then_inc(done, 1)


def project_tokens(c, srcT, w, bank0, done):
    for t in range(NT):
        ins = c.nc.tensor.matmul(c.ps[:, bank0 + t // 4, (t % 4) * P:(t % 4 + 1) * P],
                                 srcT[:, t * P:(t + 1) * P], w, start=True, stop=True)
        if t % 4 == 3:
            ins.then_inc(done, 1)


def evacuate(c, act, src_bank, dst, done, first, out_ready, bias=0.0, scale=1.0):
    for k in range(NC):
        act.wait_ge(done, first + k + 1)
        c.nc.scalar.activation(dst[:, k * 512:(k + 1) * 512], c.ps[:, src_bank + k, :], ACT.Identity,
                               bias=bias, scale=scale).then_inc(out_ready, 1)


def constants(c, ins):
    nc = c.nc
    zeroed, x_loaded = c.sem("identity_zeroed"), c.sem("x_loaded")
    with nc.Block() as block:
        @block.sync
        def _(sp):
            sp.dma_start(c.x[:, :, :], ins["L0_attn_x"][0].rearrange("(t p) d -> p t d", p=P)).then_inc(x_loaded, 16)
            sp.wait_ge(x_loaded, 16)

        @block.gpsimd
        def _(pool):
            nc.gpsimd.memset(c.ident[:, :], 0.0).then_inc(zeroed, 1)
            nc.gpsimd.memset(c.identb[:, :], 0.0).then_inc(zeroed, 1)
            pool.wait_ge(zeroed, 2)
            for m in (c.ident, c.identb):
                nc.gpsimd.affine_select(out=m[:, :], in_=m[:, :], compare_op=ALU.not_equal, fill=1.0, base=0,
                                        pattern=[[-1, P]], channel_multiplier=1).then_inc(zeroed, 1)
            pool.wait_ge(zeroed, 4)


class Attention:

    def __init__(self, c, ctx):
        sb, nc = c.sb, c.nc
        self.hi = sb(ctx, "part_hi", [P, T], BF16)
        self.mid = sb(ctx, "part_mid", [P, T], BF16)
        self.lo = sb(ctx, "part_lo", [P, T], BF16)
        self.kx = sb(ctx, "k_parts", [P, 2, NPAIR, T], BF16)
        self.v = sb(ctx, "v_and_ones", [P, 2, NT, H, HD + 1], F32)
        self.q1 = sb(ctx, "q_parts", [P, 2, NPAIR, 2, P], BF16)
        self.q2 = sb(ctx, "q_parts_and_max", [P, NPAIR, 2, P], BF16)
        self.prob = c.qk[:, :, :].rearrange("p a (b k j q) -> p (a b) k j q", b=2, k=2, j=4)
        self.mx = sb(ctx, "chunk_max", [P, H, 4], F32)
        self.negm = sb(ctx, "minus_max", [P, H], F32)
        self.rest = sb(ctx, "minus_max_rest", [P, 4, 4], F32)
        self.mparts = sb(ctx, "minus_max_parts", [P, 4, 4, 3], BF16)
        self.mrow = sb(ctx, "minus_max_rows", [12, 4, P], BF16)
        self.oTs = sb(ctx, "out_channels", [P, 512], F32)
        self.rden = sb(ctx, "denominators", [P, H], F32)
        self.start = sb(ctx, "start_credit", [P, 1], F32)
        self.tick = sb(ctx, "tick", [P, 2], F32)
        self.wp = sb(ctx, "w_head_order", [P, 2, P], F32)
        self.q_dram = nc.dram_tensor(f"{c.layer}q_parts_dram", [2, NR, HD, NPAIR, T], BF16, kind="Internal").ap()
        self.k_dram = nc.dram_tensor(f"{c.layer}k_parts_dram", [8, 2, 3, HD, NPAIR, T], BF16, kind="Internal").ap()


def attention_constants(c, at, buffers):
    nc = c.nc
    filled, ones_set, zeroed = c.sem("attn_filled"), c.sem("attn_ones_set"), c.sem("attn_zeroed")
    ones = at.hi[0:3, :]
    with nc.Block() as block:
        @block.vector
        def _(dve):
            nc.vector.memset(ones, 1.0).then_inc(filled, 1)
            for k in range(buffers):
                nc.vector.memset(at.kx[:, k, :, :].bitcast(F32), 0.0).then_inc(filled, 1)

        @block.gpsimd
        def _(pool):
            nc.gpsimd.memset(at.q1[:, :, :, :, :].bitcast(F32), 0.0).then_inc(zeroed, 1)
            nc.gpsimd.memset(at.v[:, :, :, :, :], 1.0).then_inc(zeroed, 1)
            nc.gpsimd.memset(at.oTs[:, :], 1.0).then_inc(zeroed, 1)
            nc.gpsimd.memset(at.tick[:, :], 0.0).then_inc(zeroed, 1)
            pool.wait_ge(zeroed, 4)

        @block.sync
        def _(sp):
            sp.wait_ge(filled, 1 + buffers)
            for k in range(buffers):
                for j in range(2):
                    for p in range(NPAIR):
                        sp.dma_start(at.kx[64 * j + ROWS:64 * j + ROWS + 3, k, p, :], ones).then_inc(ones_set, 16)
            sp.wait_ge(ones_set, 16 * 2 * NPAIR * buffers)


def split_vector(c, at, dve, link, src, parts_ready, parts_stored, stores):
    v = c.nc.vector
    rest = c.b[:, :, :].rearrange("p t d -> p (t d)")
    if stores is not None:
        dve.wait_ge(parts_stored, stores)
    link(v.tensor_copy(at.hi[:, :], src))
    link(v.tensor_tensor(rest, src, at.hi[:, :], ALU.subtract))
    link(v.tensor_copy(at.mid[:, :], rest))
    v.tensor_tensor(at.lo[:, :], rest, at.mid[:, :], ALU.subtract).then_inc(parts_ready, 1)


def store_queries(c, at, eng, parts_ready, count, parts_stored):
    eng.wait_ge(parts_ready, count)
    parts = (at.hi, at.mid, at.lo)
    for r, which in enumerate(PARTS_Q):
        eng.dma_start(at.q_dram[:, r].rearrange("j d p t -> j (d p) t"), parts[which][:, :]).then_inc(parts_stored, 16)


def store_keys(c, at, eng, e, parts_ready, count, parts_stored):
    eng.wait_ge(parts_ready, count)
    for which, part in enumerate((at.hi, at.mid, at.lo)):
        eng.dma_start(at.k_dram[bass.ds(e, 1), :, which].rearrange("e j d p t -> (e j) (d p) t"), part[:, :]).then_inc(parts_stored, 16)


def load_keys(c, at, eng, buf, e, pairs, k_loaded):
    for j in range(2):
        for first, n in RUNS_K:
            row = 64 * j + first * HD
            eng.dma_start(at.kx[row:row + n * HD, buf, pairs, :],
                          at.k_dram[bass.ds(e, 1), j, 0:n, :, pairs, :].rearrange("e r d p t -> (e r d) p t")).then_inc(k_loaded, 16)


class Span:

    def __init__(self, causal):
        self.causal = causal

    def key_tiles(self, tile, u):
        return [kt for kt in (2 * u, 2 * u + 1) if not self.causal or kt <= tile]

    def steps(self, tile):
        return tile // 2 + 1 if self.causal else NT // 2

    def chunks(self, tile):
        return tile // 4 + 1 if self.causal else NC

    def width(self, tile, chunk):
        return P * (tile % 4 + 1) if self.causal and chunk == tile // 4 else 512

    def step_base(self, tile):
        return sum(4 * self.steps(i) for i in range(tile)) if self.causal else tile * (2 * NT)

    def max_base(self, tile):
        return sum(H * self.chunks(i) for i in range(tile)) if self.causal else tile * (H * NC)


def share(n, u, steps):
    return range(u * n // steps, (u + 1) * n // steps)


def attention_loop(c, at, tri=None, routed=None):
    nc = c.nc
    G = 4
    tiles = routed.tiles if routed else NT
    span = Span(tri is not None)
    s2 = (c.ps[:, 0:2, :], c.ps[:, 2:4, :])
    s1 = (c.ps[:, 4, :], c.ps[:, 5, :])
    oT, misc = c.ps[:, 6, :], c.ps[:, 7, :]
    miscb = misc.bitcast(BF16)

    ORDER = {0: ["rows3", "out"], 1: ["rows0"], 2: ["rows1"], 3: ["rows2"]}
    FIRST = ["rows0", "rows1", "rows2"]
    if routed:
        ORDER = {0: ["rows3", "out", "outT"], 1: ["proj", "rows0", "q"], 2: ["rows1"], 3: ["rows2"]}
        FIRST = ["q", "q"] + FIRST
    FLAT = [t for g in range(G) for t in ORDER[g]]
    LAST = ["out", "outT", "proj"] if routed else ["out"]

    def turn(i, name):
        return i * len(FLAT) + (len(FIRST) + FLAT.index(name))

    after_loop = turn(tiles - 1, "out") + 1 if tri is not None else turn(tiles, FLAT[0])

    def turns(i, g, u, late):
        steps = span.steps(i)
        due = [name for k, name in enumerate(ORDER[g]) if min(2 * k + 1 + late, steps - 1) == u]
        return [name for name in due if follows(i) or name in ("rows3", "out")]

    def follows(i):
        return tri is None or i + 1 < tiles

    def each_tile(eng, body):
        if tri is not None:
            for i in range(tiles):
                body(i, i % 2, i // 2)
        else:
            with eng.Fori(0, tiles // 2) as r:
                for k in range(2):
                    body(r * 2 + k, k, r)

    def kx(k):
        return at.kx[:, k if routed else 0]

    def vx(k):
        return at.v[:, k if routed else 0]

    q1_loaded = [c.sem(f"attn_q1_loaded{k}") for k in range(2)]
    q2_loaded = [c.sem(f"attn_q2_loaded{g}") for g in range(G)]
    s1_ready, s1_read = c.sem("attn_s1_ready"), c.sem("attn_s1_read")
    s2_ready, exp_done, pv_done = c.sem("attn_s2_ready"), c.sem("attn_exp_done"), c.sem("attn_pv_done")
    q_copied, mparts_ready = c.sem("attn_q_copied"), c.sem("attn_mparts_ready")
    misc_ready, misc_read, oT_copied = c.sem("attn_misc_ready"), c.sem("attn_misc_read"), c.sem("attn_oT_copied")
    dve_chain, oT_zeroed = c.sem("attn_dve_chain"), c.sem("attn_oT_zeroed")
    if routed:
        k_loaded = [[c.sem(f"attn_k_loaded{k}{g}") for g in range(G)] for k in range(2)]
        v_loaded = [c.sem(f"attn_v_loaded{k}") for k in range(2)]
        ticked, list_loaded, gathered = c.sem("attn_ticked"), c.sem("attn_list_loaded"), [c.sem(f"attn_gathered{k}") for k in range(2)]
        qparts_ready, w_out_loaded, y_stored = c.sem("attn_qparts_ready"), c.sem("attn_w_out_loaded"), c.sem("attn_y_stored")
    Q1 = 16 * (2 * NR if routed else 2)
    KX = 16 * 2 * len(RUNS_K)

    with nc.Block() as block:
        @block.sync
        def _(sp):
            def load_q(k, tile):
                if routed:
                    sp.wait_ge(qparts_ready, tile + 1)
                    for j in range(2):
                        for r, which in enumerate(PARTS_Q):
                            sp.dma_start(at.q1[64 * j + r * HD:64 * j + (r + 1) * HD, k, :, j, :],
                                         routed.qparts[64 * j:64 * j + 64, which, :]).then_inc(q1_loaded[k], 16)
                else:
                    for j in range(2):
                        sp.dma_start(at.q1[64 * j:64 * j + ROWS, k, :, j, :],
                                     at.q_dram[j].rearrange("r d p t -> (r d) p t")[:, :, bass.ds(tile * P, P)]).then_inc(q1_loaded[k], 16)

            def load_max(g, before):
                sp.wait_ge(misc_read, before + 1)
                for pp in range(2):
                    for j in range(2):
                        h = 2 * pp + j
                        sp.dma_start(at.q2[64 * j + ROWS:64 * j + ROWS + 3, 2 * g + pp, j, :],
                                     at.mrow[3 * h:3 * h + 3, g, :]).then_inc(q2_loaded[g], 16)

            def pairs(g):
                return slice(2 * g, 2 * g + 2)

            def expert(tile):
                return sp.value_load(routed.expert_of[0:1, bass.ds(tile, 1)], min_val=0, max_val=routed.E - 1)

            def load_values(k, e):
                sp.dma_start(at.v[:, k], routed.v_dram[bass.ds(e, 1)].rearrange("e p t h d -> (e p) t h d")).then_inc(v_loaded[k], 16)

            def load_w_out(e):
                sp.dma_start(routed.w_out_now[:, :], routed.w_out_dram[bass.ds(e, 1)].rearrange("e p d -> (e p) d")).then_inc(w_out_loaded, 16)

            def store_y(i):
                sp.dma_start(routed.y_dram[bass.ds(i, 1)].rearrange("a p d -> (a p) d"), routed.y[:, :]).then_inc(y_stored, 16)

            def tile_loads(i, k, r):
                sp.wait_ge(q_copied, i * G + G)
                load_max(3, turn(i, "rows3"))
                if tri is None and not routed:
                    load_q(k, (i + 2) % tiles)
                elif tri is not None and i + 2 < tiles:
                    load_q(k, i + 2)
                for g in range(G - 1):
                    if follows(i):
                        load_max(g, turn(i, f"rows{g}"))

            def routed_loads(i, k, r):
                this, following, e = expert(i), expert(i + 1), expert(i + 2)
                sp.wait_ge(pv_done, span.step_base(i) + 4)
                load_values(1 - k, following)
                load_max(3, turn(i, "rows3"))
                for g in range(G):
                    sp.wait_ge(s2_ready, span.step_base(i) + (g + 1) * (NT // 2))
                    load_keys(c, at, sp, k, e, pairs(g), k_loaded[k][g])
                    if g == 0:
                        sp.wait_ge(misc_read, turn(i, "proj") + 1)
                        store_y(i)
                        load_w_out(this)
                    if g < 3:
                        load_max(g, turn(i, f"rows{g}"))
                    if g == 0:
                        load_q(k, i + 2)

            if routed:
                for k in range(2):
                    e = expert(k)
                    if k == 0:
                        load_w_out(e)
                        load_values(0, e)
                    for g in range(G):
                        load_keys(c, at, sp, k, e, pairs(g), k_loaded[k][g])
            for k in range(2):
                load_q(k, k)
            for g in range(G - 1):
                load_max(g, len(FIRST) - 3 + g)
            each_tile(sp, routed_loads if routed else tile_loads)
            for k in range(2):
                sp.wait_ge(q1_loaded[k], Q1 * (tiles // 2 + (1 if tri is None else 0)))
            for g in range(G):
                sp.wait_ge(q2_loaded[g], 64 * (tiles + (1 if g < 3 and tri is None else 0)))
            if routed:
                for k in range(2):
                    sp.wait_ge(v_loaded[k], 16 * (tiles // 2 + (1 - k)))
                    for g in range(G):
                        sp.wait_ge(k_loaded[k][g], KX * (tiles // 2 + 1))
                sp.wait_ge(misc_read, after_loop + len(LAST))
                store_y(tiles)
                sp.wait_ge(y_stored, 16 * (tiles + 2))

        if routed:
            @block.gpsimd
            def _(pool):
                def gather(tile, k):
                    pool.dma_start(routed.index[:, k:k + 1],
                                   routed.list_dram[bass.ds(tile, 1)].rearrange("a (p b) -> (a p) b", b=1)).then_inc(list_loaded, 16)
                    pool.wait_ge(list_loaded, tile * 16 + 16)
                    nc.gpsimd.tensor_tensor(at.tick[:, 1:2], at.tick[:, 0:1], at.tick[:, 0:1], ALU.add).then_inc(ticked, 1)
                    nc.gpsimd.indirect_dma_start(out=routed.q[:, k, :], out_offset=None, in_=routed.q_dram[:, :],
                                                 in_offset=bass.IndirectOffsetOnAxis(ap=routed.index[:, k:k + 1], axis=0)).then_inc(gathered[k], 16)

                def next_gather(i, k, r):
                    pool.wait_ge(ticked, i + 2)
                    pool.wait_ge(qparts_ready, i + 1)
                    gather(i + 2, k)

                gather(0, 0)
                pool.wait_ge(ticked, 1)
                gather(1, 1)
                each_tile(pool, next_gather)
                for k in range(2):
                    pool.wait_ge(gathered[k], 16 * (tiles // 2 + 1))

        @block.tensor
        def _(pe):
            def first_pass(g, unit, tile, k, r):
                chunks = span.chunks(tile)
                head, chunk = unit // chunks, unit % chunks
                if unit == 0:
                    if g == 0:
                        pe.wait_ge(q1_loaded[k], r * Q1 + Q1)
                    if routed:
                        pe.wait_ge(k_loaded[k][g], r * KX + KX)
                pair, j = 2 * g + head // 2, head % 2
                n = g * 4 * chunks + unit
                width = span.width(tile, chunk)
                diagonal = tri is not None and chunk == chunks - 1
                pe.wait_ge(s1_read, span.max_base(tile) + (n + 1))
                last = nc.tensor.matmul(s1[n % 2][:, 0:width], at.q1[:, k, pair, j, :], kx(k)[:, pair, chunk * 512:chunk * 512 + width],
                                        start=True, stop=not diagonal)
                if diagonal:
                    last = nc.tensor.matmul(s1[n % 2][:, width - P:width], c.identb[:, :], tri.query[:, :], start=False, stop=True)
                last.then_inc(s1_ready, 1)

            def second_pass(s, i, k):
                steps, base = span.steps(i), span.step_base(i)
                g, u = s // steps, s % steps
                if u == 0:
                    pe.wait_ge(q2_loaded[g], i * 64 + 64)
                pe.wait_ge(exp_done, base + (s + 1))
                for kk, kt in enumerate(span.key_tiles(i, u)):
                    diagonal = tri is not None and kt == i
                    for pp in range(2):
                        last = nc.tensor.matmul(s2[s % 2][:, kk, pp * 256:(pp + 1) * 256], kx(k)[:, 2 * g + pp, kt * P:(kt + 1) * P],
                                                at.q2[:, 2 * g + pp, :, :].rearrange("p j q -> p (j q)"),
                                                start=not diagonal or pp == 0, stop=not diagonal)
                    if diagonal:
                        last = nc.tensor.matmul(s2[s % 2][:, kk, :], c.identb[:, :], tri.key[:, :].unsqueeze(1).to_broadcast([P, 4, P]),
                                                start=False, stop=True)
                last.then_inc(s2_ready, 1)

            def weighted_values(s, i, k, r):
                steps, base = span.steps(i), span.step_base(i)
                g, u = s // steps, s % steps
                if s == 0:
                    pe.wait_ge(oT_copied, i + 1)
                    if routed:
                        pe.wait_ge(v_loaded[k], r * 16 + 16)
                pe.wait_ge(exp_done, base + (s + 3))
                kts = span.key_tiles(i, u)
                for kk, kt in enumerate(kts):
                    for j in range(4):
                        last = nc.tensor.matmul(oT[32 * j:32 * j + HD + 1, g * P:(g + 1) * P], vx(k)[:, kt, 4 * g + j, :],
                                                at.prob[:, s % 4, kk, j, :], start=kt == 0, stop=u == steps - 1 and kt == kts[-1])
                last.then_inc(pv_done, 1)

            def fill_misc(name, i, k, r, before):
                if not (isinstance(before, int) and before == 0):
                    pe.wait_ge(misc_read, before)
                if name == "out":
                    pe.wait_ge(oT_copied, i + 1)
                    for g in range(G):
                        last = nc.tensor.transpose(misc[:, g * P:(g + 1) * P], at.oTs[:, g * P:(g + 1) * P], c.ident[:, :])
                    last.then_inc(misc_ready, 1)
                elif name == "outT":
                    nc.tensor.transpose(misc[:, 0:P], c.heads[:, 0, :], c.ident[:, :]).then_inc(misc_ready, 1)
                elif name == "proj":
                    pe.wait_ge(w_out_loaded, i * 16 + 16)
                    nc.tensor.matmul(misc[:, 0:P], routed.outT[:, :], routed.w_out_now[:, :], start=True, stop=True).then_inc(misc_ready, 1)
                elif name == "q":
                    pe.wait_ge(gathered[k], r * 16 + 32)
                    nc.tensor.transpose(misc[:, 0:P], routed.q[:, k, :], c.ident[:, :]).then_inc(misc_ready, 1)
                else:
                    g = int(name[4])
                    pe.wait_ge(mparts_ready, (i if g == 3 else i + 1) * G + (g + 1))
                    nc.tensor.transpose(miscb[0:12, 0:P], at.mparts[:, g, :, :].rearrange("p h r -> p (h r)"),
                                        c.identb[:, :]).then_inc(misc_ready, 1)

            def whole_tile(i, k, r):
                steps = span.steps(i)
                for s in range(G * steps):
                    g, u = s // steps, s % steps
                    if s + 1 < G * steps:
                        second_pass(s + 1, i, k)
                    if follows(i):
                        for unit in share(4 * span.chunks(i + 1), u, steps):
                            first_pass(g, unit, i + 1, 1 - k, r + k)
                    for name in turns(i, g, u, 0):
                        fill_misc(name, i, k, r, turn(i, name))
                    if s + 1 == G * steps and follows(i):
                        second_pass(0, i + 1, 1 - k)
                    weighted_values(s, i, k, r)

            pe.wait_ge(oT_zeroed, 1)
            if routed:
                for k in range(2):
                    fill_misc("q", k - 2, k, -1, k)
            for g in range(G):
                for unit in range(4 * span.chunks(0)):
                    first_pass(g, unit, 0, 0, 0)
                if g < 3:
                    fill_misc(f"rows{g}", -1, 1, -1, len(FIRST) - 3 + g)
            second_pass(0, 0, 0)
            each_tile(pe, whole_tile)
            for n, name in enumerate(LAST):
                fill_misc(name, tiles, 0, 0, after_loop + n)

        @block.scalar
        def _(act):
            def exps(i, k, r):
                steps, base = span.steps(i), span.step_base(i)
                for s in range(G * steps):
                    n = len(span.key_tiles(i, s % steps))
                    act.wait_ge(s2_ready, base + (s + 1))
                    act.wait_ge(pv_done, base + (s + 1))
                    nc.scalar.activation(at.prob[:, s % 4, 0:n, :, :].rearrange("p k j q -> p (k j q)"),
                                         s2[s % 2][:, 0:n, :].rearrange("p k n -> p (k n)"), ACT.Exp, scale=SCALE).then_inc(exp_done, 1)

            nc.scalar.activation(at.start[:, :], c.ident[:, 0:1], ACT.Exp).then_inc(exp_done, 2)
            each_tile(act, exps)

        @block.vector
        def _(dve):
            v = nc.vector

            class Link:

                def __init__(self, base):
                    self.base, self.k = base, 0

                def __call__(self, ins):
                    self.k += 1
                    ins.then_inc(dve_chain, 1)
                    dve.wait_ge(dve_chain, self.base + self.k)

            def maximum(g, unit, tile):
                chunks = span.chunks(tile)
                n = g * 4 * chunks + unit
                dve.wait_ge(s1_ready, span.max_base(tile) + (n + 1))
                v.tensor_reduce(at.mx[:, 4 * g + unit // chunks, unit % chunks:unit % chunks + 1],
                                s1[n % 2][:, 0:span.width(tile, unit % chunks)], X, ALU.max).then_inc(s1_read, 1)

            def finish_max(g, tile, link):
                chunks = span.chunks(tile)
                dve.wait_ge(s1_read, span.max_base(tile) + ((g + 1) * 4 * chunks + 2))
                m = at.negm[:, 4 * g:4 * g + 4]
                link(v.tensor_reduce(m, at.mx[:, 4 * g:4 * g + 4, 0:chunks], X, ALU.max, negate=True))
                link(v.tensor_copy(at.mparts[:, g, :, 0], m))
                link(v.tensor_tensor(at.rest[:, g, :], m, at.mparts[:, g, :, 0], ALU.subtract))
                link(v.tensor_copy(at.mparts[:, g, :, 1], at.rest[:, g, :]))
                v.tensor_tensor(at.mparts[:, g, :, 2], at.rest[:, g, :], at.mparts[:, g, :, 1],
                                ALU.subtract).then_inc(mparts_ready, 1)

            def copy_q(g, k):
                v.tensor_copy(at.q2[:, 2 * g:2 * g + 2, :, :], at.q1[:, k, 2 * g:2 * g + 2, :, :]).then_inc(q_copied, 1)

            def read_misc(name, i, k, r, before, link):
                dve.wait_ge(misc_ready, before + 1)
                if name == "out":
                    o = misc.rearrange("p (h n) -> p h n", n=32)
                    link(v.reciprocal(at.rden[:, :], o[:, :, HD]))
                    dst = c.heads[:, 0:1, :] if routed else c.heads[:, bass.ds(i, 1), :]
                    v.tensor_tensor(dst.rearrange("p a (h d) -> p (a h) d", d=HD), o[:, :, 0:HD],
                                    at.rden[:, :].unsqueeze(2).to_broadcast([P, H, HD]), ALU.mult).then_inc(misc_read, 1)
                elif name == "outT":
                    v.tensor_copy(routed.outT[:, :], misc[:, 0:P]).then_inc(misc_read, 1)
                elif name == "proj":
                    dve.wait_ge(y_stored, i * 16 + 16)
                    v.tensor_copy(routed.y[:, :], misc[:, 0:P]).then_inc(misc_read, 1)
                elif name == "q":
                    if not (isinstance(i, int) and i == -2):
                        dve.wait_ge(q1_loaded[1 - k], (r + k) * Q1 + Q1)
                    link(v.tensor_copy(routed.qparts[:, 0, :], misc[:, 0:P]))
                    v.tensor_tensor(routed.qrest[:, :], misc[:, 0:P], routed.qparts[:, 0, :], ALU.subtract).then_inc(misc_read, 1)
                    dve.wait_ge(misc_read, before + 1)
                    link(v.tensor_copy(routed.qparts[:, 1, :], routed.qrest[:, :]))
                    v.tensor_tensor(routed.qparts[:, 2, :], routed.qrest[:, :], routed.qparts[:, 1, :], ALU.subtract).then_inc(qparts_ready, 1)
                else:
                    v.tensor_copy(at.mrow[:, int(name[4]), :], miscb[0:12, 0:P]).then_inc(misc_read, 1)

            v.memset(oT, 0.0).then_inc(oT_zeroed, 1)
            v.memset(at.rest[:, 0, 0:1], 0.0).then_inc(s1_read, 2)
            v.memset(at.rest[:, 0, 1:2], 0.0).then_inc(pv_done, 4)
            v.memset(at.rest[:, 0, 2:3], 0.0).then_inc(oT_copied, 1)
            if routed:
                v.memset(at.rest[:, 0, 3:4], 0.0).then_inc(y_stored, 16)
            link = Link(0)
            if routed:
                for k in range(2):
                    read_misc("q", k - 2, k, -1, k, link)
            for g in range(G):
                for unit in range(4 * span.chunks(0)):
                    maximum(g, unit, 0)
                finish_max(g, 0, link)
                copy_q(g, 0)
                if g < 3:
                    read_misc(f"rows{g}", -1, 1, -1, len(FIRST) - 3 + g, link)
            before_loop, per_tile = link.k, 4 * G + (3 if routed else 1)

            def whole_tile(i, k, r):
                steps, base = span.steps(i), span.step_base(i)
                tile_link = link if tri is not None else Link(i * per_tile + before_loop)
                for g in range(G):
                    for u in range(steps):
                        if follows(i):
                            for unit in share(4 * span.chunks(i + 1), u, steps):
                                maximum(g, unit, i + 1)
                        for name in turns(i, g, u, 1):
                            read_misc(name, i, k, r, turn(i, name), tile_link)
                    if follows(i):
                        finish_max(g, i + 1, tile_link)
                        dve.wait_ge(s2_ready, base + (g + 1) * steps)
                        copy_q(g, 1 - k)
                dve.wait_ge(pv_done, base + (G * steps + 4))
                v.tensor_copy(at.oTs[:, :], oT).then_inc(oT_copied, 1)
                assert tri is not None or tile_link.k == per_tile

            each_tile(dve, whole_tile)
            end = link if tri is not None else Link(tiles * per_tile + before_loop)
            for n, name in enumerate(LAST):
                read_misc(name, tiles, 0, 0, after_loop + n, end)
            dve.wait_ge(misc_read, after_loop + len(LAST))


def l0_attention(c, at, ins):
    nc = c.nc
    c.layer = "l0a_"
    with ExitStack() as ctx:
        w = c.sb(ctx, "w_qkv", [P, 3 * P], F32)
        w_out = c.sb(ctx, "w_out", [P, P], F32)
        gamma, beta = c.sb(ctx, "gamma", [P, 1], F32), c.sb(ctx, "beta", [P, 1], F32)
        bq, bk = c.sb(ctx, "b_q", [P, 1], F32), c.sb(ctx, "b_k", [P, 1], F32)
        bv, b_out = c.sb(ctx, "b_v", [P, P], F32), c.sb(ctx, "b_out", [P, P], F32)
        b_qkv = ins["L0_attn_b_qkv"]
        pairs = [(w[:, :], ins["L0_attn_w_qkv"]), (w_out[:, :], ins["L0_attn_w_out"]),
                 (gamma[:, :], column(ins["L0_attn_ln_gamma"])), (beta[:, :], column(ins["L0_attn_ln_beta"])),
                 (bv[:, :], row_view(b_qkv[2 * P:3 * P], P)), (b_out[:, :], row_view(ins["L0_attn_b_out"], P))]
        for j in range(2):
            pairs.append((bq[64 * j:64 * j + 64, :], head_column(b_qkv[0:P])[j]))
            pairs.append((bk[64 * j:64 * j + 64, :], head_column(b_qkv[P:2 * P])[j]))
        attention_layer(c, at, pairs, [(eps, None, None) for eps in (1e-5,)] + [(1e-5, gamma, beta)],
                        w[:, 0:P], w[:, P:2 * P], w[:, 2 * P:3 * P], bq, bk, bv)
        attention_loop(c, at)
        attention_out(c, w_out, b_out, c.n, then_into_x=True)


def attention_layer(c, at, loads, norms, wq, wk, wv, bq, bk, bv):
    nc = c.nc
    w_loaded, var_ready, std_ready, chain = c.sem("w_loaded"), c.sem("var_ready"), c.sem("std_ready"), c.sem("chain")
    w_ordered = c.sem("w_ordered")
    h_ready, hT_psum, hT_ready = c.sem("h_ready"), c.sem("hT_psum"), c.sem("hT_ready")
    q_psum, k_psum, v_psum = c.sem("q_psum"), c.sem("k_psum"), c.sem("v_psum")
    q_ready, k_ready, v_ready = c.sem("q_ready"), c.sem("k_ready"), c.sem("v_ready")
    parts_ready, parts_stored, k_loaded = c.sem("parts_ready"), c.sem("parts_stored"), c.sem("k_loaded")
    ps = c.ps
    with nc.Block() as block:
        @block.sync
        def _(sp):
            for dst, src in loads:
                sp.dma_start(dst, src, allow_slow_non_contiguous=True).then_inc(w_loaded, 16)
            store_keys(c, at, sp, 0, parts_ready, 1, parts_stored)
            sp.wait_ge(parts_stored, 16 * 3)
            load_keys(c, at, sp, 0, 0, slice(0, NPAIR), k_loaded)
            store_queries(c, at, sp, parts_ready, 2, parts_stored)
            sp.wait_ge(parts_stored, 16 * (3 + NR))
            sp.wait_ge(k_loaded, 16 * 2 * len(RUNS_K))

        @block.vector
        def _(dve):
            link = Chain(dve, chain)
            dve.wait_ge(w_loaded, 16 * len(loads))
            nc.vector.tensor_copy(split_heads(at.wp[:, 0, :]), head_order(wq)).then_inc(w_ordered, 1)
            nc.vector.tensor_copy(split_heads(at.wp[:, 1, :]), head_order(wk)).then_inc(w_ordered, 1)
            link(layer_norm_vector(c, dve, link, c.x[:, :, :], c.n[:, :, :], c.b[:, :, :], var_ready, std_ready, 1, norms[0][0]))
            layer_norm_vector(c, dve, link, c.n[:, :, :], c.a[:, :, :], c.b[:, :, :], var_ready, std_ready, 2,
                              norms[1][0]).then_inc(h_ready, 1)
            dve.wait_ge(k_ready, NC)
            split_vector(c, at, dve, link, c.kT, parts_ready, parts_stored, None)
            for b in range(4):
                dve.wait_ge(v_psum, b + 1)
                nc.vector.tensor_tensor(at.v[:, 0, 4 * b:4 * b + 4, :, 0:HD], ps[:, 4 + b, :].rearrange("p (t h d) -> p t h d", t=4, h=H),
                                        bv[:, :].rearrange("p (h d) -> p h d", h=H).unsqueeze(1).to_broadcast([P, 4, H, HD]),
                                        ALU.add).then_inc(v_ready, 1)
            dve.wait_ge(q_ready, NC)
            split_vector(c, at, dve, link, c.qT, parts_ready, parts_stored, 16 * 3)
            dve.wait_ge(v_ready, 4)

        @block.tensor
        def _(pe):
            pe.wait_ge(h_ready, 1)
            transpose_tokens(c, c.a, 0, hT_psum)
            pe.wait_ge(w_loaded, 16 * len(loads))
            pe.wait_ge(w_ordered, 2)
            pe.wait_ge(hT_ready, NC)
            project_channels(c, at.wp[:, 1, :], c.nT, 4, k_psum)
            project_channels(c, at.wp[:, 0, :], c.nT, 0, q_psum)
            pe.wait_ge(k_ready, NC)
            project_tokens(c, c.nT, wv, 4, v_psum)

        @block.scalar
        def _(act):
            layer_norm_scalar(c, act, var_ready, std_ready, 1)
            layer_norm_scalar(c, act, var_ready, std_ready, 2)
            act.wait_ge(w_loaded, 16 * len(loads))
            _, gamma, beta = norms[1]
            evacuate(c, act, 0, c.nT, hT_psum, 0, hT_ready, beta[:, :], gamma[:, :])
            evacuate(c, act, 4, c.kT, k_psum, 0, k_ready, bk[:, :])
            evacuate(c, act, 0, c.qT, q_psum, 0, q_ready, bq[:, :])


def attention_out(c, w_out, b_out, into, then_into_x):
    nc = c.nc
    aT_psum, aT_ready, y_psum, chain = c.sem("aT_psum"), c.sem("aT_ready"), c.sem("y_psum"), c.sem("out_chain")
    with nc.Block() as block:
        @block.tensor
        def _(pe):
            transpose_tokens(c, c.a, 0, aT_psum)
            pe.wait_ge(aT_ready, NC)
            project_tokens(c, c.nT, w_out[:, :], 4, y_psum)

        @block.scalar
        def _(act):
            evacuate(c, act, 0, c.nT, aT_psum, 0, aT_ready)

        @block.vector
        def _(dve):
            link = Chain(dve, chain)
            link(nc.vector.tensor_tensor(into[:, :, :], into[:, :, :], b_out[:, :].unsqueeze(1).to_broadcast([P, NT, P]), ALU.add))
            add_banks(c, dve, link, into, 4, y_psum)
            if then_into_x:
                link(nc.vector.tensor_tensor(c.x[:, :, :], c.x[:, :, :], into[:, :, :], ALU.add))


def add_banks(c, dve, link, into, bank0, ready):
    for b in range(4):
        sl = slice(4 * b, 4 * b + 4)
        dve.wait_ge(ready, b + 1)
        link(c.nc.vector.tensor_tensor(into[:, sl, :], into[:, sl, :], c.ps[:, bank0 + b, :].rearrange("p (t d) -> p t d", t=4), ALU.add))


class DiagonalMask:

    def __init__(self, c, ctx):
        self.query = c.sb(ctx, "mask_by_query", [P, P], BF16)
        self.key = c.sb(ctx, "mask_by_key", [P, P], BF16)
        nc = c.nc
        drawn = c.sem("mask_drawn")
        with nc.Block() as block:
            @block.gpsimd
            def _(pool):
                nc.gpsimd.memset(self.query[:, :], 0.0).then_inc(drawn, 1)
                nc.gpsimd.memset(self.key[:, :], 0.0).then_inc(drawn, 1)
                pool.wait_ge(drawn, 2)
                nc.gpsimd.affine_select(out=self.query[:, :], in_=self.query[:, :], compare_op=ALU.is_ge, fill=MASKED,
                                        base=0, pattern=[[-1, P]], channel_multiplier=1).then_inc(drawn, 1)
                nc.gpsimd.affine_select(out=self.key[:, :], in_=self.key[:, :], compare_op=ALU.is_ge, fill=MASKED,
                                        base=0, pattern=[[1, P]], channel_multiplier=-1).then_inc(drawn, 1)
                pool.wait_ge(drawn, 4)


def l0_ffn(c, at, ins):
    nc = c.nc
    c.layer = "l0f_"
    E = 8
    with ExitStack() as ctx:
        w_out, b_out = c.sb(ctx, "w_out", [P, P], F32), c.sb(ctx, "b_out", [P, P], F32)
        with ExitStack() as actx:
            w = c.sb(actx, "w_qkv", [P, 3, P], F32)
            gamma, beta = c.sb(actx, "gamma", [P, 1], F32), c.sb(actx, "beta", [P, 1], F32)
            bq, bk, bv = c.sb(actx, "b_q", [P, 1], F32), c.sb(actx, "b_k", [P, 1], F32), c.sb(actx, "b_v", [P, P], F32)
            loads = [(w[:, k, :], ins[f"L0_ffn_W{m}"]) for k, m in enumerate("qkv")]
            loads += [(w_out[:, :], ins["L0_ffn_Wo"]), (gamma[:, :], column(ins["L0_ffn_ln1_g"])),
                      (beta[:, :], column(ins["L0_ffn_ln1_b"])), (bv[:, :], row_view(ins["L0_ffn_bv"], P)),
                      (b_out[:, :], row_view(ins["L0_ffn_bo"], P))]
            for j in range(2):
                loads.append((bq[64 * j:64 * j + 64, :], head_column(ins["L0_ffn_bq"])[j]))
                loads.append((bk[64 * j:64 * j + 64, :], head_column(ins["L0_ffn_bk"])[j]))
            attention_layer(c, at, loads, [(1e-5, None, None), (1e-5, gamma, beta)], w[:, 0, :], w[:, 1, :], w[:, 2, :], bq, bk, bv)
            attention_loop(c, at, tri=DiagonalMask(c, actx))
        attention_out(c, w_out, b_out, c.n, then_into_x=False)
        mix = c.sb(ctx, "expert_weights", [P, NT, E], F32)
        bias = c.sb(ctx, "b1_columns", [P, E * 4], F32)
        l0_router(c, ctx, ins, E, mix, bias)
        experts(c, ctx, E, ins["L0_ffn_e_w1"], lambda e: ins["L0_ffn_e_w2"][bass.ds(e, 1)], bias, mix)
        add_to_residual(c)


def top_choice(c, v, link, logits, best, tie, order, choice, width):
    def wide(s):
        return s.unsqueeze(2).to_broadcast([P, NT, width])
    link(v.tensor_reduce(best, logits, X, ALU.max))
    link(v.tensor_tensor(choice, logits, wide(best), ALU.is_equal))
    link(v.tensor_tensor(choice, choice, order.unsqueeze(1).to_broadcast([P, NT, width]), ALU.mult))
    link(v.tensor_reduce(tie, choice, X, ALU.max))
    link(v.tensor_tensor(choice, choice, wide(tie), ALU.is_equal))


def draw_order(c, pool, order, width, drawn):
    for e in range(width):
        c.nc.gpsimd.memset(order[:, e:e + 1], float(width - e)).then_inc(drawn, 1)


def l0_router(c, ctx, ins, E, mix, bias):
    nc = c.nc
    ps = c.ps
    with ExitStack() as rctx:
        gamma, beta = c.sb(rctx, "gamma2", [P, 1], F32), c.sb(rctx, "beta2", [P, 1], F32)
        wr, br = c.sb(rctx, "w_router", [P, E], F32), c.sb(rctx, "b_router", [P, E], F32)
        b1, b2 = c.sb(rctx, "b1_rows", [E * 4, P], F32), c.sb(rctx, "b2_rows", [E, P], F32)
        lg, ch, ex = (c.sb(rctx, n, [P, NT, E], F32) for n in ("logits", "choice", "rest"))
        best, second, tie = (c.sb(rctx, n, [P, NT], F32) for n in ("best", "second", "tie"))
        order = c.sb(rctx, "order", [P, E], F32)
        mixT = c.sb(rctx, "mix_rows", [E, T], F32)
        w_loaded, var_ready, std_ready, chain = c.sem("r_w_loaded"), c.sem("r_var_ready"), c.sem("r_std_ready"), c.sem("r_chain")
        h_ready, hT_psum, hT_ready, drawn = c.sem("r_h_ready"), c.sem("r_hT_psum"), c.sem("r_hT_ready"), c.sem("r_order_drawn")
        b1_psum, b1_ready, lg_psum, shifted, exp_ready = (c.sem("r_" + n) for n in ("b1_psum", "b1_ready", "lg_psum", "shifted", "exp_ready"))
        mix_ready, mixT_psum, mixT_ready, b2_psum = (c.sem("r_" + n) for n in ("mix_ready", "mixT_psum", "mixT_ready", "b2_psum"))
        loads = [(gamma[:, :], column(ins["L0_ffn_ln2_g"])), (beta[:, :], column(ins["L0_ffn_ln2_b"])),
                 (wr[:, :], ins["L0_ffn_Wr"]), (br[:, :], row_view(ins["L0_ffn_br"], E)),
                 (b1[:, :], ins["L0_ffn_e_b1"].rearrange("e (f p) -> (e f) p", p=P)), (b2[:, :], ins["L0_ffn_e_b2"])]
        with nc.Block() as block:
            @block.sync
            def _(sp):
                for dst, src in loads:
                    sp.dma_start(dst, src).then_inc(w_loaded, 16)

            @block.gpsimd
            def _(pool):
                draw_order(c, pool, order, E, drawn)

            @block.tensor
            def _(pe):
                pe.wait_ge(h_ready, 1)
                transpose_tokens(c, c.a, 0, hT_psum)
                pe.wait_ge(w_loaded, 16 * len(loads))
                nc.tensor.transpose(ps[:, 4, 0:E * 4], b1[:, :], c.ident[0:E * 4, 0:E * 4]).then_inc(b1_psum, 1)
                pe.wait_ge(hT_ready, NC)
                for t in range(NT):
                    last = nc.tensor.matmul(ps[:, 5, t * E:(t + 1) * E], c.nT[:, t * P:(t + 1) * P], wr[:, :], start=True, stop=True)
                last.then_inc(lg_psum, 1)
                pe.wait_ge(mix_ready, 1)
                for t in range(NT):
                    ins_ = nc.tensor.transpose(ps[0:E, t // 4, (t % 4) * P:(t % 4 + 1) * P], mix[:, t, :], c.ident[:, :])
                    if t % 4 == 3:
                        ins_.then_inc(mixT_psum, 1)
                pe.wait_ge(mixT_ready, NC)
                for t in range(NT):
                    ins_ = nc.tensor.matmul(ps[:, 4 + t // 4, (t % 4) * P:(t % 4 + 1) * P], mixT[:, t * P:(t + 1) * P], b2[:, :],
                                            start=True, stop=True)
                    if t % 4 == 3:
                        ins_.then_inc(b2_psum, 1)

            @block.scalar
            def _(act):
                layer_norm_scalar(c, act, var_ready, std_ready, 1)
                act.wait_ge(w_loaded, 16 * len(loads))
                evacuate(c, act, 0, c.nT, hT_psum, 0, hT_ready, beta[:, :], gamma[:, :])
                act.wait_ge(b1_psum, 1)
                nc.scalar.activation(bias[:, :], ps[:, 4, 0:E * 4], ACT.Copy).then_inc(b1_ready, 1)
                act.wait_ge(shifted, 1)
                nc.scalar.activation(ex[:, :, :], ex[:, :, :], ACT.Exp).then_inc(exp_ready, 1)
                for k in range(NC):
                    act.wait_ge(mixT_psum, k + 1)
                    nc.scalar.activation(mixT[:, k * 512:(k + 1) * 512], ps[0:E, k, :], ACT.Copy).then_inc(mixT_ready, 1)
                act.wait_ge(b1_ready, 1)

            @block.vector
            def _(dve):
                v = nc.vector
                link = Chain(dve, chain)

                def wide(s):
                    return s.unsqueeze(2).to_broadcast([P, NT, E])

                layer_norm_vector(c, dve, link, c.n[:, :, :], c.a[:, :, :], c.b[:, :, :], var_ready, std_ready, 1, 1e-5).then_inc(h_ready, 1)
                dve.wait_ge(w_loaded, 16 * len(loads))
                dve.wait_ge(drawn, E)
                dve.wait_ge(lg_psum, 1)
                link(v.tensor_tensor(lg[:, :, :], ps[:, 5, 0:NT * E].rearrange("p (t e) -> p t e", e=E),
                                     br[:, :].unsqueeze(1).to_broadcast([P, NT, E]), ALU.add))
                top_choice(c, v, link, lg[:, :, :], best[:, :], tie[:, :], order[:, :], ch[:, :, :], E)
                link(v.scalar_tensor_tensor(ex[:, :, :], ch[:, :, :], MASKED, lg[:, :, :], ALU.mult, ALU.add))
                link(v.tensor_reduce(second[:, :], ex[:, :, :], X, ALU.max))
                link(v.tensor_tensor(ch[:, :, :], lg[:, :, :], wide(second[:, :]), ALU.is_ge))
                v.tensor_tensor(ex[:, :, :], lg[:, :, :], wide(best[:, :]), ALU.subtract).then_inc(shifted, 1)
                dve.wait_ge(exp_ready, 1)
                link(v.tensor_tensor(ex[:, :, :], ex[:, :, :], ch[:, :, :], ALU.mult))
                link(v.tensor_reduce(tie[:, :], ex[:, :, :], X, ALU.add))
                link(v.reciprocal(best[:, :], tie[:, :]))
                v.tensor_tensor(mix[:, :, :], ex[:, :, :], wide(best[:, :]), ALU.mult).then_inc(mix_ready, 1)
                for b in range(4):
                    sl = slice(4 * b, 4 * b + 4)
                    dve.wait_ge(b2_psum, b + 1)
                    link(v.tensor_tensor(c.n[:, sl, :], c.n[:, sl, :], ps[:, 4 + b, :].rearrange("p (t d) -> p t d", t=4), ALU.add))


def experts(c, ctx, E, w1_dram, w2_of, bias, mix):
    nc = c.nc
    ps = c.ps
    F = 4
    K = 2 * NC
    with ExitStack() as ectx:
        w1 = c.sb(ectx, "w1", [P, 2, F * P], F32)
        w2 = c.sb(ectx, "w2", [P, 2, F, P], F32)
        mid = c.sb(ectx, "hidden", [P, 2, F, 512], F32)
        bnow = c.sb(ectx, "b1_now", [P, 2, F], F32)
        start = c.sb(ectx, "e_start_credit", [P, 3], F32)
        w_loaded = [c.sem(f"e_w_loaded{k}") for k in range(2)]
        mid_psum, gelu_done, y_psum, y_added = (c.sem("e_" + n) for n in ("mid_psum", "gelu_done", "y_psum", "y_added"))
        with nc.Block() as block:
            @block.sync
            def _(sp):
                def load(k, e):
                    sp.dma_start(w1[:, k, :], w1_dram[bass.ds(e, 1)].rearrange("a d f -> d (a f)")).then_inc(w_loaded[k], 16)
                    sp.dma_start(bnow[:, k, :], bias[:, bass.ds(e * F, F)]).then_inc(w_loaded[k], 16)
                    sp.dma_start(w2[:, k, :, :], w2_of(e).rearrange("a (f p) d -> p (a f) d", p=P)).then_inc(w_loaded[k], 16)

                for k in range(2):
                    load(k, k)
                with sp.Fori(0, E // 2 - 1) as r:
                    for k in range(2):
                        sp.wait_ge(y_psum, r * K + (NC * (k + 1) + 2))
                        load(k, r * 2 + (2 + k))

            @block.tensor
            def _(pe):
                def up(r, k):
                    e, ch = k // NC, k % NC
                    if ch == 0:
                        pe.wait_ge(w_loaded[e], r * 48 + 48)
                    for f in range(F):
                        pe.wait_ge(gelu_done, r * K * F + (k * F + f + 1))
                        nc.tensor.matmul(ps[:, f, :], w1[:, e, f * P:(f + 1) * P], c.nT[:, ch * 512:(ch + 1) * 512],
                                         start=True, stop=True).then_inc(mid_psum, 1)

                def down(r, k):
                    e = k // NC
                    pe.wait_ge(gelu_done, r * K * F + (k * F + 2 * F))
                    pe.wait_ge(y_added, r * K + (k + 3))
                    for t in range(4):
                        for f in range(F):
                            last = nc.tensor.matmul(ps[:, 4 + k % 2, t * P:(t + 1) * P], mid[:, k % 2, f, t * P:(t + 1) * P],
                                                    w2[:, e, f, :], start=f == 0, stop=f == F - 1)
                    last.then_inc(y_psum, 1)

                with pe.Fori(0, E // 2) as r:
                    up(r, 0)
                    for k in range(K):
                        if k + 1 < K:
                            up(r, k + 1)
                        down(r, k)

            @block.scalar
            def _(act):
                nc.scalar.activation(start[:, 0:1], bias[:, 0:1], ACT.Copy).then_inc(gelu_done, 4)
                with act.Fori(0, E // 2) as r:
                    for k in range(K):
                        if k % NC == 0:
                            act.wait_ge(w_loaded[k // NC], r * 48 + 48)
                        act.wait_ge(y_psum, r * K + (k + 1))
                        for f in range(F):
                            act.wait_ge(mid_psum, r * K * F + (k * F + f + 1))
                            nc.scalar.activation(mid[:, k % 2, f, :], ps[:, f, :], ACT.Gelu,
                                                 bias=bnow[:, k // NC, f:f + 1]).then_inc(gelu_done, 1)

            @block.vector
            def _(dve):
                v = nc.vector
                v.memset(start[:, 1:2], 0.0).then_inc(y_psum, 2)
                v.memset(start[:, 2:3], 0.0).then_inc(y_added, 4)
                with dve.Fori(0, E // 2) as r:
                    for k in range(K):
                        e, ch = k // NC, k % NC
                        dve.wait_ge(y_psum, r * K + (k + 3))
                        dve.wait_ge(y_added, r * K + (k + 1))
                        for t in range(4):
                            tile = 4 * ch + t
                            last = v.scalar_tensor_tensor(c.n[:, tile, :], ps[:, 4 + k % 2, t * P:(t + 1) * P],
                                                          mix[:, tile, bass.ds(r * 2 + e, 1)], c.n[:, tile, :], ALU.mult, ALU.add)
                        last.then_inc(y_added, 1)
                dve.wait_ge(y_added, E * NC + 4)


def add_to_residual(c):
    nc = c.nc
    done = c.sem("residual_done")
    with nc.Block() as block:
        @block.vector
        def _(dve):
            nc.vector.tensor_tensor(c.x[:, :, :], c.x[:, :, :], c.n[:, :, :], ALU.add).then_inc(done, 1)
            dve.wait_ge(done, 1)


class NormBlock:

    def __init__(self, c, prefix="n_"):
        self.c = c
        self.var_ready, self.std_ready = c.sem(prefix + "var_ready"), c.sem(prefix + "std_ready")
        self.n_ready, self.nT_psum, self.nT_ready = c.sem(prefix + "n_ready"), c.sem(prefix + "nT_psum"), c.sem(prefix + "nT_ready")

    def vector(self, dve, link, eps=1e-5):
        c = self.c
        layer_norm_vector(c, dve, link, c.x[:, :, :], c.n[:, :, :], c.b[:, :, :], self.var_ready, self.std_ready, 1,
                          eps).then_inc(self.n_ready, 1)

    def tensor(self, pe):
        pe.wait_ge(self.n_ready, 1)
        transpose_tokens(self.c, self.c.n, 0, self.nT_psum)

    def scalar(self, act, dst):
        layer_norm_scalar(self.c, act, self.var_ready, self.std_ready, 1)
        evacuate(self.c, act, 0, dst, self.nT_psum, 0, self.nT_ready)


def softplus_scalar(c, act, link, x, bias, magnitude, tail):
    link(c.nc.scalar.activation(magnitude, x, ACT.Abs, bias=bias))
    link(c.nc.scalar.activation(magnitude, magnitude, ACT.Exp, scale=-1.0))
    return c.nc.scalar.activation(tail, magnitude, ACT.Ln, bias=1.0)


def l1_mamba(c, ins):
    nc = c.nc
    c.layer = "l1a_"
    DI, DS, KC, R = 2 * P, 16, 4, 8
    ps = c.ps
    dram = nc.dram_tensor("ssm_rows_dram", [2 * DS, T], F32, kind="Internal").ap()
    with ExitStack() as ctx:
        xv = c.sb(ctx, "xv", [P, 2, T], F32)
        dx = c.sb(ctx, "delta_x", [P, 2, T], F32)
        delta = c.sb(ctx, "delta", [P, 2, T], F32)
        a = c.sb(ctx, "a", [P, 2, DS], F32)
        w_out, dvec = c.sb(ctx, "w_out", [P, 2, P], F32), c.sb(ctx, "d", [P, 2], F32)
        with ExitStack() as pctx:
            w_in, conv_w, conv_b = c.sb(pctx, "w_in", [P, DI], F32), c.sb(pctx, "conv_w", [P, 2, KC], F32), c.sb(pctx, "conv_b", [P, 2], F32)
            w_x, w_dt, b_dt = c.sb(pctx, "w_x", [P, 2, R + 2 * DS], F32), c.sb(pctx, "w_dt", [R, DI], F32), c.sb(pctx, "b_dt", [P, 2], F32)
            xp = c.sb(pctx, "x_padded", [P, 2, KC - 1 + T], F32)
            ssm = c.sb(pctx, "ssm", [R, T], F32)
            ssm_bc = c.sb(pctx, "ssm_bc", [2 * DS, T], F32)
            norm = NormBlock(c)
            w_loaded, chain, act_chain = c.sem("w_loaded"), c.sem("chain"), c.sem("act_chain")
            xp_psum, xp_ready, conv_ready, xv_ready = c.sem("xp_psum"), c.sem("xp_ready"), c.sem("conv_ready"), c.sem("xv_ready")
            ssm_psum, ssm_ready, ssm_stored, dt_psum, tail_ready, delta_ready = (c.sem(n) for n in (
                "ssm_psum", "ssm_ready", "ssm_stored", "dt_psum", "tail_ready", "delta_ready"))

            def halves(v):
                return v.rearrange("(h p) -> p h", p=P)

            loads = [(w_in[:, :], ins["L1_attn_W_in"]), (conv_w[:, :, :], ins["L1_attn_conv_w"].rearrange("(h p) a k -> p h (a k)", p=P)),
                     (conv_b[:, :], halves(ins["L1_attn_conv_b"])), (w_x[:, :, :], ins["L1_attn_W_x"].rearrange("(h p) r -> p h r", p=P)),
                     (w_dt[:, :], ins["L1_attn_W_dt"]), (b_dt[:, :], halves(ins["L1_attn_b_dt"])),
                     (a[:, :, :], ins["L1_attn_A_log"].rearrange("(h p) n -> p h n", p=P)),
                     (w_out[:, :, :], ins["L1_attn_W_out"].rearrange("(h p) d -> p h d", p=P)), (dvec[:, :], halves(ins["L1_attn_D"]))]
            with nc.Block() as block:
                @block.sync
                def _(sp):
                    for dst, src in loads:
                        sp.dma_start(dst, src, allow_slow_non_contiguous=True).then_inc(w_loaded, 16)
                    sp.wait_ge(ssm_ready, 2 * NC)
                    sp.dma_start(dram[:, :], ssm_bc[:, :]).then_inc(ssm_stored, 16)
                    sp.wait_ge(ssm_stored, 16)

                @block.tensor
                def _(pe):
                    norm.tensor(pe)
                    pe.wait_ge(w_loaded, 16 * len(loads))
                    pe.wait_ge(norm.nT_ready, NC)
                    project_channels(c, w_in[:, P:2 * P], c.nT, 4, xp_psum)
                    project_channels(c, w_in[:, 0:P], c.nT, 0, xp_psum)
                    pe.wait_ge(xv_ready, 2)
                    pe.wait_ge(xp_ready, 2 * NC)
                    for k in range(NC):
                        for h in range(2):
                            last = nc.tensor.matmul(ps[0:R, k, :], w_x[:, h, 0:R], xv[:, h, k * 512:(k + 1) * 512],
                                                    start=h == 0, stop=h == 1)
                        last.then_inc(ssm_psum, 1)
                    for k in range(NC):
                        for h in range(2):
                            last = nc.tensor.matmul(ps[0:2 * DS, 4 + k, :], w_x[:, h, R:R + 2 * DS], xv[:, h, k * 512:(k + 1) * 512],
                                                    start=h == 0, stop=h == 1)
                        last.then_inc(ssm_psum, 1)
                    pe.wait_ge(ssm_ready, 2 * NC)
                    for h in range(2):
                        for k in range(NC):
                            last = nc.tensor.matmul(ps[:, 4 * h + k, :], w_dt[:, h * P:(h + 1) * P], ssm[:, k * 512:(k + 1) * 512],
                                                    start=True, stop=True)
                        last.then_inc(dt_psum, 1)

                @block.scalar
                def _(act):
                    link = Chain(act, act_chain)
                    norm.scalar(act, c.nT)
                    for h in (1, 0):
                        evacuate(c, act, 4 * h, xp[:, h, KC - 1:], xp_psum, (1 - h) * NC, xp_ready)
                    for h in range(2):
                        act.wait_ge(conv_ready, h + 1)
                        nc.scalar.activation(xv[:, h, :], xv[:, h, :], ACT.Silu).then_inc(xv_ready, 1)
                    for part in range(2):
                        for k in range(NC):
                            act.wait_ge(ssm_psum, part * NC + k + 1)
                            dst = ssm_bc if part else ssm
                            nc.scalar.activation(dst[:, k * 512:(k + 1) * 512], ps[0:dst.shape[0], 4 * part + k, :], ACT.Copy).then_inc(ssm_ready, 1)
                    for h in range(2):
                        act.wait_ge(dt_psum, h + 1)
                        softplus_scalar(c, act, link, ps[:, 4 * h:4 * h + 4, :].rearrange("p b n -> p (b n)"), b_dt[:, h:h + 1],
                                        dx[:, h, :], delta[:, h, :]).then_inc(tail_ready, 1)
                    act.wait_ge(w_loaded, 16 * len(loads))
                    link(nc.scalar.activation(a[:, :, :], a[:, :, :], ACT.Exp))
                    act.wait_ge(tail_ready, 2)
                    link(nc.scalar.activation(a[:, :, :], a[:, :, :], ACT.Copy, scale=-1.0))

                @block.vector
                def _(dve):
                    v = nc.vector
                    link = Chain(dve, chain)
                    link(v.memset(xp[:, :, 0:KC - 1], 0.0))
                    norm.vector(dve, link)
                    dve.wait_ge(w_loaded, 16 * len(loads))
                    for h in range(2):
                        dve.wait_ge(xp_ready, 2 * NC)
                        link(v.tensor_scalar(xv[:, h, :], xp[:, h, 0:T], conv_w[:, h, 0:1], conv_b[:, h:h + 1], ALU.mult, ALU.add))
                        for k in range(1, KC):
                            last = v.scalar_tensor_tensor(xv[:, h, :], xp[:, h, k:k + T], conv_w[:, h, k:k + 1], xv[:, h, :], ALU.mult, ALU.add)
                            if k < KC - 1:
                                link(last)
                        last.then_inc(conv_ready, 1)
                    for h in range(2):
                        dve.wait_ge(tail_ready, h + 1)
                        link(v.tensor_scalar(dx[:, h, :], ps[:, 4 * h:4 * h + 4, :].rearrange("p b n -> p (b n)"), b_dt[:, h:h + 1], 0.0,
                                             ALU.add, ALU.max))
                        link(v.tensor_tensor(delta[:, h, :], delta[:, h, :], dx[:, h, :], ALU.add))
                        dve.wait_ge(xv_ready, 2)
                        link(v.tensor_tensor(dx[:, h, :], delta[:, h, :], xv[:, h, :], ALU.mult))

        mamba_scan(c, ctx, dram, DS, a, dvec, delta, dx, xv)
        y = dx
        y_ready, out_psum, chain2 = c.sem("y_ready"), c.sem("out_psum"), c.sem("chain2")
        with nc.Block() as block:
            @block.scalar
            def _(act):
                for h in range(2):
                    nc.scalar.activation(y[:, h, :], ps[:, 4 * h:4 * h + 4, :].rearrange("p b n -> p (b n)"), ACT.Copy).then_inc(y_ready, 1)

            @block.tensor
            def _(pe):
                pe.wait_ge(y_ready, 2)
                for t in range(NT):
                    for h in range(2):
                        last = nc.tensor.matmul(ps[:, t // 4, (t % 4) * P:(t % 4 + 1) * P], y[:, h, t * P:(t + 1) * P], w_out[:, h, :],
                                                start=h == 0, stop=h == 1)
                    if t % 4 == 3:
                        last.then_inc(out_psum, 1)

            @block.vector
            def _(dve):
                add_banks(c, dve, Chain(dve, chain2), c.x, 0, out_psum)


def mamba_scan(c, ctx, dram, DS, a, dvec, delta, dx, xv):
    nc = c.nc
    ps = c.ps
    with ExitStack() as sctx:
        rows = c.sb(sctx, "bc_rows", [P, 2, 2, T], F32)
        da = c.sb(sctx, "decay", [P, 2, T], F32)
        u = c.sb(sctx, "input", [P, 2, T], F32)
        hc = c.sb(sctx, "state_c", [P, 2, T], F32)
        anow = c.sb(sctx, "a_now", [P, 2, 2], F32)
        diag = c.sb(sctx, "d_diagonal", [P, 2, P], F32)
        start = c.sb(sctx, "start_credit", [P, 4], F32)
        rows_loaded = [c.sem(f"rows_loaded{k}") for k in range(2)]
        da_ready, u_ready, scanned, hc_ready, added, diag_ready = (c.sem("s_" + n) for n in (
            "da_ready", "u_ready", "scanned", "hc_ready", "added", "diag_ready"))
        L = 3 * 16
        with nc.Block() as block:
            @block.sync
            def _(sp):
                def load(k, n):
                    sp.dma_start(rows[:, k, 0, :], dram[bass.ds(n, 1), :].to_broadcast([P, T])).then_inc(rows_loaded[k], 16)
                    sp.dma_start(rows[:, k, 1, :], dram[bass.ds(n + DS, 1), :].to_broadcast([P, T])).then_inc(rows_loaded[k], 16)
                    sp.dma_start(anow[:, k, :], a[:, :, bass.ds(n, 1)].rearrange("p h a -> p (h a)"),
                                 allow_slow_non_contiguous=True).then_inc(rows_loaded[k], 16)

                for k in range(2):
                    load(k, k)
                with sp.Fori(0, DS // 2 - 1) as r:
                    for k in range(2):
                        sp.wait_ge(hc_ready, r * 4 + (2 * k + 4))
                        load(k, r * 2 + (2 + k))

            @block.scalar
            def _(act):
                def decays(r, k):
                    act.wait_ge(rows_loaded[k], r * L + L)
                    for h in range(2):
                        act.wait_ge(scanned, r * 4 + (2 * k + h + 1))
                        nc.scalar.activation(da[:, h, :], delta[:, h, :], ACT.Exp, scale=anow[:, k, h:h + 1]).then_inc(da_ready, 1)

                with act.Fori(0, DS // 2 - 1) as r:
                    for k in range(2):
                        decays(r, k)
                for k in range(2):
                    decays(DS // 2 - 1, k)

            @block.gpsimd
            def _(pool):
                def inputs(r, k):
                    pool.wait_ge(rows_loaded[k], r * L + L)
                    for h in range(2):
                        pool.wait_ge(hc_ready, r * 4 + (2 * k + h + 1))
                        nc.gpsimd.tensor_tensor(u[:, h, :], dx[:, h, :], rows[:, k, 0, :], ALU.mult).then_inc(u_ready, 1)

                with pool.Fori(0, DS // 2 - 1) as r:
                    for k in range(2):
                        inputs(r, k)
                for k in range(2):
                    inputs(DS // 2 - 1, k)

            @block.vector
            def _(dve):
                v = nc.vector

                def states(r, k):
                    for h in range(2):
                        step = 2 * k + h
                        dve.wait_ge(da_ready, r * 4 + (step + 1))
                        dve.wait_ge(u_ready, r * 4 + (step + 1))
                        v.tensor_tensor_scan(u[:, h, :], da[:, h, :], u[:, h, :], 0.0, ALU.mult, ALU.add).then_inc(scanned, 1)
                        dve.wait_ge(scanned, r * 4 + (step + 3))
                        dve.wait_ge(added, r * 4 + (step + 1))
                        v.tensor_tensor(hc[:, h, :], u[:, h, :], rows[:, k, 1, :], ALU.mult).then_inc(hc_ready, 1)

                for h in range(2):
                    v.tensor_scalar(diag[:, h, :], c.ident[:, :], dvec[:, h:h + 1], None, ALU.mult).then_inc(diag_ready, 1)
                v.memset(start[:, 0:1], 0.0).then_inc(scanned, 2)
                v.memset(start[:, 1:2], 0.0).then_inc(hc_ready, 2)
                v.memset(start[:, 2:3], 0.0).then_inc(added, 2)
                with dve.Fori(0, DS // 2 - 1) as r:
                    for k in range(2):
                        states(r, k)
                for k in range(2):
                    states(DS // 2 - 1, k)

            @block.tensor
            def _(pe):
                def add_state(r, k, closing):
                    for h in range(2):
                        pe.wait_ge(hc_ready, r * 4 + (2 * k + h + 3))
                        for b in range(NC):
                            last = nc.tensor.matmul(ps[:, 4 * h + b, :], c.ident[:, :], hc[:, h, b * 512:(b + 1) * 512],
                                                    start=False, stop=closing)
                        last.then_inc(added, 1)

                pe.wait_ge(diag_ready, 2)
                for h in range(2):
                    for b in range(NC):
                        nc.tensor.matmul(ps[:, 4 * h + b, :], diag[:, h, :], xv[:, h, b * 512:(b + 1) * 512], start=True, stop=False)
                with pe.Fori(0, DS // 2 - 1) as r:
                    for k in range(2):
                        add_state(r, k, False)
                for k in range(2):
                    add_state(DS // 2 - 1, k, k == 1)


def l1_ternary(c, ins):
    nc = c.nc
    c.layer = "l1f_"
    ps = c.ps
    with ExitStack() as ctx:
        w, wt = c.sb(ctx, "w", [P, P], F32), c.sb(ctx, "w_ternary", [P, 2, P], F32)
        wT = c.sb(ctx, "wT", [P, P], F32)
        alpha, bias = c.sb(ctx, "alpha", [P, 1], F32), c.sb(ctx, "bias", [P, P], F32)
        ones, thr = c.sb(ctx, "ones", [P, P], F32), c.sb(ctx, "threshold", [P, 3], F32)
        norm = NormBlock(c)
        w_loaded, chain, sums_ready, total_psum, w_ready, wT_psum, wT_ready, y_psum = (c.sem(n) for n in (
            "w_loaded", "chain", "sums_ready", "total_psum", "w_ready", "wT_psum", "wT_ready", "y_psum"))
        loads = [(w[:, :], ins["L1_ffn_weight"]), (alpha[:, :], row_view(ins["L1_ffn_alpha"], 1)), (bias[:, :], row_view(ins["L1_ffn_bias"], P))]
        with nc.Block() as block:
            @block.sync
            def _(sp):
                for dst, src in loads:
                    sp.dma_start(dst, src).then_inc(w_loaded, 16)

            @block.vector
            def _(dve):
                v = nc.vector
                link = Chain(dve, chain)
                link(v.memset(ones[:, :], 1.0))
                dve.wait_ge(w_loaded, 16 * len(loads))
                v.tensor_reduce(thr[:, 0:1], w[:, :], X, ALU.add, apply_absolute_value=True).then_inc(sums_ready, 1)
                dve.wait_ge(total_psum, 1)
                link(v.tensor_scalar(thr[:, 1:2], ps[:, 7, 0:1], 1.0 / (P * P), 0.7, ALU.mult, ALU.mult))
                link(v.tensor_scalar(thr[:, 2:3], thr[:, 1:2], -1.0, None, ALU.mult))
                link(v.tensor_scalar(wt[:, 0, :], w[:, :], thr[:, 1:2], alpha[:, :], ALU.is_gt, ALU.mult))
                link(v.tensor_scalar(wt[:, 1, :], w[:, :], thr[:, 2:3], alpha[:, :], ALU.is_lt, ALU.mult))
                v.tensor_tensor(wt[:, 0, :], wt[:, 0, :], wt[:, 1, :], ALU.subtract).then_inc(w_ready, 1)
                norm.vector(dve, link)
                link(v.tensor_tensor(c.x[:, :, :], c.x[:, :, :], bias[:, :].unsqueeze(1).to_broadcast([P, NT, P]), ALU.add))
                add_banks(c, dve, link, c.x, 4, y_psum)

            @block.tensor
            def _(pe):
                pe.wait_ge(sums_ready, 1)
                nc.tensor.matmul(ps[:, 7, 0:1], ones[:, :], thr[:, 0:1], start=True, stop=True).then_inc(total_psum, 1)
                pe.wait_ge(w_ready, 1)
                nc.tensor.transpose(ps[:, 6, 0:P], wt[:, 0, :], c.ident[:, :]).then_inc(wT_psum, 1)
                norm.tensor(pe)
                pe.wait_ge(wT_ready, 1)
                pe.wait_ge(norm.nT_ready, NC)
                project_tokens(c, c.nT, wT[:, :], 4, y_psum)

            @block.scalar
            def _(act):
                act.wait_ge(wT_psum, 1)
                nc.scalar.activation(wT[:, :], ps[:, 6, 0:P], ACT.Copy).then_inc(wT_ready, 1)
                norm.scalar(act, c.nT)


def l2_performer(c, ins):
    nc = c.nc
    c.layer = "l2a_"
    M, G, EPS = 32, 4, 1e-6
    W = 4 * (HD + 1)
    ps = c.ps
    with ExitStack() as ctx:
        b_out, woT = c.sb(ctx, "b_out", [P, P], F32), c.sb(ctx, "woT", [P, P], F32)
        with ExitStack() as fctx:
            w, wT = c.sb(fctx, "w", [P, 4, P], F32), c.sb(fctx, "wT", [P, 3, P], F32)
            bq, bk, bv = c.sb(fctx, "b_q", [P, 1], F32), c.sb(fctx, "b_k", [P, 1], F32), c.sb(fctx, "b_v", [P, P], F32)
            orf, orf_all = c.sb(fctx, "orf", [M, HD], F32), c.sb(fctx, "orf_all", [M, H, HD], F32)
            own, own4 = c.sb(fctx, "own_head", [P, H, M], F32), c.sb(fctx, "own_of_four", [P, 4, HD + 1], F32)
            feat, minus_norm = c.sb(fctx, "features", [P, H * M], F32), c.sb(fctx, "minus_norm", [P, H * M], F32)
            v1 = c.sb(fctx, "v_and_ones", [P, NT, H, HD + 1], F32)
            q2, k2 = c.sb(fctx, "q_squared", [P, T], F32), c.sb(fctx, "k_squared", [P, T], F32)
            phik, phiq = c.sb(fctx, "phi_k", [P, 4, H * M], F32), c.sb(fctx, "phi_q", [P, G, T], F32)
            kv = c.sb(fctx, "kv", [P, G, W], F32)
            rden = c.sb(fctx, "denominators", [P, NT, H], F32)
            norm = NormBlock(c)
            (w_loaded, chain, drawn, wT_psum, wT_ready, orf_ready, orf_psum, feat_ready, q_psum, q_ready, k_psum, k_ready, v_psum, v_ready,
             q2_ready, k2_ready, pk_psum, pk_exp, pk_ready, kv_psum, kv_ready, pq_psum, pq_exp, pq_ready, num_psum) = (c.sem(n) for n in (
                 "w_loaded", "chain", "drawn", "wT_psum", "wT_ready", "orf_ready", "orf_psum", "feat_ready", "q_psum", "q_ready", "k_psum",
                 "k_ready", "v_psum", "v_ready", "q2_ready", "k2_ready", "pk_psum", "pk_exp", "pk_ready", "kv_psum", "kv_ready",
                 "pq_psum", "pq_exp", "pq_ready", "num_psum"))
            loads = [(w[:, k, :], ins[f"L2_attn_W{m}"]) for k, m in enumerate("qkvo")]
            loads += [(bq[:, :], column(ins["L2_attn_bq"])), (bk[:, :], column(ins["L2_attn_bk"])),
                      (bv[:, :], row_view(ins["L2_attn_bv"], P)), (b_out[:, :], row_view(ins["L2_attn_bo"], P)), (orf[:, :], ins["L2_attn_orf"])]
            with nc.Block() as block:
                @block.sync
                def _(sp):
                    for dst, src in loads:
                        sp.dma_start(dst, src).then_inc(w_loaded, 16)

                @block.gpsimd
                def _(pool):
                    nc.gpsimd.memset(own[:, :, :], 1.0).then_inc(drawn, 1)
                    nc.gpsimd.memset(own4[:, :, :], 1.0).then_inc(drawn, 1)
                    for m, n, step, width in ((own, H, HD, M), (own4, 4, M, HD + 1)):
                        pool.wait_ge(drawn, 2 if m is own else 4)
                        nc.gpsimd.affine_select(out=m[:, :, :], in_=m[:, :, :], compare_op=ALU.is_ge, fill=0.0, base=0,
                                                pattern=[[-step, n], [0, width]], channel_multiplier=1).then_inc(drawn, 1)
                        pool.wait_ge(drawn, 3 if m is own else 5)
                        nc.gpsimd.affine_select(out=m[:, :, :], in_=m[:, :, :], compare_op=ALU.is_ge, fill=0.0, base=step - 1,
                                                pattern=[[step, n], [0, width]], channel_multiplier=-1).then_inc(drawn, 1)

                @block.tensor
                def _(pe):
                    pe.wait_ge(w_loaded, 16 * len(loads))
                    for k in range(4):
                        nc.tensor.transpose(ps[:, 6, k * P:(k + 1) * P], w[:, k, :], c.ident[:, :]).then_inc(wT_psum, 1)
                    pe.wait_ge(orf_ready, 1)
                    nc.tensor.transpose(ps[:, 7, 0:M], orf_all[:, :, :].rearrange("m h d -> m (h d)"), c.ident[0:M, 0:M]).then_inc(orf_psum, 1)
                    norm.tensor(pe)
                    pe.wait_ge(wT_ready, 2)
                    pe.wait_ge(feat_ready, 1)
                    pe.wait_ge(norm.nT_ready, NC)
                    project_channels(c, wT[:, 1, :], c.nT, 4, k_psum)
                    project_channels(c, wT[:, 0, :], c.nT, 0, q_psum)
                    pe.wait_ge(k_ready, NC)
                    project_tokens(c, c.nT, wT[:, 2, :], 4, v_psum)
                    pe.wait_ge(q_ready, NC)
                    pe.wait_ge(k2_ready, 1)
                    pe.wait_ge(v_ready, 4)

                    def keys(t):
                        if t >= 4:
                            pe.wait_ge(pk_exp, t - 3)
                        tok = slice(t * P, (t + 1) * P)
                        nc.tensor.matmul(ps[:, t % 4, :], c.kT[:, tok], feat[:, :], start=True, stop=False)
                        nc.tensor.matmul(ps[:, t % 4, :], k2[:, tok], minus_norm[:, :], start=False, stop=True).then_inc(pk_psum, 1)

                    keys(0)
                    keys(1)
                    for t in range(NT):
                        if t + 2 < NT:
                            keys(t + 2)
                        pe.wait_ge(pk_ready, t + 1)
                        for g in range(G):
                            last = nc.tensor.matmul(ps[:, 4 + g, 0:W], phik[:, t % 4, g * P:(g + 1) * P],
                                                    v1[:, t, 4 * g:4 * g + 4, :].rearrange("p h d -> p (h d)"), start=t == 0, stop=t == NT - 1)
                        last.then_inc(kv_psum, 1)
                    pe.wait_ge(q2_ready, 1)
                    for g in range(G):
                        for k in range(NC):
                            n = g * NC + k
                            if n == 0:
                                pe.wait_ge(pk_exp, NT)
                            if n >= 4:
                                pe.wait_ge(pq_exp, n - 3)
                            tok = slice(k * 512, (k + 1) * 512)
                            nc.tensor.matmul(ps[:, n % 4, :], feat[:, g * P:(g + 1) * P], c.qT[:, tok], start=True, stop=False)
                            nc.tensor.matmul(ps[:, n % 4, :], minus_norm[:, g * P:(g + 1) * P], q2[:, tok], start=False, stop=True).then_inc(pq_psum, 1)
                    pe.wait_ge(kv_ready, G)
                    pe.wait_ge(pq_exp, G * NC)
                    pe.wait_ge(pq_ready, G * NC)
                    for t in range(NT):
                        for g in range(G):
                            at = (t % 2) * G * W + g * W
                            last = nc.tensor.matmul(ps[:, t // 2, at:at + W], phiq[:, g, t * P:(t + 1) * P], kv[:, g, :], start=True, stop=True)
                        if t % 2:
                            last.then_inc(num_psum, 1)

                @block.scalar
                def _(act):
                    norm.scalar(act, c.nT)
                    act.wait_ge(w_loaded, 16 * len(loads))
                    evacuate(c, act, 4, c.kT, k_psum, 0, k_ready, bk[:, :])
                    evacuate(c, act, 0, c.qT, q_psum, 0, q_ready, bq[:, :])
                    for t in range(NT):
                        act.wait_ge(pk_psum, t + 1)
                        if t >= 4:
                            act.wait_ge(kv_psum, t - 3)
                        nc.scalar.activation(phik[:, t % 4, :], ps[:, t % 4, :], ACT.Exp).then_inc(pk_exp, 1)
                    for n in range(G * NC):
                        act.wait_ge(pq_psum, n + 1)
                        nc.scalar.activation(phiq[:, n // NC, (n % NC) * 512:(n % NC + 1) * 512], ps[:, n % 4, :], ACT.Exp).then_inc(pq_exp, 1)

                @block.vector
                def _(dve):
                    v = nc.vector
                    link = Chain(dve, chain)
                    dve.wait_ge(w_loaded, 16 * len(loads))
                    v.tensor_copy(orf_all[:, :, :], orf[:, :].unsqueeze(1).to_broadcast([M, H, HD])).then_inc(orf_ready, 1)
                    link(v.memset(v1[:, :, :, :], 1.0))
                    norm.vector(dve, link)
                    dve.wait_ge(wT_psum, 4)
                    v.tensor_copy(wT[:, :, :], ps[:, 6, 0:3 * P].rearrange("p (k n) -> p k n", k=3)).then_inc(wT_ready, 1)
                    v.tensor_copy(woT[:, :], ps[:, 6, 3 * P:4 * P]).then_inc(wT_ready, 1)
                    dve.wait_ge(drawn, 6)
                    dve.wait_ge(orf_psum, 1)
                    link(v.tensor_copy(rden[:, 0:2, :].rearrange("p a b -> p (a b)"), ps[:, 7, 0:M]))
                    feat3 = feat[:, :].rearrange("p (h m) -> p h m", h=H)
                    link(v.tensor_tensor(feat3, own[:, :, :], rden[:, 0:2, :].rearrange("p a b -> p (a b)").unsqueeze(1).to_broadcast([P, H, M]), ALU.mult))
                    link(v.tensor_scalar(feat[:, :], feat[:, :], HD ** -0.25, None, ALU.mult))
                    v.tensor_scalar(minus_norm[:, :].rearrange("p (h m) -> p h m", h=H), own[:, :, :], -0.5 * HD ** -0.5, None, ALU.mult).then_inc(feat_ready, 1)
                    for b in range(4):
                        dve.wait_ge(v_psum, b + 1)
                        v.tensor_tensor(v1[:, 4 * b:4 * b + 4, :, 0:HD], ps[:, 4 + b, :].rearrange("p (t h d) -> p t h d", t=4, h=H),
                                        bv[:, :].rearrange("p (h d) -> p h d", h=H).unsqueeze(1).to_broadcast([P, 4, H, HD]), ALU.add).then_inc(v_ready, 1)
                    dve.wait_ge(k_ready, NC)
                    v.tensor_tensor(k2[:, :], c.kT[:, :], c.kT[:, :], ALU.mult).then_inc(k2_ready, 1)
                    dve.wait_ge(q_ready, NC)
                    v.tensor_tensor(q2[:, :], c.qT[:, :], c.qT[:, :], ALU.mult).then_inc(q2_ready, 1)
                    for t in range(NT):
                        dve.wait_ge(pk_exp, t + 1)
                        v.tensor_scalar(phik[:, t % 4, :], phik[:, t % 4, :], EPS, M ** -0.5, ALU.add, ALU.mult).then_inc(pk_ready, 1)
                    dve.wait_ge(kv_psum, NT)
                    for g in range(G):
                        v.tensor_tensor(kv[:, g, :], ps[:, 4 + g, 0:W], own4[:, :, :].rearrange("p h d -> p (h d)"), ALU.mult).then_inc(kv_ready, 1)
                    for n in range(G * NC):
                        dve.wait_ge(pq_exp, n + 1)
                        part = phiq[:, n // NC, (n % NC) * 512:(n % NC + 1) * 512]
                        v.tensor_scalar(part, part, EPS, M ** -0.5, ALU.add, ALU.mult).then_inc(pq_ready, 1)
                    for b in range(8):
                        dve.wait_ge(num_psum, b + 1)
                        num = ps[:, b, 0:2 * G * W].rearrange("p (t h d) -> p t h d", t=2, h=H)
                        two = slice(2 * b, 2 * b + 2)
                        link(v.reciprocal(rden[:, two, :], num[:, :, :, HD]))
                        link(v.tensor_tensor(c.a[:, two, :].rearrange("p t (h d) -> p t h d", h=H), num[:, :, :, 0:HD],
                                             rden[:, two, :].unsqueeze(3).to_broadcast([P, 2, H, HD]), ALU.mult))
        attention_out(c, woT, b_out, c.x, then_into_x=False)


class Routed:

    def __init__(self, c, ctx, E, K):
        nc, sb = c.nc, c.sb
        self.E = E
        self.tiles = (K * T + E * (P - 1)) // P + 1
        self.listed = self.tiles + 2
        self.expert_of = sb(ctx, "expert_of_tile", [1, self.listed], mybir.dt.int32)
        self.q = sb(ctx, "gathered_q", [P, 2, P], F32)
        self.index = sb(ctx, "gathered_index", [P, 2], mybir.dt.uint32)
        self.qparts = sb(ctx, "gathered_q_parts", [P, 3, P], BF16)
        self.qrest = sb(ctx, "gathered_q_rest", [P, P], F32)
        self.outT = sb(ctx, "outT", [P, P], F32)
        self.y = sb(ctx, "y", [P, P], F32)
        self.w_out_now = sb(ctx, "w_out_now", [P, P], F32)
        self.list_dram = nc.dram_tensor("query_list_dram", [self.listed, P], mybir.dt.uint32, kind="Internal").ap()
        self.q_dram = nc.dram_tensor("expert_q_dram", [E * T, P], F32, kind="Internal").ap()
        self.v_dram = nc.dram_tensor("expert_v_dram", [E, P, NT, H, HD + 1], F32, kind="Internal").ap()
        self.w_out_dram = nc.dram_tensor("expert_w_out_dram", [E, P, P], F32, kind="Internal").ap()
        self.y_dram = nc.dram_tensor("expert_y_dram", [self.tiles + 1, P, P], F32, kind="Internal").ap()


def l2_ffn(c, at, ins):
    c.layer = "l2f_"
    E, K = 8, 2
    with ExitStack() as ctx:
        rt = Routed(c, ctx, E, K)
        gate = c.sb(ctx, "gate", [P, K, NT], F32)
        slot = c.sb(ctx, "slot", [P, K, NT], mybir.dt.uint32)
        row = c.sb(ctx, "row", [P, K, NT], mybir.dt.uint32)
        y_row = c.sb(ctx, "y_row", [P, K, NT], mybir.dt.uint32)
        l2_router(c, ins, rt, E, K, gate, slot, row, y_row)
        l2_prepare(c, at, ins, rt, slot, row)
        attention_loop(c, at, routed=rt)
        l2_collect(c, rt, gate, y_row)


def l2_router(c, ins, rt, E, K, gate, slot, row, y_row):
    nc, ps = c.nc, c.ps
    W = P // 2
    with ExitStack() as ctx:
        w1, w2, ob = c.sb(ctx, "rw1", [W, P], F32), c.sb(ctx, "rw2", [E, W], F32), c.sb(ctx, "ob", [E, P], F32)
        b1, g1, g0, b2 = (c.sb(ctx, n, [P, w], F32) for n, w in (("rb1", W), ("ln_g", W), ("ln_b", W), ("rb2", E)))
        w1T, w2T = c.sb(ctx, "rw1T", [P, W], F32), c.sb(ctx, "rw2T", [W, E], F32)
        h, hh = c.sb(ctx, "hidden", [P, NT, W], F32), c.sb(ctx, "hidden_squared", [P, NT, W], F32)
        hT = c.sb(ctx, "hiddenT", [W, T], F32)
        probs, masked, sel, mix, tmp = (c.sb(ctx, n, [P, NT, E], F32) for n in ("probs", "masked", "selected", "mix", "tmp"))
        choice = c.sb(ctx, "choice", [P, K, NT, E], F32)
        best = c.sb(ctx, "best", [P, K, NT], F32)
        tie, total = c.sb(ctx, "tie", [P, NT], F32), c.sb(ctx, "total", [P, NT], F32)
        order, edge = c.sb(ctx, "order", [P, E], F32), c.sb(ctx, "edge", [P, NT], F32)
        before, ones = c.sb(ctx, "before", [P, P], F32), c.sb(ctx, "ones", [P, P], F32)
        counts, offset = c.sb(ctx, "tile_counts", [P, NT, E], F32), c.sb(ctx, "tile_offset", [P, NT, E], F32)
        more, tiles_of = c.sb(ctx, "more", [P, E, NT], F32), c.sb(ctx, "tiles_of", [P, E], F32)
        first, end, index = c.sb(ctx, "first_tile", [P, E], F32), c.sb(ctx, "end_tile", [P, E], F32), c.sb(ctx, "partition", [P, 1], F32)
        passed, of_tile = c.sb(ctx, "passed", [P, E], F32), c.sb(ctx, "of_tile", [P, 1], F32)
        where = c.sb(ctx, "where", [P, NT], F32)
        mixT = c.sb(ctx, "mixT", [E, T], F32)
        norm = NormBlock(c)
        (w_loaded, drawn, chain, wT_psum, wT_ready, h_psum, hvar_ready, hstd_ready, h_ready, hT_psum, hT_ready, lg_psum, shifted, exp_ready,
         sel_ready, rank_psum, mix_ready, mixT_psum, mixT_ready, ranked, of_tile_ready, of_tile_psum, ob_psum) = (c.sem("r_" + n) for n in (
             "w_loaded", "drawn", "chain", "wT_psum", "wT_ready", "h_psum", "hvar_ready", "hstd_ready", "h_ready", "hT_psum", "hT_ready",
             "lg_psum", "shifted", "exp_ready", "sel_ready", "rank_psum", "mix_ready", "mixT_psum", "mixT_ready", "ranked", "of_tile_ready",
             "of_tile_psum", "ob_psum"))
        loads = [(w1[:, :], ins["L2_ffn_rW1"]), (w2[:, :], ins["L2_ffn_rW2"]), (ob[:, :], ins["L2_ffn_ob"]),
                 (b1[:, :], row_view(ins["L2_ffn_rb1"], W)), (g1[:, :], row_view(ins["L2_ffn_ln_g"], W)),
                 (g0[:, :], row_view(ins["L2_ffn_ln_b"], W)), (b2[:, :], row_view(ins["L2_ffn_rb2"], E))]
        DRAWN = E + NT + 3

        def per_token(s, width):
            return s.unsqueeze(2).to_broadcast([P, NT, width])

        def per_column(s, width):
            return s.unsqueeze(1).to_broadcast([P, NT, width])

        with nc.Block() as block:
            @block.sync
            def _(sp):
                for dst, src in loads:
                    sp.dma_start(dst, src).then_inc(w_loaded, 16)

            @block.gpsimd
            def _(pool):
                draw_order(c, pool, order, E, drawn)
                for t in range(NT):
                    nc.gpsimd.memset(edge[:, t:t + 1], float(P * t)).then_inc(drawn, 1)
                nc.gpsimd.memset(ones[:, :], 1.0).then_inc(drawn, 1)
                nc.gpsimd.memset(before[:, :], 1.0).then_inc(drawn, 1)
                pool.wait_ge(drawn, DRAWN - 1)
                nc.gpsimd.affine_select(out=before[:, :], in_=before[:, :], compare_op=ALU.is_gt, fill=0.0, base=0,
                                        pattern=[[1, P]], channel_multiplier=-1).then_inc(drawn, 1)

            @block.tensor
            def _(pe):
                pe.wait_ge(w_loaded, 16 * len(loads))
                nc.tensor.transpose(ps[:, 4, 0:W], w1[:, :], c.ident[0:W, 0:W])
                nc.tensor.transpose(ps[0:W, 4, W:W + E], w2[:, :], c.ident[0:E, 0:E]).then_inc(wT_psum, 1)
                norm.tensor(pe)
                pe.wait_ge(wT_ready, 2)
                pe.wait_ge(norm.nT_ready, NC)
                for t in range(NT):
                    ins_ = nc.tensor.matmul(ps[:, 4 + t // 8, (t % 8) * W:(t % 8 + 1) * W], c.nT[:, t * P:(t + 1) * P], w1T[:, :],
                                            start=True, stop=True)
                    if t % 8 == 7:
                        ins_.then_inc(h_psum, 1)
                pe.wait_ge(h_ready, 1)
                for t in range(NT):
                    ins_ = nc.tensor.transpose(ps[0:W, t // 4, (t % 4) * P:(t % 4 + 1) * P], h[:, t, :], c.ident[:, :])
                    if t % 4 == 3:
                        ins_.then_inc(hT_psum, 1)
                pe.wait_ge(hT_ready, NC)
                for t in range(NT):
                    last = nc.tensor.matmul(ps[:, 6, t * E:(t + 1) * E], hT[:, t * P:(t + 1) * P], w2T[:, :], start=True, stop=True)
                last.then_inc(lg_psum, 1)
                pe.wait_ge(drawn, DRAWN)
                pe.wait_ge(sel_ready, 1)
                chosen = sel[:, :, :].rearrange("p t e -> p (t e)")
                nc.tensor.matmul(ps[:, 7, 0:P], before[:, :], chosen, start=True, stop=True)
                nc.tensor.matmul(ps[:, 7, P:2 * P], ones[:, :], chosen, start=True, stop=True)
                nc.tensor.matmul(ps[:, 7, 2 * P:2 * P + 1], before[:, :], ones[:, 0:1], start=True, stop=True).then_inc(rank_psum, 1)
                pe.wait_ge(mix_ready, 1)
                for t in range(NT):
                    ins_ = nc.tensor.transpose(ps[0:E, t // 4, (t % 4) * P:(t % 4 + 1) * P], mix[:, t, :], c.ident[:, :])
                    if t % 4 == 3:
                        ins_.then_inc(mixT_psum, 1)
                pe.wait_ge(of_tile_ready, 1)
                nc.tensor.transpose(ps[0:1, 6, 0:P], of_tile[:, :], c.ident[:, :]).then_inc(of_tile_psum, 1)
                pe.wait_ge(mixT_ready, NC)
                pe.wait_ge(ranked, 1)
                for t in range(NT):
                    ins_ = nc.tensor.matmul(ps[:, 4 + t // 4, (t % 4) * P:(t % 4 + 1) * P], mixT[:, t * P:(t + 1) * P], ob[:, :],
                                            start=True, stop=True)
                    if t % 4 == 3:
                        ins_.then_inc(ob_psum, 1)

            @block.scalar
            def _(act):
                act.wait_ge(wT_psum, 1)
                nc.scalar.activation(w1T[:, :], ps[:, 4, 0:W], ACT.Copy).then_inc(wT_ready, 1)
                nc.scalar.activation(w2T[:, :], ps[0:W, 4, W:W + E], ACT.Copy).then_inc(wT_ready, 1)
                norm.scalar(act, c.nT)
                act.wait_ge(hvar_ready, 1)
                nc.scalar.activation(total[:, :], total[:, :], ACT.Sqrt).then_inc(hstd_ready, 1)
                for k in range(NC):
                    act.wait_ge(hT_psum, k + 1)
                    nc.scalar.activation(hT[:, k * 512:(k + 1) * 512], ps[0:W, k, :], ACT.Copy).then_inc(hT_ready, 1)
                act.wait_ge(shifted, 1)
                nc.scalar.activation(probs[:, :, :], probs[:, :, :], ACT.Exp).then_inc(exp_ready, 1)
                for k in range(NC):
                    act.wait_ge(mixT_psum, k + 1)
                    nc.scalar.activation(mixT[:, k * 512:(k + 1) * 512], ps[0:E, k, :], ACT.Copy).then_inc(mixT_ready, 1)

            @block.vector
            def _(dve):
                v = nc.vector
                link = Chain(dve, chain)
                norm.vector(dve, link)
                dve.wait_ge(w_loaded, 16 * len(loads))
                for b in range(2):
                    dve.wait_ge(h_psum, b + 1)
                    link(v.tensor_tensor(h[:, 8 * b:8 * b + 8, :], ps[:, 4 + b, :].rearrange("p (t w) -> p t w", w=W),
                                         b1[:, :].unsqueeze(1).to_broadcast([P, 8, W]), ALU.add))
                link(v.tensor_reduce(total[:, :], h[:, :, :], X, ALU.add))
                link(v.tensor_scalar(tie[:, :], total[:, :], 1.0 / W, None, ALU.mult))
                link(v.tensor_tensor(h[:, :, :], h[:, :, :], per_token(tie[:, :], W), ALU.subtract))
                link(v.tensor_tensor(hh[:, :, :], h[:, :, :], h[:, :, :], ALU.mult))
                link(v.tensor_reduce(tie[:, :], hh[:, :, :], X, ALU.add))
                v.tensor_scalar(total[:, :], tie[:, :], 1.0 / W, 1e-5, ALU.mult, ALU.add).then_inc(hvar_ready, 1)
                dve.wait_ge(hstd_ready, 1)
                link(v.reciprocal(tie[:, :], total[:, :]))
                link(v.tensor_tensor(h[:, :, :], h[:, :, :], per_token(tie[:, :], W), ALU.mult))
                link(v.tensor_tensor(h[:, :, :], h[:, :, :], per_column(g1[:, :], W), ALU.mult))
                link(v.tensor_tensor(h[:, :, :], h[:, :, :], per_column(g0[:, :], W), ALU.add))
                v.tensor_scalar(h[:, :, :], h[:, :, :], 0.0, None, ALU.max).then_inc(h_ready, 1)
                dve.wait_ge(lg_psum, 1)
                link(v.tensor_tensor(masked[:, :, :], ps[:, 6, 0:NT * E].rearrange("p (t e) -> p t e", e=E), per_column(b2[:, :], E), ALU.add))
                link(v.tensor_reduce(tie[:, :], masked[:, :, :], X, ALU.max))
                v.tensor_tensor(probs[:, :, :], masked[:, :, :], per_token(tie[:, :], E), ALU.subtract).then_inc(shifted, 1)
                dve.wait_ge(exp_ready, 1)
                link(v.tensor_reduce(total[:, :], probs[:, :, :], X, ALU.add))
                link(v.reciprocal(tie[:, :], total[:, :]))
                link(v.tensor_tensor(probs[:, :, :], probs[:, :, :], per_token(tie[:, :], E), ALU.mult))
                dve.wait_ge(drawn, DRAWN)
                top_choice(c, v, link, probs[:, :, :], best[:, 0, :], tie[:, :], order[:, :], choice[:, 0], E)
                link(v.scalar_tensor_tensor(masked[:, :, :], choice[:, 0], MASKED, probs[:, :, :], ALU.mult, ALU.add))
                top_choice(c, v, link, masked[:, :, :], best[:, 1, :], tie[:, :], order[:, :], choice[:, 1], E)
                v.tensor_tensor(sel[:, :, :], choice[:, 0], choice[:, 1], ALU.add).then_inc(sel_ready, 1)
                link(v.tensor_tensor(total[:, :], best[:, 0, :], best[:, 1, :], ALU.add))
                link(v.reciprocal(tie[:, :], total[:, :]))
                for k in range(K):
                    link(v.tensor_tensor(gate[:, k, :], best[:, k, :], tie[:, :], ALU.mult))
                link(v.tensor_tensor(mix[:, :, :], choice[:, 0], per_token(gate[:, 0, :], E), ALU.mult))
                link(v.tensor_tensor(tmp[:, :, :], choice[:, 1], per_token(gate[:, 1, :], E), ALU.mult))
                v.tensor_tensor(mix[:, :, :], mix[:, :, :], tmp[:, :, :], ALU.add).then_inc(mix_ready, 1)
                dve.wait_ge(mix_ready, 1)
                dve.wait_ge(rank_psum, 1)
                link(v.tensor_copy(counts[:, :, :], ps[:, 7, P:2 * P].rearrange("p (t e) -> p t e", e=E)))
                link(v.tensor_copy(index[:, :], ps[:, 7, 2 * P:2 * P + 1]))
                link(v.memset(offset[:, 0, :], 0.0))
                for t in range(1, NT):
                    link(v.tensor_tensor(offset[:, t, :], offset[:, t - 1, :], counts[:, t - 1, :], ALU.add))
                link(v.tensor_tensor(end[:, :], offset[:, NT - 1, :], counts[:, NT - 1, :], ALU.add))
                link(v.tensor_tensor(more[:, :, :], end[:, :].unsqueeze(2).to_broadcast([P, E, NT]),
                                     edge[:, :].unsqueeze(1).to_broadcast([P, E, NT]), ALU.is_gt))
                link(v.tensor_reduce(tiles_of[:, :], more[:, :, :], X, ALU.add))
                link(v.memset(first[:, 0:1], 0.0))
                for e in range(1, E):
                    link(v.tensor_tensor(first[:, e:e + 1], first[:, e - 1:e], tiles_of[:, e - 1:e], ALU.add))
                link(v.tensor_tensor(end[:, :], first[:, :], tiles_of[:, :], ALU.add))
                link(v.tensor_scalar(passed[:, :], end[:, :], index[:, 0:1], None, ALU.is_le))
                link(v.tensor_reduce(of_tile[:, :], passed[:, :], X, ALU.add))
                v.tensor_scalar(of_tile[:, :], of_tile[:, :], float(E - 1), None, ALU.min).then_inc(of_tile_ready, 1)
                link(v.tensor_scalar(first[:, :], first[:, :], float(P), None, ALU.mult))
                link(v.tensor_tensor(offset[:, :, :], offset[:, :, :], per_column(first[:, :], E), ALU.add))
                link(v.tensor_tensor(offset[:, :, :], offset[:, :, :], ps[:, 7, 0:P].rearrange("p (t e) -> p t e", e=E), ALU.add))
                for k in range(K):
                    link(v.tensor_tensor(tmp[:, :, :], choice[:, k], offset[:, :, :], ALU.mult))
                    link(v.tensor_reduce(where[:, :], tmp[:, :, :], X, ALU.add))
                    link(v.tensor_copy(slot[:, k, :], where[:, :]))
                    link(v.tensor_scalar(y_row[:, k, :], where[:, :], float(P), None, ALU.add))
                    link(v.tensor_tensor(tmp[:, :, :], choice[:, k], per_column(order[:, :], E), ALU.mult))
                    link(v.tensor_reduce(where[:, :], tmp[:, :, :], X, ALU.add))
                    link(v.tensor_scalar(where[:, :], where[:, :], -float(T), float(E * T), ALU.mult, ALU.add))
                    link(v.tensor_tensor(where[:, :], where[:, :], edge[:, :], ALU.add))
                    link(v.tensor_scalar(row[:, k, :], where[:, :], index[:, 0:1], None, ALU.add))
                dve.wait_ge(of_tile_psum, 1)
                v.tensor_copy(rt.expert_of[:, :], ps[0:1, 6, 0:rt.listed]).then_inc(ranked, 1)
                add_banks(c, dve, link, c.x, 4, ob_psum)


def l2_prepare(c, at, ins, rt, slot, row):
    nc, ps = c.nc, c.ps
    E, K = rt.E, 2
    with ExitStack() as ctx:
        w = c.sb(ctx, "w_qkvo", [P, 2, 4, P], F32)
        bq, bv, bk = c.sb(ctx, "b_q", [P, 2, P], F32), c.sb(ctx, "b_v", [P, 2, P], F32), c.sb(ctx, "b_k", [P, 2], F32)
        wT = c.sb(ctx, "wT_qkvo", [P, 4, P], F32)
        blank = c.sb(ctx, "blank_list", [rt.listed, P], mybir.dt.uint32)
        start = c.sb(ctx, "p_start_credit", [P, 8], F32)
        w_loaded = [c.sem(f"p_w_loaded{k}") for k in range(2)]
        (wT_psum, wT_ready, k_psum, k_ready, v_psum, v_ready, q_psum, q_ready, parts_ready, chain, parts_stored, v_stored, q_stored, o_stored,
         blanked, scattered) = (c.sem("p_" + n) for n in (
             "wT_psum", "wT_ready", "k_psum", "k_ready", "v_psum", "v_ready", "q_psum", "q_ready", "parts_ready", "chain", "parts_stored",
             "v_stored", "q_stored", "o_stored", "blanked", "scattered"))
        LOADS = 4 + 2 + 2
        with nc.Block() as block:
            def each_expert(eng, body):
                with eng.Fori(0, E // 2) as r:
                    for k in range(2):
                        body(r * 2 + k, k, r)

            @block.sync
            def _(sp):
                def load(k, e):
                    def vector(name):
                        return ins[name][bass.ds(e, 1)]
                    for n, m in enumerate("qkvo"):
                        sp.dma_start(w[:, k, n, :], ins[f"L2_ffn_{m}W"][bass.ds(e, 1)].rearrange("e p d -> (e p) d")).then_inc(w_loaded[k], 16)
                    sp.dma_start(bq[:, k, :], vector("L2_ffn_qb").to_broadcast([P, P])).then_inc(w_loaded[k], 16)
                    sp.dma_start(bv[:, k, :], vector("L2_ffn_vb").to_broadcast([P, P])).then_inc(w_loaded[k], 16)
                    for j in range(2):
                        sp.dma_start(bk[64 * j:64 * j + 64, k:k + 1], vector("L2_ffn_kb").rearrange("e (p j d) -> j d p e", p=NPAIR, j=2)[j],
                                     allow_slow_non_contiguous=True).then_inc(w_loaded[k], 16)

                def stores(e, k, r):
                    sp.wait_ge(wT_ready, e * 3 + 3)
                    sp.dma_start(rt.w_out_dram[bass.ds(e, 1)].rearrange("e p d -> (e p) d"), wT[:, 3, :]).then_inc(o_stored, 16)
                    store_keys(c, at, sp, e, parts_ready, e + 2, parts_stored)
                    sp.wait_ge(v_ready, e * 4 + 8)
                    sp.dma_start(rt.v_dram[bass.ds(e, 1)].rearrange("e p t h d -> (e p) (t h d)"),
                                 at.v[:, 0].rearrange("p t h d -> p (t h d)")).then_inc(v_stored, 16)
                    sp.wait_ge(q_ready, e * 4 + 8)
                    sp.dma_start(rt.q_dram[bass.ds(e * T, T), :].rearrange("(t p) d -> p t d", p=P), c.a).then_inc(q_stored, 16)
                    load(k, (e + 2) % E)

                for k in range(2):
                    load(k, k)
                each_expert(sp, stores)
                for k in range(2):
                    sp.wait_ge(w_loaded[k], 16 * LOADS * (E // 2 + 1))
                sp.wait_ge(parts_stored, 48 * (E + 1))
                for s in (v_stored, q_stored, o_stored):
                    sp.wait_ge(s, 16 * (E + 1))

            @block.gpsimd
            def _(pool):
                nc.gpsimd.memset(blank[:, :], 0).then_inc(blanked, 1)
                pool.wait_ge(blanked, 1)
                pool.dma_start(rt.list_dram[:, :], blank[:, :]).then_inc(scattered, 16)
                pool.wait_ge(scattered, 16)
                for t in range(NT):
                    for k in range(K):
                        nc.gpsimd.indirect_dma_start(out=rt.list_dram.rearrange("i (p a) -> (i p) a", a=1),
                                                     out_offset=bass.IndirectOffsetOnAxis(ap=slot[:, k, t:t + 1], axis=0),
                                                     in_=row[:, k, t:t + 1], in_offset=None).then_inc(scattered, 16)
                pool.wait_ge(scattered, 16 * (1 + K * NT))

            @block.tensor
            def _(pe):
                def project(e, k, r):
                    pe.wait_ge(w_loaded[k], r * (16 * LOADS) + 16 * LOADS)
                    pe.wait_ge(v_ready, e * 4 + 4)
                    for n in range(4):
                        last = nc.tensor.transpose(ps[:, 7, n * P:(n + 1) * P], w[:, k, n, :], c.ident[:, :])
                    last.then_inc(wT_psum, 1)
                    pe.wait_ge(wT_ready, e * 3 + 3)
                    pe.wait_ge(q_ready, e * 4 + 4)
                    project_channels(c, wT[:, 1, :], c.nT, 0, k_psum)
                    project_tokens(c, c.nT, wT[:, 2, :], 4, v_psum)
                    pe.wait_ge(k_ready, e * 4 + 4)
                    project_tokens(c, c.nT, wT[:, 0, :], 0, q_psum)

                each_expert(pe, project)

            @block.scalar
            def _(act):
                def copies(e, k, r):
                    act.wait_ge(wT_psum, e + 1)
                    act.wait_ge(q_psum, e * 4 + 4)
                    act.wait_ge(o_stored, e * 16 + 16)
                    for n in range(2):
                        nc.scalar.activation(split_heads(wT[:, n, :]), head_order(ps[:, 7, n * P:(n + 1) * P]), ACT.Copy).then_inc(wT_ready, 1)
                    nc.scalar.activation(wT[:, 2:4, :].rearrange("p n d -> p (n d)"), ps[:, 7, 2 * P:4 * P], ACT.Copy).then_inc(wT_ready, 1)
                    act.wait_ge(parts_ready, e + 1)
                    act.wait_ge(w_loaded[k], r * (16 * LOADS) + 16 * LOADS)
                    for n in range(NC):
                        act.wait_ge(k_psum, e * 4 + (n + 1))
                        nc.scalar.activation(c.kT[:, n * 512:(n + 1) * 512], ps[:, n, :], ACT.Identity, bias=bk[:, k:k + 1]).then_inc(k_ready, 1)

                each_expert(act, copies)

            @block.vector
            def _(dve):
                v = nc.vector
                rest = c.b[:, :, :].rearrange("p t d -> p (t d)")
                for n, (s, credit) in enumerate(((parts_ready, 1), (q_psum, 4), (q_ready, 4), (v_ready, 4), (parts_stored, 48),
                                                 (v_stored, 16), (q_stored, 16), (o_stored, 16))):
                    v.memset(start[:, n:n + 1], 0.0).then_inc(s, credit)

                def biases(e, k, r):
                    dve.wait_ge(w_loaded[k], r * (16 * LOADS) + 16 * LOADS)
                    dve.wait_ge(k_ready, e * 4 + 4)
                    dve.wait_ge(parts_stored, e * 48 + 48)
                    v.tensor_copy(at.hi[:, :], c.kT).then_inc(chain, 1)
                    dve.wait_ge(chain, e * 3 + 1)
                    v.tensor_tensor(rest, c.kT, at.hi[:, :], ALU.subtract).then_inc(chain, 1)
                    dve.wait_ge(chain, e * 3 + 2)
                    v.tensor_copy(at.mid[:, :], rest).then_inc(chain, 1)
                    dve.wait_ge(chain, e * 3 + 3)
                    v.tensor_tensor(at.lo[:, :], rest, at.mid[:, :], ALU.subtract).then_inc(parts_ready, 1)
                    dve.wait_ge(v_stored, e * 16 + 16)
                    for b in range(4):
                        dve.wait_ge(v_psum, e * 4 + (b + 1))
                        v.tensor_tensor(at.v[:, 0, 4 * b:4 * b + 4, :, 0:HD], ps[:, 4 + b, :].rearrange("p (t h d) -> p t h d", t=4, h=H),
                                        bv[:, k, :].rearrange("p (h d) -> p h d", h=H).unsqueeze(1).to_broadcast([P, 4, H, HD]),
                                        ALU.add).then_inc(v_ready, 1)
                    dve.wait_ge(q_stored, e * 16 + 16)
                    for b in range(4):
                        dve.wait_ge(q_psum, e * 4 + (b + 5))
                        for t in range(4 * b, 4 * b + 4):
                            last = v.tensor_tensor(split_heads(c.a[:, t, :]), split_heads(ps[:, b, (t % 4) * P:(t % 4 + 1) * P]),
                                                   head_order(bq[:, k, :]), ALU.add)
                        last.then_inc(q_ready, 1)

                each_expert(dve, biases)


def l2_collect(c, rt, gate, y_row):
    nc = c.nc
    gathered, added = [c.sem(f"c_gathered{k}") for k in range(2)], c.sem("c_added")
    y = (c.a, c.b)
    with nc.Block() as block:
        @block.gpsimd
        def _(pool):
            for t in range(NT):
                for k in range(2):
                    nc.gpsimd.indirect_dma_start(out=y[k][:, t, :], out_offset=None, in_=rt.y_dram.rearrange("i p d -> (i p) d"),
                                                 in_offset=bass.IndirectOffsetOnAxis(ap=y_row[:, k, t:t + 1], axis=0)).then_inc(gathered[k], 16)
                    pool.wait_ge(gathered[k], 16 * (t + 1))

        @block.vector
        def _(dve):
            for t in range(NT):
                for k in range(2):
                    dve.wait_ge(gathered[k], 16 * (t + 1))
                    nc.vector.scalar_tensor_tensor(c.x[:, t, :], y[k][:, t, :], gate[:, k, t:t + 1], c.x[:, t, :],
                                                   ALU.mult, ALU.add).then_inc(added, 1)
                    dve.wait_ge(added, 2 * t + k + 1)


def l3_state(c, ins):
    nc = c.nc
    c.layer = "l3a_"
    N, KC = 64, 4
    ps = c.ps
    with ExitStack() as ctx:
        xp = c.sb(ctx, "n_padded", [P, KC - 1 + T], F32)
        conv, conv_w, conv_b = c.sb(ctx, "conv", [P, T], F32), c.sb(ctx, "conv_w", [P, KC], F32), c.sb(ctx, "conv_b", [P, 1], F32)
        wp, ws, w_out, b_out = c.sb(ctx, "wp", [P, 2 * N], F32), c.sb(ctx, "ws", [P, N], F32), c.sb(ctx, "w_out", [N, P], F32), c.sb(ctx, "b_out", [P, P], F32)
        bp, bs = c.sb(ctx, "bp", [N, 2], F32), c.sb(ctx, "bs", [N, 1], F32)
        log, sp_, tl = c.sb(ctx, "a_dt_log", [N, 2], F32), c.sb(ctx, "a_dt", [N, 2], F32), c.sb(ctx, "a_dt_tail", [N, 2], F32)
        decay = c.sb(ctx, "decay", [N, 1], F32)
        u, b_t, c_t, mag = (c.sb(ctx, n, [N, T], F32) for n in ("u", "b_t", "c_t", "magnitude"))
        norm = NormBlock(c)
        w_loaded, chain, act_chain, conv_ready, u_psum, u_ready, p_psum, c_ready, tail_ready, dt_ready, y_ready, y_psum = (c.sem(n) for n in (
            "w_loaded", "chain", "act_chain", "conv_ready", "u_psum", "u_ready", "p_psum", "c_ready", "tail_ready", "dt_ready", "y_ready", "y_psum"))
        loads = [(conv_w[:, :], ins["L3_attn_conv_w"].rearrange("k a d -> d (k a)")), (conv_b[:, :], column(ins["L3_attn_conv_b"])),
                 (wp[:, :], ins["L3_attn_Wp"]), (bp[:, :], ins["L3_attn_bp"].rearrange("(k n) -> n k", n=N)), (ws[:, :], ins["L3_attn_Ws"]),
                 (bs[:, :], column(ins["L3_attn_bs"])), (log[:, 0:1], column(ins["L3_attn_A_log"])), (log[:, 1:2], column(ins["L3_attn_dt_log"])),
                 (w_out[:, :], ins["L3_attn_Wo"]), (b_out[:, :], row_view(ins["L3_attn_bo"], P))]

        def flat(bank0):
            return ps[0:N, bank0:bank0 + 4, :].rearrange("p b n -> p (b n)")

        with nc.Block() as block:
            @block.sync
            def _(sp):
                for dst, src in loads:
                    sp.dma_start(dst, src, allow_slow_non_contiguous=True).then_inc(w_loaded, 16)

            @block.tensor
            def _(pe):
                norm.tensor(pe)
                pe.wait_ge(w_loaded, 16 * len(loads))
                pe.wait_ge(norm.nT_ready, NC)
                for k in range(NC):
                    last = nc.tensor.matmul(ps[0:N, 4 + k, :], ws[:, :], xp[:, KC - 1 + k * 512:KC - 1 + (k + 1) * 512], start=True, stop=True)
                last.then_inc(u_psum, 1)
                pe.wait_ge(conv_ready, 1)
                for part in range(2):
                    if part:
                        pe.wait_ge(u_ready, 1)
                    for k in range(NC):
                        last = nc.tensor.matmul(ps[0:N, 4 * part + k, :], wp[:, part * N:(part + 1) * N], conv[:, k * 512:(k + 1) * 512],
                                                start=True, stop=True)
                    last.then_inc(p_psum, 1)
                pe.wait_ge(y_ready, 1)
                project_tokens(c, c_t, w_out[:, :], 4, y_psum)

            @block.scalar
            def _(act):
                link = Chain(act, act_chain)
                norm.scalar(act, xp[:, KC - 1:])
                act.wait_ge(w_loaded, 16 * len(loads))
                act.wait_ge(u_psum, 1)
                nc.scalar.activation(u[:, :], flat(4), ACT.Identity, bias=bs[:, :]).then_inc(u_ready, 1)
                softplus_scalar(c, act, link, log[:, :], 0.0, sp_[:, :], tl[:, :]).then_inc(dt_ready, 1)
                act.wait_ge(p_psum, 1)
                softplus_scalar(c, act, link, flat(0), bp[:, 0:1], mag[:, :], b_t[:, :]).then_inc(tail_ready, 1)
                act.wait_ge(p_psum, 2)
                nc.scalar.activation(c_t[:, :], flat(4), ACT.Tanh, bias=bp[:, 1:2]).then_inc(c_ready, 1)

            @block.vector
            def _(dve):
                v = nc.vector
                link = Chain(dve, chain)
                link(v.memset(xp[:, 0:KC - 1], 0.0))
                norm.vector(dve, link)
                dve.wait_ge(w_loaded, 16 * len(loads))
                dve.wait_ge(norm.nT_ready, NC)
                link(v.tensor_scalar(conv[:, :], xp[:, 0:T], conv_w[:, 0:1], conv_b[:, :], ALU.mult, ALU.add))
                for k in range(1, KC):
                    last = v.scalar_tensor_tensor(conv[:, :], xp[:, k:k + T], conv_w[:, k:k + 1], conv[:, :], ALU.mult, ALU.add)
                    if k < KC - 1:
                        link(last)
                last.then_inc(conv_ready, 1)
                dve.wait_ge(dt_ready, 1)
                link(v.scalar_tensor_tensor(sp_[:, :], log[:, :], 0.0, tl[:, :], ALU.max, ALU.add))
                link(v.tensor_tensor(decay[:, :], sp_[:, 0:1], sp_[:, 1:2], ALU.mult))
                link(v.tensor_scalar(decay[:, :], decay[:, :], -1.0, 1.0, ALU.mult, ALU.add))
                dve.wait_ge(tail_ready, 1)
                link(v.tensor_scalar(mag[:, :], flat(0), bp[:, 0:1], 0.0, ALU.add, ALU.max))
                link(v.tensor_tensor(b_t[:, :], b_t[:, :], mag[:, :], ALU.add))
                dve.wait_ge(u_ready, 1)
                link(v.scalar_tensor_tensor(u[:, :], b_t[:, :], sp_[:, 1:2], u[:, :], ALU.mult, ALU.mult))
                link(v.tensor_tensor_scan(b_t[:, :], decay[:, :].to_broadcast([N, T]), u[:, :], 0.0, ALU.mult, ALU.add))
                dve.wait_ge(c_ready, 1)
                v.tensor_tensor(c_t[:, :], c_t[:, :], b_t[:, :], ALU.mult).then_inc(y_ready, 1)
                link(v.tensor_tensor(c.x[:, :, :], c.x[:, :, :], b_out[:, :].unsqueeze(1).to_broadcast([P, NT, P]), ALU.add))
                add_banks(c, dve, link, c.x, 4, y_psum)


def l3_ffn(c, ins):
    nc = c.nc
    c.layer = "l3f_"
    E = 4
    ps = c.ps
    with ExitStack() as ctx:
        gamma, beta = c.sb(ctx, "gamma", [P, P], F32), c.sb(ctx, "beta", [P, P], F32)
        choice, bias = c.sb(ctx, "choice", [P, NT, E], F32), c.sb(ctx, "b1_columns", [P, E * 4], F32)
        with ExitStack() as rctx:
            wr, b_out = c.sb(rctx, "w_router", [P, E], F32), c.sb(rctx, "b_out", [P, P], F32)
            b1, lg, order = c.sb(rctx, "b1_rows", [E * 4, P], F32), c.sb(rctx, "logits", [P, NT, E], F32), c.sb(rctx, "order", [P, E], F32)
            best, tie = c.sb(rctx, "best", [P, NT], F32), c.sb(rctx, "tie", [P, NT], F32)
            norm = NormBlock(c)
            w_loaded, chain, drawn, b1_psum, b1_ready, lg_psum = (c.sem(n) for n in ("w_loaded", "chain", "drawn", "b1_psum", "b1_ready", "lg_psum"))
            loads = [(wr[:, :], ins["L3_ffn_W_router"]), (b_out[:, :], row_view(ins["L3_ffn_bo"], P)),
                     (b1[:, :], ins["L3_ffn_b1"].rearrange("e (f p) -> (e f) p", p=P)),
                     (gamma[:, :], row_view(ins["L3_ffn_ln_gamma"], P)), (beta[:, :], row_view(ins["L3_ffn_ln_beta"], P))]
            with nc.Block() as block:
                @block.sync
                def _(sp):
                    for dst, src in loads:
                        sp.dma_start(dst, src).then_inc(w_loaded, 16)

                @block.gpsimd
                def _(pool):
                    draw_order(c, pool, order, E, drawn)

                @block.tensor
                def _(pe):
                    norm.tensor(pe)
                    pe.wait_ge(w_loaded, 16 * len(loads))
                    nc.tensor.transpose(ps[:, 4, 0:E * 4], b1[:, :], c.ident[0:E * 4, 0:E * 4]).then_inc(b1_psum, 1)
                    pe.wait_ge(norm.nT_ready, NC)
                    for t in range(NT):
                        last = nc.tensor.matmul(ps[:, 5, t * E:(t + 1) * E], c.nT[:, t * P:(t + 1) * P], wr[:, :], start=True, stop=True)
                    last.then_inc(lg_psum, 1)

                @block.scalar
                def _(act):
                    norm.scalar(act, c.nT)
                    act.wait_ge(b1_psum, 1)
                    nc.scalar.activation(bias[:, :], ps[:, 4, 0:E * 4], ACT.Copy).then_inc(b1_ready, 1)

                @block.vector
                def _(dve):
                    link = Chain(dve, chain)
                    norm.vector(dve, link)
                    dve.wait_ge(w_loaded, 16 * len(loads))
                    dve.wait_ge(drawn, E)
                    dve.wait_ge(lg_psum, 1)
                    link(nc.vector.tensor_copy(lg[:, :, :], ps[:, 5, 0:NT * E].rearrange("p (t e) -> p t e", e=E)))
                    top_choice(c, nc.vector, link, lg[:, :, :], best[:, :], tie[:, :], order[:, :], choice[:, :, :], E)
                    dve.wait_ge(norm.nT_psum, 4)
                    link(nc.vector.tensor_tensor(c.n[:, :, :], c.n[:, :, :], b_out[:, :].unsqueeze(1).to_broadcast([P, NT, P]), ALU.add))
        experts(c, ctx, E, ins["L3_ffn_W1"], lambda e: ins["L3_ffn_Wo"].rearrange("(a i) d -> a i d", a=1), bias, choice)
        var_ready, std_ready, chain = c.sem("f_var_ready"), c.sem("f_std_ready"), c.sem("f_chain")
        with nc.Block() as block:
            @block.scalar
            def _(act):
                layer_norm_scalar(c, act, var_ready, std_ready, 1)

            @block.vector
            def _(dve):
                v = nc.vector
                link = Chain(dve, chain)
                link(layer_norm_vector(c, dve, link, c.n[:, :, :], c.a[:, :, :], c.b[:, :, :], var_ready, std_ready, 1, 1e-12))
                link(v.tensor_tensor(c.a[:, :, :], c.a[:, :, :], gamma[:, :].unsqueeze(1).to_broadcast([P, NT, P]), ALU.mult))
                link(v.tensor_tensor(c.x[:, :, :], c.x[:, :, :], beta[:, :].unsqueeze(1).to_broadcast([P, NT, P]), ALU.add))
                link(v.tensor_tensor(c.x[:, :, :], c.x[:, :, :], c.a[:, :, :], ALU.add))


def store_output(c, out):
    nc = c.nc
    stored = c.sem("x_stored")
    with nc.Block() as block:
        @block.sync
        def _(sp):
            sp.dma_start(out[0].rearrange("(t p) d -> p t d", p=P), c.x[:, :, :]).then_inc(stored, 16)
            sp.wait_ge(stored, 16)


def build(nc, ins, out, layers=range(8)):
    with ExitStack() as ctx:
        c = Core(nc, ctx)
        constants(c, ins)
        with ExitStack() as actx:
            if 0 in layers or 1 in layers:
                at = Attention(c, actx)
                attention_constants(c, at, 1)
            if 0 in layers:
                l0_attention(c, at, ins)
                c.end_sublayer()
            if 1 in layers:
                l0_ffn(c, at, ins)
                c.end_sublayer()
        if 2 in layers:
            l1_mamba(c, ins)
            c.end_sublayer()
        if 3 in layers:
            l1_ternary(c, ins)
        if 4 in layers:
            l2_performer(c, ins)
            c.end_sublayer()
        if 5 in layers:
            with ExitStack() as actx:
                c.layer = "l2f_"
                at = Attention(c, actx)
                attention_constants(c, at, 2)
                l2_ffn(c, at, ins)
                c.end_sublayer()
        if 6 in layers:
            l3_state(c, ins)
        if 7 in layers:
            l3_ffn(c, ins)
        store_output(c, out)


_INS = [
    'L0_attn_x', 'L0_attn_ln_gamma', 'L0_attn_ln_beta', 'L0_attn_w_qkv', 'L0_attn_b_qkv', 'L0_attn_w_out',
    'L0_attn_b_out', 'L0_ffn_ln1_g', 'L0_ffn_ln1_b', 'L0_ffn_ln2_g', 'L0_ffn_ln2_b', 'L0_ffn_Wq', 'L0_ffn_bq',
    'L0_ffn_Wk', 'L0_ffn_bk', 'L0_ffn_Wv', 'L0_ffn_bv', 'L0_ffn_Wo', 'L0_ffn_bo', 'L0_ffn_Wr', 'L0_ffn_br',
    'L0_ffn_e_w1', 'L0_ffn_e_b1', 'L0_ffn_e_w2', 'L0_ffn_e_b2', 'L1_attn_W_in', 'L1_attn_conv_w', 'L1_attn_conv_b',
    'L1_attn_W_x', 'L1_attn_W_dt', 'L1_attn_b_dt', 'L1_attn_A_log', 'L1_attn_D', 'L1_attn_W_out', 'L1_ffn_weight',
    'L1_ffn_alpha', 'L1_ffn_bias', 'L2_attn_Wq', 'L2_attn_bq', 'L2_attn_Wk', 'L2_attn_bk', 'L2_attn_Wv', 'L2_attn_bv',
    'L2_attn_Wo', 'L2_attn_bo', 'L2_attn_orf', 'L2_ffn_rW1', 'L2_ffn_rb1', 'L2_ffn_ln_g', 'L2_ffn_ln_b', 'L2_ffn_rW2',
    'L2_ffn_rb2', 'L2_ffn_qW', 'L2_ffn_qb', 'L2_ffn_kW', 'L2_ffn_kb', 'L2_ffn_vW', 'L2_ffn_vb', 'L2_ffn_oW',
    'L2_ffn_ob', 'L3_attn_conv_w', 'L3_attn_conv_b', 'L3_attn_Wp', 'L3_attn_bp', 'L3_attn_Ws', 'L3_attn_bs',
    'L3_attn_A_log', 'L3_attn_dt_log', 'L3_attn_Wo', 'L3_attn_bo', 'L3_ffn_W_router', 'L3_ffn_W1', 'L3_ffn_b1',
    'L3_ffn_Wo', 'L3_ffn_bo', 'L3_ffn_ln_gamma', 'L3_ffn_ln_beta']
_OUTS = [((1, 2048, 128), 'float32')]


def kernel(**inputs):
    import numpy as _np
    import concourse.bacc as _bacc
    from concourse import mybir as _mybir
    from concourse.bass_utils import run_bass_kernel_spmd as _run

    nc = _bacc.Bacc("TRN2", target_bir_lowering=False, num_devices=1)
    arrays, ins = {}, {}
    for name in _INS:
        a = _np.ascontiguousarray(inputs[name])
        arrays[f"in_{name}_dram"] = a
        ins[name] = nc.dram_tensor(f"in_{name}_dram", a.shape, _mybir.dt.from_np(a.dtype), kind="ExternalInput").ap()
    outs = []
    for i, (shape, dtype) in enumerate(_OUTS):
        dt = _mybir.dt.from_np(_np.dtype(dtype))
        outs.append(nc.dram_tensor(f"out_{i}_dram", shape, dt, kind="ExternalOutput").ap())
    build(nc, ins, outs[0])
    r = _run(nc, [arrays], core_ids=[0])
    return r.results[0]["out_0_dram"]
```

```python
import concourse.bass as bass
from concourse import mybir
from contextlib import ExitStack
import numpy as np

F32 = mybir.dt.float32
BF16 = mybir.dt.bfloat16
ALU = mybir.AluOpType
ACT = mybir.ActivationFunctionType
X = mybir.AxisListType.X

P = 128
T = 2048
NT = T // P
NC = T // 512
H = 16
HD = P // H
NPAIR = H // 2
PARTS_Q = (0, 0, 0, 1, 1, 2)
PARTS_K = (0, 1, 2, 0, 1, 0)
RUNS_K = ((0, 3), (3, 2), (5, 1))
NR = len(PARTS_Q)
ROWS = NR * HD
SCALE = HD ** -0.5
MASKED = -1e30


class Chain:

    def __init__(self, eng, sem):
        self.eng, self.sem, self.n = eng, sem, 0

    def __call__(self, ins):
        self.n += 1
        ins.then_inc(self.sem, 1)
        self.eng.wait_ge(self.sem, self.n)


class Core:

    def __init__(self, nc, ctx):
        self.nc, self.layer, self.sems = nc, "", []
        sb = self.sb
        self.x = sb(ctx, "x_residual", [P, NT, P], F32)
        self.n = sb(ctx, "x_normalised", [P, NT, P], F32)
        self.heads = sb(ctx, "heads_out", [P, NT + 1, P], F32)
        self.a = self.heads[:, 1:NT + 1, :]
        self.b = sb(ctx, "tokens_b", [P, NT, P], F32)
        self.nT = sb(ctx, "channels_n", [P, T], F32)
        self.qk = sb(ctx, "channels_qk", [P, 2, T], F32)
        self.qT, self.kT = self.qk[:, 0, :], self.qk[:, 1, :]
        self.moments, self.mean_var = sb(ctx, "ln_moments", [P, NT, 6], F32), sb(ctx, "ln_mean_var", [P, NT, 2], F32)
        self.var, self.std, self.rstd = (sb(ctx, "ln_" + n, [P, NT], F32) for n in ("var", "std", "rstd"))
        self.ident = sb(ctx, "identity", [P, P], F32)
        self.identb = sb(ctx, "identity_bf16", [P, P], BF16)
        self.ps = ctx.enter_context(nc.psum_tensor("psum", [P, 8, 512], F32))

    def sb(self, ctx, name, shape, dtype):
        return ctx.enter_context(self.nc.sbuf_tensor(f"{self.layer}{name}", shape, dtype))

    def sem(self, name):
        s = self.nc.alloc_semaphore(name=f"{self.layer}{name}")
        self.sems.append(s)
        return s

    def end_sublayer(self):
        self.nc.clear_and_free_semaphores(self.sems)
        self.sems = []
        self.nc.all_engine_barrier()


def row_view(v, n):
    return v.rearrange("(a n) -> a n", a=1).to_broadcast([P, n])


def column(v):
    return v.rearrange("(p a) -> p a", a=1)


def head_order(v):
    return v.rearrange("c (p j d) -> c j d p", p=NPAIR, j=2)


def split_heads(v):
    return v.rearrange("c (j d p) -> c j d p", p=NPAIR, j=2)


def head_column(v):
    return v.rearrange("(p j d a) -> j d p a", p=NPAIR, j=2, a=1)


def layer_norm_vector(c, dve, link, src, dst, var_ready, std_ready, count, eps, done):
    v = c.nc.vector
    for t in range(NT):
        last = v.bn_stats(c.moments[:, t, :], src[:, t, :])
    link(last)
    for t in range(NT):
        last = v.bn_aggr(c.mean_var[:, t, :], c.moments[:, t, :])
    link(last)
    v.tensor_scalar(c.var[:, :], c.mean_var[:, :, 1], eps, None, ALU.add).then_inc(var_ready, 1)
    dve.wait_ge(std_ready, count)
    link(v.reciprocal(c.rstd[:, :], c.std[:, :]))
    for t in range(NT):
        last = v.tensor_scalar(dst[:, t, :], src[:, t, :], c.mean_var[:, t, 0:1], c.rstd[:, t:t + 1], ALU.subtract, ALU.mult)
        if t % 4 == 3:
            last.then_inc(done, 1)


def layer_norm_scalar(c, act, var_ready, std_ready, count):
    act.wait_ge(var_ready, count)
    c.nc.scalar.activation(c.std[:, :], c.var[:, :], ACT.Sqrt).then_inc(std_ready, 1)


def transpose_tokens(c, pe, src, bank0, done, src_ready=None):
    for t in range(NT):
        if src_ready and t % 4 == 0:
            pe.wait_ge(src_ready, t // 4 + 1)
        ins = c.nc.tensor.transpose(c.ps[:, bank0 + t // 4, (t % 4) * P:(t % 4 + 1) * P], src[:, t, :], c.ident[:, :])
        if t % 4 == 3:
            ins.then_inc(done, 1)


def project_channels(c, w, rhs, bank0, done):
    for k in range(NC):
        c.nc.tensor.matmul(c.ps[:, bank0 + k, :], w, rhs[:, k * 512:(k + 1) * 512], start=True, stop=True).then_inc(done, 1)


def project_tokens(c, srcT, w, bank0, done):
    for t in range(NT):
        ins = c.nc.tensor.matmul(c.ps[:, bank0 + t // 4, (t % 4) * P:(t % 4 + 1) * P],
                                 srcT[:, t * P:(t + 1) * P], w, start=True, stop=True)
        if t % 4 == 3:
            ins.then_inc(done, 1)


def evacuate(c, act, src_bank, dst, done, first, out_ready, bias=0.0, scale=1.0):
    for k in range(NC):
        act.wait_ge(done, first + k + 1)
        c.nc.scalar.activation(dst[:, k * 512:(k + 1) * 512], c.ps[:, src_bank + k, :], ACT.Identity,
                               bias=bias, scale=scale).then_inc(out_ready, 1)


def constants(c, ins):
    nc = c.nc
    zeroed, x_loaded = c.sem("identity_zeroed"), c.sem("x_loaded")
    with nc.Block() as block:
        @block.sync
        def _(sp):
            sp.dma_start(c.x[:, :, :], ins["L0_attn_x"][0].rearrange("(t p) d -> p t d", p=P)).then_inc(x_loaded, 16)
            sp.wait_ge(x_loaded, 16)

        @block.gpsimd
        def _(pool):
            nc.gpsimd.memset(c.ident[:, :], 0.0).then_inc(zeroed, 1)
            nc.gpsimd.memset(c.identb[:, :], 0.0).then_inc(zeroed, 1)
            pool.wait_ge(zeroed, 2)
            for m in (c.ident, c.identb):
                nc.gpsimd.affine_select(out=m[:, :], in_=m[:, :], compare_op=ALU.not_equal, fill=1.0, base=0,
                                        pattern=[[-1, P]], channel_multiplier=1).then_inc(zeroed, 1)
            pool.wait_ge(zeroed, 4)


class Attention:

    def __init__(self, c, ctx):
        sb, nc = c.sb, c.nc
        self.hi = sb(ctx, "part_hi", [P, T], BF16)
        self.mid = sb(ctx, "part_mid", [P, T], BF16)
        self.lo = sb(ctx, "part_lo", [P, T], BF16)
        self.kx = sb(ctx, "k_parts", [P, 2, NPAIR, T], BF16)
        self.v = sb(ctx, "v_and_ones", [P, 2, NT, H, HD + 1], F32)
        self.q1 = sb(ctx, "q_parts", [P, 2, NPAIR, 2, P], BF16)
        self.q2 = sb(ctx, "q_parts_and_max", [P, NPAIR, 2, P], BF16)
        self.prob = c.qk[:, :, :].rearrange("p a (b k j q) -> p (a b) k j q", b=2, k=2, j=4)
        self.mx = sb(ctx, "chunk_max", [P, H, 4], F32)
        self.negm = sb(ctx, "minus_max", [P, H], F32)
        self.rest = sb(ctx, "minus_max_rest", [P, 4, 4], F32)
        self.mparts = sb(ctx, "minus_max_parts", [P, 4, 2, 3, 2], BF16)
        self.mrow = sb(ctx, "minus_max_rows", [12, 4, P], BF16)
        self.oTs = sb(ctx, "out_channels", [P, 512], F32)
        self.rden = sb(ctx, "denominators", [P, H], F32)
        self.start = sb(ctx, "start_credit", [P, 5], F32)
        self.one, self.oneb = sb(ctx, "one", [P, 1], F32), sb(ctx, "one_bf16", [P, 1], BF16)
        self.wp = sb(ctx, "w_head_order", [P, 2, P], F32)
        self.q_dram = nc.dram_tensor(f"{c.layer}q_parts_dram", [2, NR, HD, NPAIR, T], BF16, kind="Internal").ap()
        self.k_dram = nc.dram_tensor(f"{c.layer}k_parts_dram", [8, 2, 3, HD, NPAIR, T], BF16, kind="Internal").ap()


class AttentionConstants:

    def __init__(self, c, at, buffers):
        self.c, self.at, self.buffers = c, at, buffers
        self.filled, self.ones_set = c.sem("attn_filled"), c.sem("attn_ones_set")
        self.FILLS = 6 + buffers

    def gpsimd(self):
        g, at = self.c.nc.gpsimd, self.at
        g.memset(at.q2[0:3, :, :, :], 1.0).then_inc(self.filled, 1)
        g.memset(at.v[:, :, :, :, :], 1.0).then_inc(self.filled, 1)
        for k in range(self.buffers):
            g.memset(at.kx[:, k, :, :].bitcast(F32), 0.0).then_inc(self.filled, 1)
        g.memset(at.q1[:, :, :, :, :].bitcast(F32), 0.0).then_inc(self.filled, 1)
        g.memset(at.oTs[:, :], 1.0).then_inc(self.filled, 1)
        g.memset(at.one[:, :], 1.0).then_inc(self.filled, 1)
        g.memset(at.oneb[:, :], 1.0).then_inc(self.filled, 1)

    def wait(self, eng):
        eng.wait_ge(self.filled, self.FILLS)

    def sync(self, sp):
        self.wait(sp)
        at = self.at
        ones = at.q2[0:3, :, :, :].rearrange("p a j q -> p (a j q)").unsqueeze(1).to_broadcast([3, NPAIR, T])
        for k in range(self.buffers):
            for j in range(2):
                sp.dma_start(at.kx[64 * j + ROWS:64 * j + ROWS + 3, k, :, :], ones).then_inc(self.ones_set, 16)

    def sync_end(self, sp):
        sp.wait_ge(self.ones_set, 16 * 2 * self.buffers)


def store_queries(c, at, eng, parts, part_ready, parts_stored):
    for which, part in enumerate(parts):
        sem, count = part_ready[which]
        eng.wait_ge(sem, count)
        for r in range(NR):
            if PARTS_Q[r] == which:
                eng.dma_start(at.q_dram[:, r].rearrange("j d p t -> j (d p) t"), part).then_inc(parts_stored, 16)


def place_keys(c, at, eng, part_ready, parts_placed):
    for which, part in enumerate((at.hi, at.mid, at.lo)):
        sem, count = part_ready[which]
        eng.wait_ge(sem, count)
        for r in range(NR):
            if PARTS_K[r] == which:
                for j in range(2):
                    eng.dma_start(at.kx[64 * j + r * HD:64 * j + (r + 1) * HD, 0, :, :], part[64 * j:64 * j + 64, :]).then_inc(parts_placed, 16)


def store_keys(at, eng, e, parts, parts_ready, count, parts_stored):
    eng.wait_ge(parts_ready, count)
    for which, part in enumerate(parts):
        eng.dma_start(at.k_dram[bass.ds(e, 1), :, which].rearrange("e j d p t -> (e j) (d p) t"), part[:, :]).then_inc(parts_stored, 16)


def load_keys(c, at, eng, buf, e, pairs, k_loaded):
    for j in range(2):
        for first, n in RUNS_K:
            row = 64 * j + first * HD
            eng.dma_start(at.kx[row:row + n * HD, buf, pairs, :],
                          at.k_dram[bass.ds(e, 1), j, 0:n, :, pairs, :].rearrange("e r d p t -> (e r d) p t")).then_inc(k_loaded, 16)


class Span:

    def __init__(self, causal):
        self.causal = causal

    def key_tiles(self, tile, u):
        return [kt for kt in (2 * u, 2 * u + 1) if not self.causal or kt <= tile]

    def steps(self, tile):
        return tile // 2 + 1 if self.causal else NT // 2

    def chunks(self, tile):
        return tile // 4 + 1 if self.causal else NC

    def width(self, tile, chunk):
        return P * (tile % 4 + 1) if self.causal and chunk == tile // 4 else 512

    def step_base(self, tile):
        return sum(4 * self.steps(i) for i in range(tile)) if self.causal else tile * (2 * NT)

    def max_base(self, tile):
        return sum(H * self.chunks(i) for i in range(tile)) if self.causal else tile * (H * NC)


def share(n, u, steps):
    return range(u * n // steps, (u + 1) * n // steps)


def attention_loop(c, at, lead, tri=None, routed=None):
    nc = c.nc
    G = 4
    tiles = routed.tiles if routed else NT
    span = Span(tri is not None)
    s2 = (c.ps[:, 0:2, :], c.ps[:, 2:4, :])
    s1 = (c.ps[:, 4, :], c.ps[:, 5, :])
    oT, misc = c.ps[:, 6, :], c.ps[:, 7, :]
    miscb = misc.bitcast(BF16)

    def rows_in(g):
        return f"rows{(g + lead - 1) % G}"

    ORDER = {g: [rows_in(g)] for g in range(G)}
    ORDER[0] += ["out"]
    FIRST = [f"rows{g}" for g in range(lead - 1)]
    if routed:
        ORDER[0] += ["outT"]
        ORDER[1] += ["proj", "q"]
        FIRST = ["q", "q"] + FIRST
    FLAT = [t for g in range(G) for t in ORDER[g]]
    LAST = ["out", "outT", "proj"] if routed else ["out"]

    def turn(i, name):
        return i * len(FLAT) + (len(FIRST) + FLAT.index(name))

    def after_loop(done):
        if tri is None:
            return turn(done, FLAT[0])
        return turn(done - 1, [name for name in FLAT if name == "out" or tile_of(name, 0) == 0][-1]) + 1

    def turns(i, g, u, late):
        steps = span.steps(i)
        due = [name for k, name in enumerate(ORDER[g]) if min(2 * k + 2 + late, steps - 1) == u]
        return [name for name in due if not name.startswith("rows") or exists(tile_of(name, i))]

    def tile_of(name, i):
        return i if int(name[4]) >= lead - 1 else i + 1

    def first_pass_of(i, g, k, r):
        ahead, group = divmod(g + lead, G)
        return (group, i + 1, 1 - k, r + k) if ahead else (group, i, k, r)

    def exists(tile):
        return tri is None or tile < tiles

    def each_tile(eng, body):
        if tri is not None:
            for i in range(tiles):
                body(i, i % 2, i // 2)
            return tiles // 2
        if not routed:
            with eng.Fori(0, tiles // 2) as r:
                for k in range(2):
                    body(r * 2 + k, k, r)
            return tiles // 2
        rounds = eng.value_load(routed.rounds[0:1, 0:1], min_val=routed.least_rounds, max_val=tiles // 2)
        with eng.Fori(0, tiles // 2) as r:
            with eng.If(r < rounds):
                for k in range(2):
                    body(r * 2 + k, k, r)
        return rounds

    def kx(k):
        return at.kx[:, k if routed else 0]

    def vx(k):
        return at.v[:, k if routed else 0]

    q1_loaded = [c.sem(f"attn_q1_loaded{k}") for k in range(2)]
    q2_loaded = [c.sem(f"attn_q2_loaded{g}") for g in range(G)]
    s1_ready, s1_read = c.sem("attn_s1_ready"), c.sem("attn_s1_read")
    s2_ready, exp_done, pv_done = c.sem("attn_s2_ready"), c.sem("attn_exp_done"), c.sem("attn_pv_done")
    q_copied, mparts_ready = c.sem("attn_q_copied"), c.sem("attn_mparts_ready")
    misc_ready, misc_read, oT_copied = c.sem("attn_misc_ready"), c.sem("attn_misc_read"), c.sem("attn_oT_copied")
    pool_chain, negm_ready = c.sem("attn_pool_chain"), c.sem("attn_negm_ready")
    rden_ready, oT_zeroed = c.sem("attn_rden_ready"), c.sem("attn_oT_zeroed")
    if routed:
        k_loaded = [[c.sem(f"attn_k_loaded{k}{half}") for half in range(2)] for k in range(2)]
        v_loaded = [c.sem(f"attn_v_loaded{k}") for k in range(2)]
        list_loaded, gathered = c.sem("attn_list_loaded"), [c.sem(f"attn_gathered{k}") for k in range(2)]
        last_y_stored = c.sem("attn_last_y_stored")
        qparts_ready, w_out_loaded, y_stored = c.sem("attn_qparts_ready"), c.sem("attn_w_out_loaded"), c.sem("attn_y_stored")
    Q1 = 16 * (2 * NR if routed else 2)
    KX = 16 * 2 * len(RUNS_K)

    with nc.Block() as block:
        @block.sync
        def _(sp):
            def pairs(g):
                return slice(2 * g, 2 * g + 2)

            def load_half_keys(k, half, e):
                load_keys(c, at, sp, k, e, slice(4 * half, 4 * half + 4), k_loaded[k][half])

            def load_q(k, tile):
                if routed:
                    sp.wait_ge(qparts_ready, tile + 1)
                    for j in range(2):
                        for r, which in enumerate(PARTS_Q):
                            sp.dma_start(at.q1[64 * j + r * HD:64 * j + (r + 1) * HD, k, :, j, :],
                                         routed.qparts[64 * j:64 * j + 64, which, :]).then_inc(q1_loaded[k], 16)
                else:
                    for j in range(2):
                        sp.dma_start(at.q1[64 * j:64 * j + ROWS, k, :, j, :],
                                     at.q_dram[j].rearrange("r d p t -> (r d) p t")[:, :, bass.ds(tile * P, P)]).then_inc(q1_loaded[k], 16)

            def load_max(g, before):
                sp.wait_ge(misc_read, before + 1)
                for j in range(2):
                    sp.dma_start(at.q2[64 * j + ROWS:64 * j + ROWS + 3, pairs(g), j, :],
                                 at.mrow[6 * j:6 * j + 6, g, :]).then_inc(q2_loaded[g], 16)

            def expert(tile):
                return sp.value_load(routed.expert_of[0:1, bass.ds(tile, 1)], min_val=0, max_val=routed.E - 1)

            def load_values(k, e):
                sp.dma_start(at.v[:, k], routed.v_dram[bass.ds(e, 1)].rearrange("e p t h d -> (e p) t h d")).then_inc(v_loaded[k], 16)

            def load_w_out(e):
                sp.dma_start(routed.w_out_now[:, :], routed.w_out_dram[bass.ds(e, 1)].rearrange("e p d -> (e p) d")).then_inc(w_out_loaded, 16)

            def store_y(i, stored):
                sp.dma_start(routed.y_dram[bass.ds(i, 1)].rearrange("a p d -> (a p) d"), routed.y[:, :]).then_inc(stored, 16)

            def tile_loads(i, k, r):
                for g in range(G):
                    name = rows_in(g)
                    if exists(tile_of(name, i)):
                        load_max(int(name[4]), turn(i, name))
                    if name == "rows3":
                        if tri is None:
                            load_q(k, (i + 2) % tiles)
                        elif i + 2 < tiles:
                            load_q(k, i + 2)

            def routed_loads(i, k, r):
                this, following, e = expert(i), expert(i + 1), expert(i + 2)
                for g in range(G):
                    load_max(int(rows_in(g)[4]), turn(i, rows_in(g)))
                    if g == 0:
                        load_half_keys(1 - k, 1, following)
                        sp.wait_ge(pv_done, span.step_base(i) + 4)
                        load_values(1 - k, following)
                    elif g == 1:
                        sp.wait_ge(misc_read, turn(i, "proj") + 1)
                        store_y(i, y_stored)
                        load_w_out(this)
                    elif g == 2:
                        load_half_keys(k, 0, e)
                        load_q(k, i + 2)

            if routed:
                first, second = expert(0), expert(1)
                load_half_keys(0, 0, first)
            load_q(0, 0)
            if routed:
                load_half_keys(0, 1, first)
            load_q(1, 1)
            if routed:
                load_w_out(first)
                load_values(0, first)
                load_half_keys(1, 0, second)
            for g in range(lead - 1):
                load_max(g, len(FIRST) - (lead - 1) + g)
            rounds = each_tile(sp, routed_loads if routed else tile_loads)
            more = 1 if tri is None else 0
            for k in range(2):
                sp.wait_ge(q1_loaded[k], rounds * Q1 + more * Q1)
            for g in range(G):
                sp.wait_ge(q2_loaded[g], rounds * 64 + (32 * more if g < lead - 1 else 0))
            if routed:
                for k in range(2):
                    sp.wait_ge(v_loaded[k], rounds * 16 + (1 - k) * 16)
                    for half in range(2):
                        sp.wait_ge(k_loaded[k][half], rounds * KX + (0 if k and half else KX))
                sp.wait_ge(misc_read, after_loop(rounds * 2) + len(LAST))
                sp.wait_ge(y_stored, rounds * 32 + 16)
                store_y(rounds * 2, last_y_stored)
                sp.wait_ge(last_y_stored, 16)

        @block.gpsimd
        def _(pool):
            g_ = nc.gpsimd

            class Link:

                def __init__(self, base):
                    self.base, self.k = base, 0

                def __call__(self, ins):
                    self.k += 1
                    ins.then_inc(pool_chain, 1)
                    pool.wait_ge(pool_chain, self.base + self.k)

            def same(dst, src, one=at.one):
                ones = one[:, :] if len(src.shape) == 2 else one[:, :].unsqueeze(2)
                return g_.tensor_tensor(dst, src, ones.to_broadcast(list(src.shape)), ALU.mult)

            def split(src, parts, rest, link, ready):
                link(same(parts[0], src))
                link(g_.tensor_tensor(rest, src, parts[0], ALU.subtract))
                link(same(parts[1], rest))
                g_.tensor_tensor(parts[2], rest, parts[1], ALU.subtract).then_inc(ready, 1)

            def split_max(g, tile, link):
                pool.wait_ge(q_copied, tile * G + (g + 1))
                pool.wait_ge(negm_ready, tile * G + (g + 1))
                split(at.negm[:, 4 * g:4 * g + 4].rearrange("p (a j) -> p j a", j=2), [at.mparts[:, g, :, n, :] for n in range(3)],
                      at.rest[:, g, :].rearrange("p (j a) -> p j a", j=2), link, mparts_ready)

            def copy_q(g, k):
                same(at.q2[:, 2 * g:2 * g + 2, :, :].rearrange("p a j q -> p (a j q)"),
                     at.q1[:, k, 2 * g:2 * g + 2, :, :].rearrange("p a j q -> p (a j q)"), at.oneb).then_inc(q_copied, 1)

            def load_index(tile, k):
                pool.dma_start(routed.index[:, k:k + 1],
                               routed.list_dram[bass.ds(tile, 1)].rearrange("a (p b) -> (a p) b", b=1)).then_inc(list_loaded, 16)

            def gather(k):
                g_.indirect_dma_start(out=routed.q[:, k, :], out_offset=None, in_=routed.q_dram[:, :],
                                      in_offset=bass.IndirectOffsetOnAxis(ap=routed.index[:, k:k + 1], axis=0)).then_inc(gathered[k], 16)

            def split_q(before, link):
                pool.wait_ge(misc_read, before + 1)
                split(routed.qT[:, :], [routed.qparts[:, n, :] for n in range(3)], routed.qrest[:, :], link, qparts_ready)

            link = Link(0)
            if routed:
                load_index(0, 0)
                pool.wait_ge(list_loaded, 16)
                gather(0)
                load_index(1, 1)
                split_q(0, link)
                pool.wait_ge(list_loaded, 32)
                gather(1)
                pool.wait_ge(q1_loaded[0], Q1)
                split_q(1, link)
            for g in range(lead):
                pool.wait_ge(q1_loaded[0], Q1)
                copy_q(g, 0)
                split_max(g, 0, link)
            before_loop, per_tile = link.k, 3 * (G + (1 if routed else 0))

            def whole_tile(i, k, r):
                tile_link = link if tri is not None else Link(i * per_tile + before_loop)
                if routed:
                    load_index(i + 2, k)
                for g in range(G):
                    group, tile, parity, load_round = first_pass_of(i, g, k, r)
                    if exists(tile):
                        if routed and g == 0:
                            pool.wait_ge(list_loaded, i * 16 + 48)
                        pool.wait_ge(s2_ready, span.step_base(i) + (g + 1) * span.steps(i) if lead == G else span.step_base(i) + (g * span.steps(i) + 1))
                        if group == 0:
                            pool.wait_ge(q1_loaded[parity], load_round * Q1 + Q1)
                        copy_q(group, parity)
                        if routed and g == 0:
                            gather(k)
                        split_max(group, tile, tile_link)
                    if routed and g == 1:
                        split_q(turn(i, "q"), tile_link)
                assert tri is not None or tile_link.k == per_tile

            rounds = each_tile(pool, whole_tile)
            if routed:
                for k in range(2):
                    pool.wait_ge(gathered[k], rounds * 16 + 16)

        @block.tensor
        def _(pe):
            def first_pass(g, unit, tile, k, r):
                chunks = span.chunks(tile)
                head, chunk = unit // chunks, unit % chunks
                if unit == 0:
                    if g == 0:
                        pe.wait_ge(q1_loaded[k], r * Q1 + Q1)
                    if routed and g % 2 == 0:
                        pe.wait_ge(k_loaded[k][g // 2], r * KX + KX)
                pair, j = 2 * g + head // 2, head % 2
                n = g * 4 * chunks + unit
                width = span.width(tile, chunk)
                diagonal = tri is not None and chunk == chunks - 1
                pe.wait_ge(s1_read, span.max_base(tile) + (n + 1))
                last = nc.tensor.matmul(s1[n % 2][:, 0:width], at.q1[:, k, pair, j, :], kx(k)[:, pair, chunk * 512:chunk * 512 + width],
                                        start=True, stop=not diagonal)
                if diagonal:
                    last = nc.tensor.matmul(s1[n % 2][:, width - P:width], c.identb[:, :], tri.query[:, :], start=False, stop=True)
                last.then_inc(s1_ready, 1)

            def second_pass(s, i, k):
                steps, base = span.steps(i), span.step_base(i)
                g, u = s // steps, s % steps
                if u == 0:
                    pe.wait_ge(q2_loaded[g], i * 32 + 32)
                pe.wait_ge(exp_done, base + (s + 1))
                for kk, kt in enumerate(span.key_tiles(i, u)):
                    diagonal = tri is not None and kt == i
                    for pp in range(2):
                        last = nc.tensor.matmul(s2[s % 2][:, kk, pp * 256:(pp + 1) * 256], kx(k)[:, 2 * g + pp, kt * P:(kt + 1) * P],
                                                at.q2[:, 2 * g + pp, :, :].rearrange("p j q -> p (j q)"),
                                                start=not diagonal or pp == 0, stop=not diagonal)
                    if diagonal:
                        last = nc.tensor.matmul(s2[s % 2][:, kk, :], c.identb[:, :], tri.key[:, :].unsqueeze(1).to_broadcast([P, 4, P]),
                                                start=False, stop=True)
                last.then_inc(s2_ready, 1)

            def weighted_values(s, kk, i, k, r):
                steps, base = span.steps(i), span.step_base(i)
                g, u = s // steps, s % steps
                kts = span.key_tiles(i, u)
                if kk == len(kts):
                    return
                if s == 0 and kk == 0:
                    pe.wait_ge(oT_copied, i + 1)
                    if routed:
                        pe.wait_ge(v_loaded[k], r * 16 + 16)
                if kk == 0:
                    pe.wait_ge(exp_done, base + (s + 3))
                kt = kts[kk]
                for j in range(4):
                    last = nc.tensor.matmul(oT[32 * j:32 * j + HD + 1, g * P:(g + 1) * P], vx(k)[:, kt, 4 * g + j, :],
                                            at.prob[:, s % 4, kk, j, :], start=kt == 0, stop=u == steps - 1 and kt == kts[-1])
                if kt == kts[-1]:
                    last.then_inc(pv_done, 1)

            def fill_misc(name, i, k, r, before):
                if not (isinstance(before, int) and before == 0):
                    pe.wait_ge(misc_read, before)
                if name == "out":
                    pe.wait_ge(oT_copied, i + 1)
                    for g in range(G):
                        last = nc.tensor.transpose(misc[:, g * P:(g + 1) * P], at.oTs[:, g * P:(g + 1) * P], c.ident[:, :])
                    last.then_inc(misc_ready, 1)
                elif name == "outT":
                    nc.tensor.transpose(misc[:, 0:P], c.heads[:, 0, :], c.ident[:, :]).then_inc(misc_ready, 1)
                elif name == "proj":
                    pe.wait_ge(w_out_loaded, i * 16 + 16)
                    nc.tensor.matmul(misc[:, 0:P], routed.outT[:, :], routed.w_out_now[:, :], start=True, stop=True).then_inc(misc_ready, 1)
                elif name == "q":
                    pe.wait_ge(gathered[k], r * 16 + 32)
                    nc.tensor.transpose(misc[:, 0:P], routed.q[:, k, :], c.ident[:, :]).then_inc(misc_ready, 1)
                else:
                    g = int(name[4])
                    pe.wait_ge(mparts_ready, tile_of(name, i) * G + (g + 1))
                    nc.tensor.transpose(miscb[0:12, 0:P], at.mparts[:, g, :, :, :].rearrange("p j r a -> p (j r a)"),
                                        c.identb[:, :]).then_inc(misc_ready, 1)

            def whole_tile(i, k, r):
                steps = span.steps(i)
                for s in range(G * steps):
                    g, u = s // steps, s % steps
                    group, tile, parity, load_round = first_pass_of(i, g, k, r)
                    units = list(share(4 * span.chunks(tile), u, steps)) if exists(tile) else []
                    early, late = len(units) // 3, (len(units) + 1) // 3
                    for unit in units[:early]:
                        first_pass(group, unit, tile, parity, load_round)
                    if s + 1 < G * steps:
                        second_pass(s + 1, i, k)
                    for unit in units[early:len(units) - late]:
                        first_pass(group, unit, tile, parity, load_round)
                    for name in turns(i, g, u, 0):
                        fill_misc(name, i, k, r, turn(i, name))
                    if s + 1 == G * steps and exists(i + 1):
                        second_pass(0, i + 1, 1 - k)
                    weighted_values(s, 0, i, k, r)
                    for unit in units[len(units) - late:]:
                        first_pass(group, unit, tile, parity, load_round)
                    weighted_values(s, 1, i, k, r)

            pe.wait_ge(oT_zeroed, 1)
            if routed:
                for k in range(2):
                    fill_misc("q", k - 2, k, -1, k)
            for g in range(lead):
                for unit in range(4 * span.chunks(0)):
                    first_pass(g, unit, 0, 0, 0)
                    if g > 0 and unit == 3:
                        fill_misc(f"rows{g - 1}", -1, 1, -1, len(FIRST) - (lead - 1) + g - 1)
            second_pass(0, 0, 0)
            done = each_tile(pe, whole_tile) * 2
            for n, name in enumerate(LAST):
                fill_misc(name, done, 0, 0, after_loop(done) + n)

        @block.scalar
        def _(act):
            def read_misc(name, i, before):
                act.wait_ge(misc_ready, before + 1)
                if name == "q":
                    if not (isinstance(i, int) and i == -2):
                        act.wait_ge(qparts_ready, i + 2)
                    dst, src = routed.qT[:, :], misc[:, 0:P]
                elif name == "outT":
                    dst, src = routed.outT[:, :], misc[:, 0:P]
                elif name == "proj":
                    act.wait_ge(y_stored, i * 16 + 16)
                    dst, src = routed.y[:, :], misc[:, 0:P]
                else:
                    dst, src = at.mrow[:, int(name[4]), :], miscb[0:12, 0:P]
                nc.scalar.activation(dst, src, ACT.Copy).then_inc(misc_read, 1)

            def exps(i, k, r):
                steps, base = span.steps(i), span.step_base(i)
                for s in range(G * steps):
                    n = len(span.key_tiles(i, s % steps))
                    act.wait_ge(s2_ready, base + (s + 1))
                    act.wait_ge(pv_done, base + (s + 1))
                    nc.scalar.activation(at.prob[:, s % 4, 0:n, :, :].rearrange("p k j q -> p (k j q)"),
                                         s2[s % 2][:, 0:n, :].rearrange("p k n -> p (k n)"), ACT.Exp, scale=SCALE).then_inc(exp_done, 1)
                    for name in turns(i, s // steps, s % steps, 1):
                        if name != "out":
                            read_misc(name, i, turn(i, name))

            nc.scalar.activation(at.start[:, 0:1], c.ident[:, 0:1], ACT.Exp).then_inc(exp_done, 2)
            for n, name in enumerate(FIRST):
                read_misc(name, n - 2, n)
            done = each_tile(act, exps) * 2
            for n, name in enumerate(LAST):
                if name != "out":
                    read_misc(name, done, after_loop(done) + n)

        @block.vector
        def _(dve):
            v = nc.vector

            def maximum(g, unit, tile):
                chunks = span.chunks(tile)
                n = g * 4 * chunks + unit
                dve.wait_ge(s1_ready, span.max_base(tile) + (n + 1))
                v.tensor_reduce(at.mx[:, 4 * g + unit // chunks, unit % chunks:unit % chunks + 1],
                                s1[n % 2][:, 0:span.width(tile, unit % chunks)], X, ALU.max).then_inc(s1_read, 1)

            def finish_max(g, tile):
                chunks = span.chunks(tile)
                dve.wait_ge(s1_read, span.max_base(tile) + ((g + 1) * 4 * chunks + 2))
                v.tensor_reduce(at.negm[:, 4 * g:4 * g + 4], at.mx[:, 4 * g:4 * g + 4, 0:chunks], X, ALU.max, negate=True).then_inc(negm_ready, 1)

            def read_out(i, before):
                dve.wait_ge(misc_ready, before + 1)
                o = misc.rearrange("p (h n) -> p h n", n=32)
                v.reciprocal(at.rden[:, :], o[:, :, HD]).then_inc(rden_ready, 1)
                dve.wait_ge(rden_ready, i + 1)
                dst = c.heads[:, 0:1, :] if routed else c.heads[:, bass.ds(i, 1), :]
                v.tensor_tensor(dst.rearrange("p a (h d) -> p (a h) d", d=HD), o[:, :, 0:HD],
                                at.rden[:, :].unsqueeze(2).to_broadcast([P, H, HD]), ALU.mult).then_inc(misc_read, 1)

            v.memset(oT, 0.0).then_inc(oT_zeroed, 1)
            v.memset(at.start[:, 1:2], 0.0).then_inc(s1_read, 2)
            v.memset(at.start[:, 2:3], 0.0).then_inc(pv_done, 4)
            v.memset(at.start[:, 3:4], 0.0).then_inc(oT_copied, 1)
            if routed:
                v.memset(at.start[:, 4:5], 0.0).then_inc(y_stored, 16)
            for g in range(lead):
                for unit in range(4 * span.chunks(0)):
                    maximum(g, unit, 0)
                finish_max(g, 0)

            def whole_tile(i, k, r):
                steps, base = span.steps(i), span.step_base(i)
                for g in range(G):
                    group, tile, _, _ = first_pass_of(i, g, k, r)
                    for u in range(steps):
                        if exists(tile):
                            for unit in share(4 * span.chunks(tile), u, steps):
                                maximum(group, unit, tile)
                        if "out" in turns(i, g, u, 1):
                            read_out(i, turn(i, "out"))
                    if exists(tile):
                        finish_max(group, tile)
                dve.wait_ge(pv_done, base + (G * steps + 4))
                v.tensor_copy(at.oTs[:, :], oT).then_inc(oT_copied, 1)

            done = each_tile(dve, whole_tile) * 2
            read_out(done, after_loop(done))
            if not routed:
                dve.wait_ge(misc_read, after_loop(done) + 1)


def l0_attention(c, at, ins, fixed):
    nc = c.nc
    c.layer = "l0a_"
    with ExitStack() as ctx:
        w = c.sb(ctx, "w_qkv", [P, 3 * P], F32)
        w_out = c.sb(ctx, "w_out", [P, P], F32)
        gamma, beta = c.sb(ctx, "gamma", [P, 1], F32), c.sb(ctx, "beta", [P, 1], F32)
        bq, bk = c.sb(ctx, "b_q", [P, 1], F32), c.sb(ctx, "b_k", [P, 1], F32)
        bv, b_out = c.sb(ctx, "b_v", [P, P], F32), c.sb(ctx, "b_out", [P, P], F32)
        b_qkv = ins["L0_attn_b_qkv"]
        pairs = [(w[:, :], ins["L0_attn_w_qkv"]), (w_out[:, :], ins["L0_attn_w_out"]),
                 (gamma[:, :], column(ins["L0_attn_ln_gamma"])), (beta[:, :], column(ins["L0_attn_ln_beta"])),
                 (bv[:, :], row_view(b_qkv[2 * P:3 * P], P)), (b_out[:, :], row_view(ins["L0_attn_b_out"], P))]
        for j in range(2):
            pairs.append((bq[64 * j:64 * j + 64, :], head_column(b_qkv[0:P])[j]))
            pairs.append((bk[64 * j:64 * j + 64, :], head_column(b_qkv[P:2 * P])[j]))
        attention_layer(c, at, pairs, [(eps, None, None) for eps in (1e-5,)] + [(1e-5, gamma, beta)],
                        w[:, 0:P], w[:, P:2 * P], w[:, 2 * P:3 * P], bq, bk, bv, fixed)
        attention_loop(c, at, 2)
        attention_out(c, w_out, b_out, c.n, then_into_x=True)


def attention_layer(c, at, loads, norms, wq, wk, wv, bq, bk, bv, fixed):
    nc = c.nc
    w_loaded, var_ready, std_ready, chain = c.sem("w_loaded"), c.sem("var_ready"), c.sem("std_ready"), c.sem("chain")
    w_ordered = c.sem("w_ordered")
    n_ready, h_ready, hT_psum, hT_ready = c.sem("n_ready"), c.sem("h_ready"), c.sem("hT_psum"), c.sem("hT_ready")
    q_psum, k_psum, v_psum = c.sem("q_psum"), c.sem("k_psum"), c.sem("v_psum")
    whole_ready, v_ready = [c.sem("k_ready"), c.sem("q_ready")], c.sem("v_ready")
    hi_ready, rest_ready, mid_ready, lo_ready = ([c.sem(f"{n}_ready{m}") for m in "kq"] for n in ("hi", "rest", "mid", "lo"))
    parts_placed, parts_stored = c.sem("parts_placed"), c.sem("parts_stored")
    ps = c.ps

    def free(v):
        return v.rearrange("p t d -> p (t d)").bitcast(BF16)

    parts = ((at.hi[:, :], at.mid[:, :], at.lo[:, :]),
             (free(c.a[:, 0:NT // 2, :]), free(c.a[:, NT // 2:, :]), at.q2[:, :, :, :].rearrange("p a j q -> p (a j q)")))
    whole = (c.kT, c.qT)
    with nc.Block() as block:
        @block.sync
        def _(sp):
            for dst, src in loads:
                sp.dma_start(dst, src, allow_slow_non_contiguous=True).then_inc(w_loaded, 16)
            if fixed:
                fixed.sync(sp)
            place_keys(c, at, sp, [(hi_ready[0], NC), (mid_ready[0], 1), (lo_ready[0], 1)], parts_placed)
            store_queries(c, at, sp, parts[1], [(hi_ready[1], NC), (mid_ready[1], 1), (lo_ready[1], 1)], parts_stored)
            sp.wait_ge(parts_placed, 16 * 2 * NR)
            sp.wait_ge(parts_stored, 16 * NR)

        if fixed:
            @block.gpsimd
            def _(pool):
                fixed.gpsimd()
                fixed.wait(pool)

        @block.vector
        def _(dve):
            v = nc.vector
            link = Chain(dve, chain)
            layer_norm_vector(c, dve, link, c.x, c.n, var_ready, std_ready, 1, norms[0][0], n_ready)
            dve.wait_ge(n_ready, NC)
            layer_norm_vector(c, dve, link, c.n, c.a, var_ready, std_ready, 2, norms[1][0], h_ready)
            dve.wait_ge(w_loaded, 16 * len(loads))
            v.tensor_copy(split_heads(at.wp[:, 1, :]), head_order(wk)).then_inc(w_ordered, 1)
            v.tensor_copy(split_heads(at.wp[:, 0, :]), head_order(wq)).then_inc(w_ordered, 1)
            for m in range(2):
                dve.wait_ge(hi_ready[m], NC)
                dve.wait_ge(whole_ready[m], NC)
                v.tensor_tensor(whole[m], whole[m], parts[m][0], ALU.subtract).then_inc(rest_ready[m], 1)
            if fixed:
                fixed.wait(dve)
            for b in range(4):
                dve.wait_ge(v_psum, b + 1)
                v.tensor_tensor(at.v[:, 0, 4 * b:4 * b + 4, :, 0:HD], ps[:, 4 + b, :].rearrange("p (t h d) -> p t h d", t=4, h=H),
                                bv[:, :].rearrange("p (h d) -> p h d", h=H).unsqueeze(1).to_broadcast([P, 4, H, HD]),
                                ALU.add).then_inc(v_ready, 1)
            for m in range(2):
                dve.wait_ge(mid_ready[m], 1)
                if m == 1 and fixed:
                    fixed.sync_end(dve)
                v.tensor_tensor(parts[m][2], whole[m], parts[m][1], ALU.subtract).then_inc(lo_ready[m], 1)
            dve.wait_ge(v_ready, 4)

        @block.tensor
        def _(pe):
            transpose_tokens(c, pe, c.a, 0, hT_psum, h_ready)
            pe.wait_ge(w_ordered, 2)
            pe.wait_ge(hT_ready, NC)
            project_channels(c, at.wp[:, 1, :], c.nT, 4, k_psum)
            project_channels(c, at.wp[:, 0, :], c.nT, 0, q_psum)
            pe.wait_ge(whole_ready[0], NC)
            pe.wait_ge(hi_ready[0], NC)
            project_tokens(c, c.nT, wv, 4, v_psum)

        @block.scalar
        def _(act):
            layer_norm_scalar(c, act, var_ready, std_ready, 1)
            layer_norm_scalar(c, act, var_ready, std_ready, 2)
            act.wait_ge(w_loaded, 16 * len(loads))
            _, gamma, beta = norms[1]
            evacuate(c, act, 0, c.nT, hT_psum, 0, hT_ready, beta[:, :], gamma[:, :])
            for m, bank, psum, bias in ((0, 4, k_psum, bk), (1, 0, q_psum, bq)):
                evacuate(c, act, bank, parts[m][0], psum, 0, hi_ready[m], bias[:, :])
                evacuate(c, act, bank, whole[m], psum, 0, whole_ready[m], bias[:, :])
            for m in range(2):
                act.wait_ge(rest_ready[m], 1)
                nc.scalar.activation(parts[m][1], whole[m], ACT.Copy).then_inc(mid_ready[m], 1)


def attention_out(c, w_out, b_out, into, then_into_x):
    nc = c.nc
    aT_psum, aT_ready, y_psum, chain = c.sem("aT_psum"), c.sem("aT_ready"), c.sem("y_psum"), c.sem("out_chain")
    with nc.Block() as block:
        @block.tensor
        def _(pe):
            transpose_tokens(c, pe, c.a, 0, aT_psum)
            pe.wait_ge(aT_ready, NC)
            project_tokens(c, c.nT, w_out[:, :], 4, y_psum)

        @block.scalar
        def _(act):
            evacuate(c, act, 0, c.nT, aT_psum, 0, aT_ready)

        @block.vector
        def _(dve):
            link = Chain(dve, chain)
            link(nc.vector.tensor_tensor(into[:, :, :], into[:, :, :], b_out[:, :].unsqueeze(1).to_broadcast([P, NT, P]), ALU.add))
            add_banks(c, dve, link, into, 4, y_psum)
            if then_into_x:
                link(nc.vector.tensor_tensor(c.x[:, :, :], c.x[:, :, :], into[:, :, :], ALU.add))


def add_banks(c, dve, link, into, bank0, ready):
    for b in range(4):
        sl = slice(4 * b, 4 * b + 4)
        dve.wait_ge(ready, b + 1)
        link(c.nc.vector.tensor_tensor(into[:, sl, :], into[:, sl, :], c.ps[:, bank0 + b, :].rearrange("p (t d) -> p t d", t=4), ALU.add))


class DiagonalMask:

    def __init__(self, c, ctx):
        self.query = c.sb(ctx, "mask_by_query", [P, P], BF16)
        self.key = c.sb(ctx, "mask_by_key", [P, P], BF16)
        nc = c.nc
        drawn = c.sem("mask_drawn")
        with nc.Block() as block:
            @block.gpsimd
            def _(pool):
                nc.gpsimd.memset(self.query[:, :], 0.0).then_inc(drawn, 1)
                nc.gpsimd.memset(self.key[:, :], 0.0).then_inc(drawn, 1)
                pool.wait_ge(drawn, 2)
                nc.gpsimd.affine_select(out=self.query[:, :], in_=self.query[:, :], compare_op=ALU.is_ge, fill=MASKED,
                                        base=0, pattern=[[-1, P]], channel_multiplier=1).then_inc(drawn, 1)
                nc.gpsimd.affine_select(out=self.key[:, :], in_=self.key[:, :], compare_op=ALU.is_ge, fill=MASKED,
                                        base=0, pattern=[[1, P]], channel_multiplier=-1).then_inc(drawn, 1)
                pool.wait_ge(drawn, 4)


def l0_ffn(c, at, ins, fixed):
    nc = c.nc
    c.layer = "l0f_"
    E = 8
    with ExitStack() as ctx:
        w_out, b_out = c.sb(ctx, "w_out", [P, P], F32), c.sb(ctx, "b_out", [P, P], F32)
        with ExitStack() as actx:
            w = c.sb(actx, "w_qkv", [P, 3, P], F32)
            gamma, beta = c.sb(actx, "gamma", [P, 1], F32), c.sb(actx, "beta", [P, 1], F32)
            bq, bk, bv = c.sb(actx, "b_q", [P, 1], F32), c.sb(actx, "b_k", [P, 1], F32), c.sb(actx, "b_v", [P, P], F32)
            loads = [(w[:, k, :], ins[f"L0_ffn_W{m}"]) for k, m in enumerate("qkv")]
            loads += [(w_out[:, :], ins["L0_ffn_Wo"]), (gamma[:, :], column(ins["L0_ffn_ln1_g"])),
                      (beta[:, :], column(ins["L0_ffn_ln1_b"])), (bv[:, :], row_view(ins["L0_ffn_bv"], P)),
                      (b_out[:, :], row_view(ins["L0_ffn_bo"], P))]
            for j in range(2):
                loads.append((bq[64 * j:64 * j + 64, :], head_column(ins["L0_ffn_bq"])[j]))
                loads.append((bk[64 * j:64 * j + 64, :], head_column(ins["L0_ffn_bk"])[j]))
            attention_layer(c, at, loads, [(1e-5, None, None), (1e-5, gamma, beta)], w[:, 0, :], w[:, 1, :], w[:, 2, :], bq, bk, bv, fixed)
            attention_loop(c, at, 4, tri=DiagonalMask(c, actx))
        attention_out(c, w_out, b_out, c.n, then_into_x=False)
        mix = c.sb(ctx, "expert_weights", [P, NT, E], F32)
        bias = c.sb(ctx, "b1_columns", [P, E * 4], F32)
        l0_router(c, ctx, ins, E, mix, bias)
        experts(c, ctx, E, ins["L0_ffn_e_w1"], lambda e: ins["L0_ffn_e_w2"][bass.ds(e, 1)], bias, mix)
        add_to_residual(c)


def top_choice(c, v, link, logits, best, tie, order, choice, width):
    def wide(s):
        return s.unsqueeze(2).to_broadcast([P, NT, width])
    link(v.tensor_reduce(best, logits, X, ALU.max))
    link(v.tensor_tensor(choice, logits, wide(best), ALU.is_equal))
    link(v.tensor_tensor(choice, choice, order.unsqueeze(1).to_broadcast([P, NT, width]), ALU.mult))
    link(v.tensor_reduce(tie, choice, X, ALU.max))
    link(v.tensor_tensor(choice, choice, wide(tie), ALU.is_equal))


def draw_order(c, pool, order, width, drawn):
    for e in range(width):
        c.nc.gpsimd.memset(order[:, e:e + 1], float(width - e)).then_inc(drawn, 1)


def l0_router(c, ctx, ins, E, mix, bias):
    nc = c.nc
    ps = c.ps
    with ExitStack() as rctx:
        gamma, beta = c.sb(rctx, "gamma2", [P, 1], F32), c.sb(rctx, "beta2", [P, 1], F32)
        wr, br = c.sb(rctx, "w_router", [P, E], F32), c.sb(rctx, "b_router", [P, E], F32)
        b1, b2 = c.sb(rctx, "b1_rows", [E * 4, P], F32), c.sb(rctx, "b2_rows", [E, P], F32)
        lg, ch, ex = (c.sb(rctx, n, [P, NT, E], F32) for n in ("logits", "choice", "rest"))
        best, second, tie = (c.sb(rctx, n, [P, NT], F32) for n in ("best", "second", "tie"))
        order = c.sb(rctx, "order", [P, E], F32)
        mixT = c.sb(rctx, "mix_rows", [E, T], F32)
        w_loaded, var_ready, std_ready, chain = c.sem("r_w_loaded"), c.sem("r_var_ready"), c.sem("r_std_ready"), c.sem("r_chain")
        h_ready, hT_psum, hT_ready, drawn = c.sem("r_h_ready"), c.sem("r_hT_psum"), c.sem("r_hT_ready"), c.sem("r_order_drawn")
        b1_psum, b1_ready, lg_psum, shifted, exp_ready = (c.sem("r_" + n) for n in ("b1_psum", "b1_ready", "lg_psum", "shifted", "exp_ready"))
        mix_ready, mixT_psum, mixT_ready, b2_psum = (c.sem("r_" + n) for n in ("mix_ready", "mixT_psum", "mixT_ready", "b2_psum"))
        loads = [(gamma[:, :], column(ins["L0_ffn_ln2_g"])), (beta[:, :], column(ins["L0_ffn_ln2_b"])),
                 (wr[:, :], ins["L0_ffn_Wr"]), (br[:, :], row_view(ins["L0_ffn_br"], E)),
                 (b1[:, :], ins["L0_ffn_e_b1"].rearrange("e (f p) -> (e f) p", p=P)), (b2[:, :], ins["L0_ffn_e_b2"])]
        with nc.Block() as block:
            @block.sync
            def _(sp):
                for dst, src in loads:
                    sp.dma_start(dst, src).then_inc(w_loaded, 16)

            @block.gpsimd
            def _(pool):
                draw_order(c, pool, order, E, drawn)

            @block.tensor
            def _(pe):
                transpose_tokens(c, pe, c.a, 0, hT_psum, h_ready)
                pe.wait_ge(w_loaded, 16 * len(loads))
                nc.tensor.transpose(ps[:, 4, 0:E * 4], b1[:, :], c.ident[0:E * 4, 0:E * 4]).then_inc(b1_psum, 1)
                pe.wait_ge(hT_ready, NC)
                for t in range(NT):
                    last = nc.tensor.matmul(ps[:, 5, t * E:(t + 1) * E], c.nT[:, t * P:(t + 1) * P], wr[:, :], start=True, stop=True)
                last.then_inc(lg_psum, 1)
                pe.wait_ge(mix_ready, 1)
                for t in range(NT):
                    ins_ = nc.tensor.transpose(ps[0:E, t // 4, (t % 4) * P:(t % 4 + 1) * P], mix[:, t, :], c.ident[:, :])
                    if t % 4 == 3:
                        ins_.then_inc(mixT_psum, 1)
                pe.wait_ge(mixT_ready, NC)
                for t in range(NT):
                    ins_ = nc.tensor.matmul(ps[:, 4 + t // 4, (t % 4) * P:(t % 4 + 1) * P], mixT[:, t * P:(t + 1) * P], b2[:, :],
                                            start=True, stop=True)
                    if t % 4 == 3:
                        ins_.then_inc(b2_psum, 1)

            @block.scalar
            def _(act):
                layer_norm_scalar(c, act, var_ready, std_ready, 1)
                act.wait_ge(w_loaded, 16 * len(loads))
                evacuate(c, act, 0, c.nT, hT_psum, 0, hT_ready, beta[:, :], gamma[:, :])
                act.wait_ge(b1_psum, 1)
                nc.scalar.activation(bias[:, :], ps[:, 4, 0:E * 4], ACT.Copy).then_inc(b1_ready, 1)
                act.wait_ge(shifted, 1)
                nc.scalar.activation(ex[:, :, :], ex[:, :, :], ACT.Exp).then_inc(exp_ready, 1)
                for k in range(NC):
                    act.wait_ge(mixT_psum, k + 1)
                    nc.scalar.activation(mixT[:, k * 512:(k + 1) * 512], ps[0:E, k, :], ACT.Copy).then_inc(mixT_ready, 1)
                act.wait_ge(b1_ready, 1)

            @block.vector
            def _(dve):
                v = nc.vector
                link = Chain(dve, chain)

                def wide(s):
                    return s.unsqueeze(2).to_broadcast([P, NT, E])

                layer_norm_vector(c, dve, link, c.n, c.a, var_ready, std_ready, 1, 1e-5, h_ready)
                dve.wait_ge(w_loaded, 16 * len(loads))
                dve.wait_ge(drawn, E)
                dve.wait_ge(lg_psum, 1)
                link(v.tensor_tensor(lg[:, :, :], ps[:, 5, 0:NT * E].rearrange("p (t e) -> p t e", e=E),
                                     br[:, :].unsqueeze(1).to_broadcast([P, NT, E]), ALU.add))
                top_choice(c, v, link, lg[:, :, :], best[:, :], tie[:, :], order[:, :], ch[:, :, :], E)
                link(v.scalar_tensor_tensor(ex[:, :, :], ch[:, :, :], MASKED, lg[:, :, :], ALU.mult, ALU.add))
                link(v.tensor_reduce(second[:, :], ex[:, :, :], X, ALU.max))
                link(v.tensor_tensor(ch[:, :, :], lg[:, :, :], wide(second[:, :]), ALU.is_ge))
                v.tensor_tensor(ex[:, :, :], lg[:, :, :], wide(best[:, :]), ALU.subtract).then_inc(shifted, 1)
                dve.wait_ge(exp_ready, 1)
                link(v.tensor_tensor(ex[:, :, :], ex[:, :, :], ch[:, :, :], ALU.mult))
                link(v.tensor_reduce(tie[:, :], ex[:, :, :], X, ALU.add))
                link(v.reciprocal(best[:, :], tie[:, :]))
                v.tensor_tensor(mix[:, :, :], ex[:, :, :], wide(best[:, :]), ALU.mult).then_inc(mix_ready, 1)
                for b in range(4):
                    sl = slice(4 * b, 4 * b + 4)
                    dve.wait_ge(b2_psum, b + 1)
                    link(v.tensor_tensor(c.n[:, sl, :], c.n[:, sl, :], ps[:, 4 + b, :].rearrange("p (t d) -> p t d", t=4), ALU.add))


def experts(c, ctx, E, w1_dram, w2_of, bias, mix):
    nc = c.nc
    ps = c.ps
    F = 4
    K = 2 * NC
    with ExitStack() as ectx:
        w1 = c.sb(ectx, "w1", [P, 2, F * P], F32)
        w2 = c.sb(ectx, "w2", [P, 2, F, P], F32)
        mid = c.sb(ectx, "hidden", [P, 2, F, 512], F32)
        bnow = c.sb(ectx, "b1_now", [P, 2, F], F32)
        start = c.sb(ectx, "e_start_credit", [P, 3], F32)
        w_loaded = [c.sem(f"e_w_loaded{k}") for k in range(2)]
        mid_psum, gelu_done, y_psum, y_added = (c.sem("e_" + n) for n in ("mid_psum", "gelu_done", "y_psum", "y_added"))
        with nc.Block() as block:
            @block.sync
            def _(sp):
                def load(k, e):
                    sp.dma_start(w1[:, k, :], w1_dram[bass.ds(e, 1)].rearrange("a d f -> d (a f)")).then_inc(w_loaded[k], 16)
                    sp.dma_start(bnow[:, k, :], bias[:, bass.ds(e * F, F)]).then_inc(w_loaded[k], 16)
                    sp.dma_start(w2[:, k, :, :], w2_of(e).rearrange("a (f p) d -> p (a f) d", p=P)).then_inc(w_loaded[k], 16)

                for k in range(2):
                    load(k, k)
                with sp.Fori(0, E // 2 - 1) as r:
                    for k in range(2):
                        sp.wait_ge(y_psum, r * K + (NC * (k + 1) + 2))
                        load(k, r * 2 + (2 + k))

            @block.tensor
            def _(pe):
                def up(r, k):
                    e, ch = k // NC, k % NC
                    if ch == 0:
                        pe.wait_ge(w_loaded[e], r * 48 + 48)
                    for f in range(F):
                        pe.wait_ge(gelu_done, r * K * F + (k * F + f + 1))
                        nc.tensor.matmul(ps[:, f, :], w1[:, e, f * P:(f + 1) * P], c.nT[:, ch * 512:(ch + 1) * 512],
                                         start=True, stop=True).then_inc(mid_psum, 1)

                def down(r, k):
                    e = k // NC
                    pe.wait_ge(gelu_done, r * K * F + (k * F + 2 * F))
                    pe.wait_ge(y_added, r * K + (k + 3))
                    for t in range(4):
                        for f in range(F):
                            last = nc.tensor.matmul(ps[:, 4 + k % 2, t * P:(t + 1) * P], mid[:, k % 2, f, t * P:(t + 1) * P],
                                                    w2[:, e, f, :], start=f == 0, stop=f == F - 1)
                    last.then_inc(y_psum, 1)

                with pe.Fori(0, E // 2) as r:
                    up(r, 0)
                    for k in range(K):
                        if k + 1 < K:
                            up(r, k + 1)
                        down(r, k)

            @block.scalar
            def _(act):
                nc.scalar.activation(start[:, 0:1], bias[:, 0:1], ACT.Copy).then_inc(gelu_done, 4)
                with act.Fori(0, E // 2) as r:
                    for k in range(K):
                        if k % NC == 0:
                            act.wait_ge(w_loaded[k // NC], r * 48 + 48)
                        act.wait_ge(y_psum, r * K + (k + 1))
                        for f in range(F):
                            act.wait_ge(mid_psum, r * K * F + (k * F + f + 1))
                            nc.scalar.activation(mid[:, k % 2, f, :], ps[:, f, :], ACT.Gelu,
                                                 bias=bnow[:, k // NC, f:f + 1]).then_inc(gelu_done, 1)

            @block.vector
            def _(dve):
                v = nc.vector
                v.memset(start[:, 1:2], 0.0).then_inc(y_psum, 2)
                v.memset(start[:, 2:3], 0.0).then_inc(y_added, 4)
                with dve.Fori(0, E // 2) as r:
                    for k in range(K):
                        e, ch = k // NC, k % NC
                        dve.wait_ge(y_psum, r * K + (k + 3))
                        dve.wait_ge(y_added, r * K + (k + 1))
                        for t in range(4):
                            tile = 4 * ch + t
                            last = v.scalar_tensor_tensor(c.n[:, tile, :], ps[:, 4 + k % 2, t * P:(t + 1) * P],
                                                          mix[:, tile, bass.ds(r * 2 + e, 1)], c.n[:, tile, :], ALU.mult, ALU.add)
                        last.then_inc(y_added, 1)
                dve.wait_ge(y_added, E * NC + 4)


def add_to_residual(c):
    nc = c.nc
    done = c.sem("residual_done")
    with nc.Block() as block:
        @block.vector
        def _(dve):
            nc.vector.tensor_tensor(c.x[:, :, :], c.x[:, :, :], c.n[:, :, :], ALU.add).then_inc(done, 1)
            dve.wait_ge(done, 1)


class NormBlock:

    def __init__(self, c, prefix="n_"):
        self.c = c
        self.var_ready, self.std_ready = c.sem(prefix + "var_ready"), c.sem(prefix + "std_ready")
        self.n_ready, self.nT_psum, self.nT_ready = c.sem(prefix + "n_ready"), c.sem(prefix + "nT_psum"), c.sem(prefix + "nT_ready")

    def vector(self, dve, link, eps=1e-5):
        c = self.c
        layer_norm_vector(c, dve, link, c.x, c.n, self.var_ready, self.std_ready, 1, eps, self.n_ready)
        dve.wait_ge(self.n_ready, NC)

    def tensor(self, pe):
        transpose_tokens(self.c, pe, self.c.n, 0, self.nT_psum, self.n_ready)

    def scalar(self, act, dst):
        layer_norm_scalar(self.c, act, self.var_ready, self.std_ready, 1)
        evacuate(self.c, act, 0, dst, self.nT_psum, 0, self.nT_ready)


def softplus_scalar(c, act, link, x, bias, magnitude, tail):
    link(c.nc.scalar.activation(magnitude, x, ACT.Abs, bias=bias))
    link(c.nc.scalar.activation(magnitude, magnitude, ACT.Exp, scale=-1.0))
    return c.nc.scalar.activation(tail, magnitude, ACT.Ln, bias=1.0)


def l1_mamba(c, ins):
    nc = c.nc
    c.layer = "l1a_"
    DI, DS, KC, R = 2 * P, 16, 4, 8
    ps = c.ps
    dram = nc.dram_tensor("ssm_rows_dram", [2 * DS, T], F32, kind="Internal").ap()
    with ExitStack() as ctx:
        xv = c.sb(ctx, "xv", [P, 2, T], F32)
        dx = c.sb(ctx, "delta_x", [P, 2, T], F32)
        delta = c.sb(ctx, "delta", [P, 2, T], F32)
        a = c.sb(ctx, "a", [P, 2, DS], F32)
        w_out, dvec = c.sb(ctx, "w_out", [P, 2, P], F32), c.sb(ctx, "d", [P, 2], F32)
        with ExitStack() as pctx:
            w_in, conv_w, conv_b = c.sb(pctx, "w_in", [P, DI], F32), c.sb(pctx, "conv_w", [P, 2, KC], F32), c.sb(pctx, "conv_b", [P, 2], F32)
            w_x, w_dt, b_dt = c.sb(pctx, "w_x", [P, 2, R + 2 * DS], F32), c.sb(pctx, "w_dt", [R, DI], F32), c.sb(pctx, "b_dt", [P, 2], F32)
            xp = c.sb(pctx, "x_padded", [P, 2, KC - 1 + T], F32)
            ssm = c.sb(pctx, "ssm", [R, T], F32)
            ssm_bc = c.sb(pctx, "ssm_bc", [2 * DS, T], F32)
            norm = NormBlock(c)
            w_loaded, chain, act_chain = c.sem("w_loaded"), c.sem("chain"), c.sem("act_chain")
            xp_psum, xp_ready, conv_ready, xv_ready = c.sem("xp_psum"), c.sem("xp_ready"), c.sem("conv_ready"), c.sem("xv_ready")
            ssm_psum, ssm_ready, ssm_stored, dt_psum, tail_ready, delta_ready = (c.sem(n) for n in (
                "ssm_psum", "ssm_ready", "ssm_stored", "dt_psum", "tail_ready", "delta_ready"))

            def halves(v):
                return v.rearrange("(h p) -> p h", p=P)

            loads = [(w_in[:, :], ins["L1_attn_W_in"]), (conv_w[:, :, :], ins["L1_attn_conv_w"].rearrange("(h p) a k -> p h (a k)", p=P)),
                     (conv_b[:, :], halves(ins["L1_attn_conv_b"])), (w_x[:, :, :], ins["L1_attn_W_x"].rearrange("(h p) r -> p h r", p=P)),
                     (w_dt[:, :], ins["L1_attn_W_dt"]), (b_dt[:, :], halves(ins["L1_attn_b_dt"])),
                     (a[:, :, :], ins["L1_attn_A_log"].rearrange("(h p) n -> p h n", p=P)),
                     (w_out[:, :, :], ins["L1_attn_W_out"].rearrange("(h p) d -> p h d", p=P)), (dvec[:, :], halves(ins["L1_attn_D"]))]
            with nc.Block() as block:
                @block.sync
                def _(sp):
                    for dst, src in loads:
                        sp.dma_start(dst, src, allow_slow_non_contiguous=True).then_inc(w_loaded, 16)
                    sp.wait_ge(ssm_ready, 2 * NC)
                    sp.dma_start(dram[:, :], ssm_bc[:, :]).then_inc(ssm_stored, 16)
                    sp.wait_ge(ssm_stored, 16)

                @block.tensor
                def _(pe):
                    norm.tensor(pe)
                    pe.wait_ge(w_loaded, 16 * len(loads))
                    pe.wait_ge(norm.nT_ready, NC)
                    project_channels(c, w_in[:, P:2 * P], c.nT, 4, xp_psum)
                    project_channels(c, w_in[:, 0:P], c.nT, 0, xp_psum)
                    pe.wait_ge(xv_ready, 2)
                    pe.wait_ge(xp_ready, 2 * NC)
                    for k in range(NC):
                        for h in range(2):
                            last = nc.tensor.matmul(ps[0:R, k, :], w_x[:, h, 0:R], xv[:, h, k * 512:(k + 1) * 512],
                                                    start=h == 0, stop=h == 1)
                        last.then_inc(ssm_psum, 1)
                    for k in range(NC):
                        for h in range(2):
                            last = nc.tensor.matmul(ps[0:2 * DS, 4 + k, :], w_x[:, h, R:R + 2 * DS], xv[:, h, k * 512:(k + 1) * 512],
                                                    start=h == 0, stop=h == 1)
                        last.then_inc(ssm_psum, 1)
                    pe.wait_ge(ssm_ready, 2 * NC)
                    for h in range(2):
                        for k in range(NC):
                            last = nc.tensor.matmul(ps[:, 4 * h + k, :], w_dt[:, h * P:(h + 1) * P], ssm[:, k * 512:(k + 1) * 512],
                                                    start=True, stop=True)
                        last.then_inc(dt_psum, 1)

                @block.scalar
                def _(act):
                    link = Chain(act, act_chain)
                    norm.scalar(act, c.nT)
                    for h in (1, 0):
                        evacuate(c, act, 4 * h, xp[:, h, KC - 1:], xp_psum, (1 - h) * NC, xp_ready)
                    for h in range(2):
                        act.wait_ge(conv_ready, h + 1)
                        nc.scalar.activation(xv[:, h, :], xv[:, h, :], ACT.Silu).then_inc(xv_ready, 1)
                    for part in range(2):
                        for k in range(NC):
                            act.wait_ge(ssm_psum, part * NC + k + 1)
                            dst = ssm_bc if part else ssm
                            nc.scalar.activation(dst[:, k * 512:(k + 1) * 512], ps[0:dst.shape[0], 4 * part + k, :], ACT.Copy).then_inc(ssm_ready, 1)
                    for h in range(2):
                        act.wait_ge(dt_psum, h + 1)
                        softplus_scalar(c, act, link, ps[:, 4 * h:4 * h + 4, :].rearrange("p b n -> p (b n)"), b_dt[:, h:h + 1],
                                        dx[:, h, :], delta[:, h, :]).then_inc(tail_ready, 1)
                    act.wait_ge(w_loaded, 16 * len(loads))
                    link(nc.scalar.activation(a[:, :, :], a[:, :, :], ACT.Exp))
                    act.wait_ge(tail_ready, 2)
                    link(nc.scalar.activation(a[:, :, :], a[:, :, :], ACT.Copy, scale=-1.0))

                @block.vector
                def _(dve):
                    v = nc.vector
                    link = Chain(dve, chain)
                    link(v.memset(xp[:, :, 0:KC - 1], 0.0))
                    norm.vector(dve, link)
                    dve.wait_ge(w_loaded, 16 * len(loads))
                    for h in range(2):
                        dve.wait_ge(xp_ready, 2 * NC)
                        link(v.tensor_scalar(xv[:, h, :], xp[:, h, 0:T], conv_w[:, h, 0:1], conv_b[:, h:h + 1], ALU.mult, ALU.add))
                        for k in range(1, KC):
                            last = v.scalar_tensor_tensor(xv[:, h, :], xp[:, h, k:k + T], conv_w[:, h, k:k + 1], xv[:, h, :], ALU.mult, ALU.add)
                            if k < KC - 1:
                                link(last)
                        last.then_inc(conv_ready, 1)
                    for h in range(2):
                        dve.wait_ge(tail_ready, h + 1)
                        link(v.tensor_scalar(dx[:, h, :], ps[:, 4 * h:4 * h + 4, :].rearrange("p b n -> p (b n)"), b_dt[:, h:h + 1], 0.0,
                                             ALU.add, ALU.max))
                        link(v.tensor_tensor(delta[:, h, :], delta[:, h, :], dx[:, h, :], ALU.add))
                        dve.wait_ge(xv_ready, 2)
                        link(v.tensor_tensor(dx[:, h, :], delta[:, h, :], xv[:, h, :], ALU.mult))

        mamba_scan(c, ctx, dram, DS, a, dvec, delta, dx, xv)
        y = dx
        y_ready, out_psum, chain2 = c.sem("y_ready"), c.sem("out_psum"), c.sem("chain2")
        with nc.Block() as block:
            @block.scalar
            def _(act):
                for h in range(2):
                    nc.scalar.activation(y[:, h, :], ps[:, 4 * h:4 * h + 4, :].rearrange("p b n -> p (b n)"), ACT.Copy).then_inc(y_ready, 1)

            @block.tensor
            def _(pe):
                pe.wait_ge(y_ready, 2)
                for t in range(NT):
                    for h in range(2):
                        last = nc.tensor.matmul(ps[:, t // 4, (t % 4) * P:(t % 4 + 1) * P], y[:, h, t * P:(t + 1) * P], w_out[:, h, :],
                                                start=h == 0, stop=h == 1)
                    if t % 4 == 3:
                        last.then_inc(out_psum, 1)

            @block.vector
            def _(dve):
                add_banks(c, dve, Chain(dve, chain2), c.x, 0, out_psum)


def mamba_scan(c, ctx, dram, DS, a, dvec, delta, dx, xv):
    nc = c.nc
    ps = c.ps
    with ExitStack() as sctx:
        K = 4
        own = c.sb(sctx, "bc_rows", [P, 2, 2, T], F32)
        rows = [(own[:, 0, 0, :], own[:, 0, 1, :]), (own[:, 1, 0, :], own[:, 1, 1, :]), (c.qT, c.kT),
                (c.nT[:, :], c.b[:, :, :].rearrange("p t d -> p (t d)"))]
        da = c.sb(sctx, "decay", [P, 2, T], F32)
        u = c.sb(sctx, "input", [P, 2, T], F32)
        hc = c.sb(sctx, "state_c", [P, 2, T], F32)
        anow = c.sb(sctx, "a_now", [P, K, 2], F32)
        diag = c.sb(sctx, "d_diagonal", [P, 2, P], F32)
        start = c.sb(sctx, "start_credit", [P, 4], F32)
        rows_loaded = [c.sem(f"rows_loaded{k}") for k in range(K)]
        da_ready, u_ready, scanned, hc_ready, added, diag_ready = (c.sem("s_" + n) for n in (
            "da_ready", "u_ready", "scanned", "hc_ready", "added", "diag_ready"))
        L = 3 * 16
        with nc.Block() as block:
            @block.sync
            def _(sp):
                def load(k, n):
                    sp.dma_start(rows[k][0], dram[bass.ds(n, 1), :].to_broadcast([P, T])).then_inc(rows_loaded[k], 16)
                    sp.dma_start(rows[k][1], dram[bass.ds(n + DS, 1), :].to_broadcast([P, T])).then_inc(rows_loaded[k], 16)
                    sp.dma_start(anow[:, k, :], a[:, :, bass.ds(n, 1)].rearrange("p h a -> p (h a)"),
                                 allow_slow_non_contiguous=True).then_inc(rows_loaded[k], 16)

                for k in range(K):
                    load(k, k)
                with sp.Fori(0, DS // K - 1) as r:
                    for k in range(K):
                        sp.wait_ge(hc_ready, r * (2 * K) + (2 * k + 4))
                        load(k, r * K + (K + k))

            @block.scalar
            def _(act):
                def decays(r, k):
                    act.wait_ge(rows_loaded[k], r * L + L)
                    for h in range(2):
                        act.wait_ge(scanned, r * (2 * K) + (2 * k + h + 1))
                        nc.scalar.activation(da[:, h, :], delta[:, h, :], ACT.Exp, scale=anow[:, k, h:h + 1]).then_inc(da_ready, 1)

                with act.Fori(0, DS // K - 1) as r:
                    for k in range(K):
                        decays(r, k)
                for k in range(K):
                    decays(DS // K - 1, k)

            @block.gpsimd
            def _(pool):
                def inputs(r, k):
                    pool.wait_ge(rows_loaded[k], r * L + L)
                    for h in range(2):
                        pool.wait_ge(hc_ready, r * (2 * K) + (2 * k + h + 1))
                        nc.gpsimd.tensor_tensor(u[:, h, :], dx[:, h, :], rows[k][0], ALU.mult).then_inc(u_ready, 1)

                with pool.Fori(0, DS // K - 1) as r:
                    for k in range(K):
                        inputs(r, k)
                for k in range(K):
                    inputs(DS // K - 1, k)

            @block.vector
            def _(dve):
                v = nc.vector

                def states(r, k):
                    for h in range(2):
                        step = 2 * k + h
                        dve.wait_ge(da_ready, r * (2 * K) + (step + 1))
                        dve.wait_ge(u_ready, r * (2 * K) + (step + 1))
                        v.tensor_tensor_scan(u[:, h, :], da[:, h, :], u[:, h, :], 0.0, ALU.mult, ALU.add).then_inc(scanned, 1)
                        dve.wait_ge(scanned, r * (2 * K) + (step + 3))
                        dve.wait_ge(added, r * (2 * K) + (step + 1))
                        v.tensor_tensor(hc[:, h, :], u[:, h, :], rows[k][1], ALU.mult).then_inc(hc_ready, 1)

                for h in range(2):
                    v.tensor_scalar(diag[:, h, :], c.ident[:, :], dvec[:, h:h + 1], None, ALU.mult).then_inc(diag_ready, 1)
                v.memset(start[:, 0:1], 0.0).then_inc(scanned, 2)
                v.memset(start[:, 1:2], 0.0).then_inc(hc_ready, 2)
                v.memset(start[:, 2:3], 0.0).then_inc(added, 2)
                with dve.Fori(0, DS // K - 1) as r:
                    for k in range(K):
                        states(r, k)
                for k in range(K):
                    states(DS // K - 1, k)

            @block.tensor
            def _(pe):
                def add_state(r, k, closing):
                    for h in range(2):
                        pe.wait_ge(hc_ready, r * (2 * K) + (2 * k + h + 3))
                        for b in range(NC):
                            last = nc.tensor.matmul(ps[:, 4 * h + b, :], c.ident[:, :], hc[:, h, b * 512:(b + 1) * 512],
                                                    start=False, stop=closing)
                        last.then_inc(added, 1)

                pe.wait_ge(diag_ready, 2)
                for h in range(2):
                    for b in range(NC):
                        nc.tensor.matmul(ps[:, 4 * h + b, :], diag[:, h, :], xv[:, h, b * 512:(b + 1) * 512], start=True, stop=False)
                with pe.Fori(0, DS // K - 1) as r:
                    for k in range(K):
                        add_state(r, k, False)
                for k in range(K):
                    add_state(DS // K - 1, k, k == K - 1)


def l1_ternary(c, ins):
    nc = c.nc
    c.layer = "l1f_"
    ps = c.ps
    with ExitStack() as ctx:
        w, wt = c.sb(ctx, "w", [P, P], F32), c.sb(ctx, "w_ternary", [P, 2, P], F32)
        wT = c.sb(ctx, "wT", [P, P], F32)
        alpha, bias = c.sb(ctx, "alpha", [P, 1], F32), c.sb(ctx, "bias", [P, P], F32)
        ones, thr = c.sb(ctx, "ones", [P, P], F32), c.sb(ctx, "threshold", [P, 3], F32)
        norm = NormBlock(c)
        w_loaded, chain, sums_ready, total_psum, w_ready, wT_psum, wT_ready, y_psum = (c.sem(n) for n in (
            "w_loaded", "chain", "sums_ready", "total_psum", "w_ready", "wT_psum", "wT_ready", "y_psum"))
        loads = [(w[:, :], ins["L1_ffn_weight"]), (alpha[:, :], row_view(ins["L1_ffn_alpha"], 1)), (bias[:, :], row_view(ins["L1_ffn_bias"], P))]
        with nc.Block() as block:
            @block.sync
            def _(sp):
                for dst, src in loads:
                    sp.dma_start(dst, src).then_inc(w_loaded, 16)

            @block.vector
            def _(dve):
                v = nc.vector
                link = Chain(dve, chain)
                link(v.memset(ones[:, :], 1.0))
                dve.wait_ge(w_loaded, 16 * len(loads))
                v.tensor_reduce(thr[:, 0:1], w[:, :], X, ALU.add, apply_absolute_value=True).then_inc(sums_ready, 1)
                dve.wait_ge(total_psum, 1)
                link(v.tensor_scalar(thr[:, 1:2], ps[:, 7, 0:1], 1.0 / (P * P), 0.7, ALU.mult, ALU.mult))
                link(v.tensor_scalar(thr[:, 2:3], thr[:, 1:2], -1.0, None, ALU.mult))
                link(v.tensor_scalar(wt[:, 0, :], w[:, :], thr[:, 1:2], alpha[:, :], ALU.is_gt, ALU.mult))
                link(v.tensor_scalar(wt[:, 1, :], w[:, :], thr[:, 2:3], alpha[:, :], ALU.is_lt, ALU.mult))
                v.tensor_tensor(wt[:, 0, :], wt[:, 0, :], wt[:, 1, :], ALU.subtract).then_inc(w_ready, 1)
                norm.vector(dve, link)
                link(v.tensor_tensor(c.x[:, :, :], c.x[:, :, :], bias[:, :].unsqueeze(1).to_broadcast([P, NT, P]), ALU.add))
                add_banks(c, dve, link, c.x, 4, y_psum)

            @block.tensor
            def _(pe):
                pe.wait_ge(sums_ready, 1)
                nc.tensor.matmul(ps[:, 7, 0:1], ones[:, :], thr[:, 0:1], start=True, stop=True).then_inc(total_psum, 1)
                pe.wait_ge(w_ready, 1)
                nc.tensor.transpose(ps[:, 6, 0:P], wt[:, 0, :], c.ident[:, :]).then_inc(wT_psum, 1)
                norm.tensor(pe)
                pe.wait_ge(wT_ready, 1)
                pe.wait_ge(norm.nT_ready, NC)
                project_tokens(c, c.nT, wT[:, :], 4, y_psum)

            @block.scalar
            def _(act):
                act.wait_ge(wT_psum, 1)
                nc.scalar.activation(wT[:, :], ps[:, 6, 0:P], ACT.Copy).then_inc(wT_ready, 1)
                norm.scalar(act, c.nT)


def l2_performer(c, ins):
    nc = c.nc
    c.layer = "l2a_"
    M, G, EPS = 32, 4, 1e-6
    W = 4 * (HD + 1)
    ps = c.ps
    with ExitStack() as ctx:
        b_out, woT = c.sb(ctx, "b_out", [P, P], F32), c.sb(ctx, "woT", [P, P], F32)
        with ExitStack() as fctx:
            w, wT = c.sb(fctx, "w", [P, 4, P], F32), c.sb(fctx, "wT", [P, 3, P], F32)
            bq, bk, bv = c.sb(fctx, "b_q", [P, 1], F32), c.sb(fctx, "b_k", [P, 1], F32), c.sb(fctx, "b_v", [P, P], F32)
            orf, orf_all = c.sb(fctx, "orf", [M, HD], F32), c.sb(fctx, "orf_all", [M, H, HD], F32)
            own, own4 = c.sb(fctx, "own_head", [P, H, M], F32), c.sb(fctx, "own_of_four", [P, 4, HD + 1], F32)
            feat, minus_norm = c.sb(fctx, "features", [P, H * M], F32), c.sb(fctx, "minus_norm", [P, H * M], F32)
            v1 = c.sb(fctx, "v_and_ones", [P, NT, H, HD + 1], F32)
            q2, k2 = c.sb(fctx, "q_squared", [P, T], F32), c.sb(fctx, "k_squared", [P, T], F32)
            phik, phiq = c.sb(fctx, "phi_k", [P, 4, H * M], F32), c.sb(fctx, "phi_q", [P, G, T], F32)
            kv = c.sb(fctx, "kv", [P, G, W], F32)
            rden = c.sb(fctx, "denominators", [P, NT, H], F32)
            norm = NormBlock(c)
            (w_loaded, chain, drawn, wT_psum, wT_ready, orf_ready, orf_psum, feat_ready, q_psum, q_ready, k_psum, k_ready, v_psum, v_ready,
             q2_ready, k2_ready, pk_psum, pk_exp, pk_ready, kv_psum, kv_ready, pq_psum, pq_exp, pq_ready, num_psum) = (c.sem(n) for n in (
                 "w_loaded", "chain", "drawn", "wT_psum", "wT_ready", "orf_ready", "orf_psum", "feat_ready", "q_psum", "q_ready", "k_psum",
                 "k_ready", "v_psum", "v_ready", "q2_ready", "k2_ready", "pk_psum", "pk_exp", "pk_ready", "kv_psum", "kv_ready",
                 "pq_psum", "pq_exp", "pq_ready", "num_psum"))
            loads = [(w[:, k, :], ins[f"L2_attn_W{m}"]) for k, m in enumerate("qkvo")]
            loads += [(bq[:, :], column(ins["L2_attn_bq"])), (bk[:, :], column(ins["L2_attn_bk"])),
                      (bv[:, :], row_view(ins["L2_attn_bv"], P)), (b_out[:, :], row_view(ins["L2_attn_bo"], P)), (orf[:, :], ins["L2_attn_orf"])]
            with nc.Block() as block:
                @block.sync
                def _(sp):
                    for dst, src in loads:
                        sp.dma_start(dst, src).then_inc(w_loaded, 16)

                @block.gpsimd
                def _(pool):
                    nc.gpsimd.memset(own[:, :, :], 1.0).then_inc(drawn, 1)
                    nc.gpsimd.memset(own4[:, :, :], 1.0).then_inc(drawn, 1)
                    for m, n, step, width in ((own, H, HD, M), (own4, 4, M, HD + 1)):
                        pool.wait_ge(drawn, 2 if m is own else 4)
                        nc.gpsimd.affine_select(out=m[:, :, :], in_=m[:, :, :], compare_op=ALU.is_ge, fill=0.0, base=0,
                                                pattern=[[-step, n], [0, width]], channel_multiplier=1).then_inc(drawn, 1)
                        pool.wait_ge(drawn, 3 if m is own else 5)
                        nc.gpsimd.affine_select(out=m[:, :, :], in_=m[:, :, :], compare_op=ALU.is_ge, fill=0.0, base=step - 1,
                                                pattern=[[step, n], [0, width]], channel_multiplier=-1).then_inc(drawn, 1)

                @block.tensor
                def _(pe):
                    pe.wait_ge(w_loaded, 16 * len(loads))
                    for k in range(4):
                        nc.tensor.transpose(ps[:, 6, k * P:(k + 1) * P], w[:, k, :], c.ident[:, :]).then_inc(wT_psum, 1)
                    pe.wait_ge(orf_ready, 1)
                    nc.tensor.transpose(ps[:, 7, 0:M], orf_all[:, :, :].rearrange("m h d -> m (h d)"), c.ident[0:M, 0:M]).then_inc(orf_psum, 1)
                    norm.tensor(pe)
                    pe.wait_ge(wT_ready, 2)
                    pe.wait_ge(feat_ready, 1)
                    pe.wait_ge(norm.nT_ready, NC)
                    project_channels(c, wT[:, 1, :], c.nT, 4, k_psum)
                    project_channels(c, wT[:, 0, :], c.nT, 0, q_psum)
                    pe.wait_ge(k_ready, NC)
                    project_tokens(c, c.nT, wT[:, 2, :], 4, v_psum)
                    pe.wait_ge(q_ready, NC)
                    pe.wait_ge(k2_ready, 1)
                    pe.wait_ge(v_ready, 4)

                    def keys(t):
                        if t >= 4:
                            pe.wait_ge(pk_exp, t - 3)
                        tok = slice(t * P, (t + 1) * P)
                        nc.tensor.matmul(ps[:, t % 4, :], c.kT[:, tok], feat[:, :], start=True, stop=False)
                        nc.tensor.matmul(ps[:, t % 4, :], k2[:, tok], minus_norm[:, :], start=False, stop=True).then_inc(pk_psum, 1)

                    keys(0)
                    keys(1)
                    for t in range(NT):
                        if t + 2 < NT:
                            keys(t + 2)
                        pe.wait_ge(pk_ready, t + 1)
                        for g in range(G):
                            last = nc.tensor.matmul(ps[:, 4 + g, 0:W], phik[:, t % 4, g * P:(g + 1) * P],
                                                    v1[:, t, 4 * g:4 * g + 4, :].rearrange("p h d -> p (h d)"), start=t == 0, stop=t == NT - 1)
                        last.then_inc(kv_psum, 1)
                    pe.wait_ge(q2_ready, 1)
                    for g in range(G):
                        for k in range(NC):
                            n = g * NC + k
                            if n == 0:
                                pe.wait_ge(pk_exp, NT)
                            if n >= 4:
                                pe.wait_ge(pq_exp, n - 3)
                            tok = slice(k * 512, (k + 1) * 512)
                            nc.tensor.matmul(ps[:, n % 4, :], feat[:, g * P:(g + 1) * P], c.qT[:, tok], start=True, stop=False)
                            nc.tensor.matmul(ps[:, n % 4, :], minus_norm[:, g * P:(g + 1) * P], q2[:, tok], start=False, stop=True).then_inc(pq_psum, 1)
                    pe.wait_ge(kv_ready, G)
                    pe.wait_ge(pq_exp, G * NC)
                    pe.wait_ge(pq_ready, G * NC)
                    for t in range(NT):
                        for g in range(G):
                            at = (t % 2) * G * W + g * W
                            last = nc.tensor.matmul(ps[:, t // 2, at:at + W], phiq[:, g, t * P:(t + 1) * P], kv[:, g, :], start=True, stop=True)
                        if t % 2:
                            last.then_inc(num_psum, 1)

                @block.scalar
                def _(act):
                    norm.scalar(act, c.nT)
                    act.wait_ge(w_loaded, 16 * len(loads))
                    evacuate(c, act, 4, c.kT, k_psum, 0, k_ready, bk[:, :])
                    evacuate(c, act, 0, c.qT, q_psum, 0, q_ready, bq[:, :])
                    for t in range(NT):
                        act.wait_ge(pk_psum, t + 1)
                        if t >= 4:
                            act.wait_ge(kv_psum, t - 3)
                        nc.scalar.activation(phik[:, t % 4, :], ps[:, t % 4, :], ACT.Exp).then_inc(pk_exp, 1)
                    for n in range(G * NC):
                        act.wait_ge(pq_psum, n + 1)
                        nc.scalar.activation(phiq[:, n // NC, (n % NC) * 512:(n % NC + 1) * 512], ps[:, n % 4, :], ACT.Exp).then_inc(pq_exp, 1)

                @block.vector
                def _(dve):
                    v = nc.vector
                    link = Chain(dve, chain)
                    dve.wait_ge(w_loaded, 16 * len(loads))
                    v.tensor_copy(orf_all[:, :, :], orf[:, :].unsqueeze(1).to_broadcast([M, H, HD])).then_inc(orf_ready, 1)
                    link(v.memset(v1[:, :, :, :], 1.0))
                    norm.vector(dve, link)
                    dve.wait_ge(wT_psum, 4)
                    v.tensor_copy(wT[:, :, :], ps[:, 6, 0:3 * P].rearrange("p (k n) -> p k n", k=3)).then_inc(wT_ready, 1)
                    v.tensor_copy(woT[:, :], ps[:, 6, 3 * P:4 * P]).then_inc(wT_ready, 1)
                    dve.wait_ge(drawn, 6)
                    dve.wait_ge(orf_psum, 1)
                    link(v.tensor_copy(rden[:, 0:2, :].rearrange("p a b -> p (a b)"), ps[:, 7, 0:M]))
                    feat3 = feat[:, :].rearrange("p (h m) -> p h m", h=H)
                    link(v.tensor_tensor(feat3, own[:, :, :], rden[:, 0:2, :].rearrange("p a b -> p (a b)").unsqueeze(1).to_broadcast([P, H, M]), ALU.mult))
                    link(v.tensor_scalar(feat[:, :], feat[:, :], HD ** -0.25, None, ALU.mult))
                    v.tensor_scalar(minus_norm[:, :].rearrange("p (h m) -> p h m", h=H), own[:, :, :], -0.5 * HD ** -0.5, None, ALU.mult).then_inc(feat_ready, 1)
                    for b in range(4):
                        dve.wait_ge(v_psum, b + 1)
                        v.tensor_tensor(v1[:, 4 * b:4 * b + 4, :, 0:HD], ps[:, 4 + b, :].rearrange("p (t h d) -> p t h d", t=4, h=H),
                                        bv[:, :].rearrange("p (h d) -> p h d", h=H).unsqueeze(1).to_broadcast([P, 4, H, HD]), ALU.add).then_inc(v_ready, 1)
                    dve.wait_ge(k_ready, NC)
                    v.tensor_tensor(k2[:, :], c.kT[:, :], c.kT[:, :], ALU.mult).then_inc(k2_ready, 1)
                    dve.wait_ge(q_ready, NC)
                    v.tensor_tensor(q2[:, :], c.qT[:, :], c.qT[:, :], ALU.mult).then_inc(q2_ready, 1)
                    for t in range(NT):
                        dve.wait_ge(pk_exp, t + 1)
                        v.tensor_scalar(phik[:, t % 4, :], phik[:, t % 4, :], EPS, M ** -0.5, ALU.add, ALU.mult).then_inc(pk_ready, 1)
                    dve.wait_ge(kv_psum, NT)
                    for g in range(G):
                        v.tensor_tensor(kv[:, g, :], ps[:, 4 + g, 0:W], own4[:, :, :].rearrange("p h d -> p (h d)"), ALU.mult).then_inc(kv_ready, 1)
                    for n in range(G * NC):
                        dve.wait_ge(pq_exp, n + 1)
                        part = phiq[:, n // NC, (n % NC) * 512:(n % NC + 1) * 512]
                        v.tensor_scalar(part, part, EPS, M ** -0.5, ALU.add, ALU.mult).then_inc(pq_ready, 1)
                    for b in range(8):
                        dve.wait_ge(num_psum, b + 1)
                        num = ps[:, b, 0:2 * G * W].rearrange("p (t h d) -> p t h d", t=2, h=H)
                        two = slice(2 * b, 2 * b + 2)
                        link(v.reciprocal(rden[:, two, :], num[:, :, :, HD]))
                        link(v.tensor_tensor(c.a[:, two, :].rearrange("p t (h d) -> p t h d", h=H), num[:, :, :, 0:HD],
                                             rden[:, two, :].unsqueeze(3).to_broadcast([P, 2, H, HD]), ALU.mult))
        attention_out(c, woT, b_out, c.x, then_into_x=False)


class Routed:

    def __init__(self, c, ctx, E, K):
        nc, sb = c.nc, c.sb
        self.E = E
        self.tiles = (K * T + E * (P - 1)) // P + 1
        self.listed = self.tiles + 2
        self.least_rounds = K * T // P // 2
        self.rounds = sb(ctx, "rounds", [1, 1], mybir.dt.int32)
        self.expert_of = sb(ctx, "expert_of_tile", [1, self.listed], mybir.dt.int32)
        self.q = sb(ctx, "gathered_q", [P, 2, P], F32)
        self.index = sb(ctx, "gathered_index", [P, 2], mybir.dt.uint32)
        self.qparts = sb(ctx, "gathered_q_parts", [P, 3, P], BF16)
        self.qT = sb(ctx, "gathered_qT", [P, P], F32)
        self.qrest = sb(ctx, "gathered_q_rest", [P, P], F32)
        self.outT = sb(ctx, "outT", [P, P], F32)
        self.y = sb(ctx, "y", [P, P], F32)
        self.w_out_now = sb(ctx, "w_out_now", [P, P], F32)
        self.list_dram = nc.dram_tensor("query_list_dram", [self.listed, P], mybir.dt.uint32, kind="Internal").ap()
        self.q_dram = nc.dram_tensor("expert_q_dram", [E * T, P], F32, kind="Internal").ap()
        self.v_dram = nc.dram_tensor("expert_v_dram", [E, P, NT, H, HD + 1], F32, kind="Internal").ap()
        self.w_out_dram = nc.dram_tensor("expert_w_out_dram", [E, P, P], F32, kind="Internal").ap()
        self.y_dram = nc.dram_tensor("expert_y_dram", [self.tiles + 1, P, P], F32, kind="Internal").ap()


def l2_ffn(c, at, ins, fixed):
    c.layer = "l2f_"
    E, K = 8, 2
    with ExitStack() as ctx:
        rt = Routed(c, ctx, E, K)
        gate = c.sb(ctx, "gate", [P, K, NT], F32)
        slot = c.sb(ctx, "slot", [P, K, NT], mybir.dt.uint32)
        row = c.sb(ctx, "row", [P, K, NT], mybir.dt.uint32)
        y_row = c.sb(ctx, "y_row", [P, K, NT], mybir.dt.uint32)
        l2_router(c, ins, rt, E, K, gate, slot, row, y_row, fixed)
        l2_prepare(c, at, ins, rt, slot, row)
        attention_loop(c, at, 3, routed=rt)
        l2_collect(c, rt, gate, y_row)


def l2_router(c, ins, rt, E, K, gate, slot, row, y_row, fixed):
    nc, ps = c.nc, c.ps
    W = P // 2
    with ExitStack() as ctx:
        w1, w2, ob = c.sb(ctx, "rw1", [W, P], F32), c.sb(ctx, "rw2", [E, W], F32), c.sb(ctx, "ob", [E, P], F32)
        b1, g1, g0, b2 = (c.sb(ctx, n, [P, w], F32) for n, w in (("rb1", W), ("ln_g", W), ("ln_b", W), ("rb2", E)))
        w1T, w2T = c.sb(ctx, "rw1T", [P, W], F32), c.sb(ctx, "rw2T", [W, E], F32)
        h, hh = c.sb(ctx, "hidden", [P, NT, W], F32), c.sb(ctx, "hidden_squared", [P, NT, W], F32)
        hT = c.sb(ctx, "hiddenT", [W, T], F32)
        probs, masked, sel, mix, tmp = (c.sb(ctx, n, [P, NT, E], F32) for n in ("probs", "masked", "selected", "mix", "tmp"))
        choice = c.sb(ctx, "choice", [P, K, NT, E], F32)
        best = c.sb(ctx, "best", [P, K, NT], F32)
        tie, total = c.sb(ctx, "tie", [P, NT], F32), c.sb(ctx, "total", [P, NT], F32)
        order, edge = c.sb(ctx, "order", [P, E], F32), c.sb(ctx, "edge", [P, NT], F32)
        before, ones = c.sb(ctx, "before", [P, P], F32), c.sb(ctx, "ones", [P, P], F32)
        counts, offset = c.sb(ctx, "tile_counts", [P, NT, E], F32), c.sb(ctx, "tile_offset", [P, NT, E], F32)
        more, tiles_of = c.sb(ctx, "more", [P, E, NT], F32), c.sb(ctx, "tiles_of", [P, E], F32)
        first, end, index = c.sb(ctx, "first_tile", [P, E], F32), c.sb(ctx, "end_tile", [P, E], F32), c.sb(ctx, "partition", [P, 1], F32)
        many = c.sb(ctx, "many", [P, 2], F32)
        passed, of_tile = c.sb(ctx, "passed", [P, E], F32), c.sb(ctx, "of_tile", [P, 1], F32)
        where = c.sb(ctx, "where", [P, NT], F32)
        mixT = c.sb(ctx, "mixT", [E, T], F32)
        norm = NormBlock(c)
        (w_loaded, drawn, chain, wT_psum, wT_ready, h_psum, hvar_ready, hstd_ready, h_ready, hT_psum, hT_ready, lg_psum, shifted, exp_ready,
         sel_ready, rank_psum, mix_ready, mixT_psum, mixT_ready, ranked, of_tile_ready, of_tile_psum, ob_psum) = (c.sem("r_" + n) for n in (
             "w_loaded", "drawn", "chain", "wT_psum", "wT_ready", "h_psum", "hvar_ready", "hstd_ready", "h_ready", "hT_psum", "hT_ready",
             "lg_psum", "shifted", "exp_ready", "sel_ready", "rank_psum", "mix_ready", "mixT_psum", "mixT_ready", "ranked", "of_tile_ready",
             "of_tile_psum", "ob_psum"))
        loads = [(w1[:, :], ins["L2_ffn_rW1"]), (w2[:, :], ins["L2_ffn_rW2"]), (ob[:, :], ins["L2_ffn_ob"]),
                 (b1[:, :], row_view(ins["L2_ffn_rb1"], W)), (g1[:, :], row_view(ins["L2_ffn_ln_g"], W)),
                 (g0[:, :], row_view(ins["L2_ffn_ln_b"], W)), (b2[:, :], row_view(ins["L2_ffn_rb2"], E))]
        DRAWN = E + NT + 3

        def per_token(s, width):
            return s.unsqueeze(2).to_broadcast([P, NT, width])

        def per_column(s, width):
            return s.unsqueeze(1).to_broadcast([P, NT, width])

        with nc.Block() as block:
            @block.sync
            def _(sp):
                for dst, src in loads:
                    sp.dma_start(dst, src).then_inc(w_loaded, 16)
                fixed.sync(sp)
                fixed.sync_end(sp)

            @block.gpsimd
            def _(pool):
                draw_order(c, pool, order, E, drawn)
                for t in range(NT):
                    nc.gpsimd.memset(edge[:, t:t + 1], float(P * t)).then_inc(drawn, 1)
                nc.gpsimd.memset(ones[:, :], 1.0).then_inc(drawn, 1)
                nc.gpsimd.memset(before[:, :], 1.0).then_inc(drawn, 1)
                pool.wait_ge(drawn, DRAWN - 1)
                nc.gpsimd.affine_select(out=before[:, :], in_=before[:, :], compare_op=ALU.is_gt, fill=0.0, base=0,
                                        pattern=[[1, P]], channel_multiplier=-1).then_inc(drawn, 1)
                fixed.gpsimd()
                fixed.wait(pool)

            @block.tensor
            def _(pe):
                pe.wait_ge(w_loaded, 16 * len(loads))
                nc.tensor.transpose(ps[:, 4, 0:W], w1[:, :], c.ident[0:W, 0:W])
                nc.tensor.transpose(ps[0:W, 4, W:W + E], w2[:, :], c.ident[0:E, 0:E]).then_inc(wT_psum, 1)
                norm.tensor(pe)
                pe.wait_ge(wT_ready, 2)
                pe.wait_ge(norm.nT_ready, NC)
                for t in range(NT):
                    ins_ = nc.tensor.matmul(ps[:, 4 + t // 8, (t % 8) * W:(t % 8 + 1) * W], c.nT[:, t * P:(t + 1) * P], w1T[:, :],
                                            start=True, stop=True)
                    if t % 8 == 7:
                        ins_.then_inc(h_psum, 1)
                pe.wait_ge(h_ready, 1)
                for t in range(NT):
                    ins_ = nc.tensor.transpose(ps[0:W, t // 4, (t % 4) * P:(t % 4 + 1) * P], h[:, t, :], c.ident[:, :])
                    if t % 4 == 3:
                        ins_.then_inc(hT_psum, 1)
                pe.wait_ge(hT_ready, NC)
                for t in range(NT):
                    last = nc.tensor.matmul(ps[:, 6, t * E:(t + 1) * E], hT[:, t * P:(t + 1) * P], w2T[:, :], start=True, stop=True)
                last.then_inc(lg_psum, 1)
                pe.wait_ge(drawn, DRAWN)
                pe.wait_ge(sel_ready, 1)
                chosen = sel[:, :, :].rearrange("p t e -> p (t e)")
                nc.tensor.matmul(ps[:, 7, 0:P], before[:, :], chosen, start=True, stop=True)
                nc.tensor.matmul(ps[:, 7, P:2 * P], ones[:, :], chosen, start=True, stop=True)
                nc.tensor.matmul(ps[:, 7, 2 * P:2 * P + 1], before[:, :], ones[:, 0:1], start=True, stop=True).then_inc(rank_psum, 1)
                pe.wait_ge(mix_ready, 1)
                for t in range(NT):
                    ins_ = nc.tensor.transpose(ps[0:E, t // 4, (t % 4) * P:(t % 4 + 1) * P], mix[:, t, :], c.ident[:, :])
                    if t % 4 == 3:
                        ins_.then_inc(mixT_psum, 1)
                pe.wait_ge(of_tile_ready, 1)
                nc.tensor.transpose(ps[0:1, 6, 0:P], of_tile[:, :], c.ident[:, :]).then_inc(of_tile_psum, 1)
                pe.wait_ge(mixT_ready, NC)
                pe.wait_ge(ranked, 1)
                for t in range(NT):
                    ins_ = nc.tensor.matmul(ps[:, 4 + t // 4, (t % 4) * P:(t % 4 + 1) * P], mixT[:, t * P:(t + 1) * P], ob[:, :],
                                            start=True, stop=True)
                    if t % 4 == 3:
                        ins_.then_inc(ob_psum, 1)

            @block.scalar
            def _(act):
                act.wait_ge(wT_psum, 1)
                nc.scalar.activation(w1T[:, :], ps[:, 4, 0:W], ACT.Copy).then_inc(wT_ready, 1)
                nc.scalar.activation(w2T[:, :], ps[0:W, 4, W:W + E], ACT.Copy).then_inc(wT_ready, 1)
                norm.scalar(act, c.nT)
                act.wait_ge(hvar_ready, 1)
                nc.scalar.activation(total[:, :], total[:, :], ACT.Sqrt).then_inc(hstd_ready, 1)
                for k in range(NC):
                    act.wait_ge(hT_psum, k + 1)
                    nc.scalar.activation(hT[:, k * 512:(k + 1) * 512], ps[0:W, k, :], ACT.Copy).then_inc(hT_ready, 1)
                act.wait_ge(shifted, 1)
                nc.scalar.activation(probs[:, :, :], probs[:, :, :], ACT.Exp).then_inc(exp_ready, 1)
                for k in range(NC):
                    act.wait_ge(mixT_psum, k + 1)
                    nc.scalar.activation(mixT[:, k * 512:(k + 1) * 512], ps[0:E, k, :], ACT.Copy).then_inc(mixT_ready, 1)

            @block.vector
            def _(dve):
                v = nc.vector
                link = Chain(dve, chain)
                norm.vector(dve, link)
                dve.wait_ge(w_loaded, 16 * len(loads))
                for b in range(2):
                    dve.wait_ge(h_psum, b + 1)
                    link(v.tensor_tensor(h[:, 8 * b:8 * b + 8, :], ps[:, 4 + b, :].rearrange("p (t w) -> p t w", w=W),
                                         b1[:, :].unsqueeze(1).to_broadcast([P, 8, W]), ALU.add))
                link(v.tensor_reduce(total[:, :], h[:, :, :], X, ALU.add))
                link(v.tensor_scalar(tie[:, :], total[:, :], 1.0 / W, None, ALU.mult))
                link(v.tensor_tensor(h[:, :, :], h[:, :, :], per_token(tie[:, :], W), ALU.subtract))
                link(v.tensor_tensor(hh[:, :, :], h[:, :, :], h[:, :, :], ALU.mult))
                link(v.tensor_reduce(tie[:, :], hh[:, :, :], X, ALU.add))
                v.tensor_scalar(total[:, :], tie[:, :], 1.0 / W, 1e-5, ALU.mult, ALU.add).then_inc(hvar_ready, 1)
                dve.wait_ge(hstd_ready, 1)
                link(v.reciprocal(tie[:, :], total[:, :]))
                link(v.tensor_tensor(h[:, :, :], h[:, :, :], per_token(tie[:, :], W), ALU.mult))
                link(v.tensor_tensor(h[:, :, :], h[:, :, :], per_column(g1[:, :], W), ALU.mult))
                link(v.tensor_tensor(h[:, :, :], h[:, :, :], per_column(g0[:, :], W), ALU.add))
                v.tensor_scalar(h[:, :, :], h[:, :, :], 0.0, None, ALU.max).then_inc(h_ready, 1)
                dve.wait_ge(lg_psum, 1)
                link(v.tensor_tensor(masked[:, :, :], ps[:, 6, 0:NT * E].rearrange("p (t e) -> p t e", e=E), per_column(b2[:, :], E), ALU.add))
                link(v.tensor_reduce(tie[:, :], masked[:, :, :], X, ALU.max))
                v.tensor_tensor(probs[:, :, :], masked[:, :, :], per_token(tie[:, :], E), ALU.subtract).then_inc(shifted, 1)
                dve.wait_ge(exp_ready, 1)
                link(v.tensor_reduce(total[:, :], probs[:, :, :], X, ALU.add))
                link(v.reciprocal(tie[:, :], total[:, :]))
                link(v.tensor_tensor(probs[:, :, :], probs[:, :, :], per_token(tie[:, :], E), ALU.mult))
                dve.wait_ge(drawn, DRAWN)
                top_choice(c, v, link, probs[:, :, :], best[:, 0, :], tie[:, :], order[:, :], choice[:, 0], E)
                link(v.scalar_tensor_tensor(masked[:, :, :], choice[:, 0], MASKED, probs[:, :, :], ALU.mult, ALU.add))
                top_choice(c, v, link, masked[:, :, :], best[:, 1, :], tie[:, :], order[:, :], choice[:, 1], E)
                v.tensor_tensor(sel[:, :, :], choice[:, 0], choice[:, 1], ALU.add).then_inc(sel_ready, 1)
                link(v.tensor_tensor(total[:, :], best[:, 0, :], best[:, 1, :], ALU.add))
                link(v.reciprocal(tie[:, :], total[:, :]))
                for k in range(K):
                    link(v.tensor_tensor(gate[:, k, :], best[:, k, :], tie[:, :], ALU.mult))
                link(v.tensor_tensor(mix[:, :, :], choice[:, 0], per_token(gate[:, 0, :], E), ALU.mult))
                link(v.tensor_tensor(tmp[:, :, :], choice[:, 1], per_token(gate[:, 1, :], E), ALU.mult))
                v.tensor_tensor(mix[:, :, :], mix[:, :, :], tmp[:, :, :], ALU.add).then_inc(mix_ready, 1)
                dve.wait_ge(mix_ready, 1)
                dve.wait_ge(rank_psum, 1)
                link(v.tensor_copy(counts[:, :, :], ps[:, 7, P:2 * P].rearrange("p (t e) -> p t e", e=E)))
                link(v.tensor_copy(index[:, :], ps[:, 7, 2 * P:2 * P + 1]))
                link(v.memset(offset[:, 0, :], 0.0))
                for t in range(1, NT):
                    link(v.tensor_tensor(offset[:, t, :], offset[:, t - 1, :], counts[:, t - 1, :], ALU.add))
                link(v.tensor_tensor(end[:, :], offset[:, NT - 1, :], counts[:, NT - 1, :], ALU.add))
                link(v.tensor_tensor(more[:, :, :], end[:, :].unsqueeze(2).to_broadcast([P, E, NT]),
                                     edge[:, :].unsqueeze(1).to_broadcast([P, E, NT]), ALU.is_gt))
                link(v.tensor_reduce(tiles_of[:, :], more[:, :, :], X, ALU.add))
                link(v.memset(first[:, 0:1], 0.0))
                for e in range(1, E):
                    link(v.tensor_tensor(first[:, e:e + 1], first[:, e - 1:e], tiles_of[:, e - 1:e], ALU.add))
                link(v.tensor_tensor(end[:, :], first[:, :], tiles_of[:, :], ALU.add))
                link(v.tensor_scalar(passed[:, :], end[:, :], index[:, 0:1], None, ALU.is_le))
                link(v.tensor_reduce(of_tile[:, :], passed[:, :], X, ALU.add))
                v.tensor_scalar(of_tile[:, :], of_tile[:, :], float(E - 1), None, ALU.min).then_inc(of_tile_ready, 1)
                link(v.memset(many[:, 0:1], float(rt.least_rounds)))
                for n in range(rt.least_rounds, rt.tiles // 2):
                    link(v.tensor_scalar(many[:, 1:2], end[:, E - 1:E], 2.0 * n, None, ALU.is_gt))
                    link(v.tensor_tensor(many[:, 0:1], many[:, 0:1], many[:, 1:2], ALU.add))
                link(v.tensor_copy(rt.rounds[:, :], many[0:1, 0:1]))
                link(v.tensor_scalar(first[:, :], first[:, :], float(P), None, ALU.mult))
                link(v.tensor_tensor(offset[:, :, :], offset[:, :, :], per_column(first[:, :], E), ALU.add))
                link(v.tensor_tensor(offset[:, :, :], offset[:, :, :], ps[:, 7, 0:P].rearrange("p (t e) -> p t e", e=E), ALU.add))
                for k in range(K):
                    link(v.tensor_tensor(tmp[:, :, :], choice[:, k], offset[:, :, :], ALU.mult))
                    link(v.tensor_reduce(where[:, :], tmp[:, :, :], X, ALU.add))
                    link(v.tensor_copy(slot[:, k, :], where[:, :]))
                    link(v.tensor_scalar(y_row[:, k, :], where[:, :], float(P), None, ALU.add))
                    link(v.tensor_tensor(tmp[:, :, :], choice[:, k], per_column(order[:, :], E), ALU.mult))
                    link(v.tensor_reduce(where[:, :], tmp[:, :, :], X, ALU.add))
                    link(v.tensor_scalar(where[:, :], where[:, :], -float(T), float(E * T), ALU.mult, ALU.add))
                    link(v.tensor_tensor(where[:, :], where[:, :], edge[:, :], ALU.add))
                    link(v.tensor_scalar(row[:, k, :], where[:, :], index[:, 0:1], None, ALU.add))
                dve.wait_ge(of_tile_psum, 1)
                v.tensor_copy(rt.expert_of[:, :], ps[0:1, 6, 0:rt.listed]).then_inc(ranked, 1)
                add_banks(c, dve, link, c.x, 4, ob_psum)


def l2_prepare(c, at, ins, rt, slot, row):
    nc, ps = c.nc, c.ps
    E, K = rt.E, 2
    with ExitStack() as ctx:
        w = c.sb(ctx, "w_qkvo", [P, 2, 4, P], F32)
        bq, bv, bk = c.sb(ctx, "b_q", [P, 2, P], F32), c.sb(ctx, "b_v", [P, 2, P], F32), c.sb(ctx, "b_k", [P, 2], F32)
        bq_ordered = c.sb(ctx, "b_q_head_order", [P, P], F32)
        wT = c.sb(ctx, "wT_qkvo", [P, 2, 4, P], F32)
        used = 2 * rt.least_rounds + 1
        blank_y, y_blanked = c.sb(ctx, "blank_y", [P, P], F32), c.sem("p_y_blanked")
        blank = c.sb(ctx, "blank_list", [rt.listed, P], mybir.dt.uint32)
        start = c.sb(ctx, "p_start_credit", [P, 10], F32)
        w_loaded, b_loaded = ([c.sem(f"p_{n}_loaded{k}") for k in range(2)] for n in "wb")
        (wT_psum, wT_ready, k_psum, k_ready, v_psum, v_ready, q_psum, q_ready, rest_ready, mid_ready, parts_ready, ordered,
         v_stored, q_stored, blanked, scattered) = (c.sem("p_" + n) for n in (
             "wT_psum", "wT_ready", "k_psum", "k_ready", "v_psum", "v_ready", "q_psum", "q_ready", "rest_ready", "mid_ready", "parts_ready",
             "ordered", "v_stored", "q_stored", "blanked", "scattered"))
        o_stored, parts_stored = ([c.sem(f"p_{n}_stored{k}") for k in range(2)] for n in ("o", "parts"))
        parts = ((at.hi, at.mid, at.lo), [c.sb(ctx, f"other_{n}", [P, T], BF16) for n in ("hi", "mid", "lo")])
        LOADS = 16 * 4
        rest = c.b[:, :, :].rearrange("p t d -> p (t d)")
        with nc.Block() as block:
            def done(n, e):
                return e * n + n

            def each_expert(eng, body):
                with eng.Fori(0, E // 2) as r:
                    for k in range(2):
                        body(r * 2 + k, k, r)

            @block.sync
            def _(sp):
                def load_weights(k, e):
                    for n, m in enumerate("qkvo"):
                        sp.dma_start(w[:, k, n, :], ins[f"L2_ffn_{m}W"][bass.ds(e, 1)].rearrange("e p d -> (e p) d")).then_inc(w_loaded[k], 16)

                def load_biases(k, e):
                    def vector(name):
                        return ins[name][bass.ds(e, 1)]
                    sp.dma_start(bq[:, k, :], vector("L2_ffn_qb").to_broadcast([P, P])).then_inc(b_loaded[k], 16)
                    sp.dma_start(bv[:, k, :], vector("L2_ffn_vb").to_broadcast([P, P])).then_inc(b_loaded[k], 16)
                    for j in range(2):
                        sp.dma_start(bk[64 * j:64 * j + 64, k:k + 1], vector("L2_ffn_kb").rearrange("e (p j d) -> j d p e", p=NPAIR, j=2)[j],
                                     allow_slow_non_contiguous=True).then_inc(b_loaded[k], 16)

                def stores(e, k, r):
                    sp.wait_ge(wT_ready, e * 3 + 3)
                    load_weights(k, (e + 2) % E)
                    sp.dma_start(rt.w_out_dram[bass.ds(e, 1)].rearrange("e p d -> (e p) d"), wT[:, k, 3, :]).then_inc(o_stored[k], 16)
                    sp.wait_ge(v_ready, done(2, e + 1))
                    sp.dma_start(rt.v_dram[bass.ds(e, 1)].rearrange("e p t h d -> (e p) (t h d)"),
                                 at.v[:, 0].rearrange("p t h d -> p (t h d)")).then_inc(v_stored, 16)
                    sp.wait_ge(q_ready, done(4, e + 1))
                    sp.dma_start(rt.q_dram[bass.ds(e * T, T), :].rearrange("(t p) d -> p t d", p=P), c.a).then_inc(q_stored, 16)
                    store_keys(at, sp, e, parts[k], parts_ready, done(1, e + 1), parts_stored[k])
                    load_biases(k, (e + 2) % E)

                for k in range(2):
                    load_weights(k, k)
                    load_biases(k, k)
                each_expert(sp, stores)
                for k in range(2):
                    sp.wait_ge(w_loaded[k], LOADS * (E // 2 + 1))
                    sp.wait_ge(b_loaded[k], LOADS * (E // 2 + 1))
                for s in (v_stored, q_stored):
                    sp.wait_ge(s, done(16, E))
                for k in range(2):
                    sp.wait_ge(o_stored[k], 16 * (E // 2 + k))
                    sp.wait_ge(parts_stored[k], done(48, E // 2))

            @block.gpsimd
            def _(pool):
                nc.gpsimd.memset(blank[:, :], 0).then_inc(blanked, 1)
                nc.gpsimd.memset(blank_y[:, :], 0.0).then_inc(blanked, 1)
                pool.wait_ge(blanked, 2)
                pool.dma_start(rt.y_dram[used:].rearrange("i p d -> p i d"),
                               blank_y[:, :].unsqueeze(1).to_broadcast([P, rt.tiles + 1 - used, P])).then_inc(y_blanked, 16)
                pool.dma_start(rt.list_dram[:, :], blank[:, :]).then_inc(scattered, 16)
                pool.wait_ge(scattered, 16)
                for t in range(NT):
                    for k in range(K):
                        nc.gpsimd.indirect_dma_start(out=rt.list_dram.rearrange("i (p a) -> (i p) a", a=1),
                                                     out_offset=bass.IndirectOffsetOnAxis(ap=slot[:, k, t:t + 1], axis=0),
                                                     in_=row[:, k, t:t + 1], in_offset=None).then_inc(scattered, 16)
                pool.wait_ge(scattered, 16 * (1 + K * NT))
                pool.wait_ge(y_blanked, 16)

            @block.tensor
            def _(pe):
                def transpose_weights(k):
                    for n in range(4):
                        last = nc.tensor.transpose(ps[:, 6 + k, n * P:(n + 1) * P], w[:, k, n, :], c.ident[:, :])
                    last.then_inc(wT_psum, 1)

                def values(half, k):
                    for t in range(8):
                        tile = 8 * half + t
                        last = nc.tensor.matmul(ps[:, 4 + t // 4, (t % 4) * P:(t % 4 + 1) * P], c.nT[:, tile * P:(tile + 1) * P],
                                                wT[:, k, 2, :], start=True, stop=True)
                    last.then_inc(v_psum, 1)

                def project(e, k, r):
                    pe.wait_ge(wT_ready, e * 3 + 3)
                    pe.wait_ge(q_ready, done(4, e))
                    project_channels(c, wT[:, k, 1, :], c.nT, 0, k_psum)
                    pe.wait_ge(v_ready, done(2, e))
                    values(0, k)
                    pe.wait_ge(w_loaded[1 - k], (r + k) * LOADS + LOADS)
                    transpose_weights(1 - k)
                    pe.wait_ge(v_ready, e * 2 + 3)
                    values(1, k)
                    pe.wait_ge(k_ready, e * 8 + 8)
                    project_tokens(c, c.nT, wT[:, k, 0, :], 0, q_psum)

                pe.wait_ge(w_loaded[0], LOADS)
                transpose_weights(0)
                each_expert(pe, project)

            @block.scalar
            def _(act):
                def copy_weights(k, count):
                    act.wait_ge(wT_psum, count)
                    for n in range(2):
                        nc.scalar.activation(split_heads(wT[:, k, n, :]), head_order(ps[:, 6 + k, n * P:(n + 1) * P]), ACT.Copy).then_inc(wT_ready, 1)
                    nc.scalar.activation(wT[:, k, 2:4, :].rearrange("p n d -> p (n d)"), ps[:, 6 + k, 2 * P:4 * P], ACT.Copy).then_inc(wT_ready, 1)

                def keys(e, k, r):
                    act.wait_ge(rest_ready, done(1, e))
                    act.wait_ge(parts_stored[k], done(48, r))
                    act.wait_ge(b_loaded[k], r * LOADS + LOADS)
                    for n in range(NC):
                        act.wait_ge(k_psum, e * 4 + (n + 1))
                        for dst in (parts[k][0], c.kT):
                            nc.scalar.activation(dst[:, n * 512:(n + 1) * 512], ps[:, n, :], ACT.Identity, bias=bk[:, k:k + 1]).then_inc(k_ready, 1)
                    act.wait_ge(q_psum, done(4, e))
                    act.wait_ge(o_stored[1 - k], r * 16 + 16)
                    copy_weights(1 - k, e + 2)
                    act.wait_ge(rest_ready, done(1, e + 1))
                    nc.scalar.activation(parts[k][1][:, :], rest, ACT.Copy).then_inc(mid_ready, 1)

                copy_weights(0, 1)
                each_expert(act, keys)

            @block.vector
            def _(dve):
                v = nc.vector
                for n, (s, credit) in enumerate(((parts_ready, 1), (q_psum, 4), (q_ready, 4), (v_ready, 2), (parts_stored[0], 48), (parts_stored[1], 48),
                                                 (v_stored, 16), (q_stored, 16), (o_stored[1], 16), (rest_ready, 1))):
                    v.memset(start[:, n:n + 1], 0.0).then_inc(s, credit)

                def biases(e, k, r):
                    dve.wait_ge(b_loaded[k], r * LOADS + LOADS)
                    dve.wait_ge(q_ready, done(4, e))
                    v.tensor_copy(split_heads(bq_ordered[:, :]), head_order(bq[:, k, :])).then_inc(ordered, 1)
                    dve.wait_ge(v_stored, done(16, e))
                    for half in range(2):
                        dve.wait_ge(v_psum, e * 2 + (half + 1))
                        v.tensor_tensor(at.v[:, 0, 8 * half:8 * half + 8, :, 0:HD], ps[:, 4:6, :].rearrange("p b (t h d) -> p (b t) h d", t=4, h=H),
                                        bv[:, k, :].rearrange("p (h d) -> p h d", h=H).unsqueeze(1).to_broadcast([P, 8, H, HD]),
                                        ALU.add).then_inc(v_ready, 1)
                    dve.wait_ge(k_ready, e * 8 + 8)
                    dve.wait_ge(parts_ready, done(1, e))
                    v.tensor_tensor(rest, c.kT, parts[k][0][:, :], ALU.subtract).then_inc(rest_ready, 1)
                    dve.wait_ge(ordered, e + 1)
                    dve.wait_ge(q_stored, done(16, e))
                    for b in range(4):
                        dve.wait_ge(q_psum, e * 4 + (b + 5))
                        v.tensor_tensor(c.a[:, 4 * b:4 * b + 4, :], ps[:, b, :].rearrange("p (t d) -> p t d", t=4),
                                        bq_ordered[:, :].unsqueeze(1).to_broadcast([P, 4, P]), ALU.add).then_inc(q_ready, 1)
                    dve.wait_ge(mid_ready, e + 1)
                    v.tensor_tensor(parts[k][2][:, :], rest, parts[k][1][:, :], ALU.subtract).then_inc(parts_ready, 1)

                each_expert(dve, biases)


def l2_collect(c, rt, gate, y_row):
    nc = c.nc
    B = 2
    gathered, added = [c.sem(f"c_gathered{n}") for n in range(NT // B)], c.sem("c_added")
    y = (c.a, c.b)
    with nc.Block() as block:
        @block.gpsimd
        def _(pool):
            for t in range(NT):
                for k in range(2):
                    nc.gpsimd.indirect_dma_start(out=y[k][:, t, :], out_offset=None, in_=rt.y_dram.rearrange("i p d -> (i p) d"),
                                                 in_offset=bass.IndirectOffsetOnAxis(ap=y_row[:, k, t:t + 1], axis=0)).then_inc(gathered[t // B], 16)

        @block.vector
        def _(dve):
            for t in range(NT):
                dve.wait_ge(gathered[t // B], 16 * 2 * B)
                for k in range(2):
                    nc.vector.scalar_tensor_tensor(c.x[:, t, :], y[k][:, t, :], gate[:, k, t:t + 1], c.x[:, t, :],
                                                   ALU.mult, ALU.add).then_inc(added, 1)
                    dve.wait_ge(added, 2 * t + k + 1)


def l3_state(c, ins):
    nc = c.nc
    c.layer = "l3a_"
    N, KC = 64, 4
    ps = c.ps
    with ExitStack() as ctx:
        xp = c.sb(ctx, "n_padded", [P, KC - 1 + T], F32)
        conv, conv_w, conv_b = c.sb(ctx, "conv", [P, T], F32), c.sb(ctx, "conv_w", [P, KC], F32), c.sb(ctx, "conv_b", [P, 1], F32)
        wp, ws, w_out, b_out = c.sb(ctx, "wp", [P, 2 * N], F32), c.sb(ctx, "ws", [P, N], F32), c.sb(ctx, "w_out", [N, P], F32), c.sb(ctx, "b_out", [P, P], F32)
        bp, bs = c.sb(ctx, "bp", [N, 2], F32), c.sb(ctx, "bs", [N, 1], F32)
        log, sp_, tl = c.sb(ctx, "a_dt_log", [N, 2], F32), c.sb(ctx, "a_dt", [N, 2], F32), c.sb(ctx, "a_dt_tail", [N, 2], F32)
        decay = c.sb(ctx, "decay", [N, 1], F32)
        u, b_t, c_t, mag = (c.sb(ctx, n, [N, T], F32) for n in ("u", "b_t", "c_t", "magnitude"))
        norm = NormBlock(c)
        w_loaded, chain, act_chain, conv_ready, u_psum, u_ready, p_psum, c_ready, tail_ready, dt_ready, y_ready, y_psum = (c.sem(n) for n in (
            "w_loaded", "chain", "act_chain", "conv_ready", "u_psum", "u_ready", "p_psum", "c_ready", "tail_ready", "dt_ready", "y_ready", "y_psum"))
        loads = [(conv_w[:, :], ins["L3_attn_conv_w"].rearrange("k a d -> d (k a)")), (conv_b[:, :], column(ins["L3_attn_conv_b"])),
                 (wp[:, :], ins["L3_attn_Wp"]), (bp[:, :], ins["L3_attn_bp"].rearrange("(k n) -> n k", n=N)), (ws[:, :], ins["L3_attn_Ws"]),
                 (bs[:, :], column(ins["L3_attn_bs"])), (log[:, 0:1], column(ins["L3_attn_A_log"])), (log[:, 1:2], column(ins["L3_attn_dt_log"])),
                 (w_out[:, :], ins["L3_attn_Wo"]), (b_out[:, :], row_view(ins["L3_attn_bo"], P))]

        def flat(bank0):
            return ps[0:N, bank0:bank0 + 4, :].rearrange("p b n -> p (b n)")

        with nc.Block() as block:
            @block.sync
            def _(sp):
                for dst, src in loads:
                    sp.dma_start(dst, src, allow_slow_non_contiguous=True).then_inc(w_loaded, 16)

            @block.tensor
            def _(pe):
                norm.tensor(pe)
                pe.wait_ge(w_loaded, 16 * len(loads))
                pe.wait_ge(norm.nT_ready, NC)
                for k in range(NC):
                    last = nc.tensor.matmul(ps[0:N, 4 + k, :], ws[:, :], xp[:, KC - 1 + k * 512:KC - 1 + (k + 1) * 512], start=True, stop=True)
                last.then_inc(u_psum, 1)
                pe.wait_ge(conv_ready, 1)
                for part in range(2):
                    if part:
                        pe.wait_ge(u_ready, 1)
                    for k in range(NC):
                        last = nc.tensor.matmul(ps[0:N, 4 * part + k, :], wp[:, part * N:(part + 1) * N], conv[:, k * 512:(k + 1) * 512],
                                                start=True, stop=True)
                    last.then_inc(p_psum, 1)
                pe.wait_ge(y_ready, 1)
                project_tokens(c, c_t, w_out[:, :], 4, y_psum)

            @block.scalar
            def _(act):
                link = Chain(act, act_chain)
                norm.scalar(act, xp[:, KC - 1:])
                act.wait_ge(w_loaded, 16 * len(loads))
                act.wait_ge(u_psum, 1)
                nc.scalar.activation(u[:, :], flat(4), ACT.Identity, bias=bs[:, :]).then_inc(u_ready, 1)
                softplus_scalar(c, act, link, log[:, :], 0.0, sp_[:, :], tl[:, :]).then_inc(dt_ready, 1)
                act.wait_ge(p_psum, 1)
                softplus_scalar(c, act, link, flat(0), bp[:, 0:1], mag[:, :], b_t[:, :]).then_inc(tail_ready, 1)
                act.wait_ge(p_psum, 2)
                nc.scalar.activation(c_t[:, :], flat(4), ACT.Tanh, bias=bp[:, 1:2]).then_inc(c_ready, 1)

            @block.vector
            def _(dve):
                v = nc.vector
                link = Chain(dve, chain)
                link(v.memset(xp[:, 0:KC - 1], 0.0))
                norm.vector(dve, link)
                dve.wait_ge(w_loaded, 16 * len(loads))
                dve.wait_ge(norm.nT_ready, NC)
                link(v.tensor_scalar(conv[:, :], xp[:, 0:T], conv_w[:, 0:1], conv_b[:, :], ALU.mult, ALU.add))
                for k in range(1, KC):
                    last = v.scalar_tensor_tensor(conv[:, :], xp[:, k:k + T], conv_w[:, k:k + 1], conv[:, :], ALU.mult, ALU.add)
                    if k < KC - 1:
                        link(last)
                last.then_inc(conv_ready, 1)
                dve.wait_ge(dt_ready, 1)
                link(v.scalar_tensor_tensor(sp_[:, :], log[:, :], 0.0, tl[:, :], ALU.max, ALU.add))
                link(v.tensor_tensor(decay[:, :], sp_[:, 0:1], sp_[:, 1:2], ALU.mult))
                link(v.tensor_scalar(decay[:, :], decay[:, :], -1.0, 1.0, ALU.mult, ALU.add))
                dve.wait_ge(tail_ready, 1)
                link(v.tensor_scalar(mag[:, :], flat(0), bp[:, 0:1], 0.0, ALU.add, ALU.max))
                link(v.tensor_tensor(b_t[:, :], b_t[:, :], mag[:, :], ALU.add))
                dve.wait_ge(u_ready, 1)
                link(v.scalar_tensor_tensor(u[:, :], b_t[:, :], sp_[:, 1:2], u[:, :], ALU.mult, ALU.mult))
                link(v.tensor_tensor_scan(b_t[:, :], decay[:, :].to_broadcast([N, T]), u[:, :], 0.0, ALU.mult, ALU.add))
                dve.wait_ge(c_ready, 1)
                v.tensor_tensor(c_t[:, :], c_t[:, :], b_t[:, :], ALU.mult).then_inc(y_ready, 1)
                link(v.tensor_tensor(c.x[:, :, :], c.x[:, :, :], b_out[:, :].unsqueeze(1).to_broadcast([P, NT, P]), ALU.add))
                add_banks(c, dve, link, c.x, 4, y_psum)


def l3_ffn(c, ins):
    nc = c.nc
    c.layer = "l3f_"
    E = 4
    ps = c.ps
    with ExitStack() as ctx:
        gamma, beta = c.sb(ctx, "gamma", [P, P], F32), c.sb(ctx, "beta", [P, P], F32)
        choice, bias = c.sb(ctx, "choice", [P, NT, E], F32), c.sb(ctx, "b1_columns", [P, E * 4], F32)
        with ExitStack() as rctx:
            wr, b_out = c.sb(rctx, "w_router", [P, E], F32), c.sb(rctx, "b_out", [P, P], F32)
            b1, lg, order = c.sb(rctx, "b1_rows", [E * 4, P], F32), c.sb(rctx, "logits", [P, NT, E], F32), c.sb(rctx, "order", [P, E], F32)
            best, tie = c.sb(rctx, "best", [P, NT], F32), c.sb(rctx, "tie", [P, NT], F32)
            norm = NormBlock(c)
            w_loaded, chain, drawn, b1_psum, b1_ready, lg_psum = (c.sem(n) for n in ("w_loaded", "chain", "drawn", "b1_psum", "b1_ready", "lg_psum"))
            loads = [(wr[:, :], ins["L3_ffn_W_router"]), (b_out[:, :], row_view(ins["L3_ffn_bo"], P)),
                     (b1[:, :], ins["L3_ffn_b1"].rearrange("e (f p) -> (e f) p", p=P)),
                     (gamma[:, :], row_view(ins["L3_ffn_ln_gamma"], P)), (beta[:, :], row_view(ins["L3_ffn_ln_beta"], P))]
            with nc.Block() as block:
                @block.sync
                def _(sp):
                    for dst, src in loads:
                        sp.dma_start(dst, src).then_inc(w_loaded, 16)

                @block.gpsimd
                def _(pool):
                    draw_order(c, pool, order, E, drawn)

                @block.tensor
                def _(pe):
                    norm.tensor(pe)
                    pe.wait_ge(w_loaded, 16 * len(loads))
                    nc.tensor.transpose(ps[:, 4, 0:E * 4], b1[:, :], c.ident[0:E * 4, 0:E * 4]).then_inc(b1_psum, 1)
                    pe.wait_ge(norm.nT_ready, NC)
                    for t in range(NT):
                        last = nc.tensor.matmul(ps[:, 5, t * E:(t + 1) * E], c.nT[:, t * P:(t + 1) * P], wr[:, :], start=True, stop=True)
                    last.then_inc(lg_psum, 1)

                @block.scalar
                def _(act):
                    norm.scalar(act, c.nT)
                    act.wait_ge(b1_psum, 1)
                    nc.scalar.activation(bias[:, :], ps[:, 4, 0:E * 4], ACT.Copy).then_inc(b1_ready, 1)

                @block.vector
                def _(dve):
                    link = Chain(dve, chain)
                    norm.vector(dve, link)
                    dve.wait_ge(w_loaded, 16 * len(loads))
                    dve.wait_ge(drawn, E)
                    dve.wait_ge(lg_psum, 1)
                    link(nc.vector.tensor_copy(lg[:, :, :], ps[:, 5, 0:NT * E].rearrange("p (t e) -> p t e", e=E)))
                    top_choice(c, nc.vector, link, lg[:, :, :], best[:, :], tie[:, :], order[:, :], choice[:, :, :], E)
                    dve.wait_ge(norm.nT_psum, 4)
                    link(nc.vector.tensor_tensor(c.n[:, :, :], c.n[:, :, :], b_out[:, :].unsqueeze(1).to_broadcast([P, NT, P]), ALU.add))
        experts(c, ctx, E, ins["L3_ffn_W1"], lambda e: ins["L3_ffn_Wo"].rearrange("(a i) d -> a i d", a=1), bias, choice)
        var_ready, std_ready, chain, h_ready = c.sem("f_var_ready"), c.sem("f_std_ready"), c.sem("f_chain"), c.sem("f_h_ready")
        with nc.Block() as block:
            @block.scalar
            def _(act):
                layer_norm_scalar(c, act, var_ready, std_ready, 1)

            @block.vector
            def _(dve):
                v = nc.vector
                link = Chain(dve, chain)
                layer_norm_vector(c, dve, link, c.n, c.a, var_ready, std_ready, 1, 1e-12, h_ready)
                dve.wait_ge(h_ready, NC)
                link(v.tensor_tensor(c.a[:, :, :], c.a[:, :, :], gamma[:, :].unsqueeze(1).to_broadcast([P, NT, P]), ALU.mult))
                link(v.tensor_tensor(c.x[:, :, :], c.x[:, :, :], beta[:, :].unsqueeze(1).to_broadcast([P, NT, P]), ALU.add))
                link(v.tensor_tensor(c.x[:, :, :], c.x[:, :, :], c.a[:, :, :], ALU.add))


def store_output(c, out):
    nc = c.nc
    stored = c.sem("x_stored")
    with nc.Block() as block:
        @block.sync
        def _(sp):
            sp.dma_start(out[0].rearrange("(t p) d -> p t d", p=P), c.x[:, :, :]).then_inc(stored, 16)
            sp.wait_ge(stored, 16)


def build(nc, ins, out, layers=range(8)):
    with ExitStack() as ctx:
        c = Core(nc, ctx)
        constants(c, ins)
        with ExitStack() as actx:
            if 0 in layers or 1 in layers:
                at = Attention(c, actx)
            if 0 in layers:
                c.layer = "l0a_"
                l0_attention(c, at, ins, AttentionConstants(c, at, 1))
                c.end_sublayer()
            if 1 in layers:
                l0_ffn(c, at, ins, None if 0 in layers else AttentionConstants(c, at, 1))
                c.end_sublayer()
        if 2 in layers:
            l1_mamba(c, ins)
            c.end_sublayer()
        if 3 in layers:
            l1_ternary(c, ins)
        if 4 in layers:
            l2_performer(c, ins)
            c.end_sublayer()
        if 5 in layers:
            with ExitStack() as actx:
                c.layer = "l2f_"
                at = Attention(c, actx)
                l2_ffn(c, at, ins, AttentionConstants(c, at, 2))
                c.end_sublayer()
        if 6 in layers:
            l3_state(c, ins)
        if 7 in layers:
            l3_ffn(c, ins)
        store_output(c, out)


_INS = [
    'L0_attn_x', 'L0_attn_ln_gamma', 'L0_attn_ln_beta', 'L0_attn_w_qkv', 'L0_attn_b_qkv', 'L0_attn_w_out',
    'L0_attn_b_out', 'L0_ffn_ln1_g', 'L0_ffn_ln1_b', 'L0_ffn_ln2_g', 'L0_ffn_ln2_b', 'L0_ffn_Wq', 'L0_ffn_bq',
    'L0_ffn_Wk', 'L0_ffn_bk', 'L0_ffn_Wv', 'L0_ffn_bv', 'L0_ffn_Wo', 'L0_ffn_bo', 'L0_ffn_Wr', 'L0_ffn_br',
    'L0_ffn_e_w1', 'L0_ffn_e_b1', 'L0_ffn_e_w2', 'L0_ffn_e_b2', 'L1_attn_W_in', 'L1_attn_conv_w', 'L1_attn_conv_b',
    'L1_attn_W_x', 'L1_attn_W_dt', 'L1_attn_b_dt', 'L1_attn_A_log', 'L1_attn_D', 'L1_attn_W_out', 'L1_ffn_weight',
    'L1_ffn_alpha', 'L1_ffn_bias', 'L2_attn_Wq', 'L2_attn_bq', 'L2_attn_Wk', 'L2_attn_bk', 'L2_attn_Wv', 'L2_attn_bv',
    'L2_attn_Wo', 'L2_attn_bo', 'L2_attn_orf', 'L2_ffn_rW1', 'L2_ffn_rb1', 'L2_ffn_ln_g', 'L2_ffn_ln_b', 'L2_ffn_rW2',
    'L2_ffn_rb2', 'L2_ffn_qW', 'L2_ffn_qb', 'L2_ffn_kW', 'L2_ffn_kb', 'L2_ffn_vW', 'L2_ffn_vb', 'L2_ffn_oW',
    'L2_ffn_ob', 'L3_attn_conv_w', 'L3_attn_conv_b', 'L3_attn_Wp', 'L3_attn_bp', 'L3_attn_Ws', 'L3_attn_bs',
    'L3_attn_A_log', 'L3_attn_dt_log', 'L3_attn_Wo', 'L3_attn_bo', 'L3_ffn_W_router', 'L3_ffn_W1', 'L3_ffn_b1',
    'L3_ffn_Wo', 'L3_ffn_bo', 'L3_ffn_ln_gamma', 'L3_ffn_ln_beta']
_OUTS = [((1, 2048, 128), 'float32')]


def kernel(**inputs):
    import numpy as _np
    import concourse.bacc as _bacc
    from concourse import mybir as _mybir
    from concourse.bass_utils import run_bass_kernel_spmd as _run

    nc = _bacc.Bacc("TRN2", target_bir_lowering=False, num_devices=1)
    arrays, ins = {}, {}
    for name in _INS:
        a = _np.ascontiguousarray(inputs[name])
        arrays[f"in_{name}_dram"] = a
        ins[name] = nc.dram_tensor(f"in_{name}_dram", a.shape, _mybir.dt.from_np(a.dtype), kind="ExternalInput").ap()
    outs = []
    for i, (shape, dtype) in enumerate(_OUTS):
        dt = _mybir.dt.from_np(_np.dtype(dtype))
        outs.append(nc.dram_tensor(f"out_{i}_dram", shape, dt, kind="ExternalOutput").ap())
    build(nc, ins, outs[0])
    r = _run(nc, [arrays], core_ids=[0])
    return r.results[0]["out_0_dram"]
```

```python
import concourse.bass as bass
from concourse import mybir
from contextlib import ExitStack
import numpy as np

F32 = mybir.dt.float32
BF16 = mybir.dt.bfloat16
ALU = mybir.AluOpType
ACT = mybir.ActivationFunctionType
X = mybir.AxisListType.X

P = 128
T = 2048
NT = T // P
NC = T // 512
H = 16
HD = P // H
NPAIR = H // 2
PARTS_Q = (0, 0, 0, 1, 1, 2)
PARTS_K = (0, 1, 2, 0, 1, 0)
RUNS_K = ((0, 3), (3, 2), (5, 1))
NR = len(PARTS_Q)
ROWS = NR * HD
SCALE = HD ** -0.5
MASKED = -1e30


class Chain:

    def __init__(self, eng, sem):
        self.eng, self.sem, self.n = eng, sem, 0

    def __call__(self, ins):
        self.n += 1
        ins.then_inc(self.sem, 1)
        self.eng.wait_ge(self.sem, self.n)


class Core:

    def __init__(self, nc, ctx):
        self.nc, self.layer, self.sems = nc, "", []
        sb = self.sb
        self.x = sb(ctx, "x_residual", [P, NT, P], F32)
        self.n = sb(ctx, "x_normalised", [P, NT, P], F32)
        self.heads = sb(ctx, "heads_out", [P, NT + 1, P], F32)
        self.a = self.heads[:, 1:NT + 1, :]
        self.b = sb(ctx, "tokens_b", [P, NT, P], F32)
        self.nT = sb(ctx, "channels_n", [P, T], F32)
        self.qk = sb(ctx, "channels_qk", [P, 2, T], F32)
        self.qT, self.kT = self.qk[:, 0, :], self.qk[:, 1, :]
        self.moments, self.mean_var = sb(ctx, "ln_moments", [P, NT, 6], F32), sb(ctx, "ln_mean_var", [P, NT, 2], F32)
        self.var, self.std, self.rstd = (sb(ctx, "ln_" + n, [P, NT], F32) for n in ("var", "std", "rstd"))
        self.ident = sb(ctx, "identity", [P, P], F32)
        self.identb = sb(ctx, "identity_bf16", [P, P], BF16)
        self.ps = ctx.enter_context(nc.psum_tensor("psum", [P, 8, 512], F32))

    def sb(self, ctx, name, shape, dtype):
        return ctx.enter_context(self.nc.sbuf_tensor(f"{self.layer}{name}", shape, dtype))

    def sem(self, name):
        s = self.nc.alloc_semaphore(name=f"{self.layer}{name}")
        self.sems.append(s)
        return s

    def end_sublayer(self):
        self.nc.clear_and_free_semaphores(self.sems)
        self.sems = []
        self.nc.all_engine_barrier()


def row_view(v, n):
    return v.rearrange("(a n) -> a n", a=1).to_broadcast([P, n])


def column(v):
    return v.rearrange("(p a) -> p a", a=1)


def head_order(v):
    return v.rearrange("c (p j d) -> c j d p", p=NPAIR, j=2)


def split_heads(v):
    return v.rearrange("c (j d p) -> c j d p", p=NPAIR, j=2)


def head_column(v):
    return v.rearrange("(p j d a) -> j d p a", p=NPAIR, j=2, a=1)


def layer_norm_vector(c, dve, link, src, dst, var_ready, std_ready, count, eps, done):
    v = c.nc.vector
    for t in range(NT):
        last = v.bn_stats(c.moments[:, t, :], src[:, t, :])
    link(last)
    for t in range(NT):
        last = v.bn_aggr(c.mean_var[:, t, :], c.moments[:, t, :])
    link(last)
    v.tensor_scalar(c.var[:, :], c.mean_var[:, :, 1], eps, None, ALU.add).then_inc(var_ready, 1)
    dve.wait_ge(std_ready, count)
    link(v.reciprocal(c.rstd[:, :], c.std[:, :]))
    for t in range(NT):
        last = v.tensor_scalar(dst[:, t, :], src[:, t, :], c.mean_var[:, t, 0:1], c.rstd[:, t:t + 1], ALU.subtract, ALU.mult)
        if t % 4 == 3:
            last.then_inc(done, 1)


def layer_norm_scalar(c, act, var_ready, std_ready, count):
    act.wait_ge(var_ready, count)
    c.nc.scalar.activation(c.std[:, :], c.var[:, :], ACT.Sqrt).then_inc(std_ready, 1)


def transpose_tokens(c, pe, src, bank0, done, src_ready=None):
    for t in range(NT):
        if src_ready and t % 4 == 0:
            pe.wait_ge(src_ready, t // 4 + 1)
        ins = c.nc.tensor.transpose(c.ps[:, bank0 + t // 4, (t % 4) * P:(t % 4 + 1) * P], src[:, t, :], c.ident[:, :])
        if t % 4 == 3:
            ins.then_inc(done, 1)


def project_channels(c, w, rhs, bank0, done):
    for k in range(NC):
        c.nc.tensor.matmul(c.ps[:, bank0 + k, :], w, rhs[:, k * 512:(k + 1) * 512], start=True, stop=True).then_inc(done, 1)


def project_tokens(c, srcT, w, bank0, done):
    for t in range(NT):
        ins = c.nc.tensor.matmul(c.ps[:, bank0 + t // 4, (t % 4) * P:(t % 4 + 1) * P],
                                 srcT[:, t * P:(t + 1) * P], w, start=True, stop=True)
        if t % 4 == 3:
            ins.then_inc(done, 1)


def evacuate(c, act, src_bank, dst, done, first, out_ready, bias=0.0, scale=1.0):
    for k in range(NC):
        act.wait_ge(done, first + k + 1)
        c.nc.scalar.activation(dst[:, k * 512:(k + 1) * 512], c.ps[:, src_bank + k, :], ACT.Identity,
                               bias=bias, scale=scale).then_inc(out_ready, 1)


def constants(c, ins):
    nc = c.nc
    zeroed, x_loaded = c.sem("identity_zeroed"), c.sem("x_loaded")
    with nc.Block() as block:
        @block.sync
        def _(sp):
            sp.dma_start(c.x[:, :, :], ins["L0_attn_x"][0].rearrange("(t p) d -> p t d", p=P)).then_inc(x_loaded, 16)
            sp.wait_ge(x_loaded, 16)

        @block.gpsimd
        def _(pool):
            nc.gpsimd.memset(c.ident[:, :], 0.0).then_inc(zeroed, 1)
            nc.gpsimd.memset(c.identb[:, :], 0.0).then_inc(zeroed, 1)
            pool.wait_ge(zeroed, 2)
            for m in (c.ident, c.identb):
                nc.gpsimd.affine_select(out=m[:, :], in_=m[:, :], compare_op=ALU.not_equal, fill=1.0, base=0,
                                        pattern=[[-1, P]], channel_multiplier=1).then_inc(zeroed, 1)
            pool.wait_ge(zeroed, 4)


class Attention:

    def __init__(self, c, ctx):
        sb, nc = c.sb, c.nc
        self.hi = sb(ctx, "part_hi", [P, T], BF16)
        self.mid = sb(ctx, "part_mid", [P, T], BF16)
        self.lo = sb(ctx, "part_lo", [P, T], BF16)
        self.kx = sb(ctx, "k_parts", [P, 2, NPAIR, T], BF16)
        self.v = sb(ctx, "v_and_ones", [P, 2, NT, H, HD + 1], F32)
        self.q1 = sb(ctx, "q_parts", [P, 2, NPAIR, 2, P], BF16)
        self.q2 = sb(ctx, "q_parts_and_max", [P, NPAIR, 2, P], BF16)
        self.prob = c.qk[:, :, :].rearrange("p a (b k j q) -> p (a b) k j q", b=2, k=2, j=4)
        self.mx = sb(ctx, "chunk_max", [P, H, 4], F32)
        self.negm = sb(ctx, "minus_max", [P, H], F32)
        self.rest = sb(ctx, "minus_max_rest", [P, 4, 4], F32)
        self.mparts = sb(ctx, "minus_max_parts", [P, 4, 2, 3, 2], BF16)
        self.mrow = sb(ctx, "minus_max_rows", [12, 4, P], BF16)
        self.oTs = sb(ctx, "out_channels", [P, 512], F32)
        self.rden = sb(ctx, "denominators", [P, H], F32)
        self.start = sb(ctx, "start_credit", [P, 5], F32)
        self.one, self.oneb = sb(ctx, "one", [P, 1], F32), sb(ctx, "one_bf16", [P, 1], BF16)
        self.wp = sb(ctx, "w_head_order", [P, 2, P], F32)
        self.q_dram = nc.dram_tensor(f"{c.layer}q_parts_dram", [2, NR, HD, NPAIR, T], BF16, kind="Internal").ap()
        self.k_dram = nc.dram_tensor(f"{c.layer}k_parts_dram", [8, 2, 3, HD, NPAIR, T], BF16, kind="Internal").ap()


class AttentionConstants:

    def __init__(self, c, at, buffers):
        self.c, self.at, self.buffers = c, at, buffers
        self.filled, self.ones_set = c.sem("attn_filled"), c.sem("attn_ones_set")
        self.FILLS = 6 + buffers

    def gpsimd(self):
        g, at = self.c.nc.gpsimd, self.at
        g.memset(at.q2[0:3, :, :, :], 1.0).then_inc(self.filled, 1)
        g.memset(at.v[:, :, :, :, :], 1.0).then_inc(self.filled, 1)
        for k in range(self.buffers):
            g.memset(at.kx[:, k, :, :].bitcast(F32), 0.0).then_inc(self.filled, 1)
        g.memset(at.q1[:, :, :, :, :].bitcast(F32), 0.0).then_inc(self.filled, 1)
        g.memset(at.oTs[:, :], 1.0).then_inc(self.filled, 1)
        g.memset(at.one[:, :], 1.0).then_inc(self.filled, 1)
        g.memset(at.oneb[:, :], 1.0).then_inc(self.filled, 1)

    def wait(self, eng):
        eng.wait_ge(self.filled, self.FILLS)

    def sync(self, sp):
        self.wait(sp)
        at = self.at
        ones = at.q2[0:3, :, :, :].rearrange("p a j q -> p (a j q)").unsqueeze(1).to_broadcast([3, NPAIR, T])
        for k in range(self.buffers):
            for j in range(2):
                sp.dma_start(at.kx[64 * j + ROWS:64 * j + ROWS + 3, k, :, :], ones).then_inc(self.ones_set, 16)

    def sync_end(self, sp):
        sp.wait_ge(self.ones_set, 16 * 2 * self.buffers)


def store_queries(c, at, eng, parts, part_ready, parts_stored):
    for which, part in enumerate(parts):
        sem, count = part_ready[which]
        eng.wait_ge(sem, count)
        for r in range(NR):
            if PARTS_Q[r] == which:
                eng.dma_start(at.q_dram[:, r].rearrange("j d p t -> j (d p) t"), part).then_inc(parts_stored, 16)


def place_keys(c, at, eng, part_ready, parts_placed):
    for which, part in enumerate((at.hi, at.mid, at.lo)):
        sem, count = part_ready[which]
        eng.wait_ge(sem, count)
        for r in range(NR):
            if PARTS_K[r] == which:
                for j in range(2):
                    eng.dma_start(at.kx[64 * j + r * HD:64 * j + (r + 1) * HD, 0, :, :], part[64 * j:64 * j + 64, :]).then_inc(parts_placed, 16)


def store_keys(at, eng, e, parts, parts_ready, count, parts_stored):
    eng.wait_ge(parts_ready, count)
    for which, part in enumerate(parts):
        eng.dma_start(at.k_dram[bass.ds(e, 1), :, which].rearrange("e j d p t -> (e j) (d p) t"), part[:, :]).then_inc(parts_stored, 16)


def load_keys(c, at, eng, buf, e, pairs, k_loaded):
    for j in range(2):
        for first, n in RUNS_K:
            row = 64 * j + first * HD
            eng.dma_start(at.kx[row:row + n * HD, buf, pairs, :],
                          at.k_dram[bass.ds(e, 1), j, 0:n, :, pairs, :].rearrange("e r d p t -> (e r d) p t")).then_inc(k_loaded, 16)


class Span:

    def __init__(self, causal):
        self.causal = causal

    def key_tiles(self, tile, u):
        return [kt for kt in (2 * u, 2 * u + 1) if not self.causal or kt <= tile]

    def steps(self, tile):
        return tile // 2 + 1 if self.causal else NT // 2

    def chunks(self, tile):
        return tile // 4 + 1 if self.causal else NC

    def width(self, tile, chunk):
        return P * (tile % 4 + 1) if self.causal and chunk == tile // 4 else 512

    def step_base(self, tile):
        return sum(4 * self.steps(i) for i in range(tile)) if self.causal else tile * (2 * NT)

    def max_base(self, tile):
        return sum(H * self.chunks(i) for i in range(tile)) if self.causal else tile * (H * NC)


def share(n, u, steps):
    return range(u * n // steps, (u + 1) * n // steps)


def attention_loop(c, at, lead, tri=None, routed=None):
    nc = c.nc
    G = 4
    tiles = routed.tiles if routed else NT
    span = Span(tri is not None)
    s2 = (c.ps[:, 0:2, :], c.ps[:, 2:4, :])
    s1 = (c.ps[:, 4, :], c.ps[:, 5, :])
    oT, misc = c.ps[:, 6, :], c.ps[:, 7, :]
    miscb = misc.bitcast(BF16)

    def rows_in(g):
        return f"rows{(g + lead - 1) % G}"

    ORDER = {g: [rows_in(g)] for g in range(G)}
    ORDER[0] += ["out"]
    FIRST = [f"rows{g}" for g in range(lead - 1)]
    if routed:
        ORDER[0] += ["outT"]
        ORDER[1] += ["proj", "q"]
        FIRST = ["q", "q"] + FIRST
    FLAT = [t for g in range(G) for t in ORDER[g]]
    LAST = ["out", "outT", "proj"] if routed else ["out"]

    def turn(i, name):
        return i * len(FLAT) + (len(FIRST) + FLAT.index(name))

    def after_loop(done):
        if tri is None:
            return turn(done, FLAT[0])
        return turn(done - 1, [name for name in FLAT if name == "out" or tile_of(name, 0) == 0][-1]) + 1

    def turns(i, g, u, late):
        steps = span.steps(i)
        due = [name for k, name in enumerate(ORDER[g]) if min(2 * k + 2 + late, steps - 1) == u]
        return [name for name in due if not name.startswith("rows") or exists(tile_of(name, i))]

    def tile_of(name, i):
        return i if int(name[4]) >= lead - 1 else i + 1

    def first_pass_of(i, g, k, r):
        ahead, group = divmod(g + lead, G)
        return (group, i + 1, 1 - k, r + k) if ahead else (group, i, k, r)

    def side_work(tile, g, u, steps):
        n, out_read = 4 * span.chunks(tile), 2 * ORDER[0].index("out") + 3
        if tri is None and g == G - 1:
            return range(n - 1, n) if u == steps - 1 else share(n - 1, u, steps - 1)
        if tri is None and g == 0:
            def first(step):
                return step * n // steps + (1 if 2 <= step <= out_read else 0)
            return range(first(u), first(u + 1))
        return share(n, u, steps)

    def exists(tile):
        return tri is None or tile < tiles

    def each_tile(eng, body):
        if tri is not None:
            for i in range(tiles):
                body(i, i % 2, i // 2)
            return tiles // 2
        if not routed:
            with eng.Fori(0, tiles // 2) as r:
                for k in range(2):
                    body(r * 2 + k, k, r)
            return tiles // 2
        rounds = eng.value_load(routed.rounds[0:1, 0:1], min_val=routed.least_rounds, max_val=tiles // 2)
        with eng.Fori(0, tiles // 2) as r:
            with eng.If(r < rounds):
                for k in range(2):
                    body(r * 2 + k, k, r)
        return rounds

    def kx(k):
        return at.kx[:, k if routed else 0]

    def vx(k):
        return at.v[:, k if routed else 0]

    q1_loaded = [c.sem(f"attn_q1_loaded{k}") for k in range(2)]
    q2_loaded = [c.sem(f"attn_q2_loaded{g}") for g in range(G)]
    s1_ready, s1_read = c.sem("attn_s1_ready"), c.sem("attn_s1_read")
    s2_ready, exp_done, pv_done = c.sem("attn_s2_ready"), c.sem("attn_exp_done"), c.sem("attn_pv_done")
    q_copied, mparts_ready = c.sem("attn_q_copied"), c.sem("attn_mparts_ready")
    misc_ready, misc_read, oT_copied = c.sem("attn_misc_ready"), c.sem("attn_misc_read"), c.sem("attn_oT_copied")
    pool_chain, negm_ready = c.sem("attn_pool_chain"), c.sem("attn_negm_ready")
    rden_ready, oT_zeroed = c.sem("attn_rden_ready"), c.sem("attn_oT_zeroed")
    if routed:
        k_loaded = [[c.sem(f"attn_k_loaded{k}{half}") for half in range(2)] for k in range(2)]
        v_loaded = [c.sem(f"attn_v_loaded{k}") for k in range(2)]
        last_y_stored = c.sem("attn_last_y_stored")
        qparts_ready, w_out_loaded, y_stored = c.sem("attn_qparts_ready"), c.sem("attn_w_out_loaded"), c.sem("attn_y_stored")
    Q1 = 16 * (2 * NR if routed else 2)
    KX = 16 * 2 * len(RUNS_K)

    def load_routed_q(eng, k, j, tile):
        eng.wait_ge(qparts_ready, tile + 1)
        for r, which in enumerate(PARTS_Q):
            eng.dma_start(at.q1[64 * j + r * HD:64 * j + (r + 1) * HD, k, :, j, :],
                          routed.qparts[64 * j:64 * j + 64, which, :]).then_inc(q1_loaded[k], 16)

    with nc.Block() as block:
        @block.sync
        def _(sp):
            def pairs(g):
                return slice(2 * g, 2 * g + 2)

            def load_half_keys(k, half, e):
                load_keys(c, at, sp, k, e, slice(4 * half, 4 * half + 4), k_loaded[k][half])

            def load_q(k, tile):
                if routed:
                    for j in range(2):
                        load_routed_q(sp, k, j, tile)
                else:
                    for j in range(2):
                        sp.dma_start(at.q1[64 * j:64 * j + ROWS, k, :, j, :],
                                     at.q_dram[j].rearrange("r d p t -> (r d) p t")[:, :, bass.ds(tile * P, P)]).then_inc(q1_loaded[k], 16)

            def load_max(g, before):
                sp.wait_ge(misc_read, before + 1)
                for j in range(2):
                    sp.dma_start(at.q2[64 * j + ROWS:64 * j + ROWS + 3, pairs(g), j, :],
                                 at.mrow[6 * j:6 * j + 6, g, :]).then_inc(q2_loaded[g], 16)

            def expert(tile):
                return sp.value_load(routed.expert_of[0:1, bass.ds(tile, 1)], min_val=0, max_val=routed.E - 1)

            def load_values(k, e):
                sp.dma_start(at.v[:, k], routed.v_dram[bass.ds(e, 1)].rearrange("e p t h d -> (e p) t h d")).then_inc(v_loaded[k], 16)

            def load_w_out(e):
                sp.dma_start(routed.w_out_now[:, :], routed.w_out_dram[bass.ds(e, 1)].rearrange("e p d -> (e p) d")).then_inc(w_out_loaded, 16)

            def store_y(i, stored):
                sp.dma_start(routed.y_dram[bass.ds(i, 1)].rearrange("a p d -> (a p) d"), routed.y[:, :]).then_inc(stored, 16)

            def tile_loads(i, k, r):
                for g in range(G):
                    name = rows_in(g)
                    if exists(tile_of(name, i)):
                        load_max(int(name[4]), turn(i, name))
                    if name == "rows3":
                        if tri is None:
                            load_q(k, (i + 2) % tiles)
                        elif i + 2 < tiles:
                            load_q(k, i + 2)

            def routed_loads(i, k, r):
                this, following, e = expert(i), expert(i + 1), expert(i + 2)
                for g in range(G):
                    load_max(int(rows_in(g)[4]), turn(i, rows_in(g)))
                    if g == 0:
                        load_half_keys(1 - k, 1, following)
                        sp.wait_ge(pv_done, span.step_base(i) + 4)
                        load_values(1 - k, following)
                    elif g == 1:
                        sp.wait_ge(misc_read, turn(i, "proj") + 1)
                        store_y(i, y_stored)
                        load_w_out(this)
                    elif g == 2:
                        load_half_keys(k, 0, e)
                        load_q(k, i + 2)

            if routed:
                first, second = expert(0), expert(1)
                load_half_keys(0, 0, first)
            load_q(0, 0)
            if routed:
                load_half_keys(0, 1, first)
            load_q(1, 1)
            if routed:
                load_w_out(first)
                load_values(0, first)
                load_half_keys(1, 0, second)
            for g in range(lead - 1):
                load_max(g, len(FIRST) - (lead - 1) + g)
            rounds = each_tile(sp, routed_loads if routed else tile_loads)
            more = 1 if tri is None else 0
            for k in range(2):
                sp.wait_ge(q1_loaded[k], rounds * Q1 + more * Q1)
            for g in range(G):
                sp.wait_ge(q2_loaded[g], rounds * 64 + (32 * more if g < lead - 1 else 0))
            if routed:
                for k in range(2):
                    sp.wait_ge(v_loaded[k], rounds * 16 + (1 - k) * 16)
                    for half in range(2):
                        sp.wait_ge(k_loaded[k][half], rounds * KX + (0 if k and half else KX))
                sp.wait_ge(misc_read, after_loop(rounds * 2) + len(LAST))
                sp.wait_ge(y_stored, rounds * 32 + 16)
                store_y(rounds * 2, last_y_stored)
                sp.wait_ge(last_y_stored, 16)

        @block.gpsimd
        def _(pool):
            g_ = nc.gpsimd

            class Link:

                def __init__(self, base):
                    self.base, self.k = base, 0

                def __call__(self, ins):
                    self.k += 1
                    ins.then_inc(pool_chain, 1)
                    pool.wait_ge(pool_chain, self.base + self.k)

            def same(dst, src, one=at.one):
                ones = one[:, :] if len(src.shape) == 2 else one[:, :].unsqueeze(2)
                return g_.tensor_tensor(dst, src, ones.to_broadcast(list(src.shape)), ALU.mult)

            def split(src, parts, rest, link, ready):
                link(same(parts[0], src))
                link(g_.tensor_tensor(rest, src, parts[0], ALU.subtract))
                link(same(parts[1], rest))
                g_.tensor_tensor(parts[2], rest, parts[1], ALU.subtract).then_inc(ready, 1)

            def split_max(g, tile, link):
                pool.wait_ge(q_copied, tile * G + (g + 1))
                pool.wait_ge(negm_ready, tile * G + (g + 1))
                split(at.negm[:, 4 * g:4 * g + 4].rearrange("p (a j) -> p j a", j=2), [at.mparts[:, g, :, n, :] for n in range(3)],
                      at.rest[:, g, :].rearrange("p (j a) -> p j a", j=2), link, mparts_ready)

            def copy_q(g, k):
                same(at.q2[:, 2 * g:2 * g + 2, :, :].rearrange("p a j q -> p (a j q)"),
                     at.q1[:, k, 2 * g:2 * g + 2, :, :].rearrange("p a j q -> p (a j q)"), at.oneb).then_inc(q_copied, 1)

            def split_q(before, link):
                pool.wait_ge(misc_read, before + 1)
                split(routed.qT[:, :], [routed.qparts[:, n, :] for n in range(3)], routed.qrest[:, :], link, qparts_ready)

            link = Link(0)
            if routed:
                split_q(0, link)
                pool.wait_ge(q1_loaded[0], Q1)
                split_q(1, link)
            for g in range(lead):
                pool.wait_ge(q1_loaded[0], Q1)
                copy_q(g, 0)
                split_max(g, 0, link)
            before_loop, per_tile = link.k, 3 * (G + (1 if routed else 0))

            def whole_tile(i, k, r):
                tile_link = link if tri is not None else Link(i * per_tile + before_loop)
                if routed:
                    routed.load_index(pool, i + 2, k)
                for g in range(G):
                    group, tile, parity, load_round = first_pass_of(i, g, k, r)
                    if exists(tile):
                        if routed and g == 0:
                            pool.wait_ge(routed.list_loaded, i * 16 + 48)
                        pool.wait_ge(s2_ready, span.step_base(i) + (g + 1) * span.steps(i) if lead == G else span.step_base(i) + (g * span.steps(i) + 1))
                        if group == 0:
                            pool.wait_ge(q1_loaded[parity], load_round * Q1 + Q1)
                        copy_q(group, parity)
                        if routed and g == 0:
                            routed.gather(pool, k)
                        split_max(group, tile, tile_link)
                    if routed and g == 1:
                        split_q(turn(i, "q"), tile_link)
                assert tri is not None or tile_link.k == per_tile

            rounds = each_tile(pool, whole_tile)
            if routed:
                for k in range(2):
                    pool.wait_ge(routed.gathered[k], rounds * 16 + 16)

        @block.tensor
        def _(pe):
            def first_pass(g, unit, tile, k, r):
                chunks = span.chunks(tile)
                head, chunk = unit // chunks, unit % chunks
                if unit == 0:
                    if g == 0:
                        pe.wait_ge(q1_loaded[k], r * Q1 + Q1)
                    if routed and g % 2 == 0:
                        pe.wait_ge(k_loaded[k][g // 2], r * KX + KX)
                pair, j = 2 * g + head // 2, head % 2
                n = g * 4 * chunks + unit
                width = span.width(tile, chunk)
                diagonal = tri is not None and chunk == chunks - 1
                pe.wait_ge(s1_read, span.max_base(tile) + (n + 1))
                last = nc.tensor.matmul(s1[n % 2][:, 0:width], at.q1[:, k, pair, j, :], kx(k)[:, pair, chunk * 512:chunk * 512 + width],
                                        start=True, stop=not diagonal)
                if diagonal:
                    last = nc.tensor.matmul(s1[n % 2][:, width - P:width], c.identb[:, :], tri.query[:, :], start=False, stop=True)
                last.then_inc(s1_ready, 1)

            def second_pass(s, i, k):
                steps, base = span.steps(i), span.step_base(i)
                g, u = s // steps, s % steps
                if u == 0:
                    pe.wait_ge(q2_loaded[g], i * 32 + 32)
                pe.wait_ge(exp_done, base + (s + 1))
                for kk, kt in enumerate(span.key_tiles(i, u)):
                    diagonal = tri is not None and kt == i
                    for pp in range(2):
                        last = nc.tensor.matmul(s2[s % 2][:, kk, pp * 256:(pp + 1) * 256], kx(k)[:, 2 * g + pp, kt * P:(kt + 1) * P],
                                                at.q2[:, 2 * g + pp, :, :].rearrange("p j q -> p (j q)"),
                                                start=not diagonal or pp == 0, stop=not diagonal)
                    if diagonal:
                        last = nc.tensor.matmul(s2[s % 2][:, kk, :], c.identb[:, :], tri.key[:, :].unsqueeze(1).to_broadcast([P, 4, P]),
                                                start=False, stop=True)
                last.then_inc(s2_ready, 1)

            def weighted_values(s, kk, i, k, r):
                steps, base = span.steps(i), span.step_base(i)
                g, u = s // steps, s % steps
                kts = span.key_tiles(i, u)
                if kk == len(kts):
                    return
                if s == 0 and kk == 0:
                    pe.wait_ge(oT_copied, i + 1)
                    if routed:
                        pe.wait_ge(v_loaded[k], r * 16 + 16)
                if kk == 0:
                    pe.wait_ge(exp_done, base + (s + 3))
                kt = kts[kk]
                for j in range(4):
                    last = nc.tensor.matmul(oT[32 * j:32 * j + HD + 1, g * P:(g + 1) * P], vx(k)[:, kt, 4 * g + j, :],
                                            at.prob[:, s % 4, kk, j, :], start=kt == 0, stop=u == steps - 1 and kt == kts[-1])
                if kt == kts[-1]:
                    last.then_inc(pv_done, 1)

            def fill_misc(name, i, k, r, before):
                if not (isinstance(before, int) and before == 0):
                    pe.wait_ge(misc_read, before)
                if name == "out":
                    pe.wait_ge(oT_copied, i + 1)
                    for g in range(G):
                        last = nc.tensor.transpose(misc[:, g * P:(g + 1) * P], at.oTs[:, g * P:(g + 1) * P], c.ident[:, :])
                    last.then_inc(misc_ready, 1)
                elif name == "outT":
                    nc.tensor.transpose(misc[:, 0:P], c.heads[:, 0, :], c.ident[:, :]).then_inc(misc_ready, 1)
                elif name == "proj":
                    pe.wait_ge(w_out_loaded, i * 16 + 16)
                    nc.tensor.matmul(misc[:, 0:P], routed.outT[:, :], routed.w_out_now[:, :], start=True, stop=True).then_inc(misc_ready, 1)
                elif name == "q":
                    pe.wait_ge(routed.gathered[k], r * 16 + 32)
                    nc.tensor.transpose(misc[:, 0:P], routed.q[:, k, :], c.ident[:, :]).then_inc(misc_ready, 1)
                else:
                    g = int(name[4])
                    pe.wait_ge(mparts_ready, tile_of(name, i) * G + (g + 1))
                    nc.tensor.transpose(miscb[0:12, 0:P], at.mparts[:, g, :, :, :].rearrange("p j r a -> p (j r a)"),
                                        c.identb[:, :]).then_inc(misc_ready, 1)

            def whole_tile(i, k, r):
                steps = span.steps(i)
                for s in range(G * steps):
                    g, u = s // steps, s % steps
                    group, tile, parity, load_round = first_pass_of(i, g, k, r)
                    units = list(side_work(tile, g, u, steps)) if exists(tile) else []
                    early, late = len(units) // 3, (len(units) + 1) // 3
                    for unit in units[:early]:
                        first_pass(group, unit, tile, parity, load_round)
                    if s + 1 < G * steps:
                        second_pass(s + 1, i, k)
                    for unit in units[early:len(units) - late]:
                        first_pass(group, unit, tile, parity, load_round)
                    for name in turns(i, g, u, 0):
                        fill_misc(name, i, k, r, turn(i, name))
                    if s + 1 == G * steps and exists(i + 1):
                        second_pass(0, i + 1, 1 - k)
                    weighted_values(s, 0, i, k, r)
                    for unit in units[len(units) - late:]:
                        first_pass(group, unit, tile, parity, load_round)
                    weighted_values(s, 1, i, k, r)

            pe.wait_ge(oT_zeroed, 1)
            if routed:
                for k in range(2):
                    fill_misc("q", k - 2, k, -1, k)
            for g in range(lead):
                for unit in range(4 * span.chunks(0)):
                    first_pass(g, unit, 0, 0, 0)
                    if g > 0 and unit == 3:
                        fill_misc(f"rows{g - 1}", -1, 1, -1, len(FIRST) - (lead - 1) + g - 1)
            second_pass(0, 0, 0)
            done = each_tile(pe, whole_tile) * 2
            for n, name in enumerate(LAST):
                fill_misc(name, done, 0, 0, after_loop(done) + n)

        @block.scalar
        def _(act):
            def read_misc(name, i, before):
                act.wait_ge(misc_ready, before + 1)
                if name == "q":
                    if not (isinstance(i, int) and i == -2):
                        act.wait_ge(qparts_ready, i + 2)
                    dst, src = routed.qT[:, :], misc[:, 0:P]
                elif name == "outT":
                    dst, src = routed.outT[:, :], misc[:, 0:P]
                elif name == "proj":
                    act.wait_ge(y_stored, i * 16 + 16)
                    dst, src = routed.y[:, :], misc[:, 0:P]
                else:
                    dst, src = at.mrow[:, int(name[4]), :], miscb[0:12, 0:P]
                nc.scalar.activation(dst, src, ACT.Copy).then_inc(misc_read, 1)

            def exps(i, k, r):
                steps, base = span.steps(i), span.step_base(i)
                for s in range(G * steps):
                    n = len(span.key_tiles(i, s % steps))
                    act.wait_ge(s2_ready, base + (s + 1))
                    act.wait_ge(pv_done, base + (s + 1))
                    nc.scalar.activation(at.prob[:, s % 4, 0:n, :, :].rearrange("p k j q -> p (k j q)"),
                                         s2[s % 2][:, 0:n, :].rearrange("p k n -> p (k n)"), ACT.Exp, scale=SCALE).then_inc(exp_done, 1)
                    for name in turns(i, s // steps, s % steps, 1):
                        if name != "out":
                            read_misc(name, i, turn(i, name))

            nc.scalar.activation(at.start[:, 0:1], c.ident[:, 0:1], ACT.Exp).then_inc(exp_done, 2)
            for n, name in enumerate(FIRST):
                read_misc(name, n - 2, n)
            done = each_tile(act, exps) * 2
            for n, name in enumerate(LAST):
                if name != "out":
                    read_misc(name, done, after_loop(done) + n)

        @block.vector
        def _(dve):
            v = nc.vector

            def maximum(g, unit, tile):
                chunks = span.chunks(tile)
                n = g * 4 * chunks + unit
                dve.wait_ge(s1_ready, span.max_base(tile) + (n + 1))
                v.tensor_reduce(at.mx[:, 4 * g + unit // chunks, unit % chunks:unit % chunks + 1],
                                s1[n % 2][:, 0:span.width(tile, unit % chunks)], X, ALU.max).then_inc(s1_read, 1)

            def finish_max(g, tile):
                chunks = span.chunks(tile)
                dve.wait_ge(s1_read, span.max_base(tile) + ((g + 1) * 4 * chunks + 2))
                v.tensor_reduce(at.negm[:, 4 * g:4 * g + 4], at.mx[:, 4 * g:4 * g + 4, 0:chunks], X, ALU.max, negate=True).then_inc(negm_ready, 1)

            def read_out(i, before):
                dve.wait_ge(misc_ready, before + 1)
                o = misc.rearrange("p (h n) -> p h n", n=32)
                v.reciprocal(at.rden[:, :], o[:, :, HD]).then_inc(rden_ready, 1)
                dve.wait_ge(rden_ready, i + 1)
                dst = c.heads[:, 0:1, :] if routed else c.heads[:, bass.ds(i, 1), :]
                v.tensor_tensor(dst.rearrange("p a (h d) -> p (a h) d", d=HD), o[:, :, 0:HD],
                                at.rden[:, :].unsqueeze(2).to_broadcast([P, H, HD]), ALU.mult).then_inc(misc_read, 1)

            v.memset(oT, 0.0).then_inc(oT_zeroed, 1)
            v.memset(at.start[:, 1:2], 0.0).then_inc(s1_read, 2)
            v.memset(at.start[:, 2:3], 0.0).then_inc(pv_done, 4)
            v.memset(at.start[:, 3:4], 0.0).then_inc(oT_copied, 1)
            if routed:
                v.memset(at.start[:, 4:5], 0.0).then_inc(y_stored, 16)
            for g in range(lead):
                for unit in range(4 * span.chunks(0)):
                    maximum(g, unit, 0)
                finish_max(g, 0)

            def whole_tile(i, k, r):
                steps, base = span.steps(i), span.step_base(i)
                for g in range(G):
                    group, tile, _, _ = first_pass_of(i, g, k, r)
                    for u in range(steps):
                        if exists(tile):
                            for unit in side_work(tile, g, u, steps):
                                maximum(group, unit, tile)
                        if "out" in turns(i, g, u, 1):
                            read_out(i, turn(i, "out"))
                    if exists(tile):
                        finish_max(group, tile)
                dve.wait_ge(pv_done, base + (G * steps + 4))
                v.tensor_copy(at.oTs[:, :], oT).then_inc(oT_copied, 1)

            done = each_tile(dve, whole_tile) * 2
            read_out(done, after_loop(done))
            if not routed:
                dve.wait_ge(misc_read, after_loop(done) + 1)


def l0_attention(c, at, ins, fixed):
    nc = c.nc
    c.layer = "l0a_"
    with ExitStack() as ctx:
        w = c.sb(ctx, "w_qkv", [P, 3 * P], F32)
        w_out = c.sb(ctx, "w_out", [P, P], F32)
        gamma, beta = c.sb(ctx, "gamma", [P, 1], F32), c.sb(ctx, "beta", [P, 1], F32)
        bq, bk = c.sb(ctx, "b_q", [P, 1], F32), c.sb(ctx, "b_k", [P, 1], F32)
        bv, b_out = c.sb(ctx, "b_v", [P, P], F32), c.sb(ctx, "b_out", [P, P], F32)
        b_qkv = ins["L0_attn_b_qkv"]
        pairs = [(w[:, :], ins["L0_attn_w_qkv"]), (w_out[:, :], ins["L0_attn_w_out"]),
                 (gamma[:, :], column(ins["L0_attn_ln_gamma"])), (beta[:, :], column(ins["L0_attn_ln_beta"])),
                 (bv[:, :], row_view(b_qkv[2 * P:3 * P], P)), (b_out[:, :], row_view(ins["L0_attn_b_out"], P))]
        for j in range(2):
            pairs.append((bq[64 * j:64 * j + 64, :], head_column(b_qkv[0:P])[j]))
            pairs.append((bk[64 * j:64 * j + 64, :], head_column(b_qkv[P:2 * P])[j]))
        attention_layer(c, at, pairs, [(1e-5, None, None), (1e-5, gamma, beta)],
                        w[:, 0:P], w[:, P:2 * P], w[:, 2 * P:3 * P], bq, bk, bv, fixed)
        attention_loop(c, at, 2)
        attention_out(c, w_out, b_out, c.n, then_into_x=True)


def attention_layer(c, at, loads, norms, wq, wk, wv, bq, bk, bv, fixed):
    nc = c.nc
    w_loaded, var_ready, std_ready, chain = c.sem("w_loaded"), c.sem("var_ready"), c.sem("std_ready"), c.sem("chain")
    w_ordered = c.sem("w_ordered")
    n_ready, h_ready, hT_psum, hT_ready = c.sem("n_ready"), c.sem("h_ready"), c.sem("hT_psum"), c.sem("hT_ready")
    q_psum, k_psum, v_psum = c.sem("q_psum"), c.sem("k_psum"), c.sem("v_psum")
    v_ready = c.sem("v_ready")
    hi_ready, rest_ready, mid_ready, lo_ready = ([c.sem(f"{n}_ready{m}") for m in "kq"] for n in ("hi", "rest", "mid", "lo"))
    parts_placed, parts_stored = c.sem("parts_placed"), c.sem("parts_stored")
    ps = c.ps

    def free(v):
        return v.rearrange("p t d -> p (t d)").bitcast(BF16)

    parts = ((at.hi[:, :], at.mid[:, :], at.lo[:, :]),
             (free(c.a[:, 0:NT // 2, :]), free(c.a[:, NT // 2:, :]), at.q2[:, :, :, :].rearrange("p a j q -> p (a j q)")))
    rest = (c.kT, c.qT)
    banks = (4, 0)
    with nc.Block() as block:
        @block.sync
        def _(sp):
            for dst, src in loads:
                sp.dma_start(dst, src, allow_slow_non_contiguous=True).then_inc(w_loaded, 16)
            if fixed:
                fixed.sync(sp)
            place_keys(c, at, sp, [(hi_ready[0], NC), (mid_ready[0], 1), (lo_ready[0], 1)], parts_placed)
            store_queries(c, at, sp, parts[1], [(hi_ready[1], NC), (mid_ready[1], 1), (lo_ready[1], 1)], parts_stored)
            sp.wait_ge(parts_placed, 16 * 2 * NR)
            sp.wait_ge(parts_stored, 16 * NR)

        if fixed:
            @block.gpsimd
            def _(pool):
                fixed.gpsimd()
                fixed.wait(pool)

        @block.vector
        def _(dve):
            v = nc.vector
            link = Chain(dve, chain)
            layer_norm_vector(c, dve, link, c.x, c.n, var_ready, std_ready, 1, norms[0][0], n_ready)
            dve.wait_ge(n_ready, NC)
            layer_norm_vector(c, dve, link, c.n, c.a, var_ready, std_ready, 2, norms[1][0], h_ready)
            dve.wait_ge(w_loaded, 16 * len(loads))
            v.tensor_copy(split_heads(at.wp[:, 1, :]), head_order(wk)).then_inc(w_ordered, 1)
            v.tensor_copy(split_heads(at.wp[:, 0, :]), head_order(wq)).then_inc(w_ordered, 1)
            for m, bias in enumerate((bk, bq)):
                for b in range(NC):
                    dve.wait_ge(hi_ready[m], b + 1)
                    chunk = slice(b * 512, (b + 1) * 512)
                    v.scalar_tensor_tensor(rest[m][:, chunk], ps[:, banks[m] + b, :], bias[:, :], parts[m][0][:, chunk],
                                           ALU.add, ALU.subtract).then_inc(rest_ready[m], 1)
            for m in range(2):
                dve.wait_ge(mid_ready[m], 1)
                if m == 1 and fixed:
                    fixed.sync_end(dve)
                v.tensor_tensor(parts[m][2], rest[m], parts[m][1], ALU.subtract).then_inc(lo_ready[m], 1)
            if fixed:
                fixed.wait(dve)
            for b in range(4):
                dve.wait_ge(v_psum, b + 1)
                v.tensor_tensor(at.v[:, 0, 4 * b:4 * b + 4, :, 0:HD], ps[:, 4 + b, :].rearrange("p (t h d) -> p t h d", t=4, h=H),
                                bv[:, :].rearrange("p (h d) -> p h d", h=H).unsqueeze(1).to_broadcast([P, 4, H, HD]),
                                ALU.add).then_inc(v_ready, 1)
            dve.wait_ge(v_ready, 4)

        @block.tensor
        def _(pe):
            transpose_tokens(c, pe, c.a, 0, hT_psum, h_ready)
            pe.wait_ge(w_ordered, 2)
            pe.wait_ge(hT_ready, NC)
            project_channels(c, at.wp[:, 1, :], c.nT, 4, k_psum)
            project_channels(c, at.wp[:, 0, :], c.nT, 0, q_psum)
            pe.wait_ge(rest_ready[0], NC)
            project_tokens(c, c.nT, wv, 4, v_psum)

        @block.scalar
        def _(act):
            layer_norm_scalar(c, act, var_ready, std_ready, 1)
            layer_norm_scalar(c, act, var_ready, std_ready, 2)
            act.wait_ge(w_loaded, 16 * len(loads))
            _, gamma, beta = norms[1]
            evacuate(c, act, 0, c.nT, hT_psum, 0, hT_ready, beta[:, :], gamma[:, :])
            for m, psum, bias in ((0, k_psum, bk), (1, q_psum, bq)):
                evacuate(c, act, banks[m], parts[m][0], psum, 0, hi_ready[m], bias[:, :])
            for m in range(2):
                act.wait_ge(rest_ready[m], NC)
                nc.scalar.activation(parts[m][1], rest[m], ACT.Copy).then_inc(mid_ready[m], 1)


def attention_out(c, w_out, b_out, into, then_into_x):
    nc = c.nc
    aT_psum, aT_ready, y_psum, chain = c.sem("aT_psum"), c.sem("aT_ready"), c.sem("y_psum"), c.sem("out_chain")
    with nc.Block() as block:
        @block.tensor
        def _(pe):
            transpose_tokens(c, pe, c.a, 0, aT_psum)
            pe.wait_ge(aT_ready, NC)
            project_tokens(c, c.nT, w_out[:, :], 4, y_psum)

        @block.scalar
        def _(act):
            evacuate(c, act, 0, c.nT, aT_psum, 0, aT_ready)

        @block.vector
        def _(dve):
            link = Chain(dve, chain)
            link(nc.vector.tensor_tensor(into[:, :, :], into[:, :, :], b_out[:, :].unsqueeze(1).to_broadcast([P, NT, P]), ALU.add))
            add_banks(c, dve, link, into, 4, y_psum)
            if then_into_x:
                link(nc.vector.tensor_tensor(c.x[:, :, :], c.x[:, :, :], into[:, :, :], ALU.add))


def add_banks(c, dve, link, into, bank0, ready):
    for b in range(4):
        sl = slice(4 * b, 4 * b + 4)
        dve.wait_ge(ready, b + 1)
        link(c.nc.vector.tensor_tensor(into[:, sl, :], into[:, sl, :], c.ps[:, bank0 + b, :].rearrange("p (t d) -> p t d", t=4), ALU.add))


class DiagonalMask:

    def __init__(self, c, ctx):
        self.query = c.sb(ctx, "mask_by_query", [P, P], BF16)
        self.key = c.sb(ctx, "mask_by_key", [P, P], BF16)
        nc = c.nc
        drawn = c.sem("mask_drawn")
        with nc.Block() as block:
            @block.gpsimd
            def _(pool):
                nc.gpsimd.memset(self.query[:, :], 0.0).then_inc(drawn, 1)
                nc.gpsimd.memset(self.key[:, :], 0.0).then_inc(drawn, 1)
                pool.wait_ge(drawn, 2)
                nc.gpsimd.affine_select(out=self.query[:, :], in_=self.query[:, :], compare_op=ALU.is_ge, fill=MASKED,
                                        base=0, pattern=[[-1, P]], channel_multiplier=1).then_inc(drawn, 1)
                nc.gpsimd.affine_select(out=self.key[:, :], in_=self.key[:, :], compare_op=ALU.is_ge, fill=MASKED,
                                        base=0, pattern=[[1, P]], channel_multiplier=-1).then_inc(drawn, 1)
                pool.wait_ge(drawn, 4)


def l0_ffn(c, at, ins):
    nc = c.nc
    c.layer = "l0f_"
    E = 8
    with ExitStack() as ctx:
        w_out, b_out = c.sb(ctx, "w_out", [P, P], F32), c.sb(ctx, "b_out", [P, P], F32)
        with ExitStack() as actx:
            w = c.sb(actx, "w_qkv", [P, 3, P], F32)
            gamma, beta = c.sb(actx, "gamma", [P, 1], F32), c.sb(actx, "beta", [P, 1], F32)
            bq, bk, bv = c.sb(actx, "b_q", [P, 1], F32), c.sb(actx, "b_k", [P, 1], F32), c.sb(actx, "b_v", [P, P], F32)
            loads = [(w[:, k, :], ins[f"L0_ffn_W{m}"]) for k, m in enumerate("qkv")]
            loads += [(w_out[:, :], ins["L0_ffn_Wo"]), (gamma[:, :], column(ins["L0_ffn_ln1_g"])),
                      (beta[:, :], column(ins["L0_ffn_ln1_b"])), (bv[:, :], row_view(ins["L0_ffn_bv"], P)),
                      (b_out[:, :], row_view(ins["L0_ffn_bo"], P))]
            for j in range(2):
                loads.append((bq[64 * j:64 * j + 64, :], head_column(ins["L0_ffn_bq"])[j]))
                loads.append((bk[64 * j:64 * j + 64, :], head_column(ins["L0_ffn_bk"])[j]))
            attention_layer(c, at, loads, [(1e-5, None, None), (1e-5, gamma, beta)], w[:, 0, :], w[:, 1, :], w[:, 2, :], bq, bk, bv, None)
            attention_loop(c, at, 4, tri=DiagonalMask(c, actx))
        attention_out(c, w_out, b_out, c.n, then_into_x=False)
        mix = c.sb(ctx, "expert_weights", [P, NT, E], F32)
        bias = c.sb(ctx, "b1_columns", [P, E * 4], F32)
        l0_router(c, ctx, ins, E, mix, bias)
        experts(c, ctx, E, ins["L0_ffn_e_w1"], lambda e: ins["L0_ffn_e_w2"][bass.ds(e, 1)], bias, mix)
        add_to_residual(c)


def top_choice(c, v, link, logits, best, tie, order, choice, width):
    def wide(s):
        return s.unsqueeze(2).to_broadcast([P, NT, width])
    link(v.tensor_reduce(best, logits, X, ALU.max))
    link(v.tensor_tensor(choice, logits, wide(best), ALU.is_equal))
    link(v.tensor_tensor(choice, choice, order.unsqueeze(1).to_broadcast([P, NT, width]), ALU.mult))
    link(v.tensor_reduce(tie, choice, X, ALU.max))
    link(v.tensor_tensor(choice, choice, wide(tie), ALU.is_equal))


def draw_order(c, pool, order, width, drawn):
    for e in range(width):
        c.nc.gpsimd.memset(order[:, e:e + 1], float(width - e)).then_inc(drawn, 1)


def l0_router(c, ctx, ins, E, mix, bias):
    nc = c.nc
    ps = c.ps
    with ExitStack() as rctx:
        gamma, beta = c.sb(rctx, "gamma2", [P, 1], F32), c.sb(rctx, "beta2", [P, 1], F32)
        wr, br = c.sb(rctx, "w_router", [P, E], F32), c.sb(rctx, "b_router", [P, E], F32)
        b1, b2 = c.sb(rctx, "b1_rows", [E * 4, P], F32), c.sb(rctx, "b2_rows", [E, P], F32)
        lg, ch, ex = (c.sb(rctx, n, [P, NT, E], F32) for n in ("logits", "choice", "rest"))
        best, second, tie = (c.sb(rctx, n, [P, NT], F32) for n in ("best", "second", "tie"))
        order = c.sb(rctx, "order", [P, E], F32)
        mixT = c.sb(rctx, "mix_rows", [E, T], F32)
        w_loaded, var_ready, std_ready, chain = c.sem("r_w_loaded"), c.sem("r_var_ready"), c.sem("r_std_ready"), c.sem("r_chain")
        h_ready, hT_psum, hT_ready, drawn = c.sem("r_h_ready"), c.sem("r_hT_psum"), c.sem("r_hT_ready"), c.sem("r_order_drawn")
        b1_psum, b1_ready, lg_psum, shifted, exp_ready = (c.sem("r_" + n) for n in ("b1_psum", "b1_ready", "lg_psum", "shifted", "exp_ready"))
        mix_ready, mixT_psum, mixT_ready, b2_psum = (c.sem("r_" + n) for n in ("mix_ready", "mixT_psum", "mixT_ready", "b2_psum"))
        loads = [(gamma[:, :], column(ins["L0_ffn_ln2_g"])), (beta[:, :], column(ins["L0_ffn_ln2_b"])),
                 (wr[:, :], ins["L0_ffn_Wr"]), (br[:, :], row_view(ins["L0_ffn_br"], E)),
                 (b1[:, :], ins["L0_ffn_e_b1"].rearrange("e (f p) -> (e f) p", p=P)), (b2[:, :], ins["L0_ffn_e_b2"])]
        with nc.Block() as block:
            @block.sync
            def _(sp):
                for dst, src in loads:
                    sp.dma_start(dst, src).then_inc(w_loaded, 16)

            @block.gpsimd
            def _(pool):
                draw_order(c, pool, order, E, drawn)

            @block.tensor
            def _(pe):
                transpose_tokens(c, pe, c.a, 0, hT_psum, h_ready)
                pe.wait_ge(w_loaded, 16 * len(loads))
                nc.tensor.transpose(ps[:, 4, 0:E * 4], b1[:, :], c.ident[0:E * 4, 0:E * 4]).then_inc(b1_psum, 1)
                pe.wait_ge(hT_ready, NC)
                for t in range(NT):
                    last = nc.tensor.matmul(ps[:, 5, t * E:(t + 1) * E], c.nT[:, t * P:(t + 1) * P], wr[:, :], start=True, stop=True)
                last.then_inc(lg_psum, 1)
                pe.wait_ge(mix_ready, 1)
                for t in range(NT):
                    ins_ = nc.tensor.transpose(ps[0:E, t // 4, (t % 4) * P:(t % 4 + 1) * P], mix[:, t, :], c.ident[:, :])
                    if t % 4 == 3:
                        ins_.then_inc(mixT_psum, 1)
                pe.wait_ge(mixT_ready, NC)
                for t in range(NT):
                    ins_ = nc.tensor.matmul(ps[:, 4 + t // 4, (t % 4) * P:(t % 4 + 1) * P], mixT[:, t * P:(t + 1) * P], b2[:, :],
                                            start=True, stop=True)
                    if t % 4 == 3:
                        ins_.then_inc(b2_psum, 1)

            @block.scalar
            def _(act):
                layer_norm_scalar(c, act, var_ready, std_ready, 1)
                act.wait_ge(w_loaded, 16 * len(loads))
                evacuate(c, act, 0, c.nT, hT_psum, 0, hT_ready, beta[:, :], gamma[:, :])
                act.wait_ge(b1_psum, 1)
                nc.scalar.activation(bias[:, :], ps[:, 4, 0:E * 4], ACT.Copy).then_inc(b1_ready, 1)
                act.wait_ge(shifted, 1)
                nc.scalar.activation(ex[:, :, :], ex[:, :, :], ACT.Exp).then_inc(exp_ready, 1)
                for k in range(NC):
                    act.wait_ge(mixT_psum, k + 1)
                    nc.scalar.activation(mixT[:, k * 512:(k + 1) * 512], ps[0:E, k, :], ACT.Copy).then_inc(mixT_ready, 1)
                act.wait_ge(b1_ready, 1)

            @block.vector
            def _(dve):
                v = nc.vector
                link = Chain(dve, chain)

                def wide(s):
                    return s.unsqueeze(2).to_broadcast([P, NT, E])

                layer_norm_vector(c, dve, link, c.n, c.a, var_ready, std_ready, 1, 1e-5, h_ready)
                dve.wait_ge(w_loaded, 16 * len(loads))
                dve.wait_ge(drawn, E)
                dve.wait_ge(lg_psum, 1)
                link(v.tensor_tensor(lg[:, :, :], ps[:, 5, 0:NT * E].rearrange("p (t e) -> p t e", e=E),
                                     br[:, :].unsqueeze(1).to_broadcast([P, NT, E]), ALU.add))
                top_choice(c, v, link, lg[:, :, :], best[:, :], tie[:, :], order[:, :], ch[:, :, :], E)
                link(v.scalar_tensor_tensor(ex[:, :, :], ch[:, :, :], MASKED, lg[:, :, :], ALU.mult, ALU.add))
                link(v.tensor_reduce(second[:, :], ex[:, :, :], X, ALU.max))
                link(v.tensor_tensor(ch[:, :, :], lg[:, :, :], wide(second[:, :]), ALU.is_ge))
                v.tensor_tensor(ex[:, :, :], lg[:, :, :], wide(best[:, :]), ALU.subtract).then_inc(shifted, 1)
                dve.wait_ge(exp_ready, 1)
                link(v.tensor_tensor(ex[:, :, :], ex[:, :, :], ch[:, :, :], ALU.mult))
                link(v.tensor_reduce(tie[:, :], ex[:, :, :], X, ALU.add))
                link(v.reciprocal(best[:, :], tie[:, :]))
                v.tensor_tensor(mix[:, :, :], ex[:, :, :], wide(best[:, :]), ALU.mult).then_inc(mix_ready, 1)
                for b in range(4):
                    sl = slice(4 * b, 4 * b + 4)
                    dve.wait_ge(b2_psum, b + 1)
                    link(v.tensor_tensor(c.n[:, sl, :], c.n[:, sl, :], ps[:, 4 + b, :].rearrange("p (t d) -> p t d", t=4), ALU.add))


def experts(c, ctx, E, w1_dram, w2_of, bias, mix):
    nc = c.nc
    ps = c.ps
    F = 4
    K = 2 * NC
    with ExitStack() as ectx:
        w1 = c.sb(ectx, "w1", [P, 2, F * P], F32)
        w2 = c.sb(ectx, "w2", [P, 2, F, P], F32)
        mid = c.sb(ectx, "hidden", [P, 2, F, 512], F32)
        bnow = c.sb(ectx, "b1_now", [P, 2, F], F32)
        start = c.sb(ectx, "e_start_credit", [P, 3], F32)
        w_loaded = [c.sem(f"e_w_loaded{k}") for k in range(2)]
        mid_psum, gelu_done, y_psum, y_added = (c.sem("e_" + n) for n in ("mid_psum", "gelu_done", "y_psum", "y_added"))
        with nc.Block() as block:
            @block.sync
            def _(sp):
                def load(k, e):
                    sp.dma_start(w1[:, k, :], w1_dram[bass.ds(e, 1)].rearrange("a d f -> d (a f)")).then_inc(w_loaded[k], 16)
                    sp.dma_start(bnow[:, k, :], bias[:, bass.ds(e * F, F)]).then_inc(w_loaded[k], 16)
                    sp.dma_start(w2[:, k, :, :], w2_of(e).rearrange("a (f p) d -> p (a f) d", p=P)).then_inc(w_loaded[k], 16)

                for k in range(2):
                    load(k, k)
                with sp.Fori(0, E // 2 - 1) as r:
                    for k in range(2):
                        sp.wait_ge(y_psum, r * K + (NC * (k + 1) + 2))
                        load(k, r * 2 + (2 + k))

            @block.tensor
            def _(pe):
                def up(r, k):
                    e, ch = k // NC, k % NC
                    if ch == 0:
                        pe.wait_ge(w_loaded[e], r * 48 + 48)
                    for f in range(F):
                        pe.wait_ge(gelu_done, r * K * F + (k * F + f + 1))
                        nc.tensor.matmul(ps[:, f, :], w1[:, e, f * P:(f + 1) * P], c.nT[:, ch * 512:(ch + 1) * 512],
                                         start=True, stop=True).then_inc(mid_psum, 1)

                def down(r, k):
                    e = k // NC
                    pe.wait_ge(gelu_done, r * K * F + (k * F + 2 * F))
                    pe.wait_ge(y_added, r * K + (k + 3))
                    for t in range(4):
                        for f in range(F):
                            last = nc.tensor.matmul(ps[:, 4 + k % 2, t * P:(t + 1) * P], mid[:, k % 2, f, t * P:(t + 1) * P],
                                                    w2[:, e, f, :], start=f == 0, stop=f == F - 1)
                    last.then_inc(y_psum, 1)

                with pe.Fori(0, E // 2) as r:
                    up(r, 0)
                    for k in range(K):
                        if k + 1 < K:
                            up(r, k + 1)
                        down(r, k)

            @block.scalar
            def _(act):
                nc.scalar.activation(start[:, 0:1], bias[:, 0:1], ACT.Copy).then_inc(gelu_done, 4)
                with act.Fori(0, E // 2) as r:
                    for k in range(K):
                        if k % NC == 0:
                            act.wait_ge(w_loaded[k // NC], r * 48 + 48)
                        act.wait_ge(y_psum, r * K + (k + 1))
                        for f in range(F):
                            act.wait_ge(mid_psum, r * K * F + (k * F + f + 1))
                            nc.scalar.activation(mid[:, k % 2, f, :], ps[:, f, :], ACT.Gelu,
                                                 bias=bnow[:, k // NC, f:f + 1]).then_inc(gelu_done, 1)

            @block.vector
            def _(dve):
                v = nc.vector
                v.memset(start[:, 1:2], 0.0).then_inc(y_psum, 2)
                v.memset(start[:, 2:3], 0.0).then_inc(y_added, 4)
                with dve.Fori(0, E // 2) as r:
                    for k in range(K):
                        e, ch = k // NC, k % NC
                        dve.wait_ge(y_psum, r * K + (k + 3))
                        dve.wait_ge(y_added, r * K + (k + 1))
                        for t in range(4):
                            tile = 4 * ch + t
                            last = v.scalar_tensor_tensor(c.n[:, tile, :], ps[:, 4 + k % 2, t * P:(t + 1) * P],
                                                          mix[:, tile, bass.ds(r * 2 + e, 1)], c.n[:, tile, :], ALU.mult, ALU.add)
                        last.then_inc(y_added, 1)
                dve.wait_ge(y_added, E * NC + 4)


def add_to_residual(c):
    nc = c.nc
    done = c.sem("residual_done")
    with nc.Block() as block:
        @block.vector
        def _(dve):
            nc.vector.tensor_tensor(c.x[:, :, :], c.x[:, :, :], c.n[:, :, :], ALU.add).then_inc(done, 1)
            dve.wait_ge(done, 1)


class NormBlock:

    def __init__(self, c, prefix="n_"):
        self.c = c
        self.var_ready, self.std_ready = c.sem(prefix + "var_ready"), c.sem(prefix + "std_ready")
        self.n_ready, self.nT_psum, self.nT_ready = c.sem(prefix + "n_ready"), c.sem(prefix + "nT_psum"), c.sem(prefix + "nT_ready")

    def vector(self, dve, link, eps=1e-5):
        c = self.c
        layer_norm_vector(c, dve, link, c.x, c.n, self.var_ready, self.std_ready, 1, eps, self.n_ready)
        dve.wait_ge(self.n_ready, NC)

    def tensor(self, pe):
        transpose_tokens(self.c, pe, self.c.n, 0, self.nT_psum, self.n_ready)

    def scalar(self, act, dst):
        layer_norm_scalar(self.c, act, self.var_ready, self.std_ready, 1)
        evacuate(self.c, act, 0, dst, self.nT_psum, 0, self.nT_ready)


def softplus_scalar(c, act, link, x, bias, magnitude, tail):
    link(c.nc.scalar.activation(magnitude, x, ACT.Abs, bias=bias))
    link(c.nc.scalar.activation(magnitude, magnitude, ACT.Exp, scale=-1.0))
    return c.nc.scalar.activation(tail, magnitude, ACT.Ln, bias=1.0)


def l1_mamba(c, ins):
    nc = c.nc
    c.layer = "l1a_"
    DI, DS, KC, R = 2 * P, 16, 4, 8
    ps = c.ps
    dram = nc.dram_tensor("ssm_rows_dram", [2 * DS, T], F32, kind="Internal").ap()
    with ExitStack() as ctx:
        xv = c.sb(ctx, "xv", [P, 2, T], F32)
        dx = c.sb(ctx, "delta_x", [P, 2, T], F32)
        delta = c.sb(ctx, "delta", [P, 2, T], F32)
        a = c.sb(ctx, "a", [P, 2, DS], F32)
        rows = BroadcastRows(c, ctx, dram, DS)
        w_out, dvec = c.sb(ctx, "w_out", [P, 2, P], F32), c.sb(ctx, "d", [P, 2], F32)
        with ExitStack() as pctx:
            w_in, conv_w, conv_b = c.sb(pctx, "w_in", [P, DI], F32), c.sb(pctx, "conv_w", [P, 2, KC], F32), c.sb(pctx, "conv_b", [P, 2], F32)
            w_x, w_dt, b_dt = c.sb(pctx, "w_x", [P, 2, R + 2 * DS], F32), c.sb(pctx, "w_dt", [R, DI], F32), c.sb(pctx, "b_dt", [P, 2], F32)
            xp = c.sb(pctx, "x_padded", [P, 2, KC - 1 + T], F32)
            ssm = c.sb(pctx, "ssm", [R + 2 * DS, T], F32)
            norm = NormBlock(c)
            w_loaded, chain, act_chain = c.sem("w_loaded"), c.sem("chain"), c.sem("act_chain")
            xp_psum, xp_ready, conv_ready, xv_ready = c.sem("xp_psum"), c.sem("xp_ready"), c.sem("conv_ready"), c.sem("xv_ready")
            ssm_psum, ssm_ready, ssm_stored, dt_psum, dt_ready, size_ready, exp_ready, tail_ready = (c.sem(n) for n in (
                "ssm_psum", "ssm_ready", "ssm_stored", "dt_psum", "dt_ready", "size_ready", "exp_ready", "tail_ready"))

            def halves(v):
                return v.rearrange("(h p) -> p h", p=P)

            loads = [(w_in[:, :], ins["L1_attn_W_in"]), (conv_w[:, :, :], ins["L1_attn_conv_w"].rearrange("(h p) a k -> p h (a k)", p=P)),
                     (conv_b[:, :], halves(ins["L1_attn_conv_b"])), (w_x[:, :, :], ins["L1_attn_W_x"].rearrange("(h p) r -> p h r", p=P)),
                     (w_dt[:, :], ins["L1_attn_W_dt"]), (b_dt[:, :], halves(ins["L1_attn_b_dt"])),
                     (a[:, :, :], ins["L1_attn_A_log"].rearrange("(h p) n -> p h n", p=P)),
                     (w_out[:, :, :], ins["L1_attn_W_out"].rearrange("(h p) d -> p h d", p=P)), (dvec[:, :], halves(ins["L1_attn_D"]))]
            with nc.Block() as block:
                @block.sync
                def _(sp):
                    for dst, src in loads:
                        sp.dma_start(dst, src, allow_slow_non_contiguous=True).then_inc(w_loaded, 16)
                    sp.wait_ge(ssm_ready, NC)
                    sp.dma_start(dram[:, :], ssm[R:, :]).then_inc(ssm_stored, 16)
                    sp.wait_ge(ssm_stored, 16)
                    for k in range(2):
                        rows.load(sp, k, k)

                @block.tensor
                def _(pe):
                    norm.tensor(pe)
                    pe.wait_ge(w_loaded, 16 * len(loads))
                    pe.wait_ge(norm.nT_ready, NC)
                    project_channels(c, w_in[:, P:2 * P], c.nT, 4, xp_psum)
                    project_channels(c, w_in[:, 0:P], c.nT, 0, xp_psum)
                    for n, h in enumerate((1, 0)):
                        pe.wait_ge(xv_ready, n + 1)
                        for k in range(NC):
                            last = nc.tensor.matmul(ps[0:R + 2 * DS, 4 + k, :], w_x[:, h, :], xv[:, h, k * 512:(k + 1) * 512], start=n == 0, stop=n == 1)
                            if n == 1:
                                last.then_inc(ssm_psum, 1)
                    pe.wait_ge(xp_ready, 2 * NC)
                    for h in range(2):
                        for k in range(NC):
                            pe.wait_ge(ssm_ready, k + 1 if h == 0 else NC)
                            last = nc.tensor.matmul(ps[:, 4 * h + k, :], w_dt[:, h * P:(h + 1) * P], ssm[0:R, k * 512:(k + 1) * 512],
                                                    start=True, stop=True)
                        last.then_inc(dt_psum, 1)

                @block.scalar
                def _(act):
                    link = Chain(act, act_chain)
                    norm.scalar(act, c.nT)
                    for h in (1, 0):
                        evacuate(c, act, 4 * h, xp[:, h, KC - 1:], xp_psum, (1 - h) * NC, xp_ready)
                    for n, h in enumerate((1, 0)):
                        act.wait_ge(conv_ready, n + 1)
                        nc.scalar.activation(xv[:, h, :], xv[:, h, :], ACT.Silu).then_inc(xv_ready, 1)
                    for k in range(NC):
                        act.wait_ge(ssm_psum, k + 1)
                        nc.scalar.activation(ssm[:, k * 512:(k + 1) * 512], ps[0:R + 2 * DS, 4 + k, :], ACT.Copy).then_inc(ssm_ready, 1)
                    act.wait_ge(w_loaded, 16 * len(loads))
                    link(nc.scalar.activation(a[:, :, :], a[:, :, :], ACT.Exp))
                    link(nc.scalar.activation(a[:, :, :], a[:, :, :], ACT.Copy, scale=-1.0))
                    for h in range(2):
                        act.wait_ge(dt_psum, h + 1)
                        nc.scalar.activation(delta[:, h, :], ps[:, 4 * h:4 * h + 4, :].rearrange("p b n -> p (b n)"), ACT.Identity,
                                             bias=b_dt[:, h:h + 1]).then_inc(dt_ready, 1)
                    for h in range(2):
                        act.wait_ge(size_ready, h + 1)
                        nc.scalar.activation(dx[:, h, :], dx[:, h, :], ACT.Exp, scale=-1.0).then_inc(exp_ready, 1)
                    for h in range(2):
                        act.wait_ge(exp_ready, h + 1)
                        nc.scalar.activation(dx[:, h, :], dx[:, h, :], ACT.Ln, bias=1.0).then_inc(tail_ready, 1)

                @block.vector
                def _(dve):
                    v = nc.vector
                    link = Chain(dve, chain)
                    link(v.memset(xp[:, :, 0:KC - 1], 0.0))
                    norm.vector(dve, link)
                    dve.wait_ge(w_loaded, 16 * len(loads))
                    for n, h in enumerate((1, 0)):
                        dve.wait_ge(xp_ready, (n + 1) * NC)
                        link(v.tensor_scalar(xv[:, h, :], xp[:, h, 0:T], conv_w[:, h, 0:1], conv_b[:, h:h + 1], ALU.mult, ALU.add))
                        for k in range(1, KC):
                            last = v.scalar_tensor_tensor(xv[:, h, :], xp[:, h, k:k + T], conv_w[:, h, k:k + 1], xv[:, h, :], ALU.mult, ALU.add)
                            if k < KC - 1:
                                link(last)
                        last.then_inc(conv_ready, 1)
                    for h in range(2):
                        dve.wait_ge(dt_ready, h + 1)
                        v.scalar_tensor_tensor(dx[:, h, :], delta[:, h, :], -1.0, delta[:, h, :], ALU.mult, ALU.max).then_inc(size_ready, 1)
                    for h in range(2):
                        dve.wait_ge(tail_ready, h + 1)
                        link(v.scalar_tensor_tensor(delta[:, h, :], delta[:, h, :], 0.0, dx[:, h, :], ALU.max, ALU.add))
                        dve.wait_ge(xv_ready, 2)
                        link(v.tensor_tensor(dx[:, h, :], delta[:, h, :], xv[:, h, :], ALU.mult))

        mamba_scan(c, ctx, rows, DS, a, dvec, delta, dx, xv)
        y = dx
        y_ready, out_psum, chain2 = c.sem("y_ready"), c.sem("out_psum"), c.sem("chain2")
        with nc.Block() as block:
            @block.scalar
            def _(act):
                for k in range(NC):
                    for h in range(2):
                        nc.scalar.activation(y[:, h, k * 512:(k + 1) * 512], ps[:, 4 * h + k, :], ACT.Copy).then_inc(y_ready, 1)

            @block.tensor
            def _(pe):
                for t in range(NT):
                    if t % 4 == 0:
                        pe.wait_ge(y_ready, (t // 4 + 1) * 2)
                    for h in range(2):
                        last = nc.tensor.matmul(ps[:, t // 4, (t % 4) * P:(t % 4 + 1) * P], y[:, h, t * P:(t + 1) * P], w_out[:, h, :],
                                                start=h == 0, stop=h == 1)
                    if t % 4 == 3:
                        last.then_inc(out_psum, 1)

            @block.vector
            def _(dve):
                add_banks(c, dve, Chain(dve, chain2), c.x, 0, out_psum)


class BroadcastRows:

    STATES = 4

    def __init__(self, c, ctx, dram, n_states):
        def flat(v):
            return v.rearrange("p t d -> p (t d)")
        more = c.sb(ctx, "bc_rows", [P, 4, T], F32)
        self.buffers = [(c.qT, c.kT), (flat(c.a), flat(c.b[:, :, :])), (more[:, 0, :], more[:, 1, :]), (more[:, 2, :], more[:, 3, :])]
        self.dram, self.n_states = dram, n_states
        self.loaded = [c.sem(f"rows_loaded{k}") for k in range(self.STATES)]

    def load(self, eng, k, n):
        for row, dst in zip((n, n + self.n_states), self.buffers[k]):
            eng.dma_start(dst, self.dram[bass.ds(row, 1), :].to_broadcast([P, T])).then_inc(self.loaded[k], 16)


def mamba_scan(c, ctx, rows, DS, a, dvec, delta, dx, xv):
    nc = c.nc
    ps = c.ps
    with ExitStack() as sctx:
        K = rows.STATES
        da = c.sb(sctx, "decay", [P, 2, T], F32)
        u = c.sb(sctx, "input", [P, 2, T], F32)
        hc = c.sb(sctx, "state_c", [P, 2, T], F32)
        anow = c.sb(sctx, "a_now", [P, K, 2], F32)
        diag = c.sb(sctx, "d_diagonal", [P, 2, P], F32)
        start = c.sb(sctx, "start_credit", [P, 4], F32)
        da_ready, u_ready, scanned, hc_ready, added, diag_ready = (c.sem("s_" + n) for n in (
            "da_ready", "u_ready", "scanned", "hc_ready", "added", "diag_ready"))
        L = 3 * 16
        with nc.Block() as block:
            @block.sync
            def _(sp):
                def load_a(k, n):
                    sp.dma_start(anow[:, k, :], a[:, :, bass.ds(n, 1)].rearrange("p h a -> p (h a)"),
                                 allow_slow_non_contiguous=True).then_inc(rows.loaded[k], 16)

                for k in range(K):
                    load_a(k, k)
                for k in range(2, K):
                    rows.load(sp, k, k)
                with sp.Fori(0, DS // K - 1) as r:
                    for k in range(K):
                        sp.wait_ge(hc_ready, r * (2 * K) + (2 * k + 4))
                        rows.load(sp, k, r * K + (K + k))
                        load_a(k, r * K + (K + k))

            @block.scalar
            def _(act):
                def decays(r, k):
                    act.wait_ge(rows.loaded[k], r * L + L)
                    for h in range(2):
                        act.wait_ge(scanned, r * (2 * K) + (2 * k + h + 1))
                        nc.scalar.activation(da[:, h, :], delta[:, h, :], ACT.Exp, scale=anow[:, k, h:h + 1]).then_inc(da_ready, 1)

                with act.Fori(0, DS // K - 1) as r:
                    for k in range(K):
                        decays(r, k)
                for k in range(K):
                    decays(DS // K - 1, k)

            @block.gpsimd
            def _(pool):
                def inputs(r, k):
                    pool.wait_ge(rows.loaded[k], r * L + L)
                    for h in range(2):
                        pool.wait_ge(hc_ready, r * (2 * K) + (2 * k + h + 1))
                        nc.gpsimd.tensor_tensor(u[:, h, :], dx[:, h, :], rows.buffers[k][0], ALU.mult).then_inc(u_ready, 1)

                with pool.Fori(0, DS // K - 1) as r:
                    for k in range(K):
                        inputs(r, k)
                for k in range(K):
                    inputs(DS // K - 1, k)

            @block.vector
            def _(dve):
                v = nc.vector

                def states(r, k):
                    for h in range(2):
                        step = 2 * k + h
                        dve.wait_ge(da_ready, r * (2 * K) + (step + 1))
                        dve.wait_ge(u_ready, r * (2 * K) + (step + 1))
                        v.tensor_tensor_scan(u[:, h, :], da[:, h, :], u[:, h, :], 0.0, ALU.mult, ALU.add).then_inc(scanned, 1)
                        dve.wait_ge(scanned, r * (2 * K) + (step + 3))
                        dve.wait_ge(added, r * (2 * K) + (step + 1))
                        v.tensor_tensor(hc[:, h, :], u[:, h, :], rows.buffers[k][1], ALU.mult).then_inc(hc_ready, 1)

                for h in range(2):
                    v.tensor_scalar(diag[:, h, :], c.ident[:, :], dvec[:, h:h + 1], None, ALU.mult).then_inc(diag_ready, 1)
                v.memset(start[:, 0:1], 0.0).then_inc(scanned, 2)
                v.memset(start[:, 1:2], 0.0).then_inc(hc_ready, 2)
                v.memset(start[:, 2:3], 0.0).then_inc(added, 2)
                with dve.Fori(0, DS // K - 1) as r:
                    for k in range(K):
                        states(r, k)
                for k in range(K):
                    states(DS // K - 1, k)

            @block.tensor
            def _(pe):
                def add_state(r, k, closing):
                    for h in range(2):
                        pe.wait_ge(hc_ready, r * (2 * K) + (2 * k + h + 3))
                        for b in range(NC):
                            last = nc.tensor.matmul(ps[:, 4 * h + b, :], c.ident[:, :], hc[:, h, b * 512:(b + 1) * 512],
                                                    start=False, stop=closing)
                        last.then_inc(added, 1)

                pe.wait_ge(diag_ready, 2)
                for h in range(2):
                    for b in range(NC):
                        nc.tensor.matmul(ps[:, 4 * h + b, :], diag[:, h, :], xv[:, h, b * 512:(b + 1) * 512], start=True, stop=False)
                with pe.Fori(0, DS // K - 1) as r:
                    for k in range(K):
                        add_state(r, k, False)
                for k in range(K):
                    add_state(DS // K - 1, k, k == K - 1)


def l1_ternary(c, ins):
    nc = c.nc
    c.layer = "l1f_"
    ps = c.ps
    with ExitStack() as ctx:
        w, wt = c.sb(ctx, "w", [P, P], F32), c.sb(ctx, "w_ternary", [P, 2, P], F32)
        wT = c.sb(ctx, "wT", [P, P], F32)
        alpha, bias = c.sb(ctx, "alpha", [P, 1], F32), c.sb(ctx, "bias", [P, P], F32)
        ones, thr = c.sb(ctx, "ones", [P, P], F32), c.sb(ctx, "threshold", [P, 3], F32)
        norm = NormBlock(c)
        w_loaded, chain, sums_ready, total_psum, w_ready, wT_psum, wT_ready, y_psum = (c.sem(n) for n in (
            "w_loaded", "chain", "sums_ready", "total_psum", "w_ready", "wT_psum", "wT_ready", "y_psum"))
        loads = [(w[:, :], ins["L1_ffn_weight"]), (alpha[:, :], row_view(ins["L1_ffn_alpha"], 1)), (bias[:, :], row_view(ins["L1_ffn_bias"], P))]
        with nc.Block() as block:
            @block.sync
            def _(sp):
                for dst, src in loads:
                    sp.dma_start(dst, src).then_inc(w_loaded, 16)

            @block.vector
            def _(dve):
                v = nc.vector
                link = Chain(dve, chain)
                link(v.memset(ones[:, :], 1.0))
                dve.wait_ge(w_loaded, 16 * len(loads))
                v.tensor_reduce(thr[:, 0:1], w[:, :], X, ALU.add, apply_absolute_value=True).then_inc(sums_ready, 1)
                dve.wait_ge(total_psum, 1)
                link(v.tensor_scalar(thr[:, 1:2], ps[:, 7, 0:1], 1.0 / (P * P), 0.7, ALU.mult, ALU.mult))
                link(v.tensor_scalar(thr[:, 2:3], thr[:, 1:2], -1.0, None, ALU.mult))
                link(v.tensor_scalar(wt[:, 0, :], w[:, :], thr[:, 1:2], alpha[:, :], ALU.is_gt, ALU.mult))
                link(v.tensor_scalar(wt[:, 1, :], w[:, :], thr[:, 2:3], alpha[:, :], ALU.is_lt, ALU.mult))
                v.tensor_tensor(wt[:, 0, :], wt[:, 0, :], wt[:, 1, :], ALU.subtract).then_inc(w_ready, 1)
                norm.vector(dve, link)
                link(v.tensor_tensor(c.x[:, :, :], c.x[:, :, :], bias[:, :].unsqueeze(1).to_broadcast([P, NT, P]), ALU.add))
                add_banks(c, dve, link, c.x, 4, y_psum)

            @block.tensor
            def _(pe):
                pe.wait_ge(sums_ready, 1)
                nc.tensor.matmul(ps[:, 7, 0:1], ones[:, :], thr[:, 0:1], start=True, stop=True).then_inc(total_psum, 1)
                pe.wait_ge(w_ready, 1)
                nc.tensor.transpose(ps[:, 6, 0:P], wt[:, 0, :], c.ident[:, :]).then_inc(wT_psum, 1)
                norm.tensor(pe)
                pe.wait_ge(wT_ready, 1)
                pe.wait_ge(norm.nT_ready, NC)
                project_tokens(c, c.nT, wT[:, :], 4, y_psum)

            @block.scalar
            def _(act):
                act.wait_ge(wT_psum, 1)
                nc.scalar.activation(wT[:, :], ps[:, 6, 0:P], ACT.Copy).then_inc(wT_ready, 1)
                norm.scalar(act, c.nT)


def l2_performer(c, ins):
    nc = c.nc
    c.layer = "l2a_"
    M, G, EPS = 32, 4, 1e-6
    W = 4 * (HD + 1)
    ps = c.ps
    with ExitStack() as ctx:
        b_out, woT = c.sb(ctx, "b_out", [P, P], F32), c.sb(ctx, "woT", [P, P], F32)
        with ExitStack() as fctx:
            w, wT = c.sb(fctx, "w", [P, 4, P], F32), c.sb(fctx, "wT", [P, 3, P], F32)
            bq, bk, bv = c.sb(fctx, "b_q", [P, 1], F32), c.sb(fctx, "b_k", [P, 1], F32), c.sb(fctx, "b_v", [P, P], F32)
            orf, orf_all = c.sb(fctx, "orf", [M, HD], F32), c.sb(fctx, "orf_all", [M, H, HD], F32)
            own, own4 = c.sb(fctx, "own_head", [P, H, M], F32), c.sb(fctx, "own_of_four", [P, 4, HD], F32)
            feat, minus_norm = c.sb(fctx, "features", [P, H * M], F32), c.sb(fctx, "minus_norm", [P, H * M], F32)
            v1 = c.sb(fctx, "v_and_ones", [P, NT, H, HD + 1], F32)
            q2, k2 = c.sb(fctx, "q_squared", [P, T], F32), c.sb(fctx, "k_squared", [P, T], F32)
            phik, phiq = c.sb(fctx, "phi_k", [P, 4, H * M], F32), c.sb(fctx, "phi_q", [P, G, T], F32)
            kv, ksum = c.sb(fctx, "kv", [P, G, 4, HD], F32), c.sb(fctx, "k_sums", [P, G, 4, HD], F32)
            rden = c.sb(fctx, "denominators", [P, 512], F32)
            norm = NormBlock(c)
            (w_loaded, chain, drawn, wT_psum, wT_ready, orf_ready, orf_psum, feat_ready, q_psum, q_ready, k_psum, k_ready, v_psum, v_ready,
             q2_ready, k2_ready, pk_psum, pk_exp, pk_ready, kv_psum, kv_ready, pq_psum, pq_exp, pq_ready, num_psum, x_ready, divided, y_psum) = (c.sem(n) for n in (
                 "w_loaded", "chain", "drawn", "wT_psum", "wT_ready", "orf_ready", "orf_psum", "feat_ready", "q_psum", "q_ready", "k_psum",
                 "k_ready", "v_psum", "v_ready", "q2_ready", "k2_ready", "pk_psum", "pk_exp", "pk_ready", "kv_psum", "kv_ready",
                 "pq_psum", "pq_exp", "pq_ready", "num_psum", "x_ready", "divided", "y_psum"))
            loads = [(w[:, k, :], ins[f"L2_attn_W{m}"]) for k, m in enumerate("qkvo")]
            loads += [(bq[:, :], column(ins["L2_attn_bq"])), (bk[:, :], column(ins["L2_attn_bk"])),
                      (bv[:, :], row_view(ins["L2_attn_bv"], P)), (b_out[:, :], row_view(ins["L2_attn_bo"], P)), (orf[:, :], ins["L2_attn_orf"])]
            with nc.Block() as block:
                @block.sync
                def _(sp):
                    for dst, src in loads:
                        sp.dma_start(dst, src).then_inc(w_loaded, 16)

                @block.gpsimd
                def _(pool):
                    nc.gpsimd.memset(own[:, :, :], 1.0).then_inc(drawn, 1)
                    nc.gpsimd.memset(own4[:, :, :], 1.0).then_inc(drawn, 1)
                    for m, n, step, width in ((own, H, HD, M), (own4, 4, M, HD)):
                        pool.wait_ge(drawn, 2 if m is own else 4)
                        nc.gpsimd.affine_select(out=m[:, :, :], in_=m[:, :, :], compare_op=ALU.is_ge, fill=0.0, base=0,
                                                pattern=[[-step, n], [0, width]], channel_multiplier=1).then_inc(drawn, 1)
                        pool.wait_ge(drawn, 3 if m is own else 5)
                        nc.gpsimd.affine_select(out=m[:, :, :], in_=m[:, :, :], compare_op=ALU.is_ge, fill=0.0, base=step - 1,
                                                pattern=[[step, n], [0, width]], channel_multiplier=-1).then_inc(drawn, 1)
                    pool.wait_ge(w_loaded, 16 * len(loads))
                    pool.wait_ge(norm.n_ready, NC)
                    nc.gpsimd.tensor_tensor(c.x[:, :, :], c.x[:, :, :], b_out[:, :].unsqueeze(1).to_broadcast([P, NT, P]), ALU.add).then_inc(x_ready, 1)

                @block.tensor
                def _(pe):
                    pe.wait_ge(w_loaded, 16 * len(loads))
                    for k in range(4):
                        nc.tensor.transpose(ps[:, 6, k * P:(k + 1) * P], w[:, k, :], c.ident[:, :]).then_inc(wT_psum, 1)
                    pe.wait_ge(orf_ready, 1)
                    nc.tensor.transpose(ps[:, 7, 0:M], orf_all[:, :, :].rearrange("m h d -> m (h d)"), c.ident[0:M, 0:M]).then_inc(orf_psum, 1)
                    norm.tensor(pe)
                    pe.wait_ge(wT_ready, 2)
                    pe.wait_ge(feat_ready, 1)
                    pe.wait_ge(norm.nT_ready, NC)
                    project_channels(c, wT[:, 1, :], c.nT, 4, k_psum)
                    project_channels(c, wT[:, 0, :], c.nT, 0, q_psum)
                    pe.wait_ge(k_ready, NC)
                    project_tokens(c, c.nT, wT[:, 2, :], 4, v_psum)
                    pe.wait_ge(q_ready, NC)
                    pe.wait_ge(k2_ready, 1)
                    pe.wait_ge(v_ready, 4)

                    def keys(t):
                        if t >= 4:
                            pe.wait_ge(pk_exp, t - 3)
                        tok = slice(t * P, (t + 1) * P)
                        nc.tensor.matmul(ps[:, t % 4, :], c.kT[:, tok], feat[:, :], start=True, stop=False)
                        nc.tensor.matmul(ps[:, t % 4, :], k2[:, tok], minus_norm[:, :], start=False, stop=True).then_inc(pk_psum, 1)

                    keys(0)
                    keys(1)
                    for t in range(NT):
                        if t + 2 < NT:
                            keys(t + 2)
                        pe.wait_ge(pk_ready, t + 1)
                        for g in range(G):
                            last = nc.tensor.matmul(ps[:, 4 + g, 0:W], phik[:, t % 4, g * P:(g + 1) * P],
                                                    v1[:, t, 4 * g:4 * g + 4, :].rearrange("p h d -> p (h d)"), start=t == 0, stop=t == NT - 1)
                        last.then_inc(kv_psum, 1)
                    def queries(k):
                        for g in range(G):
                            n = k * G + g
                            if n >= 2:
                                pe.wait_ge(pq_exp, n - 1)
                            tok = slice(k * 512, (k + 1) * 512)
                            nc.tensor.matmul(ps[:, n % 2, :], feat[:, g * P:(g + 1) * P], c.qT[:, tok], start=True, stop=False)
                            nc.tensor.matmul(ps[:, n % 2, :], minus_norm[:, g * P:(g + 1) * P], q2[:, tok], start=False, stop=True).then_inc(pq_psum, 1)

                    def attend(k):
                        pe.wait_ge(pq_ready, (k + 1) * G)
                        if k >= 2:
                            pe.wait_ge(divided, k - 1)
                        tok = slice(k * 512, (k + 1) * 512)
                        for bank, of in ((4 + k, kv), (2 + k % 2, ksum)):
                            for g in range(G):
                                last = nc.tensor.matmul(ps[32 * g:32 * g + 32, bank, :], of[:, g, :, :].rearrange("p h d -> p (h d)"),
                                                        phiq[:, g, tok], start=True, stop=True)
                        last.then_inc(num_psum, 1)

                    def project(k):
                        pe.wait_ge(divided, k + 1)
                        for t in range(4):
                            last = nc.tensor.matmul(ps[:, 4 + k, t * P:(t + 1) * P], c.nT[:, (4 * k + t) * P:(4 * k + t + 1) * P], woT[:, :],
                                                    start=True, stop=True)
                        last.then_inc(y_psum, 1)

                    pe.wait_ge(q2_ready, 1)
                    pe.wait_ge(pk_exp, NT)
                    for k in range(NC):
                        queries(k)
                        if k == 0:
                            pe.wait_ge(kv_ready, 2)
                        else:
                            attend(k - 1)
                        if k >= 2:
                            project(k - 2)
                    attend(NC - 1)
                    project(NC - 2)
                    project(NC - 1)

                @block.scalar
                def _(act):
                    norm.scalar(act, c.nT)
                    act.wait_ge(w_loaded, 16 * len(loads))
                    evacuate(c, act, 4, c.kT, k_psum, 0, k_ready, bk[:, :])
                    evacuate(c, act, 0, c.qT, q_psum, 0, q_ready, bq[:, :])
                    for t in range(NT):
                        act.wait_ge(pk_psum, t + 1)
                        if t >= 4:
                            act.wait_ge(kv_psum, t - 3)
                        nc.scalar.activation(phik[:, t % 4, :], ps[:, t % 4, :], ACT.Exp).then_inc(pk_exp, 1)
                    for n in range(G * NC):
                        act.wait_ge(pq_psum, n + 1)
                        nc.scalar.activation(phiq[:, n % G, (n // G) * 512:(n // G + 1) * 512], ps[:, n % 2, :], ACT.Exp).then_inc(pq_exp, 1)

                @block.vector
                def _(dve):
                    v = nc.vector
                    link = Chain(dve, chain)
                    dve.wait_ge(w_loaded, 16 * len(loads))
                    v.tensor_copy(orf_all[:, :, :], orf[:, :].unsqueeze(1).to_broadcast([M, H, HD])).then_inc(orf_ready, 1)
                    link(v.memset(v1[:, :, :, :], 1.0))
                    norm.vector(dve, link)
                    dve.wait_ge(wT_psum, 4)
                    v.tensor_copy(wT[:, :, :], ps[:, 6, 0:3 * P].rearrange("p (k n) -> p k n", k=3)).then_inc(wT_ready, 1)
                    v.tensor_copy(woT[:, :], ps[:, 6, 3 * P:4 * P]).then_inc(wT_ready, 1)
                    dve.wait_ge(drawn, 6)
                    dve.wait_ge(orf_psum, 1)
                    link(v.tensor_copy(rden[:, 0:M], ps[:, 7, 0:M]))
                    feat3 = feat[:, :].rearrange("p (h m) -> p h m", h=H)
                    link(v.tensor_tensor(feat3, own[:, :, :], rden[:, 0:M].unsqueeze(1).to_broadcast([P, H, M]), ALU.mult))
                    link(v.tensor_scalar(feat[:, :], feat[:, :], HD ** -0.25, None, ALU.mult))
                    v.tensor_scalar(minus_norm[:, :].rearrange("p (h m) -> p h m", h=H), own[:, :, :], -0.5 * HD ** -0.5, None, ALU.mult).then_inc(feat_ready, 1)
                    for b in range(4):
                        dve.wait_ge(v_psum, b + 1)
                        v.tensor_tensor(v1[:, 4 * b:4 * b + 4, :, 0:HD], ps[:, 4 + b, :].rearrange("p (t h d) -> p t h d", t=4, h=H),
                                        bv[:, :].rearrange("p (h d) -> p h d", h=H).unsqueeze(1).to_broadcast([P, 4, H, HD]), ALU.add).then_inc(v_ready, 1)
                    dve.wait_ge(k_ready, NC)
                    v.tensor_tensor(k2[:, :], c.kT[:, :], c.kT[:, :], ALU.mult).then_inc(k2_ready, 1)
                    dve.wait_ge(q_ready, NC)
                    v.tensor_tensor(q2[:, :], c.qT[:, :], c.qT[:, :], ALU.mult).then_inc(q2_ready, 1)
                    for t in range(NT):
                        dve.wait_ge(pk_exp, t + 1)
                        v.tensor_scalar(phik[:, t % 4, :], phik[:, t % 4, :], EPS, M ** -0.5, ALU.add, ALU.mult).then_inc(pk_ready, 1)
                    dve.wait_ge(kv_psum, NT)
                    four = ps[:, 4:8, 0:W].rearrange("p g (h d) -> p g h d", h=4)
                    every = own4[:, :, :].unsqueeze(1).to_broadcast([P, G, 4, HD])
                    v.tensor_tensor(kv[:, :, :, :], four[:, :, :, 0:HD], every, ALU.mult).then_inc(kv_ready, 1)
                    v.tensor_tensor(ksum[:, :, :, :], four[:, :, :, HD:HD + 1].to_broadcast([P, G, 4, HD]), every, ALU.mult).then_inc(kv_ready, 1)

                    def divide(k):
                        dve.wait_ge(num_psum, k + 1)
                        if k:
                            dve.wait_ge(divided, k)
                        link(v.reciprocal(rden[:, :], ps[:, 2 + k % 2, :]))
                        v.tensor_tensor(c.nT[:, k * 512:(k + 1) * 512], ps[:, 4 + k, :], rden[:, :], ALU.mult).then_inc(divided, 1)

                    def add(k):
                        sl = slice(4 * k, 4 * k + 4)
                        dve.wait_ge(y_psum, k + 1)
                        if k == 0:
                            dve.wait_ge(x_ready, 1)
                        link(v.tensor_tensor(c.x[:, sl, :], c.x[:, sl, :], ps[:, 4 + k, :].rearrange("p (t d) -> p t d", t=4), ALU.add))

                    for k in range(NC):
                        for g in range(G):
                            n = k * G + g
                            dve.wait_ge(pq_exp, n + 1)
                            part = phiq[:, g, k * 512:(k + 1) * 512]
                            v.tensor_scalar(part, part, EPS, M ** -0.5, ALU.add, ALU.mult).then_inc(pq_ready, 1)
                        if k >= 1:
                            divide(k - 1)
                        if k >= 2:
                            add(k - 2)
                    divide(NC - 1)
                    add(NC - 2)
                    add(NC - 1)


class Routed:

    def __init__(self, c, ctx, E, K):
        nc, sb = c.nc, c.sb
        self.E = E
        self.tiles = (K * T + E * (P - 1)) // P + 1
        self.listed = self.tiles + 2
        self.least_rounds = K * T // P // 2
        self.rounds = sb(ctx, "rounds", [1, 1], mybir.dt.int32)
        self.expert_of = sb(ctx, "expert_of_tile", [1, self.listed], mybir.dt.int32)
        self.q = sb(ctx, "gathered_q", [P, 2, P], F32)
        self.index = sb(ctx, "gathered_index", [P, 2], mybir.dt.uint32)
        self.qparts = sb(ctx, "gathered_q_parts", [P, 3, P], BF16)
        self.qT = sb(ctx, "gathered_qT", [P, P], F32)
        self.qrest = sb(ctx, "gathered_q_rest", [P, P], F32)
        self.outT = sb(ctx, "outT", [P, P], F32)
        self.y = sb(ctx, "y", [P, P], F32)
        self.w_out_now = sb(ctx, "w_out_now", [P, P], F32)
        self.list_loaded, self.gathered = c.sem("rt_list_loaded"), [c.sem(f"rt_gathered{k}") for k in range(2)]
        self.list_dram = nc.dram_tensor("query_list_dram", [self.listed, P], mybir.dt.uint32, kind="Internal").ap()
        self.q_dram = nc.dram_tensor("expert_q_dram", [E * T, P], F32, kind="Internal").ap()
        self.v_dram = nc.dram_tensor("expert_v_dram", [E, P, NT, H, HD + 1], F32, kind="Internal").ap()
        self.w_out_dram = nc.dram_tensor("expert_w_out_dram", [E, P, P], F32, kind="Internal").ap()
        self.y_dram = nc.dram_tensor("expert_y_dram", [self.tiles + 1, P, P], F32, kind="Internal").ap()

    def load_index(self, pool, tile, k):
        pool.dma_start(self.index[:, k:k + 1], self.list_dram[bass.ds(tile, 1)].rearrange("a (p b) -> (a p) b", b=1)).then_inc(self.list_loaded, 16)

    def gather(self, pool, k):
        pool.indirect_dma_start(out=self.q[:, k, :], out_offset=None, in_=self.q_dram[:, :],
                                in_offset=bass.IndirectOffsetOnAxis(ap=self.index[:, k:k + 1], axis=0)).then_inc(self.gathered[k], 16)


def l2_ffn(c, at, ins, fixed):
    c.layer = "l2f_"
    E, K = 8, 2
    with ExitStack() as ctx:
        rt = Routed(c, ctx, E, K)
        gate = c.sb(ctx, "gate", [P, K, NT], F32)
        slot = c.sb(ctx, "slot", [P, K, NT], mybir.dt.uint32)
        row = c.sb(ctx, "row", [P, K, NT], mybir.dt.uint32)
        y_row = c.sb(ctx, "y_row", [P, K, NT], mybir.dt.uint32)
        l2_router(c, ins, rt, E, K, gate, slot, row, y_row, fixed)
        l2_prepare(c, at, ins, rt, slot, row)
        attention_loop(c, at, 3, routed=rt)
        l2_collect(c, rt, gate, y_row)


def l2_router(c, ins, rt, E, K, gate, slot, row, y_row, fixed):
    nc, ps = c.nc, c.ps
    W = P // 2
    with ExitStack() as ctx:
        w1, w2, ob = c.sb(ctx, "rw1", [W, P], F32), c.sb(ctx, "rw2", [E, W], F32), c.sb(ctx, "ob", [E, P], F32)
        b1, b2 = c.sb(ctx, "rb1", [P, W], F32), c.sb(ctx, "rb2", [P, E], F32)
        g1, g0 = c.sb(ctx, "ln_g", [W, 1], F32), c.sb(ctx, "ln_b", [W, 1], F32)
        w1T, w2T = c.sb(ctx, "rw1T", [P, W], F32), c.sb(ctx, "rw2T", [W, E], F32)
        h, hh = c.sb(ctx, "hidden", [P, NT, W], F32), c.sb(ctx, "hidden_squared", [P, NT, W], F32)
        hT = c.sb(ctx, "hiddenT", [W, T], F32)
        probs, masked, sel, mix, tmp = (c.sb(ctx, n, [P, NT, E], F32) for n in ("probs", "masked", "selected", "mix", "tmp"))
        choice = c.sb(ctx, "choice", [P, K, NT, E], F32)
        best = c.sb(ctx, "best", [P, K, NT], F32)
        tie, total = c.sb(ctx, "tie", [P, NT], F32), c.sb(ctx, "total", [P, NT], F32)
        order, edge = c.sb(ctx, "order", [P, E], F32), c.sb(ctx, "edge", [P, NT], F32)
        before, ones = c.sb(ctx, "before", [P, P], F32), c.sb(ctx, "ones", [P, P], F32)
        counts, offset = c.sb(ctx, "tile_counts", [P, NT, E], F32), c.sb(ctx, "tile_offset", [P, NT, E], F32)
        more, tiles_of = c.sb(ctx, "more", [P, E, NT], F32), c.sb(ctx, "tiles_of", [P, E], F32)
        first, end, index = c.sb(ctx, "first_tile", [P, E], F32), c.sb(ctx, "end_tile", [P, E], F32), c.sb(ctx, "partition", [P, 1], F32)
        many = c.sb(ctx, "many", [P, 2], F32)
        passed, of_tile = c.sb(ctx, "passed", [P, E], F32), c.sb(ctx, "of_tile", [P, 1], F32)
        where = c.sb(ctx, "where", [P, NT], F32)
        mixT = c.sb(ctx, "mixT", [E, T], F32)
        norm = NormBlock(c)
        (w_loaded, drawn, chain, wT_psum, wT_ready, h_psum, hvar_ready, hstd_ready, h_ready, hT_psum, hT_ready, lg_psum, shifted, exp_ready,
         sel_ready, rank_psum, mix_ready, mixT_psum, mixT_ready, ranked, of_tile_ready, of_tile_psum, ob_psum) = (c.sem("r_" + n) for n in (
             "w_loaded", "drawn", "chain", "wT_psum", "wT_ready", "h_psum", "hvar_ready", "hstd_ready", "h_ready", "hT_psum", "hT_ready",
             "lg_psum", "shifted", "exp_ready", "sel_ready", "rank_psum", "mix_ready", "mixT_psum", "mixT_ready", "ranked", "of_tile_ready",
             "of_tile_psum", "ob_psum"))
        loads = [(w1[:, :], ins["L2_ffn_rW1"]), (w2[:, :], ins["L2_ffn_rW2"]), (ob[:, :], ins["L2_ffn_ob"]),
                 (b1[:, :], row_view(ins["L2_ffn_rb1"], W)), (g1[:, :], column(ins["L2_ffn_ln_g"])),
                 (g0[:, :], column(ins["L2_ffn_ln_b"])), (b2[:, :], row_view(ins["L2_ffn_rb2"], E))]
        DRAWN = E + NT + 3

        def per_token(s, width):
            return s.unsqueeze(2).to_broadcast([P, NT, width])

        def per_column(s, width):
            return s.unsqueeze(1).to_broadcast([P, NT, width])

        with nc.Block() as block:
            @block.sync
            def _(sp):
                for dst, src in loads:
                    sp.dma_start(dst, src).then_inc(w_loaded, 16)
                fixed.sync(sp)
                fixed.sync_end(sp)

            @block.gpsimd
            def _(pool):
                draw_order(c, pool, order, E, drawn)
                for t in range(NT):
                    nc.gpsimd.memset(edge[:, t:t + 1], float(P * t)).then_inc(drawn, 1)
                nc.gpsimd.memset(ones[:, :], 1.0).then_inc(drawn, 1)
                nc.gpsimd.memset(before[:, :], 1.0).then_inc(drawn, 1)
                pool.wait_ge(drawn, DRAWN - 1)
                nc.gpsimd.affine_select(out=before[:, :], in_=before[:, :], compare_op=ALU.is_gt, fill=0.0, base=0,
                                        pattern=[[1, P]], channel_multiplier=-1).then_inc(drawn, 1)
                fixed.gpsimd()
                fixed.wait(pool)

            @block.tensor
            def _(pe):
                pe.wait_ge(w_loaded, 16 * len(loads))
                nc.tensor.transpose(ps[:, 4, 0:W], w1[:, :], c.ident[0:W, 0:W])
                nc.tensor.transpose(ps[0:W, 4, W:W + E], w2[:, :], c.ident[0:E, 0:E]).then_inc(wT_psum, 1)
                norm.tensor(pe)
                pe.wait_ge(wT_ready, 2)
                pe.wait_ge(norm.nT_ready, NC)
                for t in range(NT):
                    ins_ = nc.tensor.matmul(ps[:, 4 + t // 8, (t % 8) * W:(t % 8 + 1) * W], c.nT[:, t * P:(t + 1) * P], w1T[:, :],
                                            start=True, stop=True)
                    if t % 8 == 7:
                        ins_.then_inc(h_psum, 1)
                pe.wait_ge(h_ready, 1)
                for t in range(NT):
                    ins_ = nc.tensor.transpose(ps[0:W, t // 4, (t % 4) * P:(t % 4 + 1) * P], h[:, t, :], c.ident[:, :])
                    if t % 4 == 3:
                        ins_.then_inc(hT_psum, 1)
                pe.wait_ge(hT_ready, NC)
                for t in range(NT):
                    last = nc.tensor.matmul(ps[:, 6, t * E:(t + 1) * E], hT[:, t * P:(t + 1) * P], w2T[:, :], start=True, stop=True)
                last.then_inc(lg_psum, 1)
                pe.wait_ge(drawn, DRAWN)
                pe.wait_ge(sel_ready, 1)
                chosen = sel[:, :, :].rearrange("p t e -> p (t e)")
                nc.tensor.matmul(ps[:, 7, 0:P], before[:, :], chosen, start=True, stop=True)
                nc.tensor.matmul(ps[:, 7, P:2 * P], ones[:, :], chosen, start=True, stop=True)
                nc.tensor.matmul(ps[:, 7, 2 * P:2 * P + 1], before[:, :], ones[:, 0:1], start=True, stop=True).then_inc(rank_psum, 1)
                pe.wait_ge(mix_ready, 1)
                for t in range(NT):
                    ins_ = nc.tensor.transpose(ps[0:E, t // 4, (t % 4) * P:(t % 4 + 1) * P], mix[:, t, :], c.ident[:, :])
                    if t % 4 == 3:
                        ins_.then_inc(mixT_psum, 1)
                pe.wait_ge(of_tile_ready, 1)
                nc.tensor.transpose(ps[0:1, 6, 0:P], of_tile[:, :], c.ident[:, :]).then_inc(of_tile_psum, 1)
                pe.wait_ge(mixT_ready, NC)
                pe.wait_ge(ranked, 1)
                for t in range(NT):
                    ins_ = nc.tensor.matmul(ps[:, 4 + t // 4, (t % 4) * P:(t % 4 + 1) * P], mixT[:, t * P:(t + 1) * P], ob[:, :],
                                            start=True, stop=True)
                    if t % 4 == 3:
                        ins_.then_inc(ob_psum, 1)

            @block.scalar
            def _(act):
                act.wait_ge(wT_psum, 1)
                nc.scalar.activation(w1T[:, :], ps[:, 4, 0:W], ACT.Copy).then_inc(wT_ready, 1)
                nc.scalar.activation(w2T[:, :], ps[0:W, 4, W:W + E], ACT.Copy).then_inc(wT_ready, 1)
                norm.scalar(act, c.nT)
                act.wait_ge(w_loaded, 16 * len(loads))
                act.wait_ge(hvar_ready, 1)
                nc.scalar.activation(total[:, :], total[:, :], ACT.Sqrt).then_inc(hstd_ready, 1)
                for k in range(NC):
                    act.wait_ge(hT_psum, k + 1)
                    nc.scalar.activation(hT[:, k * 512:(k + 1) * 512], ps[0:W, k, :], ACT.Relu, bias=g0[:, :], scale=g1[:, :]).then_inc(hT_ready, 1)
                act.wait_ge(shifted, 1)
                nc.scalar.activation(probs[:, :, :], probs[:, :, :], ACT.Exp).then_inc(exp_ready, 1)
                for k in range(NC):
                    act.wait_ge(mixT_psum, k + 1)
                    nc.scalar.activation(mixT[:, k * 512:(k + 1) * 512], ps[0:E, k, :], ACT.Copy).then_inc(mixT_ready, 1)

            @block.vector
            def _(dve):
                v = nc.vector
                link = Chain(dve, chain)
                norm.vector(dve, link)
                dve.wait_ge(w_loaded, 16 * len(loads))
                for b in range(2):
                    dve.wait_ge(h_psum, b + 1)
                    link(v.tensor_tensor(h[:, 8 * b:8 * b + 8, :], ps[:, 4 + b, :].rearrange("p (t w) -> p t w", w=W),
                                         b1[:, :].unsqueeze(1).to_broadcast([P, 8, W]), ALU.add))
                link(v.tensor_reduce(total[:, :], h[:, :, :], X, ALU.add))
                link(v.tensor_scalar(tie[:, :], total[:, :], 1.0 / W, None, ALU.mult))
                link(v.tensor_tensor(h[:, :, :], h[:, :, :], per_token(tie[:, :], W), ALU.subtract))
                link(v.tensor_tensor(hh[:, :, :], h[:, :, :], h[:, :, :], ALU.mult))
                link(v.tensor_reduce(tie[:, :], hh[:, :, :], X, ALU.add))
                v.tensor_scalar(total[:, :], tie[:, :], 1.0 / W, 1e-5, ALU.mult, ALU.add).then_inc(hvar_ready, 1)
                dve.wait_ge(hstd_ready, 1)
                link(v.reciprocal(tie[:, :], total[:, :]))
                v.tensor_tensor(h[:, :, :], h[:, :, :], per_token(tie[:, :], W), ALU.mult).then_inc(h_ready, 1)
                dve.wait_ge(lg_psum, 1)
                link(v.tensor_tensor(masked[:, :, :], ps[:, 6, 0:NT * E].rearrange("p (t e) -> p t e", e=E), per_column(b2[:, :], E), ALU.add))
                link(v.tensor_reduce(tie[:, :], masked[:, :, :], X, ALU.max))
                v.tensor_tensor(probs[:, :, :], masked[:, :, :], per_token(tie[:, :], E), ALU.subtract).then_inc(shifted, 1)
                dve.wait_ge(exp_ready, 1)
                link(v.tensor_reduce(total[:, :], probs[:, :, :], X, ALU.add))
                link(v.reciprocal(tie[:, :], total[:, :]))
                link(v.tensor_tensor(probs[:, :, :], probs[:, :, :], per_token(tie[:, :], E), ALU.mult))
                dve.wait_ge(drawn, DRAWN)
                top_choice(c, v, link, probs[:, :, :], best[:, 0, :], tie[:, :], order[:, :], choice[:, 0], E)
                link(v.scalar_tensor_tensor(masked[:, :, :], choice[:, 0], MASKED, probs[:, :, :], ALU.mult, ALU.add))
                top_choice(c, v, link, masked[:, :, :], best[:, 1, :], tie[:, :], order[:, :], choice[:, 1], E)
                v.tensor_tensor(sel[:, :, :], choice[:, 0], choice[:, 1], ALU.add).then_inc(sel_ready, 1)
                link(v.tensor_tensor(total[:, :], best[:, 0, :], best[:, 1, :], ALU.add))
                link(v.reciprocal(tie[:, :], total[:, :]))
                for k in range(K):
                    link(v.tensor_tensor(gate[:, k, :], best[:, k, :], tie[:, :], ALU.mult))
                link(v.tensor_tensor(mix[:, :, :], choice[:, 0], per_token(gate[:, 0, :], E), ALU.mult))
                link(v.tensor_tensor(tmp[:, :, :], choice[:, 1], per_token(gate[:, 1, :], E), ALU.mult))
                v.tensor_tensor(mix[:, :, :], mix[:, :, :], tmp[:, :, :], ALU.add).then_inc(mix_ready, 1)
                dve.wait_ge(mix_ready, 1)
                dve.wait_ge(rank_psum, 1)
                link(v.tensor_copy(counts[:, :, :], ps[:, 7, P:2 * P].rearrange("p (t e) -> p t e", e=E)))
                link(v.tensor_copy(index[:, :], ps[:, 7, 2 * P:2 * P + 1]))
                link(v.memset(offset[:, 0, :], 0.0))
                for t in range(1, NT):
                    link(v.tensor_tensor(offset[:, t, :], offset[:, t - 1, :], counts[:, t - 1, :], ALU.add))
                link(v.tensor_tensor(end[:, :], offset[:, NT - 1, :], counts[:, NT - 1, :], ALU.add))
                link(v.tensor_tensor(more[:, :, :], end[:, :].unsqueeze(2).to_broadcast([P, E, NT]),
                                     edge[:, :].unsqueeze(1).to_broadcast([P, E, NT]), ALU.is_gt))
                link(v.tensor_reduce(tiles_of[:, :], more[:, :, :], X, ALU.add))
                link(v.memset(first[:, 0:1], 0.0))
                for e in range(1, E):
                    link(v.tensor_tensor(first[:, e:e + 1], first[:, e - 1:e], tiles_of[:, e - 1:e], ALU.add))
                link(v.tensor_tensor(end[:, :], first[:, :], tiles_of[:, :], ALU.add))
                link(v.tensor_scalar(passed[:, :], end[:, :], index[:, 0:1], None, ALU.is_le))
                link(v.tensor_reduce(of_tile[:, :], passed[:, :], X, ALU.add))
                v.tensor_scalar(of_tile[:, :], of_tile[:, :], float(E - 1), None, ALU.min).then_inc(of_tile_ready, 1)
                link(v.memset(many[:, 0:1], float(rt.least_rounds)))
                for n in range(rt.least_rounds, rt.tiles // 2):
                    link(v.tensor_scalar(many[:, 1:2], end[:, E - 1:E], 2.0 * n, None, ALU.is_gt))
                    link(v.tensor_tensor(many[:, 0:1], many[:, 0:1], many[:, 1:2], ALU.add))
                link(v.tensor_copy(rt.rounds[:, :], many[0:1, 0:1]))
                link(v.tensor_scalar(first[:, :], first[:, :], float(P), None, ALU.mult))
                link(v.tensor_tensor(offset[:, :, :], offset[:, :, :], per_column(first[:, :], E), ALU.add))
                link(v.tensor_tensor(offset[:, :, :], offset[:, :, :], ps[:, 7, 0:P].rearrange("p (t e) -> p t e", e=E), ALU.add))
                for k in range(K):
                    link(v.tensor_tensor(tmp[:, :, :], choice[:, k], offset[:, :, :], ALU.mult))
                    link(v.tensor_reduce(where[:, :], tmp[:, :, :], X, ALU.add))
                    link(v.tensor_copy(slot[:, k, :], where[:, :]))
                    link(v.tensor_scalar(y_row[:, k, :], where[:, :], float(P), None, ALU.add))
                    link(v.tensor_tensor(tmp[:, :, :], choice[:, k], per_column(order[:, :], E), ALU.mult))
                    link(v.tensor_reduce(where[:, :], tmp[:, :, :], X, ALU.add))
                    link(v.tensor_scalar(where[:, :], where[:, :], -float(T), float(E * T), ALU.mult, ALU.add))
                    link(v.tensor_tensor(where[:, :], where[:, :], edge[:, :], ALU.add))
                    link(v.tensor_scalar(row[:, k, :], where[:, :], index[:, 0:1], None, ALU.add))
                dve.wait_ge(of_tile_psum, 1)
                v.tensor_copy(rt.expert_of[:, :], ps[0:1, 6, 0:rt.listed]).then_inc(ranked, 1)
                add_banks(c, dve, link, c.x, 4, ob_psum)


def l2_prepare(c, at, ins, rt, slot, row):
    nc, ps = c.nc, c.ps
    E, K = rt.E, 2
    with ExitStack() as ctx:
        w = c.sb(ctx, "w_qkvo", [P, 2, 4, P], F32)
        bq, bv, bk = c.sb(ctx, "b_q", [P, 2, P], F32), c.sb(ctx, "b_v", [P, 2, P], F32), c.sb(ctx, "b_k", [P, 2], F32)
        bq_ordered = c.sb(ctx, "b_q_head_order", [P, P], F32)
        wT = c.sb(ctx, "wT_qkvo", [P, 2, 4, P], F32)
        used = 2 * rt.least_rounds + 1
        blank_y, y_blanked = c.sb(ctx, "blank_y", [P, P], F32), c.sem("p_y_blanked")
        blank = c.sb(ctx, "blank_list", [rt.listed, P], mybir.dt.uint32)
        start = c.sb(ctx, "p_start_credit", [P, 10], F32)
        w_loaded, b_loaded = ([c.sem(f"p_{n}_loaded{k}") for k in range(2)] for n in "wb")
        (wT_psum, wT_ready, k_psum, hi_ready, v_psum, v_ready, q_psum, q_ready, rest_ready, mid_ready, parts_ready, ordered,
         v_stored, q_stored, blanked, scattered) = (c.sem("p_" + n) for n in (
             "wT_psum", "wT_ready", "k_psum", "hi_ready", "v_psum", "v_ready", "q_psum", "q_ready", "rest_ready", "mid_ready", "parts_ready",
             "ordered", "v_stored", "q_stored", "blanked", "scattered"))
        o_stored, parts_stored = ([c.sem(f"p_{n}_stored{k}") for k in range(2)] for n in ("o", "parts"))
        parts = ((at.hi, at.mid, at.lo), [c.sb(ctx, f"other_{n}", [P, T], BF16) for n in ("hi", "mid", "lo")])
        LOADS = 16 * 4
        rest = c.b[:, :, :].rearrange("p t d -> p (t d)")
        with nc.Block() as block:
            def done(n, e):
                return e * n + n

            def each_expert(eng, body):
                with eng.Fori(0, E // 2) as r:
                    for k in range(2):
                        body(r * 2 + k, k, r)

            @block.sync
            def _(sp):
                def load_weights(k, e):
                    for n, m in enumerate("qkvo"):
                        sp.dma_start(w[:, k, n, :], ins[f"L2_ffn_{m}W"][bass.ds(e, 1)].rearrange("e p d -> (e p) d")).then_inc(w_loaded[k], 16)

                def load_biases(k, e):
                    def vector(name):
                        return ins[name][bass.ds(e, 1)]
                    sp.dma_start(bq[:, k, :], vector("L2_ffn_qb").to_broadcast([P, P])).then_inc(b_loaded[k], 16)
                    sp.dma_start(bv[:, k, :], vector("L2_ffn_vb").to_broadcast([P, P])).then_inc(b_loaded[k], 16)
                    for j in range(2):
                        sp.dma_start(bk[64 * j:64 * j + 64, k:k + 1], vector("L2_ffn_kb").rearrange("e (p j d) -> j d p e", p=NPAIR, j=2)[j],
                                     allow_slow_non_contiguous=True).then_inc(b_loaded[k], 16)

                def stores(e, k, r):
                    sp.wait_ge(wT_ready, e * 3 + 3)
                    load_weights(k, (e + 2) % E)
                    sp.dma_start(rt.w_out_dram[bass.ds(e, 1)].rearrange("e p d -> (e p) d"), wT[:, k, 3, :]).then_inc(o_stored[k], 16)
                    sp.wait_ge(v_ready, done(2, e + 1))
                    sp.dma_start(rt.v_dram[bass.ds(e, 1)].rearrange("e p t h d -> (e p) (t h d)"),
                                 at.v[:, 0].rearrange("p t h d -> p (t h d)")).then_inc(v_stored, 16)
                    sp.wait_ge(q_ready, done(4, e + 1))
                    sp.dma_start(rt.q_dram[bass.ds(e * T, T), :].rearrange("(t p) d -> p t d", p=P), c.a).then_inc(q_stored, 16)
                    store_keys(at, sp, e, parts[k], parts_ready, done(1, e + 1), parts_stored[k])
                    load_biases(k, (e + 2) % E)

                for k in range(2):
                    load_weights(k, k)
                    load_biases(k, k)
                each_expert(sp, stores)
                for k in range(2):
                    sp.wait_ge(w_loaded[k], LOADS * (E // 2 + 1))
                    sp.wait_ge(b_loaded[k], LOADS * (E // 2 + 1))
                for s in (v_stored, q_stored):
                    sp.wait_ge(s, done(16, E))
                for k in range(2):
                    sp.wait_ge(o_stored[k], 16 * (E // 2 + k))
                    sp.wait_ge(parts_stored[k], done(48, E // 2))

            @block.gpsimd
            def _(pool):
                nc.gpsimd.memset(blank[:, :], 0).then_inc(blanked, 1)
                nc.gpsimd.memset(blank_y[:, :], 0.0).then_inc(blanked, 1)
                pool.wait_ge(blanked, 2)
                pool.dma_start(rt.y_dram[used:].rearrange("i p d -> p i d"),
                               blank_y[:, :].unsqueeze(1).to_broadcast([P, rt.tiles + 1 - used, P])).then_inc(y_blanked, 16)
                pool.dma_start(rt.list_dram[:, :], blank[:, :]).then_inc(scattered, 16)
                pool.wait_ge(scattered, 16)
                for t in range(NT):
                    for k in range(K):
                        nc.gpsimd.indirect_dma_start(out=rt.list_dram.rearrange("i (p a) -> (i p) a", a=1),
                                                     out_offset=bass.IndirectOffsetOnAxis(ap=slot[:, k, t:t + 1], axis=0),
                                                     in_=row[:, k, t:t + 1], in_offset=None).then_inc(scattered, 16)
                pool.wait_ge(scattered, 16 * (1 + K * NT))
                for k in range(2):
                    rt.load_index(pool, k, k)
                pool.wait_ge(rt.list_loaded, 32)
                pool.wait_ge(q_stored, done(16, E))
                for k in range(2):
                    rt.gather(pool, k)
                pool.wait_ge(y_blanked, 16)

            @block.tensor
            def _(pe):
                def transpose_weights(k):
                    for n in range(4):
                        last = nc.tensor.transpose(ps[:, 6 + k, n * P:(n + 1) * P], w[:, k, n, :], c.ident[:, :])
                    last.then_inc(wT_psum, 1)

                def values(half, k):
                    for t in range(8):
                        tile = 8 * half + t
                        last = nc.tensor.matmul(ps[:, 4 + t // 4, (t % 4) * P:(t % 4 + 1) * P], c.nT[:, tile * P:(tile + 1) * P],
                                                wT[:, k, 2, :], start=True, stop=True)
                    last.then_inc(v_psum, 1)

                def project(e, k, r):
                    pe.wait_ge(wT_ready, e * 3 + 3)
                    pe.wait_ge(q_ready, done(4, e))
                    project_channels(c, wT[:, k, 1, :], c.nT, 0, k_psum)
                    pe.wait_ge(v_ready, done(2, e))
                    values(0, k)
                    pe.wait_ge(w_loaded[1 - k], (r + k) * LOADS + LOADS)
                    transpose_weights(1 - k)
                    pe.wait_ge(v_ready, e * 2 + 3)
                    values(1, k)
                    pe.wait_ge(rest_ready, e * 4 + 4)
                    project_tokens(c, c.nT, wT[:, k, 0, :], 0, q_psum)

                pe.wait_ge(w_loaded[0], LOADS)
                transpose_weights(0)
                each_expert(pe, project)

            @block.scalar
            def _(act):
                def copy_weights(k, count):
                    act.wait_ge(wT_psum, count)
                    for n in range(2):
                        nc.scalar.activation(split_heads(wT[:, k, n, :]), head_order(ps[:, 6 + k, n * P:(n + 1) * P]), ACT.Copy).then_inc(wT_ready, 1)
                    nc.scalar.activation(wT[:, k, 2:4, :].rearrange("p n d -> p (n d)"), ps[:, 6 + k, 2 * P:4 * P], ACT.Copy).then_inc(wT_ready, 1)

                def keys(e, k, r):
                    act.wait_ge(parts_stored[k], done(48, r))
                    act.wait_ge(b_loaded[k], r * LOADS + LOADS)
                    for n in range(NC):
                        act.wait_ge(k_psum, e * 4 + (n + 1))
                        nc.scalar.activation(parts[k][0][:, n * 512:(n + 1) * 512], ps[:, n, :], ACT.Identity, bias=bk[:, k:k + 1]).then_inc(hi_ready, 1)
                    act.wait_ge(rest_ready, e * 4 + 4)
                    nc.scalar.activation(parts[k][1][:, :], rest, ACT.Copy).then_inc(mid_ready, 1)
                    act.wait_ge(q_psum, done(4, e))
                    act.wait_ge(o_stored[1 - k], r * 16 + 16)
                    copy_weights(1 - k, e + 2)

                copy_weights(0, 1)
                each_expert(act, keys)

            @block.vector
            def _(dve):
                v = nc.vector
                for n, (s, credit) in enumerate(((parts_ready, 1), (q_psum, 4), (q_ready, 4), (v_ready, 2), (parts_stored[0], 48), (parts_stored[1], 48),
                                                 (v_stored, 16), (q_stored, 16), (o_stored[1], 16))):
                    v.memset(start[:, n:n + 1], 0.0).then_inc(s, credit)

                def biases(e, k, r):
                    dve.wait_ge(b_loaded[k], r * LOADS + LOADS)
                    dve.wait_ge(q_ready, done(4, e))
                    v.tensor_copy(split_heads(bq_ordered[:, :]), head_order(bq[:, k, :])).then_inc(ordered, 1)
                    dve.wait_ge(parts_ready, done(1, e))
                    for b in range(NC):
                        dve.wait_ge(hi_ready, e * 4 + (b + 1))
                        chunk = slice(b * 512, (b + 1) * 512)
                        v.scalar_tensor_tensor(rest[:, chunk], ps[:, b, :], bk[:, k:k + 1], parts[k][0][:, chunk],
                                               ALU.add, ALU.subtract).then_inc(rest_ready, 1)
                    dve.wait_ge(v_stored, done(16, e))
                    for half in range(2):
                        dve.wait_ge(v_psum, e * 2 + (half + 1))
                        v.tensor_tensor(at.v[:, 0, 8 * half:8 * half + 8, :, 0:HD], ps[:, 4:6, :].rearrange("p b (t h d) -> p (b t) h d", t=4, h=H),
                                        bv[:, k, :].rearrange("p (h d) -> p h d", h=H).unsqueeze(1).to_broadcast([P, 8, H, HD]),
                                        ALU.add).then_inc(v_ready, 1)
                    dve.wait_ge(ordered, e + 1)
                    dve.wait_ge(q_stored, done(16, e))
                    for b in range(4):
                        dve.wait_ge(q_psum, e * 4 + (b + 5))
                        v.tensor_tensor(c.a[:, 4 * b:4 * b + 4, :], ps[:, b, :].rearrange("p (t d) -> p t d", t=4),
                                        bq_ordered[:, :].unsqueeze(1).to_broadcast([P, 4, P]), ALU.add).then_inc(q_ready, 1)
                    dve.wait_ge(mid_ready, e + 1)
                    v.tensor_tensor(parts[k][2][:, :], rest, parts[k][1][:, :], ALU.subtract).then_inc(parts_ready, 1)

                each_expert(dve, biases)


def l2_collect(c, rt, gate, y_row):
    nc = c.nc
    B = 2
    gathered, added = [c.sem(f"c_gathered{n}") for n in range(NT // B)], c.sem("c_added")
    y = (c.a, c.b)
    with nc.Block() as block:
        @block.gpsimd
        def _(pool):
            for t in range(NT):
                for k in range(2):
                    nc.gpsimd.indirect_dma_start(out=y[k][:, t, :], out_offset=None, in_=rt.y_dram.rearrange("i p d -> (i p) d"),
                                                 in_offset=bass.IndirectOffsetOnAxis(ap=y_row[:, k, t:t + 1], axis=0)).then_inc(gathered[t // B], 16)

        @block.vector
        def _(dve):
            for t in range(NT):
                dve.wait_ge(gathered[t // B], 16 * 2 * B)
                for k in range(2):
                    nc.vector.scalar_tensor_tensor(c.x[:, t, :], y[k][:, t, :], gate[:, k, t:t + 1], c.x[:, t, :],
                                                   ALU.mult, ALU.add).then_inc(added, 1)
                    dve.wait_ge(added, 2 * t + k + 1)


def l3_state(c, ins):
    nc = c.nc
    c.layer = "l3a_"
    N, KC = 64, 4
    ps = c.ps
    with ExitStack() as ctx:
        xp = c.sb(ctx, "n_padded", [P, KC - 1 + T], F32)
        conv, conv_w, conv_b = c.sb(ctx, "conv", [P, T], F32), c.sb(ctx, "conv_w", [P, KC], F32), c.sb(ctx, "conv_b", [P, 1], F32)
        wp, ws, w_out, b_out = c.sb(ctx, "wp", [P, 2 * N], F32), c.sb(ctx, "ws", [P, N], F32), c.sb(ctx, "w_out", [N, P], F32), c.sb(ctx, "b_out", [P, P], F32)
        bp, bs = c.sb(ctx, "bp", [N, 2], F32), c.sb(ctx, "bs", [N, 1], F32)
        log, sp_, tl = c.sb(ctx, "a_dt_log", [N, 2], F32), c.sb(ctx, "a_dt", [N, 2], F32), c.sb(ctx, "a_dt_tail", [N, 2], F32)
        decay = c.sb(ctx, "decay", [N, 1], F32)
        u, b_t, c_t, mag = (c.sb(ctx, n, [N, T], F32) for n in ("u", "b_t", "c_t", "magnitude"))
        norm = NormBlock(c)
        w_loaded, chain, act_chain, conv_ready, u_psum, u_ready, p_psum, c_ready, tail_ready, dt_ready, y_ready, y_psum = (c.sem(n) for n in (
            "w_loaded", "chain", "act_chain", "conv_ready", "u_psum", "u_ready", "p_psum", "c_ready", "tail_ready", "dt_ready", "y_ready", "y_psum"))
        loads = [(conv_w[:, :], ins["L3_attn_conv_w"].rearrange("k a d -> d (k a)")), (conv_b[:, :], column(ins["L3_attn_conv_b"])),
                 (wp[:, :], ins["L3_attn_Wp"]), (bp[:, :], ins["L3_attn_bp"].rearrange("(k n) -> n k", n=N)), (ws[:, :], ins["L3_attn_Ws"]),
                 (bs[:, :], column(ins["L3_attn_bs"])), (log[:, 0:1], column(ins["L3_attn_A_log"])), (log[:, 1:2], column(ins["L3_attn_dt_log"])),
                 (w_out[:, :], ins["L3_attn_Wo"]), (b_out[:, :], row_view(ins["L3_attn_bo"], P))]

        def flat(bank0):
            return ps[0:N, bank0:bank0 + 4, :].rearrange("p b n -> p (b n)")

        with nc.Block() as block:
            @block.sync
            def _(sp):
                for dst, src in loads:
                    sp.dma_start(dst, src, allow_slow_non_contiguous=True).then_inc(w_loaded, 16)

            @block.tensor
            def _(pe):
                norm.tensor(pe)
                pe.wait_ge(w_loaded, 16 * len(loads))
                pe.wait_ge(norm.nT_ready, NC)
                for k in range(NC):
                    last = nc.tensor.matmul(ps[0:N, 4 + k, :], ws[:, :], xp[:, KC - 1 + k * 512:KC - 1 + (k + 1) * 512], start=True, stop=True)
                last.then_inc(u_psum, 1)
                pe.wait_ge(conv_ready, 1)
                for part in range(2):
                    if part:
                        pe.wait_ge(u_ready, 1)
                    for k in range(NC):
                        last = nc.tensor.matmul(ps[0:N, 4 * part + k, :], wp[:, part * N:(part + 1) * N], conv[:, k * 512:(k + 1) * 512],
                                                start=True, stop=True)
                    last.then_inc(p_psum, 1)
                pe.wait_ge(y_ready, 1)
                project_tokens(c, c_t, w_out[:, :], 4, y_psum)

            @block.scalar
            def _(act):
                link = Chain(act, act_chain)
                norm.scalar(act, xp[:, KC - 1:])
                act.wait_ge(w_loaded, 16 * len(loads))
                act.wait_ge(u_psum, 1)
                nc.scalar.activation(u[:, :], flat(4), ACT.Identity, bias=bs[:, :]).then_inc(u_ready, 1)
                softplus_scalar(c, act, link, log[:, :], 0.0, sp_[:, :], tl[:, :]).then_inc(dt_ready, 1)
                act.wait_ge(p_psum, 1)
                softplus_scalar(c, act, link, flat(0), bp[:, 0:1], mag[:, :], b_t[:, :]).then_inc(tail_ready, 1)
                act.wait_ge(p_psum, 2)
                nc.scalar.activation(c_t[:, :], flat(4), ACT.Tanh, bias=bp[:, 1:2]).then_inc(c_ready, 1)

            @block.vector
            def _(dve):
                v = nc.vector
                link = Chain(dve, chain)
                link(v.memset(xp[:, 0:KC - 1], 0.0))
                norm.vector(dve, link)
                dve.wait_ge(w_loaded, 16 * len(loads))
                dve.wait_ge(norm.nT_ready, NC)
                link(v.tensor_scalar(conv[:, :], xp[:, 0:T], conv_w[:, 0:1], conv_b[:, :], ALU.mult, ALU.add))
                for k in range(1, KC):
                    last = v.scalar_tensor_tensor(conv[:, :], xp[:, k:k + T], conv_w[:, k:k + 1], conv[:, :], ALU.mult, ALU.add)
                    if k < KC - 1:
                        link(last)
                last.then_inc(conv_ready, 1)
                dve.wait_ge(dt_ready, 1)
                link(v.scalar_tensor_tensor(sp_[:, :], log[:, :], 0.0, tl[:, :], ALU.max, ALU.add))
                link(v.tensor_tensor(decay[:, :], sp_[:, 0:1], sp_[:, 1:2], ALU.mult))
                link(v.tensor_scalar(decay[:, :], decay[:, :], -1.0, 1.0, ALU.mult, ALU.add))
                dve.wait_ge(tail_ready, 1)
                link(v.tensor_scalar(mag[:, :], flat(0), bp[:, 0:1], 0.0, ALU.add, ALU.max))
                link(v.tensor_tensor(b_t[:, :], b_t[:, :], mag[:, :], ALU.add))
                dve.wait_ge(u_ready, 1)
                link(v.scalar_tensor_tensor(u[:, :], b_t[:, :], sp_[:, 1:2], u[:, :], ALU.mult, ALU.mult))
                link(v.tensor_tensor_scan(b_t[:, :], decay[:, :].to_broadcast([N, T]), u[:, :], 0.0, ALU.mult, ALU.add))
                dve.wait_ge(c_ready, 1)
                v.tensor_tensor(c_t[:, :], c_t[:, :], b_t[:, :], ALU.mult).then_inc(y_ready, 1)
                link(v.tensor_tensor(c.x[:, :, :], c.x[:, :, :], b_out[:, :].unsqueeze(1).to_broadcast([P, NT, P]), ALU.add))
                add_banks(c, dve, link, c.x, 4, y_psum)


def l3_ffn(c, ins, out):
    nc = c.nc
    c.layer = "l3f_"
    E, F = 4, 4
    NPART, STEP = 3, 32
    K = NPART * STEP
    ps = c.ps
    with ExitStack() as ctx:
        gamma, beta, b_out = (c.sb(ctx, n, [P, P], F32) for n in ("gamma", "beta", "b_out"))
        w1, w2 = c.sb(ctx, "w1", [P, E, F * P], F32), c.sb(ctx, "wo", [P, F, P], F32)
        hot, pick = c.sb(ctx, "choice_rows", [K, T], BF16), c.sb(ctx, "pick_row", [K, E, P], BF16)
        b1, b1_rest, b1_parts = c.sb(ctx, "b1", [K, F * P], F32), c.sb(ctx, "b1_rest", [K, F * P], F32), c.sb(ctx, "b1_parts", [K, F * P], BF16)
        part = c.sb(ctx, "b1_part", [K, F * P], BF16)
        own, mid = c.sb(ctx, "own_n", [P, 2, E, 512], F32), c.sb(ctx, "hidden", [P, 2, F, 512], F32)
        wr, lg, order = c.sb(ctx, "w_router", [P, E], F32), c.sb(ctx, "logits", [P, NT, E], F32), c.sb(ctx, "order", [P, E], F32)
        choice, best, tie = c.sb(ctx, "choice", [P, NT, E], F32), c.sb(ctx, "best", [P, NT], F32), c.sb(ctx, "tie", [P, NT], F32)
        choice3 = c.sb(ctx, "choice_three_times", [P, NT, NPART, STEP], BF16)
        norm = NormBlock(c)
        w_loaded, b1_loaded, experts_loaded, chain, drawn = (c.sem(n) for n in ("w_loaded", "b1_loaded", "experts_loaded", "chain", "drawn"))
        lg_psum, choice_ready, hot_psum, hot_ready = (c.sem(n) for n in ("lg_psum", "choice_ready", "hot_psum", "hot_ready"))
        loads = [(wr[:, :], ins["L3_ffn_W_router"]), (b_out[:, :], row_view(ins["L3_ffn_bo"], P)),
                 (gamma[:, :], row_view(ins["L3_ffn_ln_gamma"], P)), (beta[:, :], row_view(ins["L3_ffn_ln_beta"], P))]
        hot_bank = ps[0:K, 6:8, :].rearrange("p b n -> p (b n)").bitcast(BF16)
        with nc.Block() as block:
            @block.sync
            def _(sp):
                for dst, src in loads:
                    sp.dma_start(dst, src).then_inc(w_loaded, 16)
                sp.wait_ge(drawn, 1)
                for n in range(NPART):
                    sp.dma_start(b1[n * STEP:n * STEP + E, :], ins["L3_ffn_b1"]).then_inc(b1_loaded, 16)
                sp.dma_start(w1[:, :, :], ins["L3_ffn_W1"].rearrange("e d f -> d e f")).then_inc(experts_loaded, 16)
                sp.dma_start(w2[:, :, :], ins["L3_ffn_Wo"].rearrange("(f p) d -> p f d", p=P)).then_inc(experts_loaded, 16)
                sp.wait_ge(experts_loaded, 32)

            @block.gpsimd
            def _(pool):
                g = nc.gpsimd
                g.memset(b1[:, :], 0.0).then_inc(drawn, 1)
                g.memset(choice3[:, :, :, :], 0.0).then_inc(drawn, 1)
                g.memset(pick[:, :, :], 0.0).then_inc(drawn, 1)
                pool.wait_ge(drawn, 3)
                g.affine_select(out=pick[:, :, :], in_=pick[:, :, :], compare_op=ALU.not_equal, fill=1.0, base=0,
                                pattern=[[-1, E], [0, P]], channel_multiplier=1).then_inc(drawn, 1)
                draw_order(c, pool, order, E, drawn)

            @block.tensor
            def _(pe):
                norm.tensor(pe)
                pe.wait_ge(w_loaded, 16 * len(loads))
                for t in range(NT):
                    if t % 4 == 0:
                        pe.wait_ge(norm.nT_ready, t // 4 + 1)
                    last = nc.tensor.matmul(ps[:, 5, t * E:(t + 1) * E], c.nT[:, t * P:(t + 1) * P], wr[:, :], start=True, stop=True)
                last.then_inc(lg_psum, 1)
                pe.wait_ge(choice_ready, 1)
                for t in range(NT):
                    last = nc.tensor.transpose(hot_bank[:, t * P:(t + 1) * P], choice3[:, t, :, :].rearrange("p n e -> p (n e)"), c.identb[:, :])
                last.then_inc(hot_psum, 1)

            @block.scalar
            def _(act):
                norm.scalar(act, c.nT)
                act.wait_ge(hot_psum, 1)
                nc.scalar.activation(hot[:, :], hot_bank, ACT.Copy).then_inc(hot_ready, 1)
                act.wait_ge(hot_ready, 1)

            @block.vector
            def _(dve):
                v = nc.vector
                link = Chain(dve, chain)
                norm.vector(dve, link)
                dve.wait_ge(b1_loaded, 16 * NPART)
                link(v.tensor_copy(b1_parts[:, :], b1[:, :]))
                link(v.tensor_tensor(b1_rest[:, :], b1[:, :], b1_parts[:, :], ALU.subtract))
                link(v.tensor_copy(part[:, :], b1_rest[:, :]))
                link(v.tensor_tensor(b1_rest[:, :], b1_rest[:, :], part[:, :], ALU.subtract))
                link(v.tensor_copy(b1_parts[STEP:2 * STEP, :], part[STEP:2 * STEP, :]))
                link(v.tensor_copy(b1_parts[2 * STEP:, :], b1_rest[2 * STEP:, :]))
                dve.wait_ge(w_loaded, 16 * len(loads))
                dve.wait_ge(drawn, 4 + E)
                dve.wait_ge(lg_psum, 1)
                link(v.tensor_copy(lg[:, :, :], ps[:, 5, 0:NT * E].rearrange("p (t e) -> p t e", e=E)))
                top_choice(c, v, link, lg[:, :, :], best[:, :], tie[:, :], order[:, :], choice[:, :, :], E)
                v.tensor_copy(choice3[:, :, :, 0:E], choice[:, :, :].unsqueeze(2).to_broadcast([P, NT, NPART, E])).then_inc(choice_ready, 1)
                dve.wait_ge(norm.nT_psum, NC)
                link(v.tensor_tensor(c.n[:, :, :], c.n[:, :, :], b_out[:, :].unsqueeze(1).to_broadcast([P, NT, P]), ALU.add))

        mask_psum, own_ready, mid_psum, gelu_done, y_psum, y_added = (c.sem(n) for n in (
            "mask_psum", "own_ready", "mid_psum", "gelu_done", "y_psum", "y_added"))
        var_ready, std_ready, x_ready, x_stored, f_chain = (c.sem(n) for n in ("var_ready", "std_ready", "x_ready", "x_stored", "f_chain"))
        with nc.Block() as block:
            @block.sync
            def _(sp):
                for k in range(NC):
                    sp.wait_ge(x_ready, k + 1)
                    sp.dma_start(out[0, k * 512:(k + 1) * 512].rearrange("(t p) d -> p t d", p=P), c.x[:, 4 * k:4 * k + 4, :]).then_inc(x_stored, 16)
                sp.wait_ge(x_stored, 16 * NC)

            @block.tensor
            def _(pe):
                def masks(k, experts):
                    for e in experts:
                        m = k * E + e
                        if m >= 2:
                            pe.wait_ge(own_ready, m - 1)
                        nc.tensor.matmul(ps[:, 6 + m % 2, :], pick[:, e, :], hot[:, k * 512:(k + 1) * 512], start=True, stop=True).then_inc(mask_psum, 1)

                def up(k, f):
                    if k > 0:
                        pe.wait_ge(gelu_done, (k - 1) * F + f + 1)
                    for e in range(E):
                        if f == 0:
                            pe.wait_ge(own_ready, k * E + e + 1)
                        nc.tensor.matmul(ps[:, f, :], w1[:, e, f * P:(f + 1) * P], own[:, k % 2, e, :], start=e == 0, stop=False)
                    nc.tensor.matmul(ps[:, f, :], b1_parts[:, f * P:(f + 1) * P], hot[:, k * 512:(k + 1) * 512],
                                     start=False, stop=True).then_inc(mid_psum, 1)

                def down(k):
                    pe.wait_ge(gelu_done, (k + 1) * F)
                    if k >= 2:
                        pe.wait_ge(y_added, k - 1)
                    for t in range(4):
                        for f in range(F):
                            last = nc.tensor.matmul(ps[:, 4 + k % 2, t * P:(t + 1) * P], mid[:, k % 2, f, t * P:(t + 1) * P],
                                                    w2[:, f, :], start=f == 0, stop=f == F - 1)
                    last.then_inc(y_psum, 1)

                masks(0, range(E))
                for k in range(NC):
                    for f in range(F):
                        up(k, f)
                        if f >= 2 and k + 1 < NC:
                            masks(k + 1, (2 * f - 4, 2 * f - 3))
                        if f == 0 and k > 0:
                            down(k - 1)
                down(NC - 1)

            @block.scalar
            def _(act):
                def std(k):
                    act.wait_ge(var_ready, k + 1)
                    sl = slice(4 * k, 4 * k + 4)
                    nc.scalar.activation(c.std[:, sl], c.var[:, sl], ACT.Sqrt).then_inc(std_ready, 1)

                for k in range(NC):
                    if k >= 2:
                        act.wait_ge(y_psum, k - 1)
                    for f in range(F):
                        act.wait_ge(mid_psum, k * F + f + 1)
                        nc.scalar.activation(mid[:, k % 2, f, :], ps[:, f, :], ACT.Gelu).then_inc(gelu_done, 1)
                        if f == 1 and k > 0:
                            std(k - 1)
                std(NC - 1)

            @block.vector
            def _(dve):
                v = nc.vector
                link = Chain(dve, f_chain)

                def own_n(k):
                    for e in range(E):
                        dve.wait_ge(mask_psum, k * E + e + 1)
                        if k >= 2 and e == 0:
                            dve.wait_ge(mid_psum, (k - 1) * F)
                        v.tensor_tensor(own[:, k % 2, e, :], c.nT[:, k * 512:(k + 1) * 512], ps[:, 6 + (k * E + e) % 2, :], ALU.mult).then_inc(own_ready, 1)

                def finish(k):
                    sl, tiles = slice(4 * k, 4 * k + 4), range(4 * k, 4 * k + 4)
                    dve.wait_ge(y_psum, k + 1)
                    v.tensor_tensor(c.n[:, sl, :], c.n[:, sl, :], ps[:, 4 + k % 2, :].rearrange("p (t d) -> p t d", t=4), ALU.add).then_inc(y_added, 1)
                    dve.wait_ge(y_added, k + 1)
                    for t in tiles:
                        last = v.bn_stats(c.moments[:, t, :], c.n[:, t, :])
                    link(last)
                    for t in tiles:
                        last = v.bn_aggr(c.mean_var[:, t, :], c.moments[:, t, :])
                    link(last)
                    v.tensor_scalar(c.var[:, sl], c.mean_var[:, sl, 1], 1e-12, None, ALU.add).then_inc(var_ready, 1)
                    for t in tiles:
                        last = v.scalar_tensor_tensor(c.a[:, t, :], c.n[:, t, :], c.mean_var[:, t, 0:1], gamma[:, :], ALU.subtract, ALU.mult)
                    link(last)
                    dve.wait_ge(std_ready, k + 1)
                    link(v.reciprocal(c.rstd[:, sl], c.std[:, sl]))
                    for t in tiles:
                        last = v.scalar_tensor_tensor(c.x[:, t, :], c.a[:, t, :], c.rstd[:, t:t + 1], c.x[:, t, :], ALU.mult, ALU.add)
                    last.then_inc(x_ready, 1)

                own_n(0)
                link(v.tensor_tensor(c.x[:, :, :], c.x[:, :, :], beta[:, :].unsqueeze(1).to_broadcast([P, NT, P]), ALU.add))
                for k in range(1, NC):
                    own_n(k)
                    finish(k - 1)
                finish(NC - 1)


def build(nc, ins, out):
    with ExitStack() as ctx:
        c = Core(nc, ctx)
        constants(c, ins)
        with ExitStack() as actx:
            at = Attention(c, actx)
            c.layer = "l0a_"
            l0_attention(c, at, ins, AttentionConstants(c, at, 1))
            c.end_sublayer()
            l0_ffn(c, at, ins)
            c.end_sublayer()
        l1_mamba(c, ins)
        c.end_sublayer()
        l1_ternary(c, ins)
        l2_performer(c, ins)
        c.end_sublayer()
        with ExitStack() as actx:
            c.layer = "l2f_"
            at = Attention(c, actx)
            l2_ffn(c, at, ins, AttentionConstants(c, at, 2))
            c.end_sublayer()
        l3_state(c, ins)
        l3_ffn(c, ins, out)


_INS = [
    'L0_attn_x', 'L0_attn_ln_gamma', 'L0_attn_ln_beta', 'L0_attn_w_qkv', 'L0_attn_b_qkv', 'L0_attn_w_out',
    'L0_attn_b_out', 'L0_ffn_ln1_g', 'L0_ffn_ln1_b', 'L0_ffn_ln2_g', 'L0_ffn_ln2_b', 'L0_ffn_Wq', 'L0_ffn_bq',
    'L0_ffn_Wk', 'L0_ffn_bk', 'L0_ffn_Wv', 'L0_ffn_bv', 'L0_ffn_Wo', 'L0_ffn_bo', 'L0_ffn_Wr', 'L0_ffn_br',
    'L0_ffn_e_w1', 'L0_ffn_e_b1', 'L0_ffn_e_w2', 'L0_ffn_e_b2', 'L1_attn_W_in', 'L1_attn_conv_w', 'L1_attn_conv_b',
    'L1_attn_W_x', 'L1_attn_W_dt', 'L1_attn_b_dt', 'L1_attn_A_log', 'L1_attn_D', 'L1_attn_W_out', 'L1_ffn_weight',
    'L1_ffn_alpha', 'L1_ffn_bias', 'L2_attn_Wq', 'L2_attn_bq', 'L2_attn_Wk', 'L2_attn_bk', 'L2_attn_Wv', 'L2_attn_bv',
    'L2_attn_Wo', 'L2_attn_bo', 'L2_attn_orf', 'L2_ffn_rW1', 'L2_ffn_rb1', 'L2_ffn_ln_g', 'L2_ffn_ln_b', 'L2_ffn_rW2',
    'L2_ffn_rb2', 'L2_ffn_qW', 'L2_ffn_qb', 'L2_ffn_kW', 'L2_ffn_kb', 'L2_ffn_vW', 'L2_ffn_vb', 'L2_ffn_oW',
    'L2_ffn_ob', 'L3_attn_conv_w', 'L3_attn_conv_b', 'L3_attn_Wp', 'L3_attn_bp', 'L3_attn_Ws', 'L3_attn_bs',
    'L3_attn_A_log', 'L3_attn_dt_log', 'L3_attn_Wo', 'L3_attn_bo', 'L3_ffn_W_router', 'L3_ffn_W1', 'L3_ffn_b1',
    'L3_ffn_Wo', 'L3_ffn_bo', 'L3_ffn_ln_gamma', 'L3_ffn_ln_beta']
_OUTS = [((1, 2048, 128), 'float32')]


def kernel(**inputs):
    import numpy as _np
    import concourse.bacc as _bacc
    from concourse import mybir as _mybir
    from concourse.bass_utils import run_bass_kernel_spmd as _run

    nc = _bacc.Bacc("TRN2", target_bir_lowering=False, num_devices=1)
    arrays, ins = {}, {}
    for name in _INS:
        a = _np.ascontiguousarray(inputs[name])
        arrays[f"in_{name}_dram"] = a
        ins[name] = nc.dram_tensor(f"in_{name}_dram", a.shape, _mybir.dt.from_np(a.dtype), kind="ExternalInput").ap()
    outs = []
    for i, (shape, dtype) in enumerate(_OUTS):
        dt = _mybir.dt.from_np(_np.dtype(dtype))
        outs.append(nc.dram_tensor(f"out_{i}_dram", shape, dt, kind="ExternalOutput").ap())
    build(nc, ins, outs[0])
    r = _run(nc, [arrays], core_ids=[0])
    return r.results[0]["out_0_dram"]
```
